# Optimizing a Trainium2 kernel written in Bass

```python
import numpy as np
import jax
import jax.numpy as jnp

def _softmax(x, axis=-1):
    return jax.nn.softmax(x, axis=axis)

def _gelu(x):
    return jax.nn.gelu(x, approximate=True)

def _silu(x):
    return jax.nn.silu(x)

def _sigmoid(x):
    return jax.nn.sigmoid(x)

def _layernorm(x, axis=-1, eps=1e-05):
    m = jnp.mean(x, axis=axis, keepdims=True)
    v = jnp.var(x, axis=axis, keepdims=True)
    return (x - m) / jnp.sqrt(v + eps)

def _scatter_add(tgt, idx, src, axis=0):
    return tgt.at[idx].add(src)

def _segment_sum(src, seg, n):
    return jax.ops.segment_sum(src, seg, n)
kernel_name = 'mk_seq_preln_d4_jaxref_r8_d75673'

def setup_inputs(seed: int=0):
    np.random.seed(seed)
    _w = jnp.asarray

    def _L0_attn_setup():
        import jax, jax.numpy as jnp
        import numpy as np
        D_MODEL = 128
        EXPAND = 2
        INNER = D_MODEL * EXPAND
        D_STATE = 64
        D_CONV = 3
        LN_EPS = 1e-05

        def _layernorm(x, gamma, beta):
            mu = jnp.mean(x, axis=-1, keepdims=True)
            var = jnp.mean(jnp.square(x - mu), axis=-1, keepdims=True)
            return (x - mu) * jax.lax.rsqrt(var + LN_EPS) * gamma + beta

        def _depthwise_conv(u, conv_w, conv_b):
            lhs = jnp.transpose(u, (0, 2, 1))
            out = jax.lax.conv_general_dilated(lhs, conv_w, window_strides=(1,), padding=[(D_CONV // 2, D_CONV // 2)], feature_group_count=INNER, dimension_numbers=('NCH', 'OIH', 'NCH'))
            out = out + conv_b[None, :, None]
            return jnp.transpose(out, (0, 2, 1))
        key = jax.random.key(seed)
        ks = jax.random.split(key, 8)
        B, L = (1, 128)
        x = jax.random.normal(ks[0], (B, L, D_MODEL), dtype=jnp.float32)
        return {'x': x, 'norm_gamma': jnp.ones((D_MODEL,), jnp.float32), 'norm_beta': jnp.zeros((D_MODEL,), jnp.float32), 'in_w': jax.random.normal(ks[1], (D_MODEL, 3 * INNER), jnp.float32) * 0.02, 'in_b': jnp.zeros((3 * INNER,), jnp.float32), 'conv_w': jax.random.normal(ks[2], (INNER, 1, D_CONV), jnp.float32) * 0.1, 'conv_b': jnp.zeros((INNER,), jnp.float32), 'A_log': jax.random.normal(ks[3], (INNER, D_STATE), jnp.float32) * 0.02, 'B_p': jax.random.normal(ks[4], (INNER, D_STATE), jnp.float32) * 0.02, 'C_p': jax.random.normal(ks[5], (INNER, D_STATE), jnp.float32) * 0.02, 'D_p': jnp.zeros((INNER,), jnp.float32), 'out_w': jax.random.normal(ks[6], (INNER, D_MODEL), jnp.float32) * 0.02, 'out_b': jnp.zeros((D_MODEL,), jnp.float32)}
    _L0_attn_in = _L0_attn_setup()

    def _L0_ffn_setup():
        import jax, jax.numpy as jnp
        import numpy as np
        B, S, D = (4, 512, 128)
        E, F_EXP = (16, 256)
        F_C = 2.0
        F_SH = 256
        key = jax.random.key(seed)
        ks = jax.random.split(key, 8)
        s = 0.02
        return {'hidden_states': jax.random.normal(ks[0], (B, S, D), jnp.float32), 'gate_w': jax.random.normal(ks[1], (E, D), jnp.float32) * s, 'Wg': jax.random.normal(ks[2], (E, F_EXP, D), jnp.float32) * s, 'Wu': jax.random.normal(ks[3], (E, F_EXP, D), jnp.float32) * s, 'Wd': jax.random.normal(ks[4], (E, D, F_EXP), jnp.float32) * s, 'Ws_g': jax.random.normal(ks[5], (F_SH, D), jnp.float32) * s, 'Ws_u': jax.random.normal(ks[6], (F_SH, D), jnp.float32) * s, 'Ws_d': jax.random.normal(ks[7], (D, F_SH), jnp.float32) * s}
    _L0_ffn_in = _L0_ffn_setup()

    def _L1_attn_setup():
        import jax, jax.numpy as jnp
        import numpy as np
        D_MODEL = 128
        LN_EPS = 1e-05
        DEN_EPS = 1e-06

        def _layer_norm(x, g, b):
            mu = jnp.mean(x, axis=-1, keepdims=True)
            var = jnp.mean(jnp.square(x - mu), axis=-1, keepdims=True)
            return (x - mu) * jax.lax.rsqrt(var + LN_EPS) * g + b
        key = jax.random.key(seed)
        ks = jax.random.split(key, 7)
        s = 1.0 / np.sqrt(D_MODEL)
        x = jax.random.normal(ks[0], (4, 256, D_MODEL), dtype=jnp.float32)
        qkv_w = jax.random.uniform(ks[1], (D_MODEL, 3 * D_MODEL), jnp.float32, -s, s)
        qkv_b = jax.random.uniform(ks[2], (3 * D_MODEL,), jnp.float32, -s, s)
        gate_w = jax.random.uniform(ks[3], (D_MODEL, D_MODEL), jnp.float32, -s, s)
        gate_b = jax.random.uniform(ks[4], (D_MODEL,), jnp.float32, -s, s)
        ln_g = jnp.ones((D_MODEL,), jnp.float32)
        ln_b = jnp.zeros((D_MODEL,), jnp.float32)
        return {'x': x, 'qkv_w': qkv_w, 'qkv_b': qkv_b, 'gate_w': gate_w, 'gate_b': gate_b, 'ln_g': ln_g, 'ln_b': ln_b}
    _L1_attn_in = _L1_attn_setup()

    def _L1_ffn_setup():
        import jax, jax.numpy as jnp
        import numpy as np
        B, S, DIM = (4, 256, 128)
        E, K, HID = (8, 2, 512)
        key = jax.random.key(seed)
        ks = jax.random.split(key, 8)
        init = lambda k, sh: jax.random.normal(k, sh, jnp.float32) * 0.02
        return {'x': jax.random.normal(ks[0], (B, S, DIM), jnp.float32), 'gate_w': init(ks[1], (DIM, E)), 'gate_b': jnp.zeros((E,), jnp.float32), 'w1': init(ks[2], (E, DIM, HID)), 'b1': jnp.zeros((E, HID), jnp.float32), 'w2': init(ks[3], (E, HID, DIM)), 'b2': jnp.zeros((E, DIM), jnp.float32), 'ws1': init(ks[4], (DIM, HID)), 'bs1': jnp.zeros((HID,), jnp.float32), 'ws2': init(ks[5], (HID, DIM)), 'bs2': jnp.zeros((DIM,), jnp.float32)}
    _L1_ffn_in = _L1_ffn_setup()

    def _L2_attn_setup():
        import math
        import jax, jax.numpy as jnp
        import numpy as np
        D_MODEL = 128
        N_HEADS = 16
        D_K = D_MODEL // N_HEADS
        D_C = 32
        B, S = (2, 256)
        key = jax.random.key(seed)
        ks = jax.random.split(key, 7)
        sd = lambda fan_in: 1.0 / math.sqrt(fan_in)
        return {'x': jax.random.normal(ks[0], (B, S, D_MODEL), dtype=jnp.float32), 'W_dq': jax.random.uniform(ks[1], (D_MODEL, D_C), minval=-sd(D_MODEL), maxval=sd(D_MODEL), dtype=jnp.float32), 'W_uq': jax.random.uniform(ks[2], (D_C, N_HEADS * D_K), minval=-sd(D_C), maxval=sd(D_C), dtype=jnp.float32), 'W_dkv': jax.random.uniform(ks[3], (D_MODEL, D_C), minval=-sd(D_MODEL), maxval=sd(D_MODEL), dtype=jnp.float32), 'W_uk': jax.random.uniform(ks[4], (D_C, N_HEADS * D_K), minval=-sd(D_C), maxval=sd(D_C), dtype=jnp.float32), 'W_uv': jax.random.uniform(ks[5], (D_C, N_HEADS * D_K), minval=-sd(D_C), maxval=sd(D_C), dtype=jnp.float32), 'W_o': jax.random.uniform(ks[6], (N_HEADS * D_K, D_MODEL), minval=-sd(N_HEADS * D_K), maxval=sd(N_HEADS * D_K), dtype=jnp.float32)}
    _L2_attn_in = _L2_attn_setup()

    def _L2_ffn_setup():
        import jax, jax.numpy as jnp
        import numpy as np
        B, S, D = (8, 512, 128)
        E, R, K = (6, 16, 2)
        key = jax.random.key(seed)
        ks = jax.random.split(key, 9)
        sc = 0.02
        return {'x': jax.random.normal(ks[0], (B, S, D), jnp.float32), 'base_W': jax.random.normal(ks[1], (D, D), jnp.float32) * sc, 'base_b': jax.random.normal(ks[2], (D,), jnp.float32) * sc, 'shared_A': jax.random.normal(ks[3], (R, D), jnp.float32) * sc, 'shared_B': jax.random.normal(ks[4], (D, R), jnp.float32) * sc, 'routed_A': jax.random.normal(ks[5], (E, R, D), jnp.float32) * sc, 'routed_B': jax.random.normal(ks[6], (E, D, R), jnp.float32) * sc, 'router_W': jax.random.normal(ks[7], (E, D), jnp.float32) * sc, 'router_b': jax.random.normal(ks[8], (E,), jnp.float32) * sc}
    _L2_ffn_in = _L2_ffn_setup()

    def _L3_attn_setup():
        import jax, jax.numpy as jnp
        import numpy as np
        DIM = 128
        BATCH = 4
        SEQ = 512
        key = jax.random.key(seed)
        ks = jax.random.split(key, 5)
        s = 1.0 / np.sqrt(DIM)
        x = jax.random.normal(ks[0], (BATCH, SEQ, DIM), dtype=jnp.float32)
        W_in = jax.random.uniform(ks[1], (DIM, DIM), jnp.float32, -s, s)
        b_in = jax.random.uniform(ks[2], (DIM,), jnp.float32, -s, s)
        W_out = jax.random.uniform(ks[3], (DIM, DIM), jnp.float32, -s, s)
        b_out = jax.random.uniform(ks[4], (DIM,), jnp.float32, -s, s)
        decay = jnp.float32(0.25)
        mix = jnp.float32(0.5)
        return {'x': x, 'W_in': W_in, 'b_in': b_in, 'W_out': W_out, 'b_out': b_out, 'decay': decay, 'mix': mix}
    _L3_attn_in = _L3_attn_setup()

    def _L3_ffn_setup():
        import jax, jax.numpy as jnp
        import numpy as np
        NHEAD = 16
        NUM_GROUPS = 4
        EXPERTS_PER_GROUP = 2
        LN_EPS = 1e-05

        def _layernorm(x, g, b):
            mu = jnp.mean(x, axis=-1, keepdims=True)
            var = jnp.mean(jnp.square(x - mu), axis=-1, keepdims=True)
            return (x - mu) * jax.lax.rsqrt(var + LN_EPS) * g + b

        def _mha(x, wi, bi, wo, bo):
            B, S, D = x.shape
            hd = D // NHEAD
            qkv = x @ wi.T + bi
            q, k, v = jnp.split(qkv, 3, axis=-1)

            def heads(t):
                return t.reshape(B, S, NHEAD, hd).transpose(0, 2, 1, 3)
            q, k, v = (heads(q), heads(k), heads(v))
            scores = jnp.einsum('bhqd,bhkd->bhqk', q, k) / jnp.sqrt(jnp.asarray(hd, x.dtype))
            attn = jax.nn.softmax(scores, axis=-1)
            o = jnp.einsum('bhqk,bhkd->bhqd', attn, v)
            o = o.transpose(0, 2, 1, 3).reshape(B, S, D)
            return o @ wo.T + bo

        def _hier_moe(x, w_group, b_group, w_expert, b_expert, w1, b1, w2, b2):
            B, S, D = x.shape
            xt = x.reshape(B * S, D)
            T = xt.shape[0]
            E = NUM_GROUPS * EXPERTS_PER_GROUP
            gp = jax.nn.softmax(xt @ w_group + b_group, axis=-1)
            g_idx = jnp.argmax(gp, axis=-1)
            g_prob = jnp.max(gp, axis=-1)
            elog = jnp.einsum('td,gde->tge', xt, w_expert) + b_expert
            ep = jax.nn.softmax(elog, axis=-1)
            ep_sel = jnp.take_along_axis(ep, g_idx[:, None, None], axis=1)[:, 0, :]
            e_idx_local = jnp.argmax(ep_sel, axis=-1)
            e_prob = jnp.max(ep_sel, axis=-1)
            flat_e = g_idx * EXPERTS_PER_GROUP + e_idx_local
            combine = jax.nn.one_hot(flat_e, E, dtype=xt.dtype) * (g_prob * e_prob)[:, None]
            h = jax.nn.relu(jnp.einsum('td,edf->etf', xt, w1) + b1[:, None, :])
            y = jnp.einsum('etf,efd->etd', h, w2) + b2[:, None, :]
            out = jnp.einsum('te,etd->td', combine, y)
            return out.reshape(B, S, D)
        key = jax.random.key(seed)
        ks = jax.random.split(key, 8)
        B, S, D, F = (2, 128, 128, 256)
        G, Epg = (NUM_GROUPS, EXPERTS_PER_GROUP)
        E = G * Epg
        sc = lambda fan: 1.0 / np.sqrt(fan)
        return {'x': jax.random.normal(ks[0], (B, S, D), jnp.float32), 'in_proj_w': jax.random.normal(ks[1], (3 * D, D), jnp.float32) * sc(D), 'in_proj_b': jnp.zeros((3 * D,), jnp.float32), 'out_proj_w': jax.random.normal(ks[2], (D, D), jnp.float32) * sc(D), 'out_proj_b': jnp.zeros((D,), jnp.float32), 'ln1_g': jnp.ones((D,), jnp.float32), 'ln1_b': jnp.zeros((D,), jnp.float32), 'ln2_g': jnp.ones((D,), jnp.float32), 'ln2_b': jnp.zeros((D,), jnp.float32), 'w_group': jax.random.normal(ks[3], (D, G), jnp.float32) * sc(D), 'b_group': jnp.zeros((G,), jnp.float32), 'w_expert': jax.random.normal(ks[4], (G, D, Epg), jnp.float32) * sc(D), 'b_expert': jnp.zeros((G, Epg), jnp.float32), 'w1': jax.random.normal(ks[5], (E, D, F), jnp.float32) * sc(D), 'b1': jnp.zeros((E, F), jnp.float32), 'w2': jax.random.normal(ks[6], (E, F, D), jnp.float32) * sc(F), 'b2': jnp.zeros((E, D), jnp.float32)}
    _L3_ffn_in = _L3_ffn_setup()
    _d = {'L0_attn_x': _L0_attn_in['x'], 'L0_attn_norm_gamma': _L0_attn_in['norm_gamma'], 'L0_attn_norm_beta': _L0_attn_in['norm_beta'], 'L0_attn_in_w': _L0_attn_in['in_w'], 'L0_attn_in_b': _L0_attn_in['in_b'], 'L0_attn_conv_w': _L0_attn_in['conv_w'], 'L0_attn_conv_b': _L0_attn_in['conv_b'], 'L0_attn_A_log': _L0_attn_in['A_log'], 'L0_attn_B_p': _L0_attn_in['B_p'], 'L0_attn_C_p': _L0_attn_in['C_p'], 'L0_attn_D_p': _L0_attn_in['D_p'], 'L0_attn_out_w': _L0_attn_in['out_w'], 'L0_attn_out_b': _L0_attn_in['out_b'], 'L0_ffn_gate_w': _L0_ffn_in['gate_w'], 'L0_ffn_Wg': _L0_ffn_in['Wg'], 'L0_ffn_Wu': _L0_ffn_in['Wu'], 'L0_ffn_Wd': _L0_ffn_in['Wd'], 'L0_ffn_Ws_g': _L0_ffn_in['Ws_g'], 'L0_ffn_Ws_u': _L0_ffn_in['Ws_u'], 'L0_ffn_Ws_d': _L0_ffn_in['Ws_d'], 'L1_attn_qkv_w': _L1_attn_in['qkv_w'], 'L1_attn_qkv_b': _L1_attn_in['qkv_b'], 'L1_attn_gate_w': _L1_attn_in['gate_w'], 'L1_attn_gate_b': _L1_attn_in['gate_b'], 'L1_attn_ln_g': _L1_attn_in['ln_g'], 'L1_attn_ln_b': _L1_attn_in['ln_b'], 'L1_ffn_gate_w': _L1_ffn_in['gate_w'], 'L1_ffn_gate_b': _L1_ffn_in['gate_b'], 'L1_ffn_w1': _L1_ffn_in['w1'], 'L1_ffn_b1': _L1_ffn_in['b1'], 'L1_ffn_w2': _L1_ffn_in['w2'], 'L1_ffn_b2': _L1_ffn_in['b2'], 'L1_ffn_ws1': _L1_ffn_in['ws1'], 'L1_ffn_bs1': _L1_ffn_in['bs1'], 'L1_ffn_ws2': _L1_ffn_in['ws2'], 'L1_ffn_bs2': _L1_ffn_in['bs2'], 'L2_attn_W_dq': _L2_attn_in['W_dq'], 'L2_attn_W_uq': _L2_attn_in['W_uq'], 'L2_attn_W_dkv': _L2_attn_in['W_dkv'], 'L2_attn_W_uk': _L2_attn_in['W_uk'], 'L2_attn_W_uv': _L2_attn_in['W_uv'], 'L2_attn_W_o': _L2_attn_in['W_o'], 'L2_ffn_base_W': _L2_ffn_in['base_W'], 'L2_ffn_base_b': _L2_ffn_in['base_b'], 'L2_ffn_shared_A': _L2_ffn_in['shared_A'], 'L2_ffn_shared_B': _L2_ffn_in['shared_B'], 'L2_ffn_routed_A': _L2_ffn_in['routed_A'], 'L2_ffn_routed_B': _L2_ffn_in['routed_B'], 'L2_ffn_router_W': _L2_ffn_in['router_W'], 'L2_ffn_router_b': _L2_ffn_in['router_b'], 'L3_attn_W_in': _L3_attn_in['W_in'], 'L3_attn_b_in': _L3_attn_in['b_in'], 'L3_attn_W_out': _L3_attn_in['W_out'], 'L3_attn_b_out': _L3_attn_in['b_out'], 'L3_attn_decay': _L3_attn_in['decay'], 'L3_attn_mix': _L3_attn_in['mix'], 'L3_ffn_in_proj_w': _L3_ffn_in['in_proj_w'], 'L3_ffn_in_proj_b': _L3_ffn_in['in_proj_b'], 'L3_ffn_out_proj_w': _L3_ffn_in['out_proj_w'], 'L3_ffn_out_proj_b': _L3_ffn_in['out_proj_b'], 'L3_ffn_ln1_g': _L3_ffn_in['ln1_g'], 'L3_ffn_ln1_b': _L3_ffn_in['ln1_b'], 'L3_ffn_ln2_g': _L3_ffn_in['ln2_g'], 'L3_ffn_ln2_b': _L3_ffn_in['ln2_b'], 'L3_ffn_w_group': _L3_ffn_in['w_group'], 'L3_ffn_b_group': _L3_ffn_in['b_group'], 'L3_ffn_w_expert': _L3_ffn_in['w_expert'], 'L3_ffn_b_expert': _L3_ffn_in['b_expert'], 'L3_ffn_w1': _L3_ffn_in['w1'], 'L3_ffn_b1': _L3_ffn_in['b1'], 'L3_ffn_w2': _L3_ffn_in['w2'], 'L3_ffn_b2': _L3_ffn_in['b2']}
    _x0 = _d['L0_attn_x']
    _d['L0_attn_x'] = jax.random.normal(jax.random.fold_in(jax.random.key(seed), 1), (32, 256, 128), dtype=_x0.dtype)
    del _x0
    return _d

def reference(L0_attn_x, L0_attn_norm_gamma, L0_attn_norm_beta, L0_attn_in_w, L0_attn_in_b, L0_attn_conv_w, L0_attn_conv_b, L0_attn_A_log, L0_attn_B_p, L0_attn_C_p, L0_attn_D_p, L0_attn_out_w, L0_attn_out_b, L0_ffn_gate_w, L0_ffn_Wg, L0_ffn_Wu, L0_ffn_Wd, L0_ffn_Ws_g, L0_ffn_Ws_u, L0_ffn_Ws_d, L1_attn_qkv_w, L1_attn_qkv_b, L1_attn_gate_w, L1_attn_gate_b, L1_attn_ln_g, L1_attn_ln_b, L1_ffn_gate_w, L1_ffn_gate_b, L1_ffn_w1, L1_ffn_b1, L1_ffn_w2, L1_ffn_b2, L1_ffn_ws1, L1_ffn_bs1, L1_ffn_ws2, L1_ffn_bs2, L2_attn_W_dq, L2_attn_W_uq, L2_attn_W_dkv, L2_attn_W_uk, L2_attn_W_uv, L2_attn_W_o, L2_ffn_base_W, L2_ffn_base_b, L2_ffn_shared_A, L2_ffn_shared_B, L2_ffn_routed_A, L2_ffn_routed_B, L2_ffn_router_W, L2_ffn_router_b, L3_attn_W_in, L3_attn_b_in, L3_attn_W_out, L3_attn_b_out, L3_attn_decay, L3_attn_mix, L3_ffn_in_proj_w, L3_ffn_in_proj_b, L3_ffn_out_proj_w, L3_ffn_out_proj_b, L3_ffn_ln1_g, L3_ffn_ln1_b, L3_ffn_ln2_g, L3_ffn_ln2_b, L3_ffn_w_group, L3_ffn_b_group, L3_ffn_w_expert, L3_ffn_b_expert, L3_ffn_w1, L3_ffn_b1, L3_ffn_w2, L3_ffn_b2):

    def _L0_attn_ref(x, norm_gamma, norm_beta, in_w, in_b, conv_w, conv_b, A_log, B_p, C_p, D_p, out_w, out_b):
        import jax, jax.numpy as jnp
        import numpy as np
        D_MODEL = 128
        EXPAND = 2
        INNER = D_MODEL * EXPAND
        D_STATE = 64
        D_CONV = 3
        LN_EPS = 1e-05

        def _layernorm(x, gamma, beta):
            mu = jnp.mean(x, axis=-1, keepdims=True)
            var = jnp.mean(jnp.square(x - mu), axis=-1, keepdims=True)
            return (x - mu) * jax.lax.rsqrt(var + LN_EPS) * gamma + beta

        def _depthwise_conv(u, conv_w, conv_b):
            lhs = jnp.transpose(u, (0, 2, 1))
            out = jax.lax.conv_general_dilated(lhs, conv_w, window_strides=(1,), padding=[(D_CONV // 2, D_CONV // 2)], feature_group_count=INNER, dimension_numbers=('NCH', 'OIH', 'NCH'))
            out = out + conv_b[None, :, None]
            return jnp.transpose(out, (0, 2, 1))
        residual = x
        h = _layernorm(x, norm_gamma, norm_beta)
        uvg = h @ in_w + in_b
        u, v, g = jnp.split(uvg, 3, axis=-1)
        u = jax.nn.silu(_depthwise_conv(u, conv_w, conv_b))
        eA = jnp.exp(-jnp.exp(A_log))

        def step(s, ut):
            s = s * eA[None] + ut[..., None] * B_p[None]
            yt = jnp.sum(s * C_p[None], axis=-1) + ut * D_p[None]
            return (s, yt)
        B_, L_, _ = u.shape
        s0 = jnp.zeros((B_, INNER, D_STATE), u.dtype)
        _, ys = jax.lax.scan(step, s0, jnp.transpose(u, (1, 0, 2)))
        y = jnp.transpose(ys, (1, 0, 2))
        y = y * jax.nn.sigmoid(g) + jax.nn.silu(v)
        y = y @ out_w + out_b
        return residual + y

    def _L0_ffn_ref(hidden_states, gate_w, Wg, Wu, Wd, Ws_g, Ws_u, Ws_d):
        import jax, jax.numpy as jnp
        import numpy as np
        B, S, D = (4, 512, 128)
        E, F_EXP = (16, 256)
        F_C = 2.0
        F_SH = 256
        b, s, d = hidden_states.shape
        e = gate_w.shape[0]
        cap = int(s * F_C / e)
        logits = jnp.einsum('bsd,ed->bse', hidden_states, gate_w)
        scores = jax.nn.softmax(logits, axis=-1).transpose(0, 2, 1)
        topk_w, topk_idx = jax.lax.top_k(scores, cap)
        x_tok = jnp.take_along_axis(hidden_states[:, None, :, :], topk_idx[..., None], axis=2)
        g = jnp.einsum('becd,efd->becf', x_tok, Wg)
        u = jnp.einsum('becd,efd->becf', x_tok, Wu)
        h = jax.nn.gelu(g, approximate=False) * u
        eo = jnp.einsum('becf,edf->becd', h, Wd) * topk_w[..., None]
        offs = (jnp.arange(b) * s)[:, None, None]
        flat_idx = (topk_idx + offs).reshape(-1)
        flat = jnp.zeros((b * s, d), hidden_states.dtype)
        flat = flat.at[flat_idx].add(eo.reshape(-1, d))
        out = flat.reshape(b, s, d)
        gs = jnp.einsum('bsd,fd->bsf', hidden_states, Ws_g)
        us = jnp.einsum('bsd,fd->bsf', hidden_states, Ws_u)
        shared = jnp.einsum('bsf,df->bsd', jax.nn.gelu(gs, approximate=False) * us, Ws_d)
        return out + shared

    def _L1_attn_ref(x, qkv_w, qkv_b, gate_w, gate_b, ln_g, ln_b):
        import jax, jax.numpy as jnp
        import numpy as np
        D_MODEL = 128
        LN_EPS = 1e-05
        DEN_EPS = 1e-06

        def _layer_norm(x, g, b):
            mu = jnp.mean(x, axis=-1, keepdims=True)
            var = jnp.mean(jnp.square(x - mu), axis=-1, keepdims=True)
            return (x - mu) * jax.lax.rsqrt(var + LN_EPS) * g + b
        B, T, D = x.shape
        xn = _layer_norm(x, ln_g, ln_b)
        qkv = xn @ qkv_w + qkv_b
        q, k, v = jnp.split(qkv, 3, axis=-1)
        gate = jax.nn.sigmoid(xn @ gate_w + gate_b)
        k = k * gate
        q = jax.nn.elu(q) + 1.0
        k = jax.nn.elu(k) + 1.0
        attn = jnp.einsum('btd,bsd->bts', q, k)
        mask = jnp.tril(jnp.ones((T, T), dtype=attn.dtype))
        attn = attn * mask
        out_num = jnp.einsum('bts,bsd->btd', attn, v)
        k_cumsum = jnp.cumsum(k, axis=1)
        out_den = jnp.sum(q * k_cumsum, axis=-1, keepdims=True) + DEN_EPS
        return out_num / out_den

    def _L1_ffn_ref(x, gate_w, gate_b, w1, b1, w2, b2, ws1, bs1, ws2, bs2):
        import jax, jax.numpy as jnp
        import numpy as np
        B, S, DIM = (4, 256, 128)
        E, K, HID = (8, 2, 512)
        orig_shape = x.shape
        xf = x.reshape(-1, DIM)
        logits = xf @ gate_w + gate_b
        top_w, top_i = jax.lax.top_k(logits, K)
        gw = jax.nn.softmax(top_w, axis=-1).astype(xf.dtype)
        combine = (gw[:, :, None] * jax.nn.one_hot(top_i, E, dtype=xf.dtype)).sum(axis=1)
        out = jnp.zeros_like(xf)
        for e in range(E):
            h = jax.nn.gelu(xf @ w1[e] + b1[e], approximate=False)
            out = out + combine[:, e:e + 1] * (h @ w2[e] + b2[e])
        shared = jax.nn.gelu(xf @ ws1 + bs1, approximate=False) @ ws2 + bs2
        return (out + shared).reshape(orig_shape)

    def _L2_attn_ref(x, W_dq, W_uq, W_dkv, W_uk, W_uv, W_o):
        import math
        import jax, jax.numpy as jnp
        import numpy as np
        D_MODEL = 128
        N_HEADS = 16
        D_K = D_MODEL // N_HEADS
        D_C = 32
        B, S = (2, 256)
        Bx, Sx, _ = x.shape
        c_q = x @ W_dq
        Q = (c_q @ W_uq).reshape(Bx, Sx, N_HEADS, D_K)
        c_kv = x @ W_dkv
        K = (c_kv @ W_uk).reshape(Bx, Sx, N_HEADS, D_K)
        V = (c_kv @ W_uv).reshape(Bx, Sx, N_HEADS, D_K)
        scores = jnp.einsum('bqhd,bkhd->bhqk', Q, K) / math.sqrt(D_K)
        causal = jnp.tril(jnp.ones((Sx, Sx), dtype=bool))
        scores = jnp.where(causal, scores, -jnp.inf)
        attn = jax.nn.softmax(scores, axis=-1)
        out = jnp.einsum('bhqk,bkhd->bqhd', attn, V).reshape(Bx, Sx, N_HEADS * D_K)
        return out @ W_o

    def _L2_ffn_ref(x, base_W, base_b, shared_A, shared_B, routed_A, routed_B, router_W, router_b):
        import jax, jax.numpy as jnp
        import numpy as np
        B, S, D = (8, 512, 128)
        E, R, K = (6, 16, 2)
        base_out = jax.lax.stop_gradient(jnp.einsum('bsi,oi->bso', x, base_W) + base_b)
        shared_out = jnp.einsum('bsr,or->bso', jnp.einsum('bsi,ri->bsr', x, shared_A), shared_B)
        logits = jnp.einsum('bsi,ei->bse', x, router_W) + router_b
        gate = jax.nn.softmax(logits, axis=-1)
        topk_w, topk_i = jax.lax.top_k(gate, K)
        sparse_w = jnp.sum(jax.nn.one_hot(topk_i, E, dtype=gate.dtype) * topk_w[..., None], axis=-2)
        sparse_w = sparse_w / (jnp.sum(sparse_w, axis=-1, keepdims=True) + 1e-06)
        h = jnp.einsum('bsi,eri->bser', x, routed_A)
        routed_outs = jnp.einsum('bser,eor->bseo', h, routed_B)
        routed_out = jnp.einsum('bseo,bse->bso', routed_outs, sparse_w)
        return base_out + shared_out + routed_out

    def _L3_attn_ref(x, W_in, b_in, W_out, b_out, decay, mix):
        import jax, jax.numpy as jnp
        import numpy as np
        DIM = 128
        BATCH = 4
        SEQ = 512
        shifted = jnp.pad(x, ((0, 0), (1, 0), (0, 0)))[:, :-1]
        inp = mix * x + (1.0 - mix) * shifted
        h = jax.nn.relu(jnp.einsum('bsd,ed->bse', inp, W_in) + b_in)

        def step(state, h_t):
            state = state * decay + h_t
            return (state, state)
        h_t_major = jnp.swapaxes(h, 0, 1)
        _, states = jax.lax.scan(step, jnp.zeros((x.shape[0], x.shape[2]), x.dtype), h_t_major)
        states = jnp.swapaxes(states, 0, 1)
        return jnp.einsum('bsd,ed->bse', states, W_out) + b_out

    def _L3_ffn_ref(x, in_proj_w, in_proj_b, out_proj_w, out_proj_b, ln1_g, ln1_b, ln2_g, ln2_b, w_group, b_group, w_expert, b_expert, w1, b1, w2, b2):
        import jax, jax.numpy as jnp
        import numpy as np
        NHEAD = 16
        NUM_GROUPS = 4
        EXPERTS_PER_GROUP = 2
        LN_EPS = 1e-05

        def _layernorm(x, g, b):
            mu = jnp.mean(x, axis=-1, keepdims=True)
            var = jnp.mean(jnp.square(x - mu), axis=-1, keepdims=True)
            return (x - mu) * jax.lax.rsqrt(var + LN_EPS) * g + b

        def _mha(x, wi, bi, wo, bo):
            B, S, D = x.shape
            hd = D // NHEAD
            qkv = x @ wi.T + bi
            q, k, v = jnp.split(qkv, 3, axis=-1)

            def heads(t):
                return t.reshape(B, S, NHEAD, hd).transpose(0, 2, 1, 3)
            q, k, v = (heads(q), heads(k), heads(v))
            scores = jnp.einsum('bhqd,bhkd->bhqk', q, k) / jnp.sqrt(jnp.asarray(hd, x.dtype))
            attn = jax.nn.softmax(scores, axis=-1)
            o = jnp.einsum('bhqk,bhkd->bhqd', attn, v)
            o = o.transpose(0, 2, 1, 3).reshape(B, S, D)
            return o @ wo.T + bo

        def _hier_moe(x, w_group, b_group, w_expert, b_expert, w1, b1, w2, b2):
            B, S, D = x.shape
            xt = x.reshape(B * S, D)
            T = xt.shape[0]
            E = NUM_GROUPS * EXPERTS_PER_GROUP
            gp = jax.nn.softmax(xt @ w_group + b_group, axis=-1)
            g_idx = jnp.argmax(gp, axis=-1)
            g_prob = jnp.max(gp, axis=-1)
            elog = jnp.einsum('td,gde->tge', xt, w_expert) + b_expert
            ep = jax.nn.softmax(elog, axis=-1)
            ep_sel = jnp.take_along_axis(ep, g_idx[:, None, None], axis=1)[:, 0, :]
            e_idx_local = jnp.argmax(ep_sel, axis=-1)
            e_prob = jnp.max(ep_sel, axis=-1)
            flat_e = g_idx * EXPERTS_PER_GROUP + e_idx_local
            combine = jax.nn.one_hot(flat_e, E, dtype=xt.dtype) * (g_prob * e_prob)[:, None]
            h = jax.nn.relu(jnp.einsum('td,edf->etf', xt, w1) + b1[:, None, :])
            y = jnp.einsum('etf,efd->etd', h, w2) + b2[:, None, :]
            out = jnp.einsum('te,etd->td', combine, y)
            return out.reshape(B, S, D)
        attn_out = _mha(x, in_proj_w, in_proj_b, out_proj_w, out_proj_b)
        x = _layernorm(x + attn_out, ln1_g, ln1_b)
        moe_out = _hier_moe(x, w_group, b_group, w_expert, b_expert, w1, b1, w2, b2)
        x = _layernorm(x + moe_out, ln2_g, ln2_b)
        return x
    x = L0_attn_x
    x = x + _L0_attn_ref(_layernorm(x, axis=-1), L0_attn_norm_gamma, L0_attn_norm_beta, L0_attn_in_w, L0_attn_in_b, L0_attn_conv_w, L0_attn_conv_b, L0_attn_A_log, L0_attn_B_p, L0_attn_C_p, L0_attn_D_p, L0_attn_out_w, L0_attn_out_b)
    x = x + _L0_ffn_ref(_layernorm(x, axis=-1), L0_ffn_gate_w, L0_ffn_Wg, L0_ffn_Wu, L0_ffn_Wd, L0_ffn_Ws_g, L0_ffn_Ws_u, L0_ffn_Ws_d)
    x = x + _L1_attn_ref(_layernorm(x, axis=-1), L1_attn_qkv_w, L1_attn_qkv_b, L1_attn_gate_w, L1_attn_gate_b, L1_attn_ln_g, L1_attn_ln_b)
    x = x + _L1_ffn_ref(_layernorm(x, axis=-1), L1_ffn_gate_w, L1_ffn_gate_b, L1_ffn_w1, L1_ffn_b1, L1_ffn_w2, L1_ffn_b2, L1_ffn_ws1, L1_ffn_bs1, L1_ffn_ws2, L1_ffn_bs2)
    x = x + _L2_attn_ref(_layernorm(x, axis=-1), L2_attn_W_dq, L2_attn_W_uq, L2_attn_W_dkv, L2_attn_W_uk, L2_attn_W_uv, L2_attn_W_o)
    x = x + _L2_ffn_ref(_layernorm(x, axis=-1), L2_ffn_base_W, L2_ffn_base_b, L2_ffn_shared_A, L2_ffn_shared_B, L2_ffn_routed_A, L2_ffn_routed_B, L2_ffn_router_W, L2_ffn_router_b)
    x = x + _L3_attn_ref(_layernorm(x, axis=-1), L3_attn_W_in, L3_attn_b_in, L3_attn_W_out, L3_attn_b_out, L3_attn_decay, L3_attn_mix)
    x = x + _L3_ffn_ref(_layernorm(x, axis=-1), L3_ffn_in_proj_w, L3_ffn_in_proj_b, L3_ffn_out_proj_w, L3_ffn_out_proj_b, L3_ffn_ln1_g, L3_ffn_ln1_b, L3_ffn_ln2_g, L3_ffn_ln2_b, L3_ffn_w_group, L3_ffn_b_group, L3_ffn_w_expert, L3_ffn_b_expert, L3_ffn_w1, L3_ffn_b1, L3_ffn_w2, L3_ffn_b2)
    return x

_drawn_inputs = setup_inputs


def setup_inputs(seed=0):
    import zlib

    import numpy as np

    out = dict(_drawn_inputs(seed))
    spreads = {'L0_attn_norm_gamma': (1.0, 0.6),
     'L0_attn_norm_beta': (0.0, 0.8),
     'L0_attn_in_b': (0.0, 0.523),
     'L0_attn_conv_b': (0.0, 0.8),
     'L0_attn_D_p': (0.0, 0.8),
     'L0_attn_out_b': (0.0, 0.1),
     'L1_attn_ln_g': (1.0, 0.6),
     'L1_attn_ln_b': (0.0, 0.1),
     'L1_ffn_gate_b': (0.0, 0.314),
     'L1_ffn_b1': (0.0, 0.711),
     'L1_ffn_b2': (0.0, 0.1),
     'L1_ffn_bs1': (0.0, 0.549),
     'L1_ffn_bs2': (0.0, 0.1),
     'L3_ffn_in_proj_b': (0.0, 0.494),
     'L3_ffn_out_proj_b': (0.0, 0.419),
     'L3_ffn_ln1_g': (1.0, 0.552),
     'L3_ffn_ln1_b': (0.0, 0.544),
     'L3_ffn_ln2_g': (1.0, 0.6),
     'L3_ffn_ln2_b': (0.0, 0.727),
     'L3_ffn_b_group': (0.0, 2.0),
     'L3_ffn_b_expert': (0.0, 2.0),
     'L3_ffn_b1': (0.0, 2.0),
     'L3_ffn_b2': (0.0, 2.0)}
    factors = {'L0_attn_conv_w': 8.0,
     'L0_attn_A_log': 8.0,
     'L0_attn_B_p': 8.0,
     'L0_attn_C_p': 8.0,
     'L0_ffn_gate_w': 8.0,
     'L0_ffn_Wg': 8.0,
     'L0_ffn_Wu': 8.0,
     'L0_ffn_Wd': 8.0,
     'L0_ffn_Ws_g': 8.0,
     'L0_ffn_Ws_u': 8.0,
     'L0_ffn_Ws_d': 8.0,
     'L1_attn_gate_w': 64.0,
     'L1_attn_gate_b': 64.0,
     'L2_attn_W_dq': 8.0,
     'L2_attn_W_uq': 8.0,
     'L2_attn_W_dkv': 2.733,
     'L2_attn_W_uk': 8.0,
     'L2_attn_W_uv': 2.876,
     'L2_attn_W_o': 2.809,
     'L2_ffn_base_b': 22.204,
     'L2_ffn_shared_A': 4.997,
     'L2_ffn_shared_B': 5.134,
     'L2_ffn_routed_A': 6.43,
     'L2_ffn_routed_B': 6.766,
     'L2_ffn_router_W': 7.816,
     'L2_ffn_router_b': 31.371,
     'L3_attn_b_in': 17.133,
     'L3_attn_W_in': 2.732,
     'L3_attn_b_out': 7.959}
    for name, (base, spread) in spreads.items():
        noise = np.random.default_rng([zlib.crc32(name.encode()), seed]).standard_normal(out[name].shape)
        drawn = base * np.exp(spread * noise) if base else spread * noise
        out[name] = jnp.asarray(drawn.astype(out[name].dtype))
    for name, factor in factors.items():
        out[name] = (out[name] * factor).astype(out[name].dtype)
    return out
```

```python
from contextlib import ExitStack, contextmanager

import concourse.bass as bass
from concourse import mybir
from concourse.alu_op_type import AluOpType as ALU

ACT = mybir.ActivationFunctionType
AX = mybir.AxisListType.X
F32 = mybir.dt.float32
BF16 = mybir.dt.bfloat16
ds = bass.ds

P = 128
NB, SEQ, D = 32, 256, 128
TPB = SEQ // P
NT = NB * TPB
UT = 4
U = UT * P
NU = NT // UT
EPS = 1e-5
INNER, NSTATE = 256, 64
CB = INNER // P
E0, F0, CAP = 16, 256, SEQ * 2 // 16
E1, F1 = 8, 512
E2, R2 = 6, 16
E3, F3, G3 = 8, 256, 4
NH, HD = 16, 8
HG = NH // 4
BIG = 1e30
CREDIT = 64

PACK = [("ident", P), ("ones", P), ("tri_st", P + SEQ), ("iota", CAP), ("tvec", SEQ),
        ("rank", 8),
        ("gam0", 1), ("bet0", 1), ("inw", 3 * INNER), ("inb", 3 * CB), ("cw", 3 * CB), ("cbias", CB),
        ("alog", CB * NSTATE), ("bp", CB * NSTATE), ("cp", CB * NSTATE), ("dp", CB), ("outw", CB * D), ("outb", D),
        ("gate0", E0), ("wsg", F0), ("wsu", F0), ("wsd", 2 * D),
        ("lng1", 1), ("lnb1", 1), ("qkvw", 3 * D), ("qkvb", 3), ("vb", D), ("gw1", D), ("gb1", 1),
        ("gate1", E1), ("gate1b", E1),
        ("wdq", 32), ("wdkv", 32), ("wuq", HG * P), ("wuk", HG * P), ("wuv", D), ("wo2", D), ("kone", HG),
        ("basew", D), ("baseb", D), ("acat", (E2 + 1) * R2), ("bcat", D), ("rout", E2), ("routb", E2),
        ("win3", D), ("bin3", 1), ("wout3", D), ("bout3", D), ("decay", 1), ("mix", 1),
        ("wq3", HG * P), ("wk3", HG * P), ("wv3", D), ("bq3", HG), ("bk3", HG), ("bv3", D), ("wo3", D), ("bo3", D),
        ("g1", D), ("b1", D), ("g2", D), ("b2", D), ("rt3", G3 + E3), ("rt3b", G3 + E3)]
OFF, NPACK = {}, 0
for _n, _c in PACK:
    OFF[_n] = (NPACK, _c)
    NPACK += _c
W0 = 3 * F0
W1 = 2 * F1 + F1 // P + U
W3 = 2 * F3 + F3 // P + U


class Signal:

    def __init__(self, semaphores, name, per):
        self.semaphores, self.name, self.per, self.held = semaphores, name, per, None

    @property
    def sem(self):
        if self.held is None:
            self.held = self.semaphores.take(self)
        return self.held[0]

    def now(self, i, k):
        return self.sem, i * self.per + (self.held[1] + k)

    def last(self, i, k):
        return self.sem, i * self.per + (self.held[1] + k - self.per)


class Semaphores:

    def __init__(self, nc, stack, count):
        self.nc, self.open = nc, []
        self.free = [stack.enter_context(nc.semaphore(f"signal{n}")) for n in range(count)]
        self.value = {s.num: CREDIT for s in self.free}
        with nc.Block() as block:
            @block.sync
            def _(sp):
                for s in self.free:
                    sp.sem_inc(s, CREDIT)

    def take(self, signal):
        held = self.free.pop(0)
        self.open.append((signal, held))
        return held, self.value[held.num]

    @contextmanager
    def loop_block(self, steps):
        with self.nc.Block() as block:
            yield block
        for signal, held in self.open:
            self.value[held.num] += signal.per * steps
            signal.held = None
            self.free.append(held)
        self.open = []


def build(nc, x_in, pack_in, maskb_in, w0_in, w1_in, w3_in, out, ktab, ychan):
    ctx = ExitStack()
    with ctx:
        pool = Semaphores(nc, ctx, 48)

        def sem(name):
            return ctx.enter_context(nc.semaphore(name))

        def sig(name, per):
            return Signal(pool, name, per)

        def sb(name, shape, dt=F32, stack=ctx):
            return stack.enter_context(nc.sbuf_tensor(name, shape, dt))

        def bank(name, stack, n=1):
            return stack.enter_context(nc.psum_tensor(name, [P, n, 512], F32))

        x_res = sb("x_res", [P, NT, D])
        pack = sb("pack", [P, NPACK])
        mean = sb("mean", [P, NT])
        rstd = sb("rstd", [P, NT])
        rstd2 = sb("rstd2", [P, NT])
        bn6 = sb("bn6", [P, NT, 6])
        tmpa = sb("tmpa", [P, NT])
        tmpb = sb("tmpb", [P, NT])
        epsc = sb("epsc", [P, 1])

        def c(name, lo=0, n=None, rows=P):
            o, w = OFF[name]
            return pack[0:rows, o + lo:o + (w if n is None else lo + n)]

        ident = c("ident")
        ones_row = c("ones", rows=1)
        loaded = sem("loaded")
        kready = sem("kready")
        chained = sem("chained")
        acted = sem("acted")
        peed = sem("peed")
        stored = sem("stored")
        n_chain, n_act, n_pe = [0], [0], [0]

        def link(dve, ins):
            n_chain[0] += 1
            ins.then_inc(chained, 1)
            dve.wait_ge(chained, n_chain[0])

        def act_done(ins):
            n_act[0] += 1
            ins.then_inc(acted, 1)

        def pe_done(ins):
            n_pe[0] += 1
            ins.then_inc(peed, 1)

        s_e = sig("decay_exp", CB)
        s_k = sig("table_sum", CB)

        class Front:
            def __init__(self, t, n):
                self.nrm = sig(t + "_normed", n)
                self.tps = sig(t + "_turned", n)
                self.hT = sig(t + "_hT_ready", n)

        fr_a = Front("a", 2)
        a_proj, a_up, a_conv, a_c3, a_c, a_silu, a_tr, a_u = (
            sig("a_proj", 4), sig("a_up", 4), sig("a_mid_tap", 4), sig("a_left_tap", 4), sig("a_convolved", 4),
            sig("a_silu", 4),
            sig("a_turned_u", 4), sig("a_u_stored", 4))
        b_tz, b_st, b_mm, b_ev, b_ea, b_out = ([sig(f"b_toeplitz{j}", 16) for j in range(2)], sig("b_staged", 2), sig("b_conv", 8),
                                              sig("b_kept_odd", 4), sig("b_kept_even", 4), [sig(f"b_y_stored{j}", 16) for j in range(2)])
        fr_c = Front("c", 2)
        c_y, c_proj, c_sig, c_t, c_z, c_out, c_x = (
            [sig(f"c_y_loaded{j}", 32) for j in range(2)], sig("c_proj", 4), sig("c_sigmoid", 8), sig("c_t", 8), sig("c_z", 4),
            sig("c_outproj", 2), sig("c_x", 2 * (UT + 2)))
        routes = {}
        for t in ("d", "m1", "m2", "m3"):
            routes[t] = (Front(t, 2), sig(t + "_logits", 2), sig(t + "_logits_kept", 2), sig(t + "_affine", 4))
        g_n, g_p, g_mm, g_x = sig("g_normed", 2), sig("g_onehot", 2), sig("g_gathered", 2), sig("g_stored", 2)
        x_w, x_gu, x_ge, x_h, x_o, x_s = ([sig(f"x_weights{j}", 16) for j in range(2)], sig("x_gate_up", 8), sig("x_gelu", 8),
                                         sig("x_hidden", 8), sig("x_down", 4), sig("x_kept", 4))
        fr_f = Front("f", 1)
        f_p, f_st, f_pt, f_ptc, f_eo, f_eoc, f_gu, f_ge, f_h, f_o, f_x = (
            sig("f_onehot", 2), sig("f_staged", 1), sig("f_turned_p", 2), sig("f_p_kept", 2), sig("f_turned_e", 1),
            sig("f_e_kept", 1), sig("f_gate_up", 1), sig("f_gelu", 1), sig("f_hidden", 1), sig("f_out", 1),
            sig("f_x", 1))
        f_h0 = sig("f_places", 2)
        fr_l = Front("l", 1)
        l_pr, l_eg, l_d1, l_ex, l_qk, l_v, l_a, l_am, l_o, l_x = (
            sig("l_proj", 2), sig("l_expgate", 1), sig("l_chain", 5), sig("l_exp", 1), sig("l_qk", 1),
            sig("l_v_kept", 1), sig("l_scores", 1), sig("l_masked", 1), sig("l_out", 1), sig("l_x", 3))
        moes = {}
        for t, nf in (("e1", F1 // P), ("e3", F3 // P)):
            moes[t] = (sem(t + "_weights_a"), sem(t + "_weights_b"), sem(t + "_weights_used"),
                       [sig(f"{t}{j}_hidden", nf) for j in range(2)], [sig(f"{t}{j}_acted", nf) for j in range(2)],
                       [sig(f"{t}{j}_out", 1) for j in range(2)], [sig(f"{t}{j}_x", UT) for j in range(2)])
        m_ts, m_tr, m_tc, m_o, m_x = (sig("m_scaled", 2), sig("m_turned", 2), sig("m_kept", 2), sig("m_out", 2),
                                      sig("m_x", 2))
        m_c = sig("m_staged", 2)
        m_h = sig("m_low", 2)
        fr_s = Front("s", 2)
        s_in, s_pr, s_re, s_sc, s_o, s_x = (sig("s_mixed", 4), sig("s_proj", 2), sig("s_relu", 2), sig("s_scan", 4),
                                            sig("s_out", 2), sig("s_x", 2))
        atts = {}
        for t in ("h2", "h3"):
            atts[t] = (Front(t, 1), {k: sig(f"{t}_{k}", n) for k, n in (
                ("low", 1), ("lowc", 1), ("pr", 3), ("qk", 2), ("qq", 2), ("half", 4), ("v", 1), ("s1", 8), ("mx", 9), ("mt", 1), ("qm", 1),
                ("s2", 8), ("ex", 8), ("pv", 4), ("ot", 4), ("tt", 1), ("nr", 2), ("t2", 1), ("t2c", 1), ("o", 1),
                ("x", 1))})
        z_n, z_a, z_d = sig("z_normed", 2), sig("z_affine", 6), [sig(f"z_stored{j}", 16) for j in range(2)]

        with nc.Block() as block:
            @block.sync
            def _(sp):
                sp.dma_start(pack[:, :], pack_in).then_inc(loaded, 16)
                sp.dma_start(x_res[:, :, :], x_in.rearrange("(t p) d -> p t d", p=P)).then_inc(loaded, 16)
                sp.wait_ge(loaded, 32)

            @block.vector
            def _(dve):
                link(dve, dve.memset(epsc[:, :], EPS))

        def stats(src, twice=False):
            with nc.Block() as block:
                k0 = n_chain[0]
                a0 = n_act[0]

                @block.vector
                def _(dve):
                    with dve.Fori(0, NT // 8) as i:
                        for t in range(8):
                            dve.bn_stats(bn6[:, ds(i * 8 + t, 1), :], src[:, ds(i * 8 + t, 1), :])
                    link(dve, dve.tensor_copy(tmpa[:, 0:1], epsc[:, 0:1]))
                    link(dve, dve.tensor_tensor(mean[:, :], bn6[:, :, 1], bn6[:, :, 4], ALU.add))
                    link(dve, dve.tensor_tensor(tmpa[:, :], bn6[:, :, 1], bn6[:, :, 4], ALU.subtract))
                    link(dve, dve.tensor_tensor(tmpb[:, :], bn6[:, :, 2], bn6[:, :, 5], ALU.add))
                    link(dve, dve.tensor_scalar(mean[:, :], mean[:, :], 0.5, None, ALU.mult))
                    link(dve, dve.tensor_tensor(tmpa[:, :], tmpa[:, :], tmpa[:, :], ALU.mult))
                    link(dve, dve.tensor_scalar(tmpa[:, :], tmpa[:, :], 0.25, EPS, ALU.mult, ALU.add))
                    link(dve, dve.scalar_tensor_tensor(tmpa[:, :], tmpb[:, :], 1.0 / D, tmpa[:, :], ALU.mult, ALU.add))

                    def root(dst):
                        n_act[0] += 1
                        dve.wait_ge(acted, n_act[0])
                        link(dve, dve.reciprocal(dst[:, :], dst[:, :]))
                        link(dve, dve.tensor_tensor(tmpb[:, :], dst[:, :], dst[:, :], ALU.mult))
                        link(dve, dve.tensor_tensor(tmpb[:, :], tmpb[:, :], tmpa[:, :], ALU.mult))
                        link(dve, dve.tensor_scalar(tmpb[:, :], tmpb[:, :], -0.5, 1.5, ALU.mult, ALU.add))
                        link(dve, dve.tensor_tensor(dst[:, :], dst[:, :], tmpb[:, :], ALU.mult))

                    root(rstd)
                    if twice:
                        link(dve, dve.tensor_scalar(tmpa[:, :], tmpa[:, :], EPS, None, ALU.subtract))
                        link(dve, dve.tensor_tensor(tmpa[:, :], tmpa[:, :], rstd[:, :], ALU.mult))
                        link(dve, dve.tensor_tensor(tmpa[:, :], tmpa[:, :], rstd[:, :], ALU.mult))
                        link(dve, dve.tensor_scalar(tmpa[:, :], tmpa[:, :], EPS, None, ALU.add))
                        root(rstd2)
                        link(dve, dve.tensor_tensor(rstd2[:, :], rstd2[:, :], rstd[:, :], ALU.mult))

                @block.scalar
                def _(act):
                    act.wait_ge(chained, k0 + 8)
                    act.activation(rstd[:, :], tmpa[:, :], ACT.Sqrt).then_inc(acted, 1)
                    if twice:
                        act.wait_ge(chained, k0 + 8 + 5 + 4)
                        act.activation(rstd2[:, :], tmpa[:, :], ACT.Sqrt).then_inc(acted, 1)

        def norm_tiles(dve, done, dst, src, first, n, r, ready_to_write, extra=None):
            dve.wait_ge(*ready_to_write)
            if extra is not None:
                dve.wait_ge(*extra)
            for t in range(n):
                ins = dve.tensor_scalar(dst[:, t, :], src[:, ds(first + t, 1), :].rearrange("p o d -> p (o d)"),
                                        mean[:, ds(first + t, 1)], r[:, ds(first + t, 1)], ALU.subtract, ALU.mult)
            ins.then_inc(done.sem, 1)

        def turn_tiles(pe, done, ps, nrm, n, *waits):
            for w in waits:
                pe.wait_ge(*w)
            for t in range(n):
                ins = pe.transpose(ps[:, t * P:(t + 1) * P], nrm[:, t, :], ident)
            ins.then_inc(done.sem, 1)

        with ExitStack() as st:
            aexp = sb("aexp", [P, CB * NSTATE], stack=st)
            cbp = sb("cbp", [P, CB * NSTATE], stack=st)
            esb = sb("esb", [P, CB, SEQ], stack=st)
            ksb = sb("ksb", [P, CB, P + SEQ], stack=st)
            with pool.loop_block(NSTATE) as block:
                a0 = n_act[0]
                k_neg = n_chain[0] + 3

                @block.scalar
                def _(act):
                    act_done(act.activation(aexp[:, :], c("alog"), ACT.Exp))
                    act.wait_ge(chained, k_neg)
                    with act.Fori(0, NSTATE) as i:
                        for b in range(CB):
                            act.wait_ge(*s_k.last(i, b + 1))
                            act.activation(esb[:, b, :], c("tvec"), ACT.Exp,
                                           scale=aexp[:, ds(i + b * NSTATE, 1)]).then_inc(s_e.sem, 1)

                @block.vector
                def _(dve):
                    link(dve, dve.memset(ksb[:, :, :], 0.0))
                    link(dve, dve.tensor_tensor(cbp[:, :], c("bp"), c("cp"), ALU.mult))
                    dve.wait_ge(acted, a0 + 1)
                    link(dve, dve.tensor_scalar(aexp[:, :], aexp[:, :], -1.0, None, ALU.mult))
                    with dve.Fori(0, NSTATE) as i:
                        for b in range(CB):
                            dve.wait_ge(*s_k.last(i, b + 1))
                            dve.wait_ge(*s_e.now(i, b + 1))
                            dve.scalar_tensor_tensor(ksb[:, b, P:], esb[:, b, :], cbp[:, ds(i + b * NSTATE, 1)],
                                                     ksb[:, b, P:], ALU.mult, ALU.add).then_inc(s_k.sem, 1)
                    dve.wait_ge(*s_k.now(NSTATE - 1, CB))
                    link(dve, dve.tensor_tensor(ksb[:, :, P], ksb[:, :, P], c("dp"), ALU.add))

                @block.sync
                def _(sp):
                    sp.wait_ge(chained, k_neg + 1)
                    sp.dma_start(ktab.rearrange("(b p) l -> p b l", p=P), ksb[:, :, :]).then_inc(kready, 16)
                    sp.wait_ge(kready, 16)

        stats(x_res, twice=True)

        with ExitStack() as st_u:
            u_all = sb("u_all", [P, TPB, NB, INNER], stack=st_u)
            with ExitStack() as st:
                nrm = [sb(f"a_nrm{j}", [P, UT, P], stack=st) for j in range(2)]
                hT = [sb(f"a_hT{j}", [P, U], stack=st) for j in range(2)]
                up = [sb(f"a_up{j}", [P, CB, 2, SEQ + 2], stack=st) for j in range(2)]
                cv = [sb(f"a_cv{j}", [P, CB, 2, SEQ], stack=st) for j in range(2)]
                rv = [sb(f"a_rv{j}", [P, CB, 2, SEQ], stack=st) for j in range(2)]
                ps_t = bank("a_ps_t", st, 2)
                ps_u = bank("a_ps_u", st, 4)
                ps_r = bank("a_ps_r", st, 2)
                with pool.loop_block(NU // 2) as block:
                    ch0 = n_chain[0] + 2

                    @block.vector
                    def _(dve):
                        for j in range(2):
                            link(dve, dve.memset(up[j][:, :, :, :], 0.0))
                        with dve.Fori(0, NU // 2) as i:
                            for j in range(2):
                                norm_tiles(dve, fr_a.nrm, nrm[j], x_res, (i * 2 + j) * UT, UT, rstd2,
                                           fr_a.tps.last(i, j + 1))
                            for b in range(CB):
                                for j in range(2):
                                    k = b * 2 + j + 1
                                    dve.wait_ge(*a_up.now(i, k))
                                    dve.wait_ge(*a_silu.last(i, k))
                                    dve.tensor_scalar(cv[j][:, b], up[j][:, b, :, 1:SEQ + 1], c("cw", b * 3 + 1, 1),
                                                      c("cbias", b, 1), ALU.mult, ALU.add).then_inc(a_conv.sem, 1)
                                    dve.wait_ge(*a_conv.now(i, k))
                                    dve.scalar_tensor_tensor(cv[j][:, b], up[j][:, b, :, 0:SEQ], c("cw", b * 3, 1),
                                                             cv[j][:, b], ALU.mult, ALU.add).then_inc(a_c3.sem, 1)
                                    dve.wait_ge(*a_c3.now(i, k))
                                    dve.scalar_tensor_tensor(cv[j][:, b], up[j][:, b, :, 2:SEQ + 2],
                                                             c("cw", b * 3 + 2, 1), cv[j][:, b],
                                                             ALU.mult, ALU.add).then_inc(a_c.sem, 1)
                            for b in range(CB):
                                for j in range(2):
                                    dve.wait_ge(*a_tr.now(i, b * 2 + j + 1))
                                    dst = u_all[:, :, ds(i * 4 + j * 2, 2), b * P:(b + 1) * P]
                                    dve.tensor_copy(dst.rearrange("p h b c -> p b h c"),
                                                    ps_r[:, j, :].rearrange("p (b h c) -> p b h c", b=2, h=TPB)
                                                    ).then_inc(a_u.sem, 1)

                    @block.tensor
                    def _(pe):
                        pe.wait_ge(chained, ch0)
                        with pe.Fori(0, NU // 2) as i:
                            for j in range(2):
                                turn_tiles(pe, fr_a.tps, ps_t[:, j, :], nrm[j], UT, fr_a.nrm.now(i, j + 1),
                                           fr_a.hT.last(i, j + 1))
                            for b in range(CB):
                                for j in range(2):
                                    pe.wait_ge(*fr_a.hT.now(i, j + 1))
                                    pe.wait_ge(*a_up.last(i, b * 2 + j + 1))
                                    pe.matmul(ps_u[:, b * 2 + j, :], c("inw", b * P, P), hT[j][:, :],
                                              start=True, stop=True).then_inc(a_proj.sem, 1)
                            for b in range(CB):
                                for j in range(2):
                                    k = b * 2 + j + 1
                                    pe.wait_ge(*a_silu.now(i, k))
                                    if b == 0:
                                        pe.wait_ge(*a_u.last(i, 2 + k))
                                    else:
                                        pe.wait_ge(*a_u.now(i, k - 2))
                                    for t in range(UT):
                                        h = TPB - 1 - t % TPB
                                        ins = pe.transpose(ps_r[:, j, t * P:(t + 1) * P],
                                                           rv[j][:, b, t // TPB, h * P:(h + 1) * P], ident)
                                    ins.then_inc(a_tr.sem, 1)

                    @block.scalar
                    def _(act):
                        act.wait_ge(chained, ch0)
                        with act.Fori(0, NU // 2) as i:
                            for j in range(2):
                                act.wait_ge(*fr_a.tps.now(i, j + 1))
                                act.wait_ge(*a_proj.last(i, 2 + j + 1))
                                act.activation(hT[j][:, :], ps_t[:, j, :], ACT.Identity, bias=c("bet0"),
                                               scale=c("gam0")).then_inc(fr_a.hT.sem, 1)
                            for b in range(CB):
                                for j in range(2):
                                    k = b * 2 + j + 1
                                    act.wait_ge(*a_proj.now(i, k))
                                    act.wait_ge(*a_c.last(i, k))
                                    act.activation(up[j][:, b, :, 1:SEQ + 1],
                                                   ps_u[:, b * 2 + j, :].rearrange("p (b t) -> p b t", b=2),
                                                   ACT.Identity, bias=c("inb", b, 1)).then_inc(a_up.sem, 1)
                            for b in range(CB):
                                for j in range(2):
                                    k = b * 2 + j + 1
                                    act.wait_ge(*a_c.now(i, k))
                                    act.wait_ge(*a_tr.last(i, k))
                                    end = cv[j][:, b, 0, SEQ - 1:SEQ]
                                    down = bass.AP(end.tensor, end.offset, [list(end.ap[0]), [SEQ, 2], [-1, SEQ]])
                                    act.activation(rv[j][:, b], down, ACT.Silu).then_inc(a_silu.sem, 1)

            with ExitStack() as st:
                GC = 16
                tz = [sb(f"b_tz{j}", [P, GC, SEQ], stack=st) for j in range(2)]
                us = [sb(f"b_us{j}", [P, TPB, GC, NB], stack=st) for j in range(2)]
                ysb = [sb(f"b_y{j}", [P, 4, SEQ], stack=st) for j in range(2)]
                ps_y = bank("b_ps_y", st, 4)
                with pool.loop_block(INNER // GC // 2) as block:
                    @block.sync
                    def _(sp):
                        with sp.Fori(0, INNER // GC // 2) as i:
                            for j in range(2):
                                sp.wait_ge(*b_mm.last(i, 4 * j + 4))
                                rows = ktab[ds((i * 2 + j) * GC, GC), :]
                                src = bass.AP(rows.tensor, rows.offset + 1, [[1, P], [P + SEQ, GC], [1, SEQ]])
                                sp.dma_start(tz[j][:, :, :], src).then_inc(b_tz[j].sem, 16)
                        for j in range(2):
                            sp.wait_ge(*b_out[j].now(INNER // GC // 2 - 1, 16))

                    @block.vector
                    def _(dve):
                        with dve.Fori(0, INNER // GC // 2) as i:
                            for j in range(2):
                                dve.wait_ge(*b_mm.last(i, 4 * j + 4))
                                dve.tensor_copy(us[j][:, :, :, :].rearrange("p h c b -> p h b c"),
                                                u_all[:, :, :, ds((i * 2 + j) * GC, GC)]).then_inc(b_st.sem, 1)
                                for q in range(1, 4, 2):
                                    dve.wait_ge(*b_mm.now(i, 4 * j + q + 1))
                                    dve.wait_ge(*b_out[j].last(i, 16))
                                    dve.tensor_copy(ysb[j][:, q, :], ps_y[:, q, 0:SEQ]).then_inc(b_ev.sem, 1)

                    @block.tensor
                    def _(pe):
                        with pe.Fori(0, INNER // GC // 2) as i:
                            for j in range(2):
                                pe.wait_ge(*b_tz[j].now(i, 16))
                                pe.wait_ge(*b_st.now(i, j + 1))
                                for q in range(4):
                                    if j == 0:
                                        pe.wait_ge(*b_ev.last(i, 4))
                                        pe.wait_ge(*b_ea.last(i, 4))
                                    else:
                                        pe.wait_ge(*b_ev.now(i, 2))
                                        pe.wait_ge(*b_ea.now(i, 2))
                                    for g in range(4):
                                        ch = 4 * q + g
                                        strip = ps_y[32 * g:32 * g + 32, q, :]
                                        pe.matmul(strip[:, 0:SEQ], us[j][:, 0, ch, :], tz[j][:, ch, :],
                                                  start=True, stop=False)
                                        ins = pe.matmul(strip[:, P:SEQ], us[j][:, 1, ch, :], tz[j][:, ch, 0:P],
                                                        start=False, stop=True)
                                    ins.then_inc(b_mm.sem, 1)

                    @block.scalar
                    def _(act):
                        with act.Fori(0, INNER // GC // 2) as i:
                            for j in range(2):
                                for q in range(0, 4, 2):
                                    act.wait_ge(*b_mm.now(i, 4 * j + q + 1))
                                    act.wait_ge(*b_out[j].last(i, 16))
                                    act.activation(ysb[j][:, q, :], ps_y[:, q, 0:SEQ], ACT.Copy).then_inc(b_ea.sem, 1)
                                act.wait_ge(*b_ea.now(i, 2 * j + 2))
                                act.wait_ge(*b_ev.now(i, 2 * j + 2))
                                dst = ychan[ds((i * 2 + j) * GC, GC)].rearrange("(q g) b t -> (g b) q t", g=4)
                                act.dma_start(dst, ysb[j][:, :, :]).then_inc(b_out[j].sem, 16)

        with ExitStack() as st:
            nrm = [sb(f"c_nrm{j}", [P, UT, P], stack=st) for j in range(2)]
            hT = [sb(f"c_hT{j}", [P, U], stack=st) for j in range(2)]
            yT = [sb(f"c_yT{j}", [P, CB, U], stack=st) for j in range(2)]
            sv = [sb(f"c_sv{j}", [P, CB, U], stack=st) for j in range(2)]
            sg = [sb(f"c_sg{j}", [P, CB, U], stack=st) for j in range(2)]
            ps_t = bank("c_ps_t", st, 2)
            ps_v = bank("c_ps_v", st, 2)
            ps_g = bank("c_ps_g", st, 2)
            ps_o = bank("c_ps_o", st, 2)
            with pool.loop_block(NU // 2) as block:
                @block.sync
                def _(sp):
                    with sp.Fori(0, NU // 2) as i:
                        for j in range(2):
                            sp.wait_ge(*c_t.last(i, 4 * j + 4))
                            for b in range(CB):
                                src = ychan[b * P:(b + 1) * P, ds((i * 2 + j) * 2, 2), :]
                                sp.dma_start(yT[j][:, b, :].rearrange("p (b t) -> p b t", b=2), src
                                             ).then_inc(c_y[j].sem, 16)

                @block.vector
                def _(dve):
                    with dve.Fori(0, NU // 2) as i:
                        for j in range(2):
                            norm_tiles(dve, fr_c.nrm, nrm[j], x_res, (i * 2 + j) * UT, UT, rstd2,
                                       fr_c.tps.last(i, j + 1))
                        for j in range(2):
                            dve.wait_ge(*c_y[j].now(i, 32))
                            for b in range(CB):
                                dve.wait_ge(*c_sig.now(i, 4 * j + 2 * b + 2))
                                dve.scalar_tensor_tensor(sv[j][:, b, :], ps_v[:, b, :], c("inb", CB + b, 1),
                                                         sv[j][:, b, :], ALU.add, ALU.mult).then_inc(c_t.sem, 1)
                                dve.tensor_tensor(sg[j][:, b, :], sg[j][:, b, :], yT[j][:, b, :],
                                                  ALU.mult).then_inc(c_t.sem, 1)
                                dve.wait_ge(*c_t.now(i, 4 * j + 2 * b + 2))
                                dve.tensor_tensor(sv[j][:, b, :], sv[j][:, b, :], sg[j][:, b, :],
                                                  ALU.add).then_inc(c_z.sem, 1)
                        for j in range(2):
                            first = (i * 2 + j) * UT
                            k0 = j * (UT + 2)
                            dve.wait_ge(*c_out.now(i, j + 1))
                            dve.wait_ge(*fr_c.tps.now(i, j + 1))
                            for t in range(UT):
                                dve.tensor_scalar(nrm[j][:, t, :],
                                                  x_res[:, ds(first + t, 1), :].rearrange("p o d -> p (o d)"),
                                                  mean[:, ds(first + t, 1)], rstd[:, ds(first + t, 1)],
                                                  ALU.subtract, ALU.mult).then_inc(c_x.sem, 1)
                            xs = x_res[:, ds(first, UT), :]
                            dve.wait_ge(*c_x.now(i, k0 + UT))
                            dve.tensor_tensor(xs, xs, nrm[j][:, :, :], ALU.add).then_inc(c_x.sem, 1)
                            dve.wait_ge(*c_x.now(i, k0 + UT + 1))
                            dve.tensor_tensor(xs, xs, ps_o[:, j, :].rearrange("p (t d) -> p t d", t=UT),
                                              ALU.add).then_inc(c_x.sem, 1)

                @block.tensor
                def _(pe):
                    with pe.Fori(0, NU // 2) as i:
                        for j in range(2):
                            turn_tiles(pe, fr_c.tps, ps_t[:, j, :], nrm[j], UT, fr_c.nrm.now(i, j + 1),
                                       fr_c.hT.last(i, j + 1))
                        for j in range(2):
                            pe.wait_ge(*fr_c.hT.now(i, j + 1))
                            for b in range(CB):
                                if j == 0:
                                    pe.wait_ge(*c_z.last(i, 2 + b + 1))
                                else:
                                    pe.wait_ge(*c_z.now(i, b + 1))
                                pe.matmul(ps_v[:, b, :], c("inw", (CB + b) * P, P), hT[j][:, :], start=True, stop=True)
                                pe.matmul(ps_g[:, b, :], c("inw", (2 * CB + b) * P, P), hT[j][:, :],
                                          start=True, stop=True).then_inc(c_proj.sem, 1)
                        for j in range(2):
                            pe.wait_ge(*c_z.now(i, 2 * j + 2))
                            pe.wait_ge(*c_x.last(i, (j + 1) * (UT + 2)))
                            for t in range(UT):
                                dst = ps_o[:, j, t * P:(t + 1) * P]
                                pe.matmul(dst, c("ones", rows=1), c("outb", rows=1), start=True, stop=False)
                                for b in range(CB):
                                    ins = pe.matmul(dst, sv[j][:, b, t * P:(t + 1) * P], c("outw", b * D, D),
                                                    start=False, stop=(b == CB - 1))
                            ins.then_inc(c_out.sem, 1)

                @block.scalar
                def _(act):
                    with act.Fori(0, NU // 2) as i:
                        for j in range(2):
                            act.wait_ge(*fr_c.tps.now(i, j + 1))
                            act.wait_ge(*c_proj.last(i, 2 * j + 2))
                            act.activation(hT[j][:, :], ps_t[:, j, :], ACT.Identity, bias=c("bet0"),
                                           scale=c("gam0")).then_inc(fr_c.hT.sem, 1)
                        for j in range(2):
                            for b in range(CB):
                                act.wait_ge(*c_proj.now(i, 2 * j + b + 1))
                                act.wait_ge(*c_out.last(i, j + 1))
                                act.activation(sv[j][:, b, :], ps_v[:, b, :], ACT.Sigmoid,
                                               bias=c("inb", CB + b, 1)).then_inc(c_sig.sem, 1)
                                act.activation(sg[j][:, b, :], ps_g[:, b, :], ACT.Sigmoid,
                                               bias=c("inb", 2 * CB + b, 1)).then_inc(c_sig.sem, 1)

        def route(tag, src, weights, bias, n_out, logits, h_all=None, affine=None):
            fr, lg, kept, aff = routes[tag]
            with ExitStack() as st:
                nrm = [sb(f"{tag}_nrm{j}", [P, UT, P], stack=st) for j in range(2)]
                hT = [sb(f"{tag}_hT{j}", [P, U], stack=st) for j in range(2)]
                ps_t = bank(f"{tag}_ps_t", st, 2)
                ps_l = bank(f"{tag}_ps_l", st, 2)
                with pool.loop_block(NU // 2) as block:
                    @block.vector
                    def _(dve):
                        with dve.Fori(0, NU // 2) as i:
                            for j in range(2):
                                first = (i * 2 + j) * UT
                                if affine is None:
                                    norm_tiles(dve, fr.nrm, nrm[j], src, first, UT, rstd, fr.tps.last(i, j + 1))
                                    continue
                                dve.wait_ge(*fr.tps.last(i, j + 1))
                                for t in range(UT):
                                    ins = dve.tensor_scalar(nrm[j][:, t, :],
                                                            src[:, ds(first + t, 1), :].rearrange("p o d -> p (o d)"),
                                                            mean[:, ds(first + t, 1)], rstd[:, ds(first + t, 1)],
                                                            ALU.subtract, ALU.mult)
                                ins.then_inc(aff.sem, 1)
                                dve.wait_ge(*aff.now(i, 2 * j + 1))
                                dve.tensor_tensor(nrm[j][:, :, :], nrm[j][:, :, :],
                                                  affine[0].unsqueeze(1).to_broadcast([P, UT, D]),
                                                  ALU.mult).then_inc(aff.sem, 1)
                                dve.wait_ge(*aff.now(i, 2 * j + 2))
                                dve.tensor_tensor(nrm[j][:, :, :], nrm[j][:, :, :],
                                                  affine[1].unsqueeze(1).to_broadcast([P, UT, D]),
                                                  ALU.add).then_inc(fr.nrm.sem, 1)
                                dve.wait_ge(*fr.nrm.now(i, j + 1))
                                dve.tensor_scalar(src[:, ds(first, UT), :], nrm[j][:, :, :], 1.0, None, ALU.mult)
                            for j in range(2):
                                dve.wait_ge(*lg.now(i, j + 1))
                                dve.tensor_copy(logits[:, ds((i * 2 + j) * UT, UT), :],
                                                ps_l[:, j, 0:UT * n_out].rearrange("p (t e) -> p t e", t=UT)
                                                ).then_inc(kept.sem, 1)

                    @block.tensor
                    def _(pe):
                        with pe.Fori(0, NU // 2) as i:
                            for j in range(2):
                                turn_tiles(pe, fr.tps, ps_t[:, j, :], nrm[j], UT, fr.nrm.now(i, j + 1),
                                           fr.hT.last(i, j + 1))
                            for j in range(2):
                                pe.wait_ge(*fr.hT.now(i, j + 1))
                                pe.wait_ge(*kept.last(i, j + 1))
                                for t in range(UT):
                                    dst = ps_l[:, j, t * n_out:(t + 1) * n_out]
                                    if bias is not None:
                                        pe.matmul(dst, c("ones", rows=1), bias, start=True, stop=False)
                                    ins = pe.matmul(dst, hT[j][:, t * P:(t + 1) * P], weights,
                                                    start=(bias is None), stop=True)
                                ins.then_inc(lg.sem, 1)

                    @block.scalar
                    def _(act):
                        with act.Fori(0, NU // 2) as i:
                            for j in range(2):
                                act.wait_ge(*fr.tps.now(i, j + 1))
                                act.wait_ge(*lg.last(i, j + 1))
                                if h_all is not None:
                                    act.activation(h_all[:, ds((i * 2 + j) * U, U)], ps_t[:, j, :], ACT.Copy)
                                act.activation(hT[j][:, :], ps_t[:, j, :], ACT.Copy).then_inc(fr.hT.sem, 1)

        def softmax_rows(dve, lg, out_e, m, s, n):
            link(dve, dve.tensor_reduce(m, lg, AX, ALU.max))
            link(dve, dve.tensor_tensor(out_e, lg, m.unsqueeze(2).to_broadcast([P, NT, n]), ALU.subtract))
            n_act[0] += 1
            dve.wait_ge(acted, n_act[0])
            link(dve, dve.tensor_reduce(s, out_e, AX, ALU.add))
            link(dve, dve.reciprocal(s, s))

        stats(x_res)
        ROWS = 8 * E0
        NG = NB // 8
        with ExitStack() as st_d:
            score = sb("d_score", [P, NT, E0], stack=st_d)
            place = sb("d_place", [P, NT, E0], stack=st_d)
            route("d", x_res, c("gate0"), None, E0, score)
            with ExitStack() as st:
                mx = sb("d_max", [P, NT], stack=st)
                rs = sb("d_rsum", [P, NT], stack=st)
                rows = sb("d_rows", [P, NG, SEQ], stack=st)
                work = sb("d_work", [P, NG, SEQ], stack=st)
                taken = sb("d_taken", [P, NG, SEQ], stack=st)
                zero = sb("d_zero", [P, SEQ], stack=st)
                top = sb("d_top", [P, NG, 8], stack=st)
                lin = sb("d_lin", [P, TPB * NG, P], stack=st)
                ps_s = bank("d_ps_s", st, 2)
                ps_p = bank("d_ps_p", st, 2)
                with nc.Block() as block:
                    k0, a0, p0 = n_chain[0], n_act[0], n_pe[0]

                    @block.vector
                    def _(dve):
                        link(dve, dve.memset(zero[:, :], 0.0))
                        softmax_rows(dve, score[:, :, :], score[:, :, :], mx[:, :], rs[:, :], E0)
                        link(dve, dve.tensor_tensor(score[:, :, :], score[:, :, :],
                                                    rs[:, :].unsqueeze(2).to_broadcast([P, NT, E0]), ALU.mult))
                        lv = lin[:, :, :].rearrange("p (g h) (b e) -> p g h b e", g=NG, b=8)
                        sv = score[:, :, :].rearrange("p (g b h) e -> p g h b e", g=NG, b=8)
                        for g in range(NG):
                            link(dve, dve.tensor_copy(lv[:, g], sv[:, g]))
                        dve.wait_ge(peed, p0 + 1)
                        link(dve, dve.tensor_copy(rows[:, :, :].rearrange("p g t -> p (g t)"),
                                                  ps_s[:, :, :].rearrange("p k n -> p (k n)")))
                        for g in range(NG):
                            src = rows
                            for _ in range(CAP // 8):
                                link(dve, dve.max(top[:, g, :], src[:, g, :]))
                                link(dve, dve.match_replace(work[:, g, :], top[:, g, :], src[:, g, :], -1.0))
                                src = work
                            link(dve, dve.tensor_scalar(taken[:, g, :], work[:, g, :], 0.0, None, ALU.is_lt))
                            link(dve, dve.tensor_tensor_scan(work[:, g, :], taken[:, g, :], zero[:, :], 0.0,
                                                             ALU.add, ALU.add))
                            link(dve, dve.tensor_tensor(rows[:, g, :], work[:, g, :], taken[:, g, :], ALU.mult))
                        dve.wait_ge(peed, p0 + 2)
                        pv = place[:, :, :].rearrange("p (g b h) e -> p g h b e", g=NG, b=8)
                        for g in range(NG):
                            half = ps_p[:, g // 2, (g % 2) * SEQ:(g % 2 + 1) * SEQ]
                            link(dve, dve.tensor_copy(pv[:, g], half.rearrange("p (h b e) -> p h b e", h=TPB, b=8)))

                    k_lin = k0 + 1 + 4 + 1 + NG
                    k_rows = k_lin + 1 + NG * (2 * (CAP // 8) + 3)

                    @block.scalar
                    def _(act):
                        act.wait_ge(chained, k0 + 3)
                        act.activation(score[:, :, :], score[:, :, :], ACT.Exp).then_inc(acted, 1)

                    @block.tensor
                    def _(pe):
                        pe.wait_ge(chained, k_lin)
                        for g in range(NG):
                            for h in range(TPB):
                                ins = pe.transpose(ps_s[:, g // 2, (g % 2) * SEQ + h * P:(g % 2) * SEQ + (h + 1) * P],
                                                   lin[:, g * TPB + h, :], ident)
                        pe_done(ins)
                        pe.wait_ge(chained, k_rows)
                        for g in range(NG):
                            for h in range(TPB):
                                ins = pe.transpose(ps_p[:, g // 2, (g % 2) * SEQ + h * P:(g % 2) * SEQ + (h + 1) * P],
                                                   rows[:, g, h * P:(h + 1) * P], ident)
                        pe_done(ins)

            SLOTS = E0 * CAP
            with ExitStack() as st_x:
                xg = sb("xg", [P, E0, NB, CAP], stack=st_x)

                with ExitStack() as st:
                    nrm = [sb(f"g_nrm{j}", [P, TPB, P], stack=st) for j in range(2)]
                    hot = [sb(f"g_hot{j}", [P, TPB, E0, CAP], stack=st) for j in range(2)]
                    ps_x = bank("g_ps_x", st, 2)
                    with pool.loop_block(NB // 2) as block:
                        @block.vector
                        def _(dve):
                            with dve.Fori(0, NB // 2) as i:
                                for j in range(2):
                                    norm_tiles(dve, g_n, nrm[j], x_res, (i * 2 + j) * TPB, TPB, rstd,
                                               g_mm.last(i, j + 1))
                                    for h in range(TPB):
                                        pl = place[:, ds((i * 2 + j) * TPB + h, 1), :].rearrange("p o e -> p (o e)")
                                        ins = dve.tensor_tensor(hot[j][:, h], pl.unsqueeze(2).to_broadcast([P, E0, CAP]),
                                                                c("iota").unsqueeze(1).to_broadcast([P, E0, CAP]),
                                                                ALU.is_equal)
                                    ins.then_inc(g_p.sem, 1)

                        @block.tensor
                        def _(pe):
                            with pe.Fori(0, NB // 2) as i:
                                for j in range(2):
                                    pe.wait_ge(*g_n.now(i, j + 1))
                                    pe.wait_ge(*g_p.now(i, j + 1))
                                    pe.wait_ge(*g_x.last(i, j + 1))
                                    for h in range(TPB):
                                        ins = pe.matmul(ps_x[:, j, :], nrm[j][:, h, :],
                                                        hot[j][:, h].rearrange("p e s -> p (e s)"),
                                                        start=(h == 0), stop=(h == TPB - 1))
                                    ins.then_inc(g_mm.sem, 1)

                        @block.scalar
                        def _(act):
                            with act.Fori(0, NB // 2) as i:
                                for j in range(2):
                                    act.wait_ge(*g_mm.now(i, j + 1))
                                    act.activation(xg[:, :, ds(i * 2 + j, 1), :].rearrange("p e o s -> p e (o s)"),
                                                   ps_x[:, j, :].rearrange("p (e s) -> p e s", e=E0),
                                                   ACT.Copy).then_inc(g_x.sem, 1)

                with ExitStack() as st:
                    w0 = [sb(f"x_w{j}", [P, W0], stack=st) for j in range(2)]
                    ge = [sb(f"x_gelu{f}", [P, 512], stack=st) for f in range(2)]
                    hu = [sb(f"x_hid{n}", [P, 2, 512], stack=st) for n in range(2)]
                    ps_g = bank("x_ps_g", st, 2)
                    ps_u = bank("x_ps_u", st, 2)
                    ps_o = bank("x_ps_o", st, 2)
                    xe = xg[:, :, :, :].rearrange("p e b s -> p (e b s)")
                    with pool.loop_block(E0 // 2) as block:
                        @block.sync
                        def _(sp):
                            with sp.Fori(0, E0 // 2) as i:
                                for j in range(2):
                                    sp.wait_ge(*x_o.last(i, 2 * j + 2))
                                    sp.dma_start(w0[j][:, :], w0_in[ds(i * 2 + j, 1)].rearrange("o p w -> p (o w)")
                                                 ).then_inc(x_w[j].sem, 16)

                        def at(i, n):
                            return xe[:, ds(i * (2 * NB * CAP) + n * 512, 512)]

                        @block.tensor
                        def _(pe):
                            with pe.Fori(0, E0 // 2) as i:
                                def down_proj(n):
                                    pe.wait_ge(*x_h.now(i, 2 * n + 2))
                                    if n >= 2:
                                        pe.wait_ge(*x_s.now(i, n - 1))
                                    else:
                                        pe.wait_ge(*x_s.last(i, n + 3))
                                    for f in range(2):
                                        ins = pe.matmul(ps_o[:, n % 2, :], w0[n // 2][:, 2 * F0 + f * D:2 * F0 + (f + 1) * D],
                                                        hu[n % 2][:, f, :], start=(f == 0), stop=(f == 1))
                                    ins.then_inc(x_o.sem, 1)

                                for n in range(4):
                                    if n % 2 == 0:
                                        pe.wait_ge(*x_w[n // 2].now(i, 16))
                                    for f in range(2):
                                        if n:
                                            pe.wait_ge(*x_h.now(i, 2 * n - 1 + f))
                                        else:
                                            pe.wait_ge(*x_h.last(i, 7 + f))
                                        pe.matmul(ps_g[:, f, :], w0[n // 2][:, f * P:(f + 1) * P], at(i, n),
                                                  start=True, stop=True)
                                        pe.matmul(ps_u[:, f, :], w0[n // 2][:, F0 + f * P:F0 + (f + 1) * P], at(i, n),
                                                  start=True, stop=True).then_inc(x_gu.sem, 1)
                                    if n:
                                        down_proj(n - 1)
                                down_proj(3)

                        @block.scalar
                        def _(act):
                            with act.Fori(0, E0 // 2) as i:
                                def keep(n):
                                    act.wait_ge(*x_o.now(i, n + 1))
                                    act.activation(at(i, n), ps_o[:, n % 2, :], ACT.Copy).then_inc(x_s.sem, 1)

                                for n in range(4):
                                    for f in range(2):
                                        k = 2 * n + f + 1
                                        act.wait_ge(*x_gu.now(i, k))
                                        if n:
                                            act.wait_ge(*x_h.now(i, k - 2))
                                        else:
                                            act.wait_ge(*x_h.last(i, 7 + f))
                                        act.activation(ge[f][:, :], ps_g[:, f, :], ACT.Gelu).then_inc(x_ge.sem, 1)
                                    if n:
                                        keep(n - 1)
                                keep(3)

                        @block.vector
                        def _(dve):
                            with dve.Fori(0, E0 // 2) as i:
                                for n in range(4):
                                    for f in range(2):
                                        dve.wait_ge(*x_ge.now(i, 2 * n + f + 1))
                                        if n >= 2:
                                            dve.wait_ge(*x_o.now(i, n - 1))
                                        else:
                                            dve.wait_ge(*x_o.last(i, n + 3))
                                        dve.tensor_tensor(hu[n % 2][:, f, :], ge[f][:, :], ps_u[:, f, :],
                                                          ALU.mult).then_inc(x_h.sem, 1)

                with ExitStack() as st:
                    nrm = sb("f_nrm", [P, TPB, P], stack=st)
                    hT = sb("f_hT", [P, SEQ], stack=st)
                    hot = sb("f_hot", [P, TPB, E0, CAP], stack=st)
                    hotT = sb("f_hotT", [P, 4, SEQ], stack=st)
                    eoT = sb("f_eoT", [P, SLOTS], stack=st)
                    eo = sb("f_eo", [P, 4, D], stack=st)
                    ge = sb("f_ge", [P, 2, SEQ], stack=st)
                    hs = sb("f_hs", [P, 2, SEQ], stack=st)
                    ps_t = bank("f_ps_t", st)
                    ps_p = bank("f_ps_p", st, 2)
                    ps_e = bank("f_ps_e", st)
                    ps_g = bank("f_ps_g", st)
                    ps_u = bank("f_ps_u", st)
                    ps_o = bank("f_ps_o", st)
                    with pool.loop_block(NB) as block:
                        @block.vector
                        def _(dve):
                            with dve.Fori(0, NB) as i:
                                norm_tiles(dve, fr_f.nrm, nrm, x_res, i * TPB, TPB, rstd, fr_f.tps.last(i, 1))
                                dve.wait_ge(*f_pt.last(i, 2))
                                for h in range(TPB):
                                    pl = place[:, ds(i * TPB + h, 1), :].rearrange("p o e -> p (o e)")
                                    dve.tensor_tensor(hot[:, h], pl.unsqueeze(2).to_broadcast([P, E0, CAP]),
                                                      c("iota").unsqueeze(1).to_broadcast([P, E0, CAP]),
                                                      ALU.is_equal).then_inc(f_h0.sem, 1)
                                for h in range(TPB):
                                    dve.wait_ge(*f_h0.now(i, h + 1))
                                    sc = score[:, ds(i * TPB + h, 1), :].rearrange("p o e -> p (o e)")
                                    dve.tensor_tensor(hot[:, h], hot[:, h], sc.unsqueeze(2).to_broadcast([P, E0, CAP]),
                                                      ALU.mult).then_inc(f_p.sem, 1)
                                dve.wait_ge(*f_eo.last(i, 1))
                                dve.tensor_copy(eoT[:, :].rearrange("p (e s) -> p e s", e=E0),
                                                xg[:, :, ds(i, 1), :].rearrange("p e o s -> p e (o s)")
                                                ).then_inc(f_st.sem, 1)
                                dve.wait_ge(*f_ge.now(i, 1))
                                dve.wait_ge(*f_o.last(i, 1))
                                dve.tensor_tensor(hs[:, :, :], ge[:, :, :],
                                                  ps_u[:, 0, :].rearrange("p (f t) -> p f t", f=2),
                                                  ALU.mult).then_inc(f_h.sem, 1)
                                dve.wait_ge(*f_eo.now(i, 1))
                                dve.tensor_copy(eo[:, :, :].rearrange("p k d -> p (k d)"), ps_e[:, 0, :]
                                                ).then_inc(f_eoc.sem, 1)
                                dve.wait_ge(*f_o.now(i, 1))
                                xs = x_res[:, ds(i * TPB, TPB), :]
                                dve.tensor_tensor(xs, xs, ps_o[:, 0, 0:SEQ].rearrange("p (t d) -> p t d", t=TPB),
                                                  ALU.add).then_inc(f_x.sem, 1)

                        @block.tensor
                        def _(pe):
                            with pe.Fori(0, NB) as i:
                                turn_tiles(pe, fr_f.tps, ps_t[:, 0, :], nrm, TPB, fr_f.nrm.now(i, 1),
                                           fr_f.hT.last(i, 1))
                                pe.wait_ge(*fr_f.hT.now(i, 1))
                                pe.wait_ge(*f_h.last(i, 1))
                                for f in range(2):
                                    pe.matmul(ps_g[:, 0, f * SEQ:(f + 1) * SEQ], c("wsg", f * P, P), hT[:, :],
                                              start=True, stop=True)
                                    ins = pe.matmul(ps_u[:, 0, f * SEQ:(f + 1) * SEQ], c("wsu", f * P, P), hT[:, :],
                                                    start=True, stop=True)
                                ins.then_inc(f_gu.sem, 1)
                                for n in range(2):
                                    pe.wait_ge(*f_p.now(i, 2))
                                    pe.wait_ge(*f_ptc.last(i, n + 1))
                                    for k in range(2 * n, 2 * n + 2):
                                        for h in range(TPB):
                                            ins = pe.transpose(
                                                ps_p[:, n, (k % 2) * SEQ + h * P:(k % 2) * SEQ + (h + 1) * P],
                                                hot[:, h].rearrange("p e s -> p (e s)")[:, k * P:(k + 1) * P], ident)
                                    ins.then_inc(f_pt.sem, 1)
                                pe.wait_ge(*f_st.now(i, 1))
                                pe.wait_ge(*f_eoc.last(i, 1))
                                for k in range(4):
                                    ins = pe.transpose(ps_e[:, 0, k * D:(k + 1) * D], eoT[:, k * P:(k + 1) * P], ident)
                                ins.then_inc(f_eo.sem, 1)
                                pe.wait_ge(*f_h.now(i, 1))
                                pe.wait_ge(*f_ptc.now(i, 2))
                                pe.wait_ge(*f_eoc.now(i, 1))
                                pe.wait_ge(*f_x.last(i, 1))
                                for h in range(TPB):
                                    dst = ps_o[:, 0, h * D:(h + 1) * D]
                                    for f in range(2):
                                        pe.matmul(dst, hs[:, f, h * P:(h + 1) * P], c("wsd", f * D, D),
                                                  start=(f == 0), stop=False)
                                    for k in range(4):
                                        ins = pe.matmul(dst, hotT[:, k, h * P:(h + 1) * P], eo[:, k, :],
                                                        start=False, stop=(k == 3))
                                ins.then_inc(f_o.sem, 1)

                        @block.scalar
                        def _(act):
                            with act.Fori(0, NB) as i:
                                act.wait_ge(*fr_f.tps.now(i, 1))
                                act.wait_ge(*f_gu.last(i, 1))
                                act.activation(hT[:, :], ps_t[:, 0, 0:SEQ], ACT.Copy).then_inc(fr_f.hT.sem, 1)
                                act.wait_ge(*f_gu.now(i, 1))
                                act.wait_ge(*f_h.last(i, 1))
                                act.activation(ge[:, :, :], ps_g[:, 0, :].rearrange("p (f t) -> p f t", f=2),
                                               ACT.Gelu).then_inc(f_ge.sem, 1)
                                for n in range(2):
                                    act.wait_ge(*f_pt.now(i, n + 1))
                                    act.wait_ge(*f_o.last(i, 1))
                                    act.activation(hotT[:, 2 * n:2 * n + 2, :],
                                                   ps_p[:, n, :].rearrange("p (k t) -> p k t", k=2),
                                                   ACT.Copy).then_inc(f_ptc.sem, 1)

        stats(x_res, twice=True)
        with ExitStack() as st:
            VW = D + 4
            nrm = sb("l_nrm", [P, TPB, P], stack=st)
            hT = sb("l_hT", [P, SEQ], stack=st)
            hgb = sb("l_hgb", [P, 1], stack=st)
            egate = sb("l_egate", [P, SEQ], stack=st)
            gate = sb("l_gate", [P, SEQ], stack=st)
            qk = sb("l_qk", [P, 2, SEQ], stack=st)
            low = sb("l_low", [P, 2, SEQ], stack=st)
            v1 = sb("l_v", [P, TPB, VW], stack=st)
            am = sb("l_am", [P, P + SEQ], stack=st)
            den = sb("l_den", [P, TPB], stack=st)
            ps_t = bank("l_ps_t", st)
            ps_q = bank("l_ps_q", st)
            ps_g = bank("l_ps_g", st)
            ps_v = bank("l_ps_v", st)
            ps_a = bank("l_ps_a", st)
            ps_o = bank("l_ps_o", st)
            with pool.loop_block(NB) as block:
                k_set = n_chain[0] + 2

                @block.vector
                def _(dve):
                    link(dve, dve.tensor_scalar(hgb[:, :], c("gb1"), 0.5, None, ALU.mult))
                    link(dve, dve.memset(v1[:, :, :], 1.0))
                    with dve.Fori(0, NB) as i:
                        norm_tiles(dve, fr_l.nrm, nrm, x_res, i * TPB, TPB, rstd2, fr_l.tps.last(i, 1))
                        dve.wait_ge(*l_eg.now(i, 1))
                        dve.tensor_scalar(gate[:, :], egate[:, :], 0.5, 0.5, ALU.mult, ALU.add).then_inc(l_d1.sem, 1)
                        dve.wait_ge(*l_a.last(i, 1))
                        dve.wait_ge(*l_pr.now(i, 2))
                        dve.tensor_scalar(qk[:, 0, :], ps_q[:, 0, 0:SEQ], c("qkvb", 0, 1), None, ALU.add
                                          ).then_inc(l_d1.sem, 1)
                        dve.wait_ge(*l_d1.now(i, 2))
                        dve.scalar_tensor_tensor(qk[:, 1, :], ps_q[:, 0, SEQ:2 * SEQ], c("qkvb", 1, 1), gate[:, :],
                                                 ALU.add, ALU.mult).then_inc(l_d1.sem, 1)
                        dve.wait_ge(*l_d1.now(i, 3))
                        dve.tensor_scalar(low[:, :, :], qk[:, :, :], 0.0, None, ALU.min).then_inc(l_d1.sem, 1)
                        dve.wait_ge(*l_v.now(i, 1))
                        dve.tensor_copy(v1[:, :, 0:D], ps_v[:, 0, 0:SEQ].rearrange("p (t d) -> p t d", t=TPB)
                                        ).then_inc(l_d1.sem, 1)
                        dve.wait_ge(*l_ex.now(i, 1))
                        dve.scalar_tensor_tensor(qk[:, :, :], qk[:, :, :], 0.0, low[:, :, :], ALU.max, ALU.add
                                                 ).then_inc(l_qk.sem, 1)
                        dve.wait_ge(*l_a.now(i, 1))
                        dve.wait_ge(*l_o.last(i, 1))
                        dve.tensor_tensor(am[:, :], ps_a[:, 0, 0:P + SEQ], c("tri_st"), ALU.mult).then_inc(l_am.sem, 1)
                        dve.wait_ge(*l_o.now(i, 1))
                        ov = ps_o[:, 0, 0:TPB * VW].rearrange("p (t w) -> p t w", t=TPB)
                        dve.tensor_scalar(den[:, :], ov[:, :, D], 1e-6, None, ALU.add).then_inc(l_x.sem, 1)
                        dve.wait_ge(*l_x.now(i, 1))
                        dve.reciprocal(den[:, :], den[:, :]).then_inc(l_x.sem, 1)
                        dve.wait_ge(*l_x.now(i, 2))
                        for t in range(TPB):
                            xs = x_res[:, ds(i * TPB + t, 1), :].rearrange("p o d -> p (o d)")
                            ins = dve.scalar_tensor_tensor(xs, ov[:, t, 0:D], den[:, t:t + 1], xs, ALU.mult, ALU.add)
                        ins.then_inc(l_x.sem, 1)

                @block.tensor
                def _(pe):
                    pe.wait_ge(chained, k_set)
                    with pe.Fori(0, NB) as i:
                        turn_tiles(pe, fr_l.tps, ps_t[:, 0, :], nrm, TPB, fr_l.nrm.now(i, 1), fr_l.hT.last(i, 1))
                        pe.wait_ge(*fr_l.hT.now(i, 1))
                        pe.wait_ge(*l_eg.last(i, 1))
                        pe.matmul(ps_g[:, 0, 0:SEQ], c("gw1"), hT[:, :], start=True, stop=True).then_inc(l_pr.sem, 1)
                        pe.wait_ge(*l_d1.last(i, 3))
                        pe.matmul(ps_q[:, 0, 0:SEQ], c("qkvw", 0, D), hT[:, :], start=True, stop=True)
                        pe.matmul(ps_q[:, 0, SEQ:2 * SEQ], c("qkvw", D, D), hT[:, :], start=True, stop=True
                                  ).then_inc(l_pr.sem, 1)
                        pe.wait_ge(*l_d1.last(i, 5))
                        for t in range(TPB):
                            dst = ps_v[:, 0, t * D:(t + 1) * D]
                            pe.matmul(dst, c("ones", rows=1), c("vb", rows=1), start=True, stop=False)
                            ins = pe.matmul(dst, hT[:, t * P:(t + 1) * P], c("qkvw", 2 * D, D), start=False, stop=True)
                        ins.then_inc(l_v.sem, 1)
                        pe.wait_ge(*l_qk.now(i, 1))
                        pe.wait_ge(*l_am.last(i, 1))
                        pe.matmul(ps_a[:, 0, 0:SEQ], qk[:, 1, 0:P], qk[:, 0, :], start=True, stop=True)
                        pe.matmul(ps_a[:, 0, SEQ:SEQ + P], qk[:, 1, P:SEQ], qk[:, 0, P:SEQ], start=True, stop=True
                                  ).then_inc(l_a.sem, 1)
                        pe.wait_ge(*l_am.now(i, 1))
                        pe.wait_ge(*l_d1.now(i, 5))
                        pe.wait_ge(*l_x.last(i, 3))
                        pe.matmul(ps_o[:, 0, 0:VW], am[:, 0:P], v1[:, 0, :], start=True, stop=True)
                        pe.matmul(ps_o[:, 0, VW:2 * VW], am[:, P:SEQ], v1[:, 0, :], start=True, stop=False)
                        pe.matmul(ps_o[:, 0, VW:2 * VW], am[:, SEQ:SEQ + P], v1[:, 1, :], start=False, stop=True
                                  ).then_inc(l_o.sem, 1)

                @block.scalar
                def _(act):
                    act.wait_ge(chained, k_set)
                    with act.Fori(0, NB) as i:
                        act.wait_ge(*fr_l.tps.now(i, 1))
                        act.wait_ge(*l_v.last(i, 1))
                        act.activation(hT[:, :], ps_t[:, 0, 0:SEQ], ACT.Identity, bias=c("lnb1"), scale=c("lng1")
                                       ).then_inc(fr_l.hT.sem, 1)
                        act.wait_ge(*l_pr.now(i, 1))
                        act.wait_ge(*l_d1.last(i, 1))
                        act.activation(egate[:, :], ps_g[:, 0, 0:SEQ], ACT.Tanh, bias=hgb[:, :], scale=0.5
                                       ).then_inc(l_eg.sem, 1)
                        act.wait_ge(*l_d1.now(i, 4))
                        act.activation(low[:, :, :], low[:, :, :], ACT.Exp).then_inc(l_ex.sem, 1)

        def experts(tag, acc, h_all, comb, w_in, n_exp, f_dim, func):
            wa, wb, used, hid, acted_h, outs, added = moes[tag]
            nf = f_dim // P
            loads = [wa, wb]
            with ExitStack() as st:
                w = [sb(f"{tag}_w{j}", [P, 2 * f_dim + nf + U], stack=st) for j in range(2)]
                hs = [sb(f"{tag}_hs{j}", [P, nf, U], stack=st) for j in range(2)]
                ps_h = bank(f"{tag}_ps_h", st, 4)
                ps_o = bank(f"{tag}_ps_o", st, 2)
                for e in range(n_exp):
                    b = e % 2
                    o_b1, o_b2 = 2 * f_dim, 2 * f_dim + nf
                    with pool.loop_block(NU // 2) as block:
                        @block.sync
                        def _(sp):
                            for n in ([0, 1] if e == 0 else [e + 1]):
                                if n < n_exp:
                                    sp.dma_start(w[n % 2][:, :], w_in[n]).then_inc(loads[n % 2], 16)

                        @block.tensor
                        def _(pe):
                            pe.wait_ge(loads[b], 16 * (e // 2 + 1))
                            with pe.Fori(0, NU // 2) as i:
                                for j in range(2):
                                    for f in range(nf):
                                        k = (j * nf + f) % 4
                                        if nf == 4:
                                            pe.wait_ge(*(acted_h[1].last(i, f + 1) if j == 0
                                                         else acted_h[0].now(i, f + 1)))
                                        else:
                                            pe.wait_ge(*acted_h[j].last(i, f + 1))
                                        pe.matmul(ps_h[:, k, :], w[b][:, f * P:(f + 1) * P],
                                                  h_all[:, ds((i * 2 + j) * U, U)], start=True, stop=True
                                                  ).then_inc(hid[j].sem, 1)
                                for j in range(2):
                                    pe.wait_ge(*added[j].last(i, UT))
                                    pe.matmul(ps_o[:, j, :], c("ones", rows=1), w[b][0:1, o_b2:o_b2 + U],
                                              start=True, stop=False, skip_group_check=True)
                                    for f in range(nf):
                                        pe.wait_ge(*acted_h[j].now(i, f + 1))
                                        for t in range(UT):
                                            ins = pe.matmul(ps_o[:, j, t * D:(t + 1) * D], hs[j][:, f, t * P:(t + 1) * P],
                                                            w[b][:, f_dim + f * D:f_dim + (f + 1) * D], start=False,
                                                            stop=(f == nf - 1 and t == UT - 1), skip_group_check=True)
                                    ins.then_inc(outs[j].sem, 1)

                        @block.scalar
                        def _(act):
                            act.wait_ge(loads[b], 16 * (e // 2 + 1))
                            with act.Fori(0, NU // 2) as i:
                                for j in range(2):
                                    for f in range(nf):
                                        act.wait_ge(*hid[j].now(i, f + 1))
                                        act.wait_ge(*outs[j].last(i, 1))
                                        act.activation(hs[j][:, f, :], ps_h[:, (j * nf + f) % 4, :], func,
                                                       bias=w[b][:, o_b1 + f:o_b1 + f + 1]).then_inc(acted_h[j].sem, 1)

                        @block.vector
                        def _(dve):
                            with dve.Fori(0, NU // 2) as i:
                                for j in range(2):
                                    dve.wait_ge(*outs[j].now(i, 1))
                                    for t in range(UT):
                                        tile = (i * 2 + j) * UT + t
                                        xs = acc[:, ds(tile, 1), :].rearrange("p o d -> p (o d)")
                                        ce = comb[:, ds(tile, 1), e:e + 1].rearrange("p o e -> p (o e)")
                                        dve.scalar_tensor_tensor(xs, ps_o[:, j, t * D:(t + 1) * D], ce, xs,
                                                                 ALU.mult, ALU.add).then_inc(added[j].sem, 1)

        def pick(dve, sel, lg, m, w3, n):
            link(dve, dve.tensor_reduce(m, lg, AX, ALU.max))
            link(dve, dve.tensor_tensor(sel, lg, m.unsqueeze(2).to_broadcast([P, NT, n]), ALU.is_equal))
            rank = c("rank", 0, n).unsqueeze(1).to_broadcast([P, NT, n])
            link(dve, dve.tensor_tensor(sel, sel, rank, ALU.mult))
            link(dve, dve.tensor_reduce(w3, sel, AX, ALU.max))
            link(dve, dve.tensor_tensor(sel, sel, w3.unsqueeze(2).to_broadcast([P, NT, n]), ALU.is_equal))

        def over_tiles(v, n):
            return v.unsqueeze(2).to_broadcast([P, NT, n])

        stats(x_res)
        with ExitStack() as st1:
            h_all = sb("h_all1", [P, NT * P], stack=st1)
            comb = sb("comb1", [P, NT, E1 + 1], stack=st1)
            lg = sb("lg1", [P, NT, E1], stack=st1)
            route("m1", x_res, c("gate1"), c("gate1b", rows=1), E1, lg, h_all)
            with ExitStack() as st:
                s1, s2 = (sb(f"m1_sel{j}", [P, NT, E1], stack=st) for j in range(2))
                m1, m2, t1 = (sb(f"m1_t{j}", [P, NT], stack=st) for j in range(3))
                with nc.Block() as block:
                    k0 = n_chain[0]

                    @block.vector
                    def _(dve):
                        link(dve, dve.memset(comb[:, :, :], 1.0))
                        pick(dve, s1[:, :, :], lg[:, :, :], m1[:, :], t1[:, :], E1)
                        link(dve, dve.scalar_tensor_tensor(lg[:, :, :], s1[:, :, :], -BIG, lg[:, :, :], ALU.mult, ALU.add))
                        pick(dve, s2[:, :, :], lg[:, :, :], m2[:, :], t1[:, :], E1)
                        link(dve, dve.tensor_tensor(m2[:, :], m2[:, :], m1[:, :], ALU.subtract))
                        n_act[0] += 1
                        dve.wait_ge(acted, n_act[0])
                        link(dve, dve.tensor_scalar(t1[:, :], m2[:, :], 1.0, None, ALU.add))
                        link(dve, dve.reciprocal(m1[:, :], t1[:, :]))
                        link(dve, dve.tensor_tensor(m2[:, :], m2[:, :], m1[:, :], ALU.mult))
                        link(dve, dve.tensor_tensor(s1[:, :, :], s1[:, :, :], over_tiles(m1[:, :], E1), ALU.mult))
                        link(dve, dve.tensor_tensor(s2[:, :, :], s2[:, :, :], over_tiles(m2[:, :], E1), ALU.mult))
                        link(dve, dve.tensor_tensor(comb[:, :, 0:E1], s1[:, :, :], s2[:, :, :], ALU.add))

                    @block.scalar
                    def _(act):
                        act.wait_ge(chained, k0 + 13)
                        act.activation(m2[:, :], m2[:, :], ACT.Exp).then_inc(acted, 1)
            experts("e1", x_res, h_all, comb, w1_in, E1 + 1, F1, ACT.Gelu)

        def attention(tag, causal, src, dst, w):
            fr, s = atts[tag]
            scale = HD ** -0.5
            low_rank = w["cq"] is not None
            with ExitStack() as st:
                nrm = sb(f"{tag}_nrm", [P, TPB, P], stack=st)
                hT = sb(f"{tag}_hT", [P, SEQ], stack=st)
                cq = sb(f"{tag}_cq", [32, 2, SEQ], stack=st)
                qx = sb(f"{tag}_qx", [P, HG, SEQ], stack=st)
                kx = sb(f"{tag}_kx", [P, HG, SEQ], stack=st)
                vx = sb(f"{tag}_vx", [P, TPB, NH, 32], stack=st)
                mx = sb(f"{tag}_mx", [P, HG, 4, TPB], stack=st)
                mp = sb(f"{tag}_mp", [P, TPB, HG, P], stack=st)
                pt = [sb(f"{tag}_pt{j}", [P, 2, TPB, SEQ], stack=st) for j in range(2)]
                ot = sb(f"{tag}_ot", [P, HG, SEQ], stack=st)
                rec = sb(f"{tag}_rec", [P, TPB, NH], stack=st)
                on = sb(f"{tag}_on", [P, TPB, NH, HD], stack=st)
                oT = sb(f"{tag}_oT", [P, SEQ], stack=st)
                if causal:
                    msk = sb(f"{tag}_msk", [P, 3 * P], stack=st)
                    mskb = sb(f"{tag}_mskb", [P, 3 * P], BF16, stack=st)
                ps_s = [bank(f"{tag}_ps_s{j}", st, 2) for j in range(2)]
                ps_1 = bank(f"{tag}_ps_1", st, 2)
                ps_2 = bank(f"{tag}_ps_2", st, 2)
                steps = NB

                with pool.loop_block(steps) as block:
                    k0 = n_chain[0]

                    if causal:
                        @block.sync
                        def _(sp):
                            sp.dma_start(msk[:, :], maskb_in).then_inc(loaded, 16)

                    @block.vector
                    def _(dve):
                        dve.memset(vx[:, :, :, :], 0.0).then_inc(chained, 1)
                        dve.memset(mp[:, :, :, :], 0.0).then_inc(chained, 1)
                        n_chain[0] += 2
                        dve.wait_ge(chained, n_chain[0])
                        link(dve, dve.memset(vx[:, :, :, HD], 1.0))
                        if causal:
                            dve.wait_ge(loaded, 48)
                            link(dve, dve.tensor_copy(mskb[:, :], msk[:, :]))
                        with dve.Fori(0, steps) as i:
                            norm_tiles(dve, fr.nrm, nrm, src, i * TPB, TPB, rstd, fr.tps.last(i, 1),
                                       None if dst is src else s["x"].last(i, 1))
                            for n in range(2):
                                dve.wait_ge(*s["pr"].now(i, 2))
                                if n == 0:
                                    dve.wait_ge(*s["s2"].last(i, 8))
                                dve.tensor_tensor(kx[:, 2 * n:2 * n + 2, :],
                                                  ps_1[:, n, :].rearrange("p (g t) -> p g t", g=2),
                                                  w["bk"][:, 2 * n:2 * n + 2].unsqueeze(2).to_broadcast([P, 2, SEQ]),
                                                  ALU.add).then_inc(s["qk"].sem, 1)
                            dve.wait_ge(*s["pr"].now(i, 3))
                            dve.wait_ge(*s["pv"].last(i, 4))
                            dve.tensor_copy(vx[:, :, :, 0:HD],
                                            ps_2[:, 0, 0:SEQ].rearrange("p (t h e) -> p t h e", t=TPB, h=NH)
                                            ).then_inc(s["v"].sem, 1)
                            for n in range(8):
                                g, jj = n // 2, n % 2
                                dve.wait_ge(*s["s1"].now(i, n + 1))
                                sv = ps_s[jj][:, :, :].rearrange("p j (q k) -> p j q k", q=TPB)
                                m2 = mx[:, g, 2 * jj:2 * jj + 2, :]
                                if causal:
                                    dve.tensor_reduce(m2[:, :, 0], sv[:, :, 0, 0:P], AX, ALU.max)
                                    dve.tensor_reduce(m2[:, :, 1], sv[:, :, 1, :], AX, ALU.max).then_inc(s["mx"].sem, 1)
                                else:
                                    dve.tensor_reduce(m2, sv, AX, ALU.max).then_inc(s["mx"].sem, 1)
                            dve.wait_ge(*s["mx"].now(i, 8))
                            dve.wait_ge(*s["mt"].last(i, 1))
                            mpv = mp[:, :, :, :].rearrange("p q g (j r) -> p q g j r", j=4)
                            for q in range(TPB):
                                ins = dve.tensor_scalar(mpv[:, q, :, :, HD], mx[:, :, :, q], -1.0, None, ALU.mult)
                            ins.then_inc(s["mx"].sem, 1)
                            dve.wait_ge(*s["mt"].now(i, 1))
                            dve.tensor_tensor(qx[:, :, :].rearrange("p g t -> p (g t)"),
                                              qx[:, :, :].rearrange("p g t -> p (g t)"),
                                              ps_1[:, :, :].rearrange("p k n -> p (k n)"), ALU.add).then_inc(s["qm"].sem, 1)
                            for g in range(HG):
                                dve.wait_ge(*s["pv"].now(i, g + 1))
                                if g == 0:
                                    dve.wait_ge(*s["tt"].last(i, 1))
                                dve.tensor_copy(ot[:, g, :], ps_2[:, g % 2, 0:SEQ]).then_inc(s["ot"].sem, 1)
                            dve.wait_ge(*s["tt"].now(i, 1))
                            tv = ps_1[:, :, :].rearrange("p q (h r) -> p q h r", r=32)
                            dve.reciprocal(rec[:, :, :], tv[:, :, :, HD]).then_inc(s["nr"].sem, 1)
                            dve.wait_ge(*s["nr"].now(i, 1))
                            dve.wait_ge(*s["t2"].last(i, 1))
                            for q in range(TPB):
                                ins = dve.tensor_tensor(on[:, q], tv[:, q, :, 0:HD],
                                                        rec[:, q, :].unsqueeze(2).to_broadcast([P, NH, HD]), ALU.mult)
                            ins.then_inc(s["nr"].sem, 1)
                            dve.wait_ge(*s["o"].now(i, 1))
                            xd = dst[:, ds(i * TPB, TPB), :]
                            base = xd if dst is src else nrm[:, :, :]
                            dve.tensor_tensor(xd, base, ps_2[:, 1, 0:SEQ].rearrange("p (t d) -> p t d", t=TPB),
                                              ALU.add).then_inc(s["x"].sem, 1)

                    k_set = k0 + 3 + (1 if causal else 0)

                    @block.tensor
                    def _(pe):
                        pe.wait_ge(chained, k_set)
                        with pe.Fori(0, steps) as i:
                            turn_tiles(pe, fr.tps, ps_1[:, 0, :], nrm, TPB, fr.nrm.now(i, 1), s["nr"].last(i, 2))
                            pe.wait_ge(*fr.hT.now(i, 1))
                            pe.wait_ge(*s["x"].last(i, 1))
                            if low_rank:
                                for n, name in enumerate(("cq", "ckv")):
                                    ins = pe.matmul(ps_1[0:32, 1, n * SEQ:(n + 1) * SEQ], w[name], hT[:, :],
                                                    start=True, stop=True)
                                ins.then_inc(s["low"].sem, 1)
                                pe.wait_ge(*s["lowc"].now(i, 1))
                                q_in, kv_in = cq[:, 0, :], cq[:, 1, :]
                            else:
                                q_in = kv_in = hT[:, :]
                            for n, (wn, ps, x_in_) in enumerate((("q", ps_2, q_in), ("k", ps_1, kv_in))):
                                for g in range(HG):
                                    ins = pe.matmul(ps[:, g // 2, (g % 2) * SEQ:(g % 2 + 1) * SEQ],
                                                    w[wn][:, g * P:(g + 1) * P], x_in_, start=True, stop=True)
                                ins.then_inc(s["pr"].sem, 1)
                            pe.wait_ge(*s["qq"].now(i, 2))
                            for t in range(TPB):
                                v_dst = ps_2[:, 0, t * D:(t + 1) * D]
                                if w["bv"] is not None:
                                    pe.matmul(v_dst, c("ones", rows=1), w["bv"], start=True, stop=False)
                                ins = pe.matmul(v_dst, kv_in[:, t * P:(t + 1) * P], w["v"],
                                                start=(w["bv"] is None), stop=True)
                            ins.then_inc(s["pr"].sem, 1)

                            def strip(t, g, j, n):
                                return t[32 * j:32 * j + n, g, :]

                            for n in range(8):
                                g, jj = n // 2, n % 2
                                if n < 2:
                                    pe.wait_ge(*s["qk"].now(i, 2))
                                    pe.wait_ge(*s["ex"].last(i, 7 + n))
                                else:
                                    pe.wait_ge(*s["mx"].now(i, n - 1))
                                for h in range(2):
                                    j = 2 * jj + h
                                    for q in range(TPB):
                                        nk = (q + 1) * P if causal else SEQ
                                        o = ps_s[jj][:, h, q * SEQ:q * SEQ + nk]
                                        ins = pe.matmul(o, strip(qx, g, j, HD)[:, q * P:(q + 1) * P],
                                                        strip(kx, g, j, HD)[:, 0:nk], start=True, stop=not causal)
                                        if causal:
                                            ins = pe.matmul(o[:, q * P:nk], mskb[:, 0:P], mskb[:, P:2 * P],
                                                            start=False, stop=True)
                                ins.then_inc(s["s1"].sem, 1)
                            pe.wait_ge(*s["mx"].now(i, 9))
                            pe.wait_ge(*s["qk"].now(i, 2))
                            for g in range(HG):
                                for q in range(TPB):
                                    ins = pe.transpose(ps_1[:, g // 2, (g % 2) * SEQ + q * P:(g % 2) * SEQ + (q + 1) * P],
                                                       mp[:, q, g, :], ident)
                            ins.then_inc(s["mt"].sem, 1)

                            def weigh(n):
                                g, jj = n // 2, n % 2
                                pe.wait_ge(*s["ex"].now(i, n + 1))
                                if jj == 0:
                                    if g == 0:
                                        pe.wait_ge(*s["v"].now(i, 1))
                                    if g >= 2:
                                        pe.wait_ge(*s["ot"].now(i, g - 1))
                                for h in range(2):
                                    j = 2 * jj + h
                                    o = ps_2[32 * j:32 * j + 32, g % 2, 0:SEQ]
                                    for t in range(TPB):
                                        q0 = t * P if causal else 0
                                        ins = pe.matmul(o[:, q0:], vx[:, t, 4 * g + j, :], pt[jj][:, h, t, q0:],
                                                        start=(t == 0), stop=(t == TPB - 1))
                                if jj == 1:
                                    ins.then_inc(s["pv"].sem, 1)
                                else:
                                    ins.then_inc(s["half"].sem, 1)

                            for n in range(8):
                                g, jj = n // 2, n % 2
                                if n < 2:
                                    pe.wait_ge(*s["qm"].now(i, 1))
                                    pe.wait_ge(*s["mx"].now(i, 7 + n))
                                else:
                                    pe.wait_ge(*s["ex"].now(i, n - 1))
                                for h in range(2):
                                    j = 2 * jj + h
                                    for t in range(TPB):
                                        q0 = t * P if causal else 0
                                        o = ps_s[jj][:, h, t * SEQ:(t + 1) * SEQ]
                                        ins = pe.matmul(o[:, q0:], strip(kx, g, j, HD + 1)[:, t * P:(t + 1) * P],
                                                        strip(qx, g, j, HD + 1)[:, q0:], start=True, stop=not causal)
                                        if causal:
                                            ins = pe.matmul(o[:, q0:q0 + P], mskb[:, 0:P], mskb[:, 2 * P:3 * P],
                                                            start=False, stop=True)
                                ins.then_inc(s["s2"].sem, 1)
                                if n:
                                    weigh(n - 1)
                            weigh(7)
                            pe.wait_ge(*s["ot"].now(i, 4))
                            for q in range(TPB):
                                for g in range(HG):
                                    ins = pe.transpose(ps_1[:, q, g * P:(g + 1) * P], ot[:, g, q * P:(q + 1) * P], ident)
                            ins.then_inc(s["tt"].sem, 1)
                            pe.wait_ge(*s["nr"].now(i, 2))
                            for q in range(TPB):
                                ins = pe.transpose(ps_2[:, 0, q * P:(q + 1) * P],
                                                   on[:, q].rearrange("p h e -> p (h e)"), ident)
                            ins.then_inc(s["t2"].sem, 1)
                            pe.wait_ge(*s["t2c"].now(i, 1))
                            for t in range(TPB):
                                o = ps_2[:, 1, t * D:(t + 1) * D]
                                if w["bo"] is not None:
                                    pe.matmul(o, c("ones", rows=1), w["bo"], start=True, stop=False)
                                ins = pe.matmul(o, oT[:, t * P:(t + 1) * P], w["o"], start=(w["bo"] is None), stop=True)
                            ins.then_inc(s["o"].sem, 1)

                    @block.scalar
                    def _(act):
                        with act.Fori(0, steps) as i:
                            act.wait_ge(*fr.tps.now(i, 1))
                            act.wait_ge(*s["pr"].last(i, 3))
                            act.activation(hT[:, :], ps_1[:, 0, 0:SEQ], ACT.Copy).then_inc(fr.hT.sem, 1)
                            if low_rank:
                                act.wait_ge(*s["low"].now(i, 1))
                                act.activation(cq[:, :, :], ps_1[0:32, 1, :].rearrange("p (n t) -> p n t", n=2), ACT.Copy
                                               ).then_inc(s["lowc"].sem, 1)
                            act.wait_ge(*s["pr"].now(i, 1))
                            act.wait_ge(*s["s2"].last(i, 8))
                            for g in range(HG):
                                x = ps_2[:, g // 2, (g % 2) * SEQ:(g % 2 + 1) * SEQ]
                                if w["bq"] is None:
                                    ins = act.activation(qx[:, g, :], x, ACT.Copy)
                                else:
                                    ins = act.activation(qx[:, g, :], x, ACT.Identity, bias=w["bq"][:, g:g + 1])
                                if g % 2:
                                    ins.then_inc(s["qq"].sem, 1)
                            for n in range(8):
                                g, jj = n // 2, n % 2
                                act.wait_ge(*s["s2"].now(i, n + 1))
                                if n >= 2:
                                    act.wait_ge(*(s["half"].now(i, g) if jj == 0 else s["pv"].now(i, g)))
                                else:
                                    act.wait_ge(*s["pv"].last(i, 4))
                                pv = pt[jj][:, :, :, :]
                                sv = ps_s[jj][:, :, :].rearrange("p j (t q) -> p j t q", t=TPB)
                                if causal:
                                    act.activation(pv[:, :, 0, :], sv[:, :, 0, :], ACT.Exp, scale=scale)
                                    act.activation(pv[:, :, 1, P:], sv[:, :, 1, P:], ACT.Exp, scale=scale
                                                   ).then_inc(s["ex"].sem, 1)
                                else:
                                    act.activation(pv, sv, ACT.Exp, scale=scale).then_inc(s["ex"].sem, 1)
                            act.wait_ge(*s["t2"].now(i, 1))
                            act.wait_ge(*s["o"].last(i, 1))
                            act.activation(oT[:, :], ps_2[:, 0, 0:SEQ], ACT.Copy).then_inc(s["t2c"].sem, 1)

        stats(x_res)
        attention("h2", True, x_res, x_res,
                  dict(cq=c("wdq"), ckv=c("wdkv"), q=c("wuq", rows=32), k=c("wuk", rows=32), v=c("wuv", rows=32),
                       bq=None, bk=c("kone"), bv=None, o=c("wo2"), bo=None))

        stats(x_res)
        RA = (E2 + 1) * R2
        with ExitStack() as st2:
            h_all = sb("h_all2", [P, NT * P], stack=st2)
            comb = sb("comb2", [P, NT, E2 + 1], stack=st2)
            lg = sb("lg2", [P, NT, E2], stack=st2)
            route("m2", x_res, c("rout"), c("routb", rows=1), E2, lg, h_all)
            with ExitStack() as st:
                s1, s2, ex = (sb(f"m2_sel{j}", [P, NT, E2], stack=st) for j in range(3))
                m1, m2, t1 = (sb(f"m2_t{j}", [P, NT], stack=st) for j in range(3))
                with nc.Block() as block:
                    k0 = n_chain[0]

                    @block.vector
                    def _(dve):
                        link(dve, dve.memset(comb[:, :, :], 1.0))
                        softmax_rows(dve, lg[:, :, :], ex[:, :, :], m1[:, :], t1[:, :], E2)
                        link(dve, dve.tensor_tensor(ex[:, :, :], ex[:, :, :], over_tiles(t1[:, :], E2), ALU.mult))
                        pick(dve, s1[:, :, :], lg[:, :, :], m1[:, :], t1[:, :], E2)
                        link(dve, dve.scalar_tensor_tensor(lg[:, :, :], s1[:, :, :], -BIG, lg[:, :, :], ALU.mult, ALU.add))
                        pick(dve, s2[:, :, :], lg[:, :, :], m2[:, :], t1[:, :], E2)
                        link(dve, dve.tensor_tensor(s1[:, :, :], s1[:, :, :], s2[:, :, :], ALU.add))
                        link(dve, dve.tensor_tensor(s1[:, :, :], s1[:, :, :], ex[:, :, :], ALU.mult))
                        link(dve, dve.tensor_reduce(t1[:, :], s1[:, :, :], AX, ALU.add))
                        link(dve, dve.tensor_scalar(t1[:, :], t1[:, :], 1e-6, None, ALU.add))
                        link(dve, dve.reciprocal(t1[:, :], t1[:, :]))
                        link(dve, dve.tensor_tensor(comb[:, :, 0:E2], s1[:, :, :], over_tiles(t1[:, :], E2), ALU.mult))

                    @block.scalar
                    def _(act):
                        act.wait_ge(chained, k0 + 3)
                        act.activation(ex[:, :, :], ex[:, :, :], ACT.Exp).then_inc(acted, 1)

            with ExitStack() as st:
                hT = [sb(f"m_hT{j}", [P, U], stack=st) for j in range(2)]
                hw = [sb(f"m_hw{j}", [P, UT, RA], stack=st) for j in range(2)]
                hwT = [sb(f"m_hwT{j}", [RA, U], stack=st) for j in range(2)]
                ps_a = bank("m_ps_a", st, 2)
                ps_t = bank("m_ps_t", st, 2)
                ps_o = bank("m_ps_o", st, 2)
                with pool.loop_block(NU // 2) as block:
                    @block.vector
                    def _(dve):
                        with dve.Fori(0, NU // 2) as i:
                            for j in range(2):
                                first = (i * 2 + j) * UT
                                dve.wait_ge(*m_h.now(i, j + 1))
                                dve.wait_ge(*m_tr.last(i, j + 1))
                                for t in range(UT):
                                    cw = comb[:, ds(first + t, 1), :].rearrange("p o e -> p (o e)")
                                    ins = dve.tensor_tensor(
                                        hw[j][:, t, :].rearrange("p (e r) -> p e r", r=R2),
                                        ps_a[:, j, t * P:t * P + RA].rearrange("p (e r) -> p e r", r=R2),
                                        cw.unsqueeze(2).to_broadcast([P, E2 + 1, R2]), ALU.mult)
                                ins.then_inc(m_ts.sem, 1)
                            for j in range(2):
                                xs = x_res[:, ds((i * 2 + j) * UT, UT), :]
                                dve.wait_ge(*m_o.now(i, j + 1))
                                dve.tensor_tensor(xs, xs, ps_o[:, j, :].rearrange("p (t d) -> p t d", t=UT), ALU.add
                                                  ).then_inc(m_x.sem, 1)

                    @block.tensor
                    def _(pe):
                        with pe.Fori(0, NU // 2) as i:
                            for j in range(2):
                                pe.wait_ge(*m_c.now(i, j + 1))
                                pe.wait_ge(*m_ts.last(i, j + 1))
                                for t in range(UT):
                                    ins = pe.matmul(ps_a[:, j, t * P:t * P + RA], hT[j][:, t * P:(t + 1) * P], c("acat"),
                                                    start=True, stop=True)
                                ins.then_inc(m_h.sem, 1)
                            for j in range(2):
                                pe.wait_ge(*m_ts.now(i, j + 1))
                                pe.wait_ge(*m_tc.last(i, j + 1))
                                for t in range(UT):
                                    ins = pe.transpose(ps_t[0:RA, j, t * P:(t + 1) * P], hw[j][:, t, :], ident)
                                ins.then_inc(m_tr.sem, 1)
                            for j in range(2):
                                pe.wait_ge(*m_tc.now(i, j + 1))
                                pe.wait_ge(*m_x.last(i, j + 1))
                                for t in range(UT):
                                    o = ps_o[:, j, t * D:(t + 1) * D]
                                    pe.matmul(o, c("ones", rows=1), c("baseb", rows=1), start=True, stop=False)
                                    pe.matmul(o, hT[j][:, t * P:(t + 1) * P], c("basew"), start=False, stop=False)
                                    ins = pe.matmul(o, hwT[j][:, t * P:(t + 1) * P], c("bcat", rows=RA),
                                                    start=False, stop=True)
                                ins.then_inc(m_o.sem, 1)

                    @block.scalar
                    def _(act):
                        with act.Fori(0, NU // 2) as i:
                            for j in range(2):
                                act.wait_ge(*m_o.last(i, j + 1))
                                act.activation(hT[j][:, :], h_all[:, ds((i * 2 + j) * U, U)], ACT.Copy
                                               ).then_inc(m_c.sem, 1)
                            for j in range(2):
                                act.wait_ge(*m_tr.now(i, j + 1))
                                act.wait_ge(*m_o.last(i, j + 1))
                                act.activation(hwT[j][:, :], ps_t[0:RA, j, :], ACT.Copy).then_inc(m_tc.sem, 1)

        stats(x_res)
        with ExitStack() as st:
            nrm = [sb(f"s_nrm{j}", [P, UT, P], stack=st) for j in range(2)]
            hT = [sb(f"s_hT{j}", [P, 2, SEQ + 1], stack=st) for j in range(2)]
            mixed = [sb(f"s_mix{j}", [P, 2, SEQ], stack=st) for j in range(2)]
            rel = [sb(f"s_rel{j}", [P, 2, SEQ], stack=st) for j in range(2)]
            state = [sb(f"s_state{j}", [P, 2, SEQ], stack=st) for j in range(2)]
            dec = sb("s_dec", [P, SEQ], stack=st)
            omix = sb("s_omix", [P, 1], stack=st)
            ps_t = bank("s_ps_t", st, 2)
            ps_h = bank("s_ps_h", st, 2)
            ps_o = bank("s_ps_o", st, 2)
            with pool.loop_block(NU // 2) as block:
                k_set = n_chain[0] + 5

                @block.vector
                def _(dve):
                    for j in range(2):
                        link(dve, dve.memset(hT[j][:, :, :], 0.0))
                    link(dve, dve.memset(dec[:, :], 1.0))
                    link(dve, dve.tensor_scalar(dec[:, :], dec[:, :], c("decay"), None, ALU.mult))
                    link(dve, dve.tensor_scalar(omix[:, :], c("mix"), -1.0, 1.0, ALU.mult, ALU.add))
                    with dve.Fori(0, NU // 2) as i:
                        for j in range(2):
                            norm_tiles(dve, fr_s.nrm, nrm[j], x_res, (i * 2 + j) * UT, UT, rstd, fr_s.tps.last(i, j + 1))
                        for j in range(2):
                            dve.wait_ge(*fr_s.hT.now(i, j + 1))
                            dve.wait_ge(*s_pr.last(i, j + 1))
                            dve.tensor_scalar(mixed[j][:, :, :], hT[j][:, :, 0:SEQ], omix[:, :], None, ALU.mult
                                              ).then_inc(s_in.sem, 1)
                            dve.wait_ge(*s_in.now(i, 2 * j + 1))
                            dve.scalar_tensor_tensor(mixed[j][:, :, :], hT[j][:, :, 1:], c("mix"), mixed[j][:, :, :],
                                                     ALU.mult, ALU.add).then_inc(s_in.sem, 1)
                        for j in range(2):
                            dve.wait_ge(*s_re.now(i, j + 1))
                            dve.wait_ge(*s_o.last(i, j + 1))
                            for b in range(2):
                                dve.tensor_tensor_scan(state[j][:, b, :], dec[:, :], rel[j][:, b, :], 0.0,
                                                       ALU.mult, ALU.add).then_inc(s_sc.sem, 1)
                        for j in range(2):
                            xs = x_res[:, ds((i * 2 + j) * UT, UT), :]
                            dve.wait_ge(*s_o.now(i, j + 1))
                            dve.tensor_tensor(xs, xs, ps_o[:, j, :].rearrange("p (t d) -> p t d", t=UT), ALU.add
                                              ).then_inc(s_x.sem, 1)

                @block.tensor
                def _(pe):
                    with pe.Fori(0, NU // 2) as i:
                        for j in range(2):
                            turn_tiles(pe, fr_s.tps, ps_t[:, j, :], nrm[j], UT, fr_s.nrm.now(i, j + 1),
                                       fr_s.hT.last(i, j + 1))
                        for j in range(2):
                            pe.wait_ge(*s_in.now(i, 2 * j + 2))
                            pe.wait_ge(*s_re.last(i, j + 1))
                            pe.matmul(ps_h[:, j, :], c("win3"), mixed[j][:, :, :].rearrange("p b t -> p (b t)"),
                                      start=True, stop=True).then_inc(s_pr.sem, 1)
                        for j in range(2):
                            pe.wait_ge(*s_sc.now(i, 2 * j + 2))
                            pe.wait_ge(*s_x.last(i, j + 1))
                            for t in range(UT):
                                o = ps_o[:, j, t * D:(t + 1) * D]
                                pe.matmul(o, c("ones", rows=1), c("bout3", rows=1), start=True, stop=False)
                                ins = pe.matmul(o, state[j][:, t // TPB, (t % TPB) * P:(t % TPB + 1) * P], c("wout3"),
                                                start=False, stop=True)
                            ins.then_inc(s_o.sem, 1)

                @block.scalar
                def _(act):
                    act.wait_ge(chained, k_set)
                    with act.Fori(0, NU // 2) as i:
                        for j in range(2):
                            act.wait_ge(*fr_s.tps.now(i, j + 1))
                            act.wait_ge(*s_in.last(i, 2 * j + 2))
                            act.activation(hT[j][:, :, 1:], ps_t[:, j, :].rearrange("p (b t) -> p b t", b=2), ACT.Copy
                                           ).then_inc(fr_s.hT.sem, 1)
                        for j in range(2):
                            act.wait_ge(*s_pr.now(i, j + 1))
                            act.wait_ge(*s_sc.last(i, 2 * j + 2))
                            act.activation(rel[j][:, :, :], ps_h[:, j, :].rearrange("p (b t) -> p b t", b=2), ACT.Relu,
                                           bias=c("bin3")).then_inc(s_re.sem, 1)

        stats(x_res)
        with ExitStack() as st3:
            x2 = sb("x2", [P, NT, D], stack=st3)
            attention("h3", False, x_res, x2,
                      dict(cq=None, q=c("wq3"), k=c("wk3"), v=c("wv3"), bq=c("bq3"), bk=c("bk3"), bv=c("bv3", rows=1),
                           o=c("wo3"), bo=c("bo3", rows=1)))
            stats(x2)
            with ExitStack() as st:
                h_all = sb("h_all3", [P, NT * P], stack=st)
                comb = sb("comb3", [P, NT, E3], stack=st)
                lg = sb("lg3", [P, NT, G3 + E3], stack=st)
                route("m3", x2, c("rt3"), c("rt3b", rows=1), G3 + E3, lg, h_all, (c("g1"), c("b1")))
                with ExitStack() as stm:
                    sel, ex = (sb(f"m3_g{j}", [P, NT, G3], stack=stm) for j in range(2))
                    el = sb("m3_el", [P, NT, 2], stack=stm)
                    tmp = sb("m3_tmp", [P, NT, 2], stack=stm)
                    sel2 = sb("m3_sel2", [P, NT, 2], stack=stm)
                    m1, t1, gp = (sb(f"m3_t{j}", [P, NT], stack=stm) for j in range(3))
                    with nc.Block() as block:
                        k0 = n_chain[0]

                        @block.vector
                        def _(dve):
                            softmax_rows(dve, lg[:, :, 0:G3], ex[:, :, :], m1[:, :], gp[:, :], G3)
                            pick(dve, sel[:, :, :], lg[:, :, 0:G3], m1[:, :], t1[:, :], G3)
                            for g in range(G3):
                                eg = lg[:, :, G3 + 2 * g:G3 + 2 * g + 2]
                                sg = over_tiles(sel[:, :, g], 2)
                                link(dve, dve.tensor_tensor(el[:, :, :] if g == 0 else tmp[:, :, :], eg, sg, ALU.mult))
                                if g:
                                    link(dve, dve.tensor_tensor(el[:, :, :], el[:, :, :], tmp[:, :, :], ALU.add))
                            softmax_rows(dve, el[:, :, :], tmp[:, :, :], m1[:, :], t1[:, :], 2)
                            link(dve, dve.tensor_tensor(gp[:, :], gp[:, :], t1[:, :], ALU.mult))
                            pick(dve, sel2[:, :, :], el[:, :, :], m1[:, :], t1[:, :], 2)
                            link(dve, dve.tensor_tensor(sel2[:, :, :], sel2[:, :, :], over_tiles(gp[:, :], 2), ALU.mult))
                            for g in range(G3):
                                link(dve, dve.tensor_tensor(comb[:, :, 2 * g:2 * g + 2], sel2[:, :, :],
                                                            over_tiles(sel[:, :, g], 2), ALU.mult))

                        @block.scalar
                        def _(act):
                            act.wait_ge(chained, k0 + 2)
                            act.activation(ex[:, :, :], ex[:, :, :], ACT.Exp).then_inc(acted, 1)
                            act.wait_ge(chained, k0 + 2 + 2 + 5 + 7 + 2)
                            act.activation(tmp[:, :, :], tmp[:, :, :], ACT.Exp).then_inc(acted, 1)
                experts("e3", x2, h_all, comb, w3_in, E3, F3, ACT.Relu)

            stats(x2)
            with ExitStack() as st:
                fin = [sb(f"z_fin{j}", [P, UT, D], stack=st) for j in range(2)]
                out_t = out.rearrange("(t p) d -> p t d", p=P)
                with pool.loop_block(NU // 2) as block:
                    @block.vector
                    def _(dve):
                        with dve.Fori(0, NU // 2) as i:
                            for j in range(2):
                                first = (i * 2 + j) * UT
                                norm_tiles(dve, z_n, fin[j], x2, first, UT, rstd, z_d[j].last(i, 16))
                                dve.wait_ge(*z_n.now(i, j + 1))
                                dve.tensor_tensor(fin[j][:, :, :], fin[j][:, :, :],
                                                  c("g2").unsqueeze(1).to_broadcast([P, UT, D]), ALU.mult
                                                  ).then_inc(z_a.sem, 1)
                                dve.wait_ge(*z_a.now(i, 3 * j + 1))
                                dve.tensor_tensor(fin[j][:, :, :], fin[j][:, :, :],
                                                  c("b2").unsqueeze(1).to_broadcast([P, UT, D]), ALU.add
                                                  ).then_inc(z_a.sem, 1)
                                dve.wait_ge(*z_a.now(i, 3 * j + 2))
                                dve.tensor_tensor(fin[j][:, :, :], fin[j][:, :, :], x_res[:, ds(first, UT), :], ALU.add
                                                  ).then_inc(z_a.sem, 1)

                    @block.sync
                    def _(sp):
                        with sp.Fori(0, NU // 2) as i:
                            for j in range(2):
                                sp.wait_ge(*z_a.now(i, 3 * j + 3))
                                sp.dma_start(out_t[:, ds((i * 2 + j) * UT, UT), :], fin[j][:, :, :]).then_inc(z_d[j].sem, 16)
                        for j in range(2):
                            sp.wait_ge(*z_d[j].now(NU // 2 - 1, 16))


def kernel(**inputs):
    import numpy as np
    import concourse.bacc as bacc
    from concourse.bass_utils import run_bass_kernel_spmd

    a = {k: np.ascontiguousarray(v) for k, v in inputs.items()}
    f32 = np.float32
    parts = {}

    def put(name, arr):
        parts[name] = arr if arr.ndim == 2 else arr[:, None]

    def blocks(arr):
        n = arr.shape[0] // P
        return arr.reshape(n, P, -1).transpose(1, 0, 2).reshape(P, -1)

    def row(arr):
        return arr.reshape(1, -1)

    def every(arr):
        return np.broadcast_to(arr.reshape(1, -1), (P, arr.size))

    def strips(w):
        o = np.zeros((w.shape[0], HG, 4, 32), f32)
        o[:, :, :, :HD] = w.reshape(w.shape[0], HG, 4, HD)
        return o.reshape(w.shape[0], HG * P)

    put("ident", np.eye(P, dtype=f32))
    put("ones", np.ones((P, P), f32))
    tri = np.triu(np.ones((P, P), f32))
    put("tri_st", np.concatenate([tri, np.ones((P, P), f32), tri], 1))
    put("iota", np.broadcast_to(np.arange(1, CAP + 1, dtype=f32), (P, CAP)))
    put("tvec", np.broadcast_to(np.arange(SEQ, dtype=f32), (P, SEQ)))
    put("rank", np.broadcast_to(np.arange(8, 0, -1, dtype=f32), (P, 8)))
    A = "L0_attn_"
    put("gam0", a[A + "norm_gamma"]); put("bet0", a[A + "norm_beta"])
    put("inw", a[A + "in_w"]); put("inb", blocks(a[A + "in_b"]))
    put("cw", blocks(a[A + "conv_w"].reshape(INNER, 3))); put("cbias", blocks(a[A + "conv_b"]))
    put("alog", blocks(a[A + "A_log"])); put("bp", blocks(a[A + "B_p"])); put("cp", blocks(a[A + "C_p"]))
    put("dp", blocks(a[A + "D_p"])); put("outw", blocks(a[A + "out_w"])); put("outb", row(a[A + "out_b"]))
    A = "L0_ffn_"
    put("gate0", a[A + "gate_w"].T); put("wsg", a[A + "Ws_g"].T); put("wsu", a[A + "Ws_u"].T)
    put("wsd", blocks(np.ascontiguousarray(a[A + "Ws_d"].T)))
    A = "L1_attn_"
    put("lng1", a[A + "ln_g"]); put("lnb1", a[A + "ln_b"]); put("qkvw", a[A + "qkv_w"])
    put("qkvb", blocks(a[A + "qkv_b"])); put("vb", row(a[A + "qkv_b"][2 * D:]))
    put("gw1", a[A + "gate_w"]); put("gb1", a[A + "gate_b"])
    A = "L1_ffn_"
    put("gate1", a[A + "gate_w"]); put("gate1b", row(a[A + "gate_b"]))
    A = "L2_attn_"
    put("wdq", a[A + "W_dq"]); put("wdkv", a[A + "W_dkv"])
    put("wuq", strips(a[A + "W_uq"])); put("wuk", strips(a[A + "W_uk"]))
    put("wuv", a[A + "W_uv"]); put("wo2", a[A + "W_o"])
    kone = np.zeros((P, HG), f32)
    kone[HD::32] = 1.0
    put("kone", kone)
    A = "L2_ffn_"
    put("basew", a[A + "base_W"].T); put("baseb", row(a[A + "base_b"]))
    put("acat", np.concatenate([a[A + "routed_A"].reshape(E2 * R2, D), a[A + "shared_A"]], 0).T)
    put("bcat", np.concatenate([a[A + "routed_B"].transpose(0, 2, 1).reshape(E2 * R2, D), a[A + "shared_B"].T], 0))
    put("rout", a[A + "router_W"].T); put("routb", row(a[A + "router_b"]))
    A = "L3_attn_"
    put("win3", a[A + "W_in"].T); put("bin3", a[A + "b_in"]); put("wout3", a[A + "W_out"].T)
    put("bout3", row(a[A + "b_out"])); put("decay", every(a[A + "decay"])); put("mix", every(a[A + "mix"]))
    A = "L3_ffn_"
    w, b = a[A + "in_proj_w"], a[A + "in_proj_b"]
    put("wq3", strips(w[:D].T)); put("wk3", strips(w[D:2 * D].T)); put("wv3", w[2 * D:].T)
    put("bq3", strips(row(b[:D])).reshape(HG, P).T)
    bk = strips(row(b[D:2 * D])).reshape(HG, P).T.copy()
    bk[HD::32] = 1.0
    put("bk3", bk)
    put("bv3", row(b[2 * D:])); put("wo3", a[A + "out_proj_w"].T); put("bo3", row(a[A + "out_proj_b"]))
    for n, s in (("g1", "ln1_g"), ("b1", "ln1_b"), ("g2", "ln2_g"), ("b2", "ln2_b")):
        put(n, every(a[A + s]))
    put("rt3", np.concatenate([a[A + "w_group"], a[A + "w_expert"].transpose(1, 0, 2).reshape(D, E3)], 1))
    put("rt3b", row(np.concatenate([a[A + "b_group"], a[A + "b_expert"].reshape(-1)])))
    pack = np.zeros((P, NPACK), f32)
    for name, (o, n) in OFF.items():
        m = parts[name]
        assert m.shape[1] == n, (name, m.shape, n)
        pack[:m.shape[0], o:o + n] = m

    def down(w, f):
        return w.reshape(w.shape[0], f // P, P, D).transpose(0, 2, 1, 3).reshape(w.shape[0], P, -1)

    A = "L0_ffn_"
    w0 = np.concatenate([a[A + "Wg"].transpose(0, 2, 1), a[A + "Wu"].transpose(0, 2, 1),
                         down(np.ascontiguousarray(a[A + "Wd"].transpose(0, 2, 1)), F0)], 2)

    def expert(wa, wb, ba, bb, f):
        e = wa.shape[0]
        o = np.zeros((e, P, 2 * f + f // P + U), f32)
        o[:, :, :f] = wa
        o[:, :, f:2 * f] = down(wb, f)
        o[:, :, 2 * f:2 * f + f // P] = ba.reshape(e, f // P, P).transpose(0, 2, 1)
        o[:, 0, 2 * f + f // P:] = np.broadcast_to(bb[:, None, :], (e, UT, D)).reshape(e, U)
        return o

    A = "L1_ffn_"
    w1 = expert(np.concatenate([a[A + "w1"], a[A + "ws1"][None]]), np.concatenate([a[A + "w2"], a[A + "ws2"][None]]),
                np.concatenate([a[A + "b1"], a[A + "bs1"][None]]), np.concatenate([a[A + "b2"], a[A + "bs2"][None]]), F1)
    A = "L3_ffn_"
    w3 = expert(a[A + "w1"], a[A + "w2"], a[A + "b1"], a[A + "b2"], F3)
    mask = np.where(np.arange(P)[None, :] <= np.arange(P)[:, None], 0.0, -BIG).astype(f32)
    masks = np.concatenate([np.eye(P, dtype=f32), mask, mask.T], 1)

    nc = bacc.Bacc("TRN2", target_bir_lowering=False, num_devices=1)
    arrays = {"x": a["L0_attn_x"].reshape(NB * SEQ, D), "pack": pack, "masks": masks,
              "w0": np.ascontiguousarray(w0), "w1": w1, "w3": w3}
    aps = [nc.dram_tensor("in_" + n, v.shape, F32, kind="ExternalInput").ap() for n, v in arrays.items()]
    out = nc.dram_tensor("out", (NB * SEQ, D), F32, kind="ExternalOutput").ap()
    ktab = nc.dram_tensor("ktab", (INNER, P + SEQ), F32).ap()
    ychan = nc.dram_tensor("ychan", (INNER, NB, SEQ), F32).ap()
    build(nc, *aps, out, ktab, ychan)
    r = run_bass_kernel_spmd(nc, [{"in_" + n: v for n, v in arrays.items()}], core_ids=[0])
    return r.results[0]["out"].reshape(NB, SEQ, D)
```

```python
from contextlib import ExitStack, contextmanager

import concourse.bass as bass
from concourse import mybir
from concourse.alu_op_type import AluOpType as ALU

ACT = mybir.ActivationFunctionType
AX = mybir.AxisListType.X
F32 = mybir.dt.float32
BF16 = mybir.dt.bfloat16
ds = bass.ds

P = 128
NB, SEQ, D = 32, 256, 128
TPB = SEQ // P
NT = NB * TPB
UT = 4
U = UT * P
NU = NT // UT
EPS = 1e-5
INNER, NSTATE = 256, 64
CB = INNER // P
E0, F0, CAP = 16, 256, SEQ * 2 // 16
E1, F1 = 8, 512
E2, R2 = 6, 16
E3, F3, G3 = 8, 256, 4
NH, HD = 16, 8
BIG = 1e30
CREDIT = 256

PACK = [("ident", P), ("ones", P), ("tri_st", P + SEQ), ("iota", CAP), ("tvec", SEQ),
        ("rank", 8),
        ("gam0", 1), ("bet0", 1), ("inw", 3 * INNER), ("inb", 3 * CB), ("cw", 3 * CB), ("cbias", CB),
        ("alog", CB * NSTATE), ("bp", CB * NSTATE), ("cp", CB * NSTATE), ("dp", CB), ("outw", CB * D), ("outb", D),
        ("gate0", E0), ("wsg", F0), ("wsu", F0), ("wsd", 2 * D),
        ("lng1", 1), ("lnb1", 1), ("qkvw", 3 * D), ("qkvb", 3), ("vb", D), ("gw1", D), ("gb1", 1),
        ("gate1", E1), ("gate1b", E1),
        ("wlow", 64), ("wuq", D), ("wuk", D), ("wuv", D), ("wo2", D),
        ("basew", D), ("baseb", D), ("acat", (E2 + 1) * R2), ("bcat", D), ("rout", E2), ("routb", E2),
        ("win3", D), ("bin3", 1), ("wout3", D), ("bout3", D), ("decay", 1), ("mix", 1),
        ("wq3", D), ("wk3", D), ("wv3", D), ("bq3", 1), ("bk3", 1), ("bv3", D), ("wo3", D), ("bo3", D),
        ("g1", D), ("b1", D), ("g2", D), ("b2", D), ("rt3", G3 + E3), ("rt3b", G3 + E3)]
OFF, NPACK = {}, 0
for _n, _c in PACK:
    OFF[_n] = (NPACK, _c)
    NPACK += _c
W0 = 3 * F0
W1 = 2 * F1 + F1 // P + U
W3 = 2 * F3 + F3 // P + U


class Signal:

    def __init__(self, semaphores, name, per):
        self.semaphores, self.name, self.per, self.held = semaphores, name, per, None

    @property
    def sem(self):
        if self.held is None:
            self.held = self.semaphores.take(self)
        return self.held[0]

    def raises(self, steps):
        return self.per * steps

    def now(self, i, k):
        return self.sem, i * self.per + (self.held[1] + k)

    def last(self, i, k):
        return self.sem, i * self.per + (self.held[1] + k - self.per)


class SlotSignal(Signal):

    def __init__(self, semaphores, name, per, u):
        super().__init__(semaphores, name, per)
        self.u = u

    def raises(self, batches):
        return self.per * len(range(self.u, batches, 4))


class Semaphores:

    def __init__(self, nc, stack, count):
        self.nc, self.open = nc, []
        self.free = [stack.enter_context(nc.semaphore(f"signal{n}")) for n in range(count)]
        self.value = {s.num: CREDIT for s in self.free}
        with nc.Block() as block:
            @block.sync
            def _(sp):
                for s in self.free:
                    sp.sem_inc(s, CREDIT)

    def take(self, signal):
        held = self.free.pop(0)
        self.open.append((signal, held))
        return held, self.value[held.num]

    @contextmanager
    def loop_block(self, steps):
        with self.nc.Block() as block:
            yield block
        for signal, held in self.open:
            self.value[held.num] += signal.raises(steps)
            signal.held = None
            self.free.append(held)
        self.open = []


def build(nc, x_in, pack_in, maskb_in, w0_in, w1_in, w3_in, out, ktab, ychan, q_stack, k_stack, v_ones, m_parts):
    ctx = ExitStack()
    with ctx:
        pool = Semaphores(nc, ctx, 48)

        def sem(name):
            return ctx.enter_context(nc.semaphore(name))

        def sig(name, per):
            return Signal(pool, name, per)

        def sb(name, shape, dt=F32, stack=ctx):
            return stack.enter_context(nc.sbuf_tensor(name, shape, dt))

        def bank(name, stack, n=1):
            return stack.enter_context(nc.psum_tensor(name, [P, n, 512], F32))

        x_res = sb("x_res", [P, NT, D])
        pack = sb("pack", [P, NPACK])
        mean = sb("mean", [P, NT])
        rstd = sb("rstd", [P, NT])
        rstd2 = sb("rstd2", [P, NT])
        bn6 = sb("bn6", [P, NT, 6])
        tmpa = sb("tmpa", [P, NT])
        tmpb = sb("tmpb", [P, NT])
        epsc = sb("epsc", [P, 1])

        def c(name, lo=0, n=None, rows=P):
            o, w = OFF[name]
            return pack[0:rows, o + lo:o + (w if n is None else lo + n)]

        ident = c("ident")
        ones_row = c("ones", rows=1)
        loaded = sem("loaded")
        kready = sem("kready")
        chained = sem("chained")
        acted = sem("acted")
        peed = sem("peed")
        stored = sem("stored")
        n_chain, n_act, n_pe = [0], [0], [0]

        def link(dve, ins):
            n_chain[0] += 1
            ins.then_inc(chained, 1)
            dve.wait_ge(chained, n_chain[0])

        def act_done(ins):
            n_act[0] += 1
            ins.then_inc(acted, 1)

        def pe_done(ins):
            n_pe[0] += 1
            ins.then_inc(peed, 1)

        s_e = sig("decay_exp", CB)
        s_k = sig("table_sum", CB)

        class Front:
            def __init__(self, t, n):
                self.nrm = sig(t + "_normed", n)
                self.tps = sig(t + "_turned", n)
                self.hT = sig(t + "_hT_ready", n)

        fr_a = Front("a", 2)
        a_proj, a_up, a_conv, a_c3, a_c, a_silu, a_tr, a_u = (
            sig("a_proj", 4), sig("a_up", 4), sig("a_mid_tap", 4), sig("a_left_tap", 4), sig("a_convolved", 4),
            sig("a_silu", 4),
            sig("a_turned_u", 4), sig("a_u_stored", 4))
        b_tz, b_st, b_mm, b_ev, b_ea, b_out = ([sig(f"b_toeplitz{j}", 16) for j in range(2)], sig("b_staged", 2), sig("b_conv", 8),
                                              sig("b_kept_odd", 4), sig("b_kept_even", 4), [sig(f"b_y_stored{j}", 16) for j in range(2)])
        fr_c = Front("c", 2)
        c_y, c_proj, c_sig, c_t, c_z, c_out, c_x = (
            [sig(f"c_y_loaded{j}", 32) for j in range(2)], sig("c_proj", 4), sig("c_sigmoid", 8), sig("c_t", 8), sig("c_z", 4),
            sig("c_outproj", 2), sig("c_x", 2 * (UT + 2)))
        routes = {}
        for t in ("d", "m1", "m2", "m3"):
            routes[t] = (Front(t, 2), sig(t + "_logits", 2), sig(t + "_logits_kept", 2), sig(t + "_affine", 4))
        g_n, g_p, g_mm, g_x = sig("g_normed", 2), sig("g_onehot", 2), sig("g_gathered", 2), sig("g_stored", 2)
        x_w, x_gu, x_ge, x_h, x_o, x_s = ([sig(f"x_weights{j}", 16) for j in range(2)], sig("x_gate_up", 8), sig("x_gelu", 8),
                                         sig("x_hidden", 8), sig("x_down", 4), sig("x_kept", 4))
        fr_f = Front("f", 1)
        f_p, f_st, f_pt, f_ptc, f_eo, f_eoc, f_gu, f_ge, f_h, f_o, f_x = (
            sig("f_onehot", 2), sig("f_staged", 1), sig("f_turned_p", 2), sig("f_p_kept", 2), sig("f_turned_e", 1),
            sig("f_e_kept", 1), sig("f_gate_up", 1), sig("f_gelu", 1), sig("f_hidden", 1), sig("f_out", 1),
            sig("f_x", 1))
        f_h0 = sig("f_places", 2)
        fr_l = Front("l", 1)
        l_pr, l_eg, l_d1, l_ex, l_qk, l_v, l_a, l_am, l_o, l_x = (
            sig("l_proj", 2), sig("l_expgate", 1), sig("l_chain", 5), sig("l_exp", 1), sig("l_qk", 1),
            sig("l_v_kept", 1), sig("l_scores", 1), sig("l_masked", 1), sig("l_out", 1), sig("l_x", 3))
        moes = {}
        for t, nf in (("e1", F1 // P), ("e3", F3 // P)):
            moes[t] = (sem(t + "_weights_a"), sem(t + "_weights_b"), sem(t + "_weights_used"),
                       [sig(f"{t}{j}_hidden", nf) for j in range(2)], [sig(f"{t}{j}_acted", nf) for j in range(2)],
                       [sig(f"{t}{j}_out", 1) for j in range(2)], [sig(f"{t}{j}_x", UT) for j in range(2)])
        m_ts, m_tr, m_tc, m_o, m_x = (sig("m_scaled", 2), sig("m_turned", 2), sig("m_kept", 2), sig("m_out", 2),
                                      sig("m_x", 2))
        m_c = sig("m_staged", 2)
        m_h = sig("m_low", 2)
        fr_s = Front("s", 2)
        s_in, s_pr, s_re, s_sc, s_o, s_x = (sig("s_mixed", 4), sig("s_proj", 2), sig("s_relu", 2), sig("s_scan", 4),
                                            sig("s_out", 2), sig("s_x", 2))
        projections = {t: (Front(t, 2), dict(
            {k: sig(f"{t}_{k}", n) for k, n in (("kept", 2), ("low", 2), ("lowc", 2), ("pr", 4), ("hi", 4), ("r1", 4),
                                               ("mid", 4), ("lo", 4), ("v", 2), ("vc", 2))},
            stored=[sig(f"{t}_stored{j}", 192) for j in range(2)],
            v_stored=[sig(f"{t}_v_stored{j}", 16) for j in range(2)])) for t in ("p2", "p3")}
        attns = {t: dict(
            {k: sig(f"{t}_{k}", n) for k, n in (
                ("s1", NH), ("mx", NH), ("nm", 1), ("mt", 1), ("mhi", 1), ("mr", 1), ("mmid", 1), ("mlo", 1), ("mout", 16),
                ("min", 16), ("s2", NH), ("ex", NH), ("pv", 4), ("ev", 4), ("tu", 4), ("rec", 4), ("on", 4), ("ot", 1),
                ("otc", 1), ("out", 1), ("x", 1))},
            loaded=[SlotSignal(pool, f"{t}_loaded{u}", 48, u) for u in range(4)]) for t in ("h2", "h3")}
        z_n, z_a, z_d = sig("z_normed", 2), sig("z_affine", 6), [sig(f"z_stored{j}", 16) for j in range(2)]

        with nc.Block() as block:
            @block.sync
            def _(sp):
                sp.dma_start(pack[:, :], pack_in).then_inc(loaded, 16)
                sp.dma_start(x_res[:, :, :], x_in.rearrange("(t p) d -> p t d", p=P)).then_inc(loaded, 16)
                sp.wait_ge(loaded, 32)

            @block.vector
            def _(dve):
                link(dve, dve.memset(epsc[:, :], EPS))

        def stats(src, twice=False):
            with nc.Block() as block:
                k0 = n_chain[0]
                a0 = n_act[0]

                @block.vector
                def _(dve):
                    with dve.Fori(0, NT // 8) as i:
                        for t in range(8):
                            dve.bn_stats(bn6[:, ds(i * 8 + t, 1), :], src[:, ds(i * 8 + t, 1), :])
                    link(dve, dve.tensor_copy(tmpa[:, 0:1], epsc[:, 0:1]))
                    link(dve, dve.tensor_tensor(mean[:, :], bn6[:, :, 1], bn6[:, :, 4], ALU.add))
                    link(dve, dve.tensor_tensor(tmpa[:, :], bn6[:, :, 1], bn6[:, :, 4], ALU.subtract))
                    link(dve, dve.tensor_tensor(tmpb[:, :], bn6[:, :, 2], bn6[:, :, 5], ALU.add))
                    link(dve, dve.tensor_scalar(mean[:, :], mean[:, :], 0.5, None, ALU.mult))
                    link(dve, dve.tensor_tensor(tmpa[:, :], tmpa[:, :], tmpa[:, :], ALU.mult))
                    link(dve, dve.tensor_scalar(tmpa[:, :], tmpa[:, :], 0.25, EPS, ALU.mult, ALU.add))
                    link(dve, dve.scalar_tensor_tensor(tmpa[:, :], tmpb[:, :], 1.0 / D, tmpa[:, :], ALU.mult, ALU.add))

                    def root(dst):
                        n_act[0] += 1
                        dve.wait_ge(acted, n_act[0])
                        link(dve, dve.reciprocal(dst[:, :], dst[:, :]))
                        link(dve, dve.tensor_tensor(tmpb[:, :], dst[:, :], dst[:, :], ALU.mult))
                        link(dve, dve.tensor_tensor(tmpb[:, :], tmpb[:, :], tmpa[:, :], ALU.mult))
                        link(dve, dve.tensor_scalar(tmpb[:, :], tmpb[:, :], -0.5, 1.5, ALU.mult, ALU.add))
                        link(dve, dve.tensor_tensor(dst[:, :], dst[:, :], tmpb[:, :], ALU.mult))

                    root(rstd)
                    if twice:
                        link(dve, dve.tensor_scalar(tmpa[:, :], tmpa[:, :], EPS, None, ALU.subtract))
                        link(dve, dve.tensor_tensor(tmpa[:, :], tmpa[:, :], rstd[:, :], ALU.mult))
                        link(dve, dve.tensor_tensor(tmpa[:, :], tmpa[:, :], rstd[:, :], ALU.mult))
                        link(dve, dve.tensor_scalar(tmpa[:, :], tmpa[:, :], EPS, None, ALU.add))
                        root(rstd2)
                        link(dve, dve.tensor_tensor(rstd2[:, :], rstd2[:, :], rstd[:, :], ALU.mult))

                @block.scalar
                def _(act):
                    act.wait_ge(chained, k0 + 8)
                    act.activation(rstd[:, :], tmpa[:, :], ACT.Sqrt).then_inc(acted, 1)
                    if twice:
                        act.wait_ge(chained, k0 + 8 + 5 + 4)
                        act.activation(rstd2[:, :], tmpa[:, :], ACT.Sqrt).then_inc(acted, 1)

        def norm_tiles(dve, done, dst, src, first, n, r, ready_to_write, extra=None):
            dve.wait_ge(*ready_to_write)
            if extra is not None:
                dve.wait_ge(*extra)
            for t in range(n):
                ins = dve.tensor_scalar(dst[:, t, :], src[:, ds(first + t, 1), :].rearrange("p o d -> p (o d)"),
                                        mean[:, ds(first + t, 1)], r[:, ds(first + t, 1)], ALU.subtract, ALU.mult)
            ins.then_inc(done.sem, 1)

        def turn_tiles(pe, done, ps, nrm, n, *waits):
            for w in waits:
                pe.wait_ge(*w)
            for t in range(n):
                ins = pe.transpose(ps[:, t * P:(t + 1) * P], nrm[:, t, :], ident)
            ins.then_inc(done.sem, 1)

        with ExitStack() as st:
            aexp = sb("aexp", [P, CB * NSTATE], stack=st)
            cbp = sb("cbp", [P, CB * NSTATE], stack=st)
            esb = sb("esb", [P, CB, SEQ], stack=st)
            ksb = sb("ksb", [P, CB, P + SEQ], stack=st)
            with pool.loop_block(NSTATE) as block:
                a0 = n_act[0]
                k_neg = n_chain[0] + 3

                @block.scalar
                def _(act):
                    act_done(act.activation(aexp[:, :], c("alog"), ACT.Exp))
                    act.wait_ge(chained, k_neg)
                    with act.Fori(0, NSTATE) as i:
                        for b in range(CB):
                            act.wait_ge(*s_k.last(i, b + 1))
                            act.activation(esb[:, b, :], c("tvec"), ACT.Exp,
                                           scale=aexp[:, ds(i + b * NSTATE, 1)]).then_inc(s_e.sem, 1)

                @block.vector
                def _(dve):
                    link(dve, dve.memset(ksb[:, :, :], 0.0))
                    link(dve, dve.tensor_tensor(cbp[:, :], c("bp"), c("cp"), ALU.mult))
                    dve.wait_ge(acted, a0 + 1)
                    link(dve, dve.tensor_scalar(aexp[:, :], aexp[:, :], -1.0, None, ALU.mult))
                    with dve.Fori(0, NSTATE) as i:
                        for b in range(CB):
                            dve.wait_ge(*s_k.last(i, b + 1))
                            dve.wait_ge(*s_e.now(i, b + 1))
                            dve.scalar_tensor_tensor(ksb[:, b, P:], esb[:, b, :], cbp[:, ds(i + b * NSTATE, 1)],
                                                     ksb[:, b, P:], ALU.mult, ALU.add).then_inc(s_k.sem, 1)
                    dve.wait_ge(*s_k.now(NSTATE - 1, CB))
                    link(dve, dve.tensor_tensor(ksb[:, :, P], ksb[:, :, P], c("dp"), ALU.add))

                @block.sync
                def _(sp):
                    sp.wait_ge(chained, k_neg + 1)
                    sp.dma_start(ktab.rearrange("(b p) l -> p b l", p=P), ksb[:, :, :]).then_inc(kready, 16)
                    sp.wait_ge(kready, 16)

        stats(x_res, twice=True)

        with ExitStack() as st_u:
            u_all = sb("u_all", [P, TPB, NB, INNER], stack=st_u)
            with ExitStack() as st:
                nrm = [sb(f"a_nrm{j}", [P, UT, P], stack=st) for j in range(2)]
                hT = [sb(f"a_hT{j}", [P, U], stack=st) for j in range(2)]
                up = [sb(f"a_up{j}", [P, CB, 2, SEQ + 2], stack=st) for j in range(2)]
                cv = [sb(f"a_cv{j}", [P, CB, 2, SEQ], stack=st) for j in range(2)]
                rv = [sb(f"a_rv{j}", [P, CB, 2, SEQ], stack=st) for j in range(2)]
                ps_t = bank("a_ps_t", st, 2)
                ps_u = bank("a_ps_u", st, 4)
                ps_r = bank("a_ps_r", st, 2)
                with pool.loop_block(NU // 2) as block:
                    ch0 = n_chain[0] + 2

                    @block.vector
                    def _(dve):
                        for j in range(2):
                            link(dve, dve.memset(up[j][:, :, :, :], 0.0))
                        with dve.Fori(0, NU // 2) as i:
                            for j in range(2):
                                norm_tiles(dve, fr_a.nrm, nrm[j], x_res, (i * 2 + j) * UT, UT, rstd2,
                                           fr_a.tps.last(i, j + 1))
                            for b in range(CB):
                                for j in range(2):
                                    k = b * 2 + j + 1
                                    dve.wait_ge(*a_up.now(i, k))
                                    dve.wait_ge(*a_silu.last(i, k))
                                    dve.tensor_scalar(cv[j][:, b], up[j][:, b, :, 1:SEQ + 1], c("cw", b * 3 + 1, 1),
                                                      c("cbias", b, 1), ALU.mult, ALU.add).then_inc(a_conv.sem, 1)
                                    dve.wait_ge(*a_conv.now(i, k))
                                    dve.scalar_tensor_tensor(cv[j][:, b], up[j][:, b, :, 0:SEQ], c("cw", b * 3, 1),
                                                             cv[j][:, b], ALU.mult, ALU.add).then_inc(a_c3.sem, 1)
                                    dve.wait_ge(*a_c3.now(i, k))
                                    dve.scalar_tensor_tensor(cv[j][:, b], up[j][:, b, :, 2:SEQ + 2],
                                                             c("cw", b * 3 + 2, 1), cv[j][:, b],
                                                             ALU.mult, ALU.add).then_inc(a_c.sem, 1)
                            for b in range(CB):
                                for j in range(2):
                                    dve.wait_ge(*a_tr.now(i, b * 2 + j + 1))
                                    dst = u_all[:, :, ds(i * 4 + j * 2, 2), b * P:(b + 1) * P]
                                    dve.tensor_copy(dst.rearrange("p h b c -> p b h c"),
                                                    ps_r[:, j, :].rearrange("p (b h c) -> p b h c", b=2, h=TPB)
                                                    ).then_inc(a_u.sem, 1)

                    @block.tensor
                    def _(pe):
                        pe.wait_ge(chained, ch0)
                        with pe.Fori(0, NU // 2) as i:
                            for j in range(2):
                                turn_tiles(pe, fr_a.tps, ps_t[:, j, :], nrm[j], UT, fr_a.nrm.now(i, j + 1),
                                           fr_a.hT.last(i, j + 1))
                            for b in range(CB):
                                for j in range(2):
                                    pe.wait_ge(*fr_a.hT.now(i, j + 1))
                                    pe.wait_ge(*a_up.last(i, b * 2 + j + 1))
                                    pe.matmul(ps_u[:, b * 2 + j, :], c("inw", b * P, P), hT[j][:, :],
                                              start=True, stop=True).then_inc(a_proj.sem, 1)
                            for b in range(CB):
                                for j in range(2):
                                    k = b * 2 + j + 1
                                    pe.wait_ge(*a_silu.now(i, k))
                                    if b == 0:
                                        pe.wait_ge(*a_u.last(i, 2 + k))
                                    else:
                                        pe.wait_ge(*a_u.now(i, k - 2))
                                    for t in range(UT):
                                        h = TPB - 1 - t % TPB
                                        ins = pe.transpose(ps_r[:, j, t * P:(t + 1) * P],
                                                           rv[j][:, b, t // TPB, h * P:(h + 1) * P], ident)
                                    ins.then_inc(a_tr.sem, 1)

                    @block.scalar
                    def _(act):
                        act.wait_ge(chained, ch0)
                        with act.Fori(0, NU // 2) as i:
                            for j in range(2):
                                act.wait_ge(*fr_a.tps.now(i, j + 1))
                                act.wait_ge(*a_proj.last(i, 2 + j + 1))
                                act.activation(hT[j][:, :], ps_t[:, j, :], ACT.Identity, bias=c("bet0"),
                                               scale=c("gam0")).then_inc(fr_a.hT.sem, 1)
                            for b in range(CB):
                                for j in range(2):
                                    k = b * 2 + j + 1
                                    act.wait_ge(*a_proj.now(i, k))
                                    act.wait_ge(*a_c.last(i, k))
                                    act.activation(up[j][:, b, :, 1:SEQ + 1],
                                                   ps_u[:, b * 2 + j, :].rearrange("p (b t) -> p b t", b=2),
                                                   ACT.Identity, bias=c("inb", b, 1)).then_inc(a_up.sem, 1)
                            for b in range(CB):
                                for j in range(2):
                                    k = b * 2 + j + 1
                                    act.wait_ge(*a_c.now(i, k))
                                    act.wait_ge(*a_tr.last(i, k))
                                    end = cv[j][:, b, 0, SEQ - 1:SEQ]
                                    down = bass.AP(end.tensor, end.offset, [list(end.ap[0]), [SEQ, 2], [-1, SEQ]])
                                    act.activation(rv[j][:, b], down, ACT.Silu).then_inc(a_silu.sem, 1)

            with ExitStack() as st:
                GC = 16
                tz = [sb(f"b_tz{j}", [P, GC, SEQ], stack=st) for j in range(2)]
                us = [sb(f"b_us{j}", [P, TPB, GC, NB], stack=st) for j in range(2)]
                ysb = [sb(f"b_y{j}", [P, 4, SEQ], stack=st) for j in range(2)]
                ps_y = bank("b_ps_y", st, 4)
                with pool.loop_block(INNER // GC // 2) as block:
                    @block.sync
                    def _(sp):
                        with sp.Fori(0, INNER // GC // 2) as i:
                            for j in range(2):
                                sp.wait_ge(*b_mm.last(i, 4 * j + 4))
                                rows = ktab[ds((i * 2 + j) * GC, GC), :]
                                src = bass.AP(rows.tensor, rows.offset + 1, [[1, P], [P + SEQ, GC], [1, SEQ]])
                                sp.dma_start(tz[j][:, :, :], src).then_inc(b_tz[j].sem, 16)
                        for j in range(2):
                            sp.wait_ge(*b_out[j].now(INNER // GC // 2 - 1, 16))

                    @block.vector
                    def _(dve):
                        with dve.Fori(0, INNER // GC // 2) as i:
                            for j in range(2):
                                dve.wait_ge(*b_mm.last(i, 4 * j + 4))
                                dve.tensor_copy(us[j][:, :, :, :].rearrange("p h c b -> p h b c"),
                                                u_all[:, :, :, ds((i * 2 + j) * GC, GC)]).then_inc(b_st.sem, 1)
                                for q in range(1, 4, 2):
                                    dve.wait_ge(*b_mm.now(i, 4 * j + q + 1))
                                    dve.wait_ge(*b_out[j].last(i, 16))
                                    dve.tensor_copy(ysb[j][:, q, :], ps_y[:, q, 0:SEQ]).then_inc(b_ev.sem, 1)

                    @block.tensor
                    def _(pe):
                        with pe.Fori(0, INNER // GC // 2) as i:
                            for j in range(2):
                                pe.wait_ge(*b_tz[j].now(i, 16))
                                pe.wait_ge(*b_st.now(i, j + 1))
                                for q in range(4):
                                    if j == 0:
                                        pe.wait_ge(*b_ev.last(i, 4))
                                        pe.wait_ge(*b_ea.last(i, 4))
                                    else:
                                        pe.wait_ge(*b_ev.now(i, 2))
                                        pe.wait_ge(*b_ea.now(i, 2))
                                    for g in range(4):
                                        ch = 4 * q + g
                                        strip = ps_y[32 * g:32 * g + 32, q, :]
                                        pe.matmul(strip[:, 0:SEQ], us[j][:, 0, ch, :], tz[j][:, ch, :],
                                                  start=True, stop=False)
                                        ins = pe.matmul(strip[:, P:SEQ], us[j][:, 1, ch, :], tz[j][:, ch, 0:P],
                                                        start=False, stop=True)
                                    ins.then_inc(b_mm.sem, 1)

                    @block.scalar
                    def _(act):
                        with act.Fori(0, INNER // GC // 2) as i:
                            for j in range(2):
                                for q in range(0, 4, 2):
                                    act.wait_ge(*b_mm.now(i, 4 * j + q + 1))
                                    act.wait_ge(*b_out[j].last(i, 16))
                                    act.activation(ysb[j][:, q, :], ps_y[:, q, 0:SEQ], ACT.Copy).then_inc(b_ea.sem, 1)
                                act.wait_ge(*b_ea.now(i, 2 * j + 2))
                                act.wait_ge(*b_ev.now(i, 2 * j + 2))
                                dst = ychan[ds((i * 2 + j) * GC, GC)].rearrange("(q g) b t -> (g b) q t", g=4)
                                act.dma_start(dst, ysb[j][:, :, :]).then_inc(b_out[j].sem, 16)

        with ExitStack() as st:
            nrm = [sb(f"c_nrm{j}", [P, UT, P], stack=st) for j in range(2)]
            hT = [sb(f"c_hT{j}", [P, U], stack=st) for j in range(2)]
            yT = [sb(f"c_yT{j}", [P, CB, U], stack=st) for j in range(2)]
            sv = [sb(f"c_sv{j}", [P, CB, U], stack=st) for j in range(2)]
            sg = [sb(f"c_sg{j}", [P, CB, U], stack=st) for j in range(2)]
            ps_t = bank("c_ps_t", st, 2)
            ps_v = bank("c_ps_v", st, 2)
            ps_g = bank("c_ps_g", st, 2)
            ps_o = bank("c_ps_o", st, 2)
            with pool.loop_block(NU // 2) as block:
                @block.sync
                def _(sp):
                    with sp.Fori(0, NU // 2) as i:
                        for j in range(2):
                            sp.wait_ge(*c_t.last(i, 4 * j + 4))
                            for b in range(CB):
                                src = ychan[b * P:(b + 1) * P, ds((i * 2 + j) * 2, 2), :]
                                sp.dma_start(yT[j][:, b, :].rearrange("p (b t) -> p b t", b=2), src
                                             ).then_inc(c_y[j].sem, 16)

                @block.vector
                def _(dve):
                    with dve.Fori(0, NU // 2) as i:
                        for j in range(2):
                            norm_tiles(dve, fr_c.nrm, nrm[j], x_res, (i * 2 + j) * UT, UT, rstd2,
                                       fr_c.tps.last(i, j + 1))
                        for j in range(2):
                            dve.wait_ge(*c_y[j].now(i, 32))
                            for b in range(CB):
                                dve.wait_ge(*c_sig.now(i, 4 * j + 2 * b + 2))
                                dve.scalar_tensor_tensor(sv[j][:, b, :], ps_v[:, b, :], c("inb", CB + b, 1),
                                                         sv[j][:, b, :], ALU.add, ALU.mult).then_inc(c_t.sem, 1)
                                dve.tensor_tensor(sg[j][:, b, :], sg[j][:, b, :], yT[j][:, b, :],
                                                  ALU.mult).then_inc(c_t.sem, 1)
                                dve.wait_ge(*c_t.now(i, 4 * j + 2 * b + 2))
                                dve.tensor_tensor(sv[j][:, b, :], sv[j][:, b, :], sg[j][:, b, :],
                                                  ALU.add).then_inc(c_z.sem, 1)
                        for j in range(2):
                            first = (i * 2 + j) * UT
                            k0 = j * (UT + 2)
                            dve.wait_ge(*c_out.now(i, j + 1))
                            dve.wait_ge(*fr_c.tps.now(i, j + 1))
                            for t in range(UT):
                                dve.tensor_scalar(nrm[j][:, t, :],
                                                  x_res[:, ds(first + t, 1), :].rearrange("p o d -> p (o d)"),
                                                  mean[:, ds(first + t, 1)], rstd[:, ds(first + t, 1)],
                                                  ALU.subtract, ALU.mult).then_inc(c_x.sem, 1)
                            xs = x_res[:, ds(first, UT), :]
                            dve.wait_ge(*c_x.now(i, k0 + UT))
                            dve.tensor_tensor(xs, xs, nrm[j][:, :, :], ALU.add).then_inc(c_x.sem, 1)
                            dve.wait_ge(*c_x.now(i, k0 + UT + 1))
                            dve.tensor_tensor(xs, xs, ps_o[:, j, :].rearrange("p (t d) -> p t d", t=UT),
                                              ALU.add).then_inc(c_x.sem, 1)

                @block.tensor
                def _(pe):
                    with pe.Fori(0, NU // 2) as i:
                        for j in range(2):
                            turn_tiles(pe, fr_c.tps, ps_t[:, j, :], nrm[j], UT, fr_c.nrm.now(i, j + 1),
                                       fr_c.hT.last(i, j + 1))
                        for j in range(2):
                            pe.wait_ge(*fr_c.hT.now(i, j + 1))
                            for b in range(CB):
                                if j == 0:
                                    pe.wait_ge(*c_z.last(i, 2 + b + 1))
                                else:
                                    pe.wait_ge(*c_z.now(i, b + 1))
                                pe.matmul(ps_v[:, b, :], c("inw", (CB + b) * P, P), hT[j][:, :], start=True, stop=True)
                                pe.matmul(ps_g[:, b, :], c("inw", (2 * CB + b) * P, P), hT[j][:, :],
                                          start=True, stop=True).then_inc(c_proj.sem, 1)
                        for j in range(2):
                            pe.wait_ge(*c_z.now(i, 2 * j + 2))
                            pe.wait_ge(*c_x.last(i, (j + 1) * (UT + 2)))
                            for t in range(UT):
                                dst = ps_o[:, j, t * P:(t + 1) * P]
                                pe.matmul(dst, c("ones", rows=1), c("outb", rows=1), start=True, stop=False)
                                for b in range(CB):
                                    ins = pe.matmul(dst, sv[j][:, b, t * P:(t + 1) * P], c("outw", b * D, D),
                                                    start=False, stop=(b == CB - 1))
                            ins.then_inc(c_out.sem, 1)

                @block.scalar
                def _(act):
                    with act.Fori(0, NU // 2) as i:
                        for j in range(2):
                            act.wait_ge(*fr_c.tps.now(i, j + 1))
                            act.wait_ge(*c_proj.last(i, 2 * j + 2))
                            act.activation(hT[j][:, :], ps_t[:, j, :], ACT.Identity, bias=c("bet0"),
                                           scale=c("gam0")).then_inc(fr_c.hT.sem, 1)
                        for j in range(2):
                            for b in range(CB):
                                act.wait_ge(*c_proj.now(i, 2 * j + b + 1))
                                act.wait_ge(*c_out.last(i, j + 1))
                                act.activation(sv[j][:, b, :], ps_v[:, b, :], ACT.Sigmoid,
                                               bias=c("inb", CB + b, 1)).then_inc(c_sig.sem, 1)
                                act.activation(sg[j][:, b, :], ps_g[:, b, :], ACT.Sigmoid,
                                               bias=c("inb", 2 * CB + b, 1)).then_inc(c_sig.sem, 1)

        def route(tag, src, weights, bias, n_out, logits, h_all=None, affine=None):
            fr, lg, kept, aff = routes[tag]
            with ExitStack() as st:
                nrm = [sb(f"{tag}_nrm{j}", [P, UT, P], stack=st) for j in range(2)]
                hT = [sb(f"{tag}_hT{j}", [P, U], stack=st) for j in range(2)]
                ps_t = bank(f"{tag}_ps_t", st, 2)
                ps_l = bank(f"{tag}_ps_l", st, 2)
                with pool.loop_block(NU // 2) as block:
                    @block.vector
                    def _(dve):
                        with dve.Fori(0, NU // 2) as i:
                            for j in range(2):
                                first = (i * 2 + j) * UT
                                if affine is None:
                                    norm_tiles(dve, fr.nrm, nrm[j], src, first, UT, rstd, fr.tps.last(i, j + 1))
                                    continue
                                dve.wait_ge(*fr.tps.last(i, j + 1))
                                for t in range(UT):
                                    ins = dve.tensor_scalar(nrm[j][:, t, :],
                                                            src[:, ds(first + t, 1), :].rearrange("p o d -> p (o d)"),
                                                            mean[:, ds(first + t, 1)], rstd[:, ds(first + t, 1)],
                                                            ALU.subtract, ALU.mult)
                                ins.then_inc(aff.sem, 1)
                                dve.wait_ge(*aff.now(i, 2 * j + 1))
                                dve.tensor_tensor(nrm[j][:, :, :], nrm[j][:, :, :],
                                                  affine[0].unsqueeze(1).to_broadcast([P, UT, D]),
                                                  ALU.mult).then_inc(aff.sem, 1)
                                dve.wait_ge(*aff.now(i, 2 * j + 2))
                                dve.tensor_tensor(nrm[j][:, :, :], nrm[j][:, :, :],
                                                  affine[1].unsqueeze(1).to_broadcast([P, UT, D]),
                                                  ALU.add).then_inc(fr.nrm.sem, 1)
                                dve.wait_ge(*fr.nrm.now(i, j + 1))
                                dve.tensor_scalar(src[:, ds(first, UT), :], nrm[j][:, :, :], 1.0, None, ALU.mult)
                            for j in range(2):
                                dve.wait_ge(*lg.now(i, j + 1))
                                dve.tensor_copy(logits[:, ds((i * 2 + j) * UT, UT), :],
                                                ps_l[:, j, 0:UT * n_out].rearrange("p (t e) -> p t e", t=UT)
                                                ).then_inc(kept.sem, 1)

                    @block.tensor
                    def _(pe):
                        with pe.Fori(0, NU // 2) as i:
                            for j in range(2):
                                turn_tiles(pe, fr.tps, ps_t[:, j, :], nrm[j], UT, fr.nrm.now(i, j + 1),
                                           fr.hT.last(i, j + 1))
                            for j in range(2):
                                pe.wait_ge(*fr.hT.now(i, j + 1))
                                pe.wait_ge(*kept.last(i, j + 1))
                                for t in range(UT):
                                    dst = ps_l[:, j, t * n_out:(t + 1) * n_out]
                                    if bias is not None:
                                        pe.matmul(dst, c("ones", rows=1), bias, start=True, stop=False)
                                    ins = pe.matmul(dst, hT[j][:, t * P:(t + 1) * P], weights,
                                                    start=(bias is None), stop=True)
                                ins.then_inc(lg.sem, 1)

                    @block.scalar
                    def _(act):
                        with act.Fori(0, NU // 2) as i:
                            for j in range(2):
                                act.wait_ge(*fr.tps.now(i, j + 1))
                                act.wait_ge(*lg.last(i, j + 1))
                                if h_all is not None:
                                    act.activation(h_all[:, ds((i * 2 + j) * U, U)], ps_t[:, j, :], ACT.Copy)
                                act.activation(hT[j][:, :], ps_t[:, j, :], ACT.Copy).then_inc(fr.hT.sem, 1)

        def softmax_rows(dve, lg, out_e, m, s, n):
            link(dve, dve.tensor_reduce(m, lg, AX, ALU.max))
            link(dve, dve.tensor_tensor(out_e, lg, m.unsqueeze(2).to_broadcast([P, NT, n]), ALU.subtract))
            n_act[0] += 1
            dve.wait_ge(acted, n_act[0])
            link(dve, dve.tensor_reduce(s, out_e, AX, ALU.add))
            link(dve, dve.reciprocal(s, s))

        stats(x_res)
        ROWS = 8 * E0
        NG = NB // 8
        with ExitStack() as st_d:
            score = sb("d_score", [P, NT, E0], stack=st_d)
            place = sb("d_place", [P, NT, E0], stack=st_d)
            route("d", x_res, c("gate0"), None, E0, score)
            with ExitStack() as st:
                mx = sb("d_max", [P, NT], stack=st)
                rs = sb("d_rsum", [P, NT], stack=st)
                rows = sb("d_rows", [P, NG, SEQ], stack=st)
                work = sb("d_work", [P, NG, SEQ], stack=st)
                taken = sb("d_taken", [P, NG, SEQ], stack=st)
                zero = sb("d_zero", [P, SEQ], stack=st)
                top = sb("d_top", [P, NG, 8], stack=st)
                lin = sb("d_lin", [P, TPB * NG, P], stack=st)
                ps_s = bank("d_ps_s", st, 2)
                ps_p = bank("d_ps_p", st, 2)
                with nc.Block() as block:
                    k0, a0, p0 = n_chain[0], n_act[0], n_pe[0]

                    @block.vector
                    def _(dve):
                        link(dve, dve.memset(zero[:, :], 0.0))
                        softmax_rows(dve, score[:, :, :], score[:, :, :], mx[:, :], rs[:, :], E0)
                        link(dve, dve.tensor_tensor(score[:, :, :], score[:, :, :],
                                                    rs[:, :].unsqueeze(2).to_broadcast([P, NT, E0]), ALU.mult))
                        lv = lin[:, :, :].rearrange("p (g h) (b e) -> p g h b e", g=NG, b=8)
                        sv = score[:, :, :].rearrange("p (g b h) e -> p g h b e", g=NG, b=8)
                        for g in range(NG):
                            link(dve, dve.tensor_copy(lv[:, g], sv[:, g]))
                        dve.wait_ge(peed, p0 + 1)
                        link(dve, dve.tensor_copy(rows[:, :, :].rearrange("p g t -> p (g t)"),
                                                  ps_s[:, :, :].rearrange("p k n -> p (k n)")))
                        for g in range(NG):
                            src = rows
                            for _ in range(CAP // 8):
                                link(dve, dve.max(top[:, g, :], src[:, g, :]))
                                link(dve, dve.match_replace(work[:, g, :], top[:, g, :], src[:, g, :], -1.0))
                                src = work
                            link(dve, dve.tensor_scalar(taken[:, g, :], work[:, g, :], 0.0, None, ALU.is_lt))
                            link(dve, dve.tensor_tensor_scan(work[:, g, :], taken[:, g, :], zero[:, :], 0.0,
                                                             ALU.add, ALU.add))
                            link(dve, dve.tensor_tensor(rows[:, g, :], work[:, g, :], taken[:, g, :], ALU.mult))
                        dve.wait_ge(peed, p0 + 2)
                        pv = place[:, :, :].rearrange("p (g b h) e -> p g h b e", g=NG, b=8)
                        for g in range(NG):
                            half = ps_p[:, g // 2, (g % 2) * SEQ:(g % 2 + 1) * SEQ]
                            link(dve, dve.tensor_copy(pv[:, g], half.rearrange("p (h b e) -> p h b e", h=TPB, b=8)))

                    k_lin = k0 + 1 + 4 + 1 + NG
                    k_rows = k_lin + 1 + NG * (2 * (CAP // 8) + 3)

                    @block.scalar
                    def _(act):
                        act.wait_ge(chained, k0 + 3)
                        act.activation(score[:, :, :], score[:, :, :], ACT.Exp).then_inc(acted, 1)

                    @block.tensor
                    def _(pe):
                        pe.wait_ge(chained, k_lin)
                        for g in range(NG):
                            for h in range(TPB):
                                ins = pe.transpose(ps_s[:, g // 2, (g % 2) * SEQ + h * P:(g % 2) * SEQ + (h + 1) * P],
                                                   lin[:, g * TPB + h, :], ident)
                        pe_done(ins)
                        pe.wait_ge(chained, k_rows)
                        for g in range(NG):
                            for h in range(TPB):
                                ins = pe.transpose(ps_p[:, g // 2, (g % 2) * SEQ + h * P:(g % 2) * SEQ + (h + 1) * P],
                                                   rows[:, g, h * P:(h + 1) * P], ident)
                        pe_done(ins)

            SLOTS = E0 * CAP
            with ExitStack() as st_x:
                xg = sb("xg", [P, E0, NB, CAP], stack=st_x)

                with ExitStack() as st:
                    nrm = [sb(f"g_nrm{j}", [P, TPB, P], stack=st) for j in range(2)]
                    hot = [sb(f"g_hot{j}", [P, TPB, E0, CAP], stack=st) for j in range(2)]
                    ps_x = bank("g_ps_x", st, 2)
                    with pool.loop_block(NB // 2) as block:
                        @block.vector
                        def _(dve):
                            with dve.Fori(0, NB // 2) as i:
                                for j in range(2):
                                    norm_tiles(dve, g_n, nrm[j], x_res, (i * 2 + j) * TPB, TPB, rstd,
                                               g_mm.last(i, j + 1))
                                    for h in range(TPB):
                                        pl = place[:, ds((i * 2 + j) * TPB + h, 1), :].rearrange("p o e -> p (o e)")
                                        ins = dve.tensor_tensor(hot[j][:, h], pl.unsqueeze(2).to_broadcast([P, E0, CAP]),
                                                                c("iota").unsqueeze(1).to_broadcast([P, E0, CAP]),
                                                                ALU.is_equal)
                                    ins.then_inc(g_p.sem, 1)

                        @block.tensor
                        def _(pe):
                            with pe.Fori(0, NB // 2) as i:
                                for j in range(2):
                                    pe.wait_ge(*g_n.now(i, j + 1))
                                    pe.wait_ge(*g_p.now(i, j + 1))
                                    pe.wait_ge(*g_x.last(i, j + 1))
                                    for h in range(TPB):
                                        ins = pe.matmul(ps_x[:, j, :], nrm[j][:, h, :],
                                                        hot[j][:, h].rearrange("p e s -> p (e s)"),
                                                        start=(h == 0), stop=(h == TPB - 1))
                                    ins.then_inc(g_mm.sem, 1)

                        @block.scalar
                        def _(act):
                            with act.Fori(0, NB // 2) as i:
                                for j in range(2):
                                    act.wait_ge(*g_mm.now(i, j + 1))
                                    act.activation(xg[:, :, ds(i * 2 + j, 1), :].rearrange("p e o s -> p e (o s)"),
                                                   ps_x[:, j, :].rearrange("p (e s) -> p e s", e=E0),
                                                   ACT.Copy).then_inc(g_x.sem, 1)

                with ExitStack() as st:
                    w0 = [sb(f"x_w{j}", [P, W0], stack=st) for j in range(2)]
                    ge = [sb(f"x_gelu{f}", [P, 512], stack=st) for f in range(2)]
                    hu = [sb(f"x_hid{n}", [P, 2, 512], stack=st) for n in range(2)]
                    ps_g = bank("x_ps_g", st, 2)
                    ps_u = bank("x_ps_u", st, 2)
                    ps_o = bank("x_ps_o", st, 2)
                    xe = xg[:, :, :, :].rearrange("p e b s -> p (e b s)")
                    with pool.loop_block(E0 // 2) as block:
                        @block.sync
                        def _(sp):
                            with sp.Fori(0, E0 // 2) as i:
                                for j in range(2):
                                    sp.wait_ge(*x_o.last(i, 2 * j + 2))
                                    sp.dma_start(w0[j][:, :], w0_in[ds(i * 2 + j, 1)].rearrange("o p w -> p (o w)")
                                                 ).then_inc(x_w[j].sem, 16)

                        def at(i, n):
                            return xe[:, ds(i * (2 * NB * CAP) + n * 512, 512)]

                        @block.tensor
                        def _(pe):
                            with pe.Fori(0, E0 // 2) as i:
                                def down_proj(n):
                                    pe.wait_ge(*x_h.now(i, 2 * n + 2))
                                    if n >= 2:
                                        pe.wait_ge(*x_s.now(i, n - 1))
                                    else:
                                        pe.wait_ge(*x_s.last(i, n + 3))
                                    for f in range(2):
                                        ins = pe.matmul(ps_o[:, n % 2, :], w0[n // 2][:, 2 * F0 + f * D:2 * F0 + (f + 1) * D],
                                                        hu[n % 2][:, f, :], start=(f == 0), stop=(f == 1))
                                    ins.then_inc(x_o.sem, 1)

                                for n in range(4):
                                    if n % 2 == 0:
                                        pe.wait_ge(*x_w[n // 2].now(i, 16))
                                    for f in range(2):
                                        if n:
                                            pe.wait_ge(*x_h.now(i, 2 * n - 1 + f))
                                        else:
                                            pe.wait_ge(*x_h.last(i, 7 + f))
                                        pe.matmul(ps_g[:, f, :], w0[n // 2][:, f * P:(f + 1) * P], at(i, n),
                                                  start=True, stop=True)
                                        pe.matmul(ps_u[:, f, :], w0[n // 2][:, F0 + f * P:F0 + (f + 1) * P], at(i, n),
                                                  start=True, stop=True).then_inc(x_gu.sem, 1)
                                    if n:
                                        down_proj(n - 1)
                                down_proj(3)

                        @block.scalar
                        def _(act):
                            with act.Fori(0, E0 // 2) as i:
                                def keep(n):
                                    act.wait_ge(*x_o.now(i, n + 1))
                                    act.activation(at(i, n), ps_o[:, n % 2, :], ACT.Copy).then_inc(x_s.sem, 1)

                                for n in range(4):
                                    for f in range(2):
                                        k = 2 * n + f + 1
                                        act.wait_ge(*x_gu.now(i, k))
                                        if n:
                                            act.wait_ge(*x_h.now(i, k - 2))
                                        else:
                                            act.wait_ge(*x_h.last(i, 7 + f))
                                        act.activation(ge[f][:, :], ps_g[:, f, :], ACT.Gelu).then_inc(x_ge.sem, 1)
                                    if n:
                                        keep(n - 1)
                                keep(3)

                        @block.vector
                        def _(dve):
                            with dve.Fori(0, E0 // 2) as i:
                                for n in range(4):
                                    for f in range(2):
                                        dve.wait_ge(*x_ge.now(i, 2 * n + f + 1))
                                        if n >= 2:
                                            dve.wait_ge(*x_o.now(i, n - 1))
                                        else:
                                            dve.wait_ge(*x_o.last(i, n + 3))
                                        dve.tensor_tensor(hu[n % 2][:, f, :], ge[f][:, :], ps_u[:, f, :],
                                                          ALU.mult).then_inc(x_h.sem, 1)

                with ExitStack() as st:
                    nrm = sb("f_nrm", [P, TPB, P], stack=st)
                    hT = sb("f_hT", [P, SEQ], stack=st)
                    hot = sb("f_hot", [P, TPB, E0, CAP], stack=st)
                    hotT = sb("f_hotT", [P, 4, SEQ], stack=st)
                    eoT = sb("f_eoT", [P, SLOTS], stack=st)
                    eo = sb("f_eo", [P, 4, D], stack=st)
                    ge = sb("f_ge", [P, 2, SEQ], stack=st)
                    hs = sb("f_hs", [P, 2, SEQ], stack=st)
                    ps_t = bank("f_ps_t", st)
                    ps_p = bank("f_ps_p", st, 2)
                    ps_e = bank("f_ps_e", st)
                    ps_g = bank("f_ps_g", st)
                    ps_u = bank("f_ps_u", st)
                    ps_o = bank("f_ps_o", st)
                    with pool.loop_block(NB) as block:
                        @block.vector
                        def _(dve):
                            with dve.Fori(0, NB) as i:
                                norm_tiles(dve, fr_f.nrm, nrm, x_res, i * TPB, TPB, rstd, fr_f.tps.last(i, 1))
                                dve.wait_ge(*f_pt.last(i, 2))
                                for h in range(TPB):
                                    pl = place[:, ds(i * TPB + h, 1), :].rearrange("p o e -> p (o e)")
                                    dve.tensor_tensor(hot[:, h], pl.unsqueeze(2).to_broadcast([P, E0, CAP]),
                                                      c("iota").unsqueeze(1).to_broadcast([P, E0, CAP]),
                                                      ALU.is_equal).then_inc(f_h0.sem, 1)
                                for h in range(TPB):
                                    dve.wait_ge(*f_h0.now(i, h + 1))
                                    sc = score[:, ds(i * TPB + h, 1), :].rearrange("p o e -> p (o e)")
                                    dve.tensor_tensor(hot[:, h], hot[:, h], sc.unsqueeze(2).to_broadcast([P, E0, CAP]),
                                                      ALU.mult).then_inc(f_p.sem, 1)
                                dve.wait_ge(*f_eo.last(i, 1))
                                dve.tensor_copy(eoT[:, :].rearrange("p (e s) -> p e s", e=E0),
                                                xg[:, :, ds(i, 1), :].rearrange("p e o s -> p e (o s)")
                                                ).then_inc(f_st.sem, 1)
                                dve.wait_ge(*f_ge.now(i, 1))
                                dve.wait_ge(*f_o.last(i, 1))
                                dve.tensor_tensor(hs[:, :, :], ge[:, :, :],
                                                  ps_u[:, 0, :].rearrange("p (f t) -> p f t", f=2),
                                                  ALU.mult).then_inc(f_h.sem, 1)
                                dve.wait_ge(*f_eo.now(i, 1))
                                dve.tensor_copy(eo[:, :, :].rearrange("p k d -> p (k d)"), ps_e[:, 0, :]
                                                ).then_inc(f_eoc.sem, 1)
                                dve.wait_ge(*f_o.now(i, 1))
                                xs = x_res[:, ds(i * TPB, TPB), :]
                                dve.tensor_tensor(xs, xs, ps_o[:, 0, 0:SEQ].rearrange("p (t d) -> p t d", t=TPB),
                                                  ALU.add).then_inc(f_x.sem, 1)

                        @block.tensor
                        def _(pe):
                            with pe.Fori(0, NB) as i:
                                turn_tiles(pe, fr_f.tps, ps_t[:, 0, :], nrm, TPB, fr_f.nrm.now(i, 1),
                                           fr_f.hT.last(i, 1))
                                pe.wait_ge(*fr_f.hT.now(i, 1))
                                pe.wait_ge(*f_h.last(i, 1))
                                for f in range(2):
                                    pe.matmul(ps_g[:, 0, f * SEQ:(f + 1) * SEQ], c("wsg", f * P, P), hT[:, :],
                                              start=True, stop=True)
                                    ins = pe.matmul(ps_u[:, 0, f * SEQ:(f + 1) * SEQ], c("wsu", f * P, P), hT[:, :],
                                                    start=True, stop=True)
                                ins.then_inc(f_gu.sem, 1)
                                for n in range(2):
                                    pe.wait_ge(*f_p.now(i, 2))
                                    pe.wait_ge(*f_ptc.last(i, n + 1))
                                    for k in range(2 * n, 2 * n + 2):
                                        for h in range(TPB):
                                            ins = pe.transpose(
                                                ps_p[:, n, (k % 2) * SEQ + h * P:(k % 2) * SEQ + (h + 1) * P],
                                                hot[:, h].rearrange("p e s -> p (e s)")[:, k * P:(k + 1) * P], ident)
                                    ins.then_inc(f_pt.sem, 1)
                                pe.wait_ge(*f_st.now(i, 1))
                                pe.wait_ge(*f_eoc.last(i, 1))
                                for k in range(4):
                                    ins = pe.transpose(ps_e[:, 0, k * D:(k + 1) * D], eoT[:, k * P:(k + 1) * P], ident)
                                ins.then_inc(f_eo.sem, 1)
                                pe.wait_ge(*f_h.now(i, 1))
                                pe.wait_ge(*f_ptc.now(i, 2))
                                pe.wait_ge(*f_eoc.now(i, 1))
                                pe.wait_ge(*f_x.last(i, 1))
                                for h in range(TPB):
                                    dst = ps_o[:, 0, h * D:(h + 1) * D]
                                    for f in range(2):
                                        pe.matmul(dst, hs[:, f, h * P:(h + 1) * P], c("wsd", f * D, D),
                                                  start=(f == 0), stop=False)
                                    for k in range(4):
                                        ins = pe.matmul(dst, hotT[:, k, h * P:(h + 1) * P], eo[:, k, :],
                                                        start=False, stop=(k == 3))
                                ins.then_inc(f_o.sem, 1)

                        @block.scalar
                        def _(act):
                            with act.Fori(0, NB) as i:
                                act.wait_ge(*fr_f.tps.now(i, 1))
                                act.wait_ge(*f_gu.last(i, 1))
                                act.activation(hT[:, :], ps_t[:, 0, 0:SEQ], ACT.Copy).then_inc(fr_f.hT.sem, 1)
                                act.wait_ge(*f_gu.now(i, 1))
                                act.wait_ge(*f_h.last(i, 1))
                                act.activation(ge[:, :, :], ps_g[:, 0, :].rearrange("p (f t) -> p f t", f=2),
                                               ACT.Gelu).then_inc(f_ge.sem, 1)
                                for n in range(2):
                                    act.wait_ge(*f_pt.now(i, n + 1))
                                    act.wait_ge(*f_o.last(i, 1))
                                    act.activation(hotT[:, 2 * n:2 * n + 2, :],
                                                   ps_p[:, n, :].rearrange("p (k t) -> p k t", k=2),
                                                   ACT.Copy).then_inc(f_ptc.sem, 1)

        stats(x_res, twice=True)
        with ExitStack() as st:
            VW = D + 4
            nrm = sb("l_nrm", [P, TPB, P], stack=st)
            hT = sb("l_hT", [P, SEQ], stack=st)
            hgb = sb("l_hgb", [P, 1], stack=st)
            egate = sb("l_egate", [P, SEQ], stack=st)
            gate = sb("l_gate", [P, SEQ], stack=st)
            qk = sb("l_qk", [P, 2, SEQ], stack=st)
            low = sb("l_low", [P, 2, SEQ], stack=st)
            v1 = sb("l_v", [P, TPB, VW], stack=st)
            am = sb("l_am", [P, P + SEQ], stack=st)
            den = sb("l_den", [P, TPB], stack=st)
            ps_t = bank("l_ps_t", st)
            ps_q = bank("l_ps_q", st)
            ps_g = bank("l_ps_g", st)
            ps_v = bank("l_ps_v", st)
            ps_a = bank("l_ps_a", st)
            ps_o = bank("l_ps_o", st)
            with pool.loop_block(NB) as block:
                k_set = n_chain[0] + 2

                @block.vector
                def _(dve):
                    link(dve, dve.tensor_scalar(hgb[:, :], c("gb1"), 0.5, None, ALU.mult))
                    link(dve, dve.memset(v1[:, :, :], 1.0))
                    with dve.Fori(0, NB) as i:
                        norm_tiles(dve, fr_l.nrm, nrm, x_res, i * TPB, TPB, rstd2, fr_l.tps.last(i, 1))
                        dve.wait_ge(*l_eg.now(i, 1))
                        dve.tensor_scalar(gate[:, :], egate[:, :], 0.5, 0.5, ALU.mult, ALU.add).then_inc(l_d1.sem, 1)
                        dve.wait_ge(*l_a.last(i, 1))
                        dve.wait_ge(*l_pr.now(i, 2))
                        dve.tensor_scalar(qk[:, 0, :], ps_q[:, 0, 0:SEQ], c("qkvb", 0, 1), None, ALU.add
                                          ).then_inc(l_d1.sem, 1)
                        dve.wait_ge(*l_d1.now(i, 2))
                        dve.scalar_tensor_tensor(qk[:, 1, :], ps_q[:, 0, SEQ:2 * SEQ], c("qkvb", 1, 1), gate[:, :],
                                                 ALU.add, ALU.mult).then_inc(l_d1.sem, 1)
                        dve.wait_ge(*l_d1.now(i, 3))
                        dve.tensor_scalar(low[:, :, :], qk[:, :, :], 0.0, None, ALU.min).then_inc(l_d1.sem, 1)
                        dve.wait_ge(*l_v.now(i, 1))
                        dve.tensor_copy(v1[:, :, 0:D], ps_v[:, 0, 0:SEQ].rearrange("p (t d) -> p t d", t=TPB)
                                        ).then_inc(l_d1.sem, 1)
                        dve.wait_ge(*l_ex.now(i, 1))
                        dve.scalar_tensor_tensor(qk[:, :, :], qk[:, :, :], 0.0, low[:, :, :], ALU.max, ALU.add
                                                 ).then_inc(l_qk.sem, 1)
                        dve.wait_ge(*l_a.now(i, 1))
                        dve.wait_ge(*l_o.last(i, 1))
                        dve.tensor_tensor(am[:, :], ps_a[:, 0, 0:P + SEQ], c("tri_st"), ALU.mult).then_inc(l_am.sem, 1)
                        dve.wait_ge(*l_o.now(i, 1))
                        ov = ps_o[:, 0, 0:TPB * VW].rearrange("p (t w) -> p t w", t=TPB)
                        dve.tensor_scalar(den[:, :], ov[:, :, D], 1e-6, None, ALU.add).then_inc(l_x.sem, 1)
                        dve.wait_ge(*l_x.now(i, 1))
                        dve.reciprocal(den[:, :], den[:, :]).then_inc(l_x.sem, 1)
                        dve.wait_ge(*l_x.now(i, 2))
                        for t in range(TPB):
                            xs = x_res[:, ds(i * TPB + t, 1), :].rearrange("p o d -> p (o d)")
                            ins = dve.scalar_tensor_tensor(xs, ov[:, t, 0:D], den[:, t:t + 1], xs, ALU.mult, ALU.add)
                        ins.then_inc(l_x.sem, 1)

                @block.tensor
                def _(pe):
                    pe.wait_ge(chained, k_set)
                    with pe.Fori(0, NB) as i:
                        turn_tiles(pe, fr_l.tps, ps_t[:, 0, :], nrm, TPB, fr_l.nrm.now(i, 1), fr_l.hT.last(i, 1))
                        pe.wait_ge(*fr_l.hT.now(i, 1))
                        pe.wait_ge(*l_eg.last(i, 1))
                        pe.matmul(ps_g[:, 0, 0:SEQ], c("gw1"), hT[:, :], start=True, stop=True).then_inc(l_pr.sem, 1)
                        pe.wait_ge(*l_d1.last(i, 3))
                        pe.matmul(ps_q[:, 0, 0:SEQ], c("qkvw", 0, D), hT[:, :], start=True, stop=True)
                        pe.matmul(ps_q[:, 0, SEQ:2 * SEQ], c("qkvw", D, D), hT[:, :], start=True, stop=True
                                  ).then_inc(l_pr.sem, 1)
                        pe.wait_ge(*l_d1.last(i, 5))
                        for t in range(TPB):
                            dst = ps_v[:, 0, t * D:(t + 1) * D]
                            pe.matmul(dst, c("ones", rows=1), c("vb", rows=1), start=True, stop=False)
                            ins = pe.matmul(dst, hT[:, t * P:(t + 1) * P], c("qkvw", 2 * D, D), start=False, stop=True)
                        ins.then_inc(l_v.sem, 1)
                        pe.wait_ge(*l_qk.now(i, 1))
                        pe.wait_ge(*l_am.last(i, 1))
                        pe.matmul(ps_a[:, 0, 0:SEQ], qk[:, 1, 0:P], qk[:, 0, :], start=True, stop=True)
                        pe.matmul(ps_a[:, 0, SEQ:SEQ + P], qk[:, 1, P:SEQ], qk[:, 0, P:SEQ], start=True, stop=True
                                  ).then_inc(l_a.sem, 1)
                        pe.wait_ge(*l_am.now(i, 1))
                        pe.wait_ge(*l_d1.now(i, 5))
                        pe.wait_ge(*l_x.last(i, 3))
                        pe.matmul(ps_o[:, 0, 0:VW], am[:, 0:P], v1[:, 0, :], start=True, stop=True)
                        pe.matmul(ps_o[:, 0, VW:2 * VW], am[:, P:SEQ], v1[:, 0, :], start=True, stop=False)
                        pe.matmul(ps_o[:, 0, VW:2 * VW], am[:, SEQ:SEQ + P], v1[:, 1, :], start=False, stop=True
                                  ).then_inc(l_o.sem, 1)

                @block.scalar
                def _(act):
                    act.wait_ge(chained, k_set)
                    with act.Fori(0, NB) as i:
                        act.wait_ge(*fr_l.tps.now(i, 1))
                        act.wait_ge(*l_v.last(i, 1))
                        act.activation(hT[:, :], ps_t[:, 0, 0:SEQ], ACT.Identity, bias=c("lnb1"), scale=c("lng1")
                                       ).then_inc(fr_l.hT.sem, 1)
                        act.wait_ge(*l_pr.now(i, 1))
                        act.wait_ge(*l_d1.last(i, 1))
                        act.activation(egate[:, :], ps_g[:, 0, 0:SEQ], ACT.Tanh, bias=hgb[:, :], scale=0.5
                                       ).then_inc(l_eg.sem, 1)
                        act.wait_ge(*l_d1.now(i, 4))
                        act.activation(low[:, :, :], low[:, :, :], ACT.Exp).then_inc(l_ex.sem, 1)

        def experts(tag, acc, h_all, comb, w_in, n_exp, f_dim, func):
            wa, wb, used, hid, acted_h, outs, added = moes[tag]
            nf = f_dim // P
            loads = [wa, wb]
            with ExitStack() as st:
                w = [sb(f"{tag}_w{j}", [P, 2 * f_dim + nf + U], stack=st) for j in range(2)]
                hs = [sb(f"{tag}_hs{j}", [P, nf, U], stack=st) for j in range(2)]
                ps_h = bank(f"{tag}_ps_h", st, 4)
                ps_o = bank(f"{tag}_ps_o", st, 2)
                for e in range(n_exp):
                    b = e % 2
                    o_b1, o_b2 = 2 * f_dim, 2 * f_dim + nf
                    with pool.loop_block(NU // 2) as block:
                        @block.sync
                        def _(sp):
                            for n in ([0, 1] if e == 0 else [e + 1]):
                                if n < n_exp:
                                    sp.dma_start(w[n % 2][:, :], w_in[n]).then_inc(loads[n % 2], 16)

                        @block.tensor
                        def _(pe):
                            pe.wait_ge(loads[b], 16 * (e // 2 + 1))
                            with pe.Fori(0, NU // 2) as i:
                                for j in range(2):
                                    for f in range(nf):
                                        k = (j * nf + f) % 4
                                        if nf == 4:
                                            pe.wait_ge(*(acted_h[1].last(i, f + 1) if j == 0
                                                         else acted_h[0].now(i, f + 1)))
                                        else:
                                            pe.wait_ge(*acted_h[j].last(i, f + 1))
                                        pe.matmul(ps_h[:, k, :], w[b][:, f * P:(f + 1) * P],
                                                  h_all[:, ds((i * 2 + j) * U, U)], start=True, stop=True
                                                  ).then_inc(hid[j].sem, 1)
                                for j in range(2):
                                    pe.wait_ge(*added[j].last(i, UT))
                                    pe.matmul(ps_o[:, j, :], c("ones", rows=1), w[b][0:1, o_b2:o_b2 + U],
                                              start=True, stop=False, skip_group_check=True)
                                    for f in range(nf):
                                        pe.wait_ge(*acted_h[j].now(i, f + 1))
                                        for t in range(UT):
                                            ins = pe.matmul(ps_o[:, j, t * D:(t + 1) * D], hs[j][:, f, t * P:(t + 1) * P],
                                                            w[b][:, f_dim + f * D:f_dim + (f + 1) * D], start=False,
                                                            stop=(f == nf - 1 and t == UT - 1), skip_group_check=True)
                                    ins.then_inc(outs[j].sem, 1)

                        @block.scalar
                        def _(act):
                            act.wait_ge(loads[b], 16 * (e // 2 + 1))
                            with act.Fori(0, NU // 2) as i:
                                for j in range(2):
                                    for f in range(nf):
                                        act.wait_ge(*hid[j].now(i, f + 1))
                                        act.wait_ge(*outs[j].last(i, 1))
                                        act.activation(hs[j][:, f, :], ps_h[:, (j * nf + f) % 4, :], func,
                                                       bias=w[b][:, o_b1 + f:o_b1 + f + 1]).then_inc(acted_h[j].sem, 1)

                        @block.vector
                        def _(dve):
                            with dve.Fori(0, NU // 2) as i:
                                for j in range(2):
                                    dve.wait_ge(*outs[j].now(i, 1))
                                    for t in range(UT):
                                        tile = (i * 2 + j) * UT + t
                                        xs = acc[:, ds(tile, 1), :].rearrange("p o d -> p (o d)")
                                        ce = comb[:, ds(tile, 1), e:e + 1].rearrange("p o e -> p (o e)")
                                        dve.scalar_tensor_tensor(xs, ps_o[:, j, t * D:(t + 1) * D], ce, xs,
                                                                 ALU.mult, ALU.add).then_inc(added[j].sem, 1)

        def pick(dve, sel, lg, m, w3, n):
            link(dve, dve.tensor_reduce(m, lg, AX, ALU.max))
            link(dve, dve.tensor_tensor(sel, lg, m.unsqueeze(2).to_broadcast([P, NT, n]), ALU.is_equal))
            rank = c("rank", 0, n).unsqueeze(1).to_broadcast([P, NT, n])
            link(dve, dve.tensor_tensor(sel, sel, rank, ALU.mult))
            link(dve, dve.tensor_reduce(w3, sel, AX, ALU.max))
            link(dve, dve.tensor_tensor(sel, sel, w3.unsqueeze(2).to_broadcast([P, NT, n]), ALU.is_equal))

        def over_tiles(v, n):
            return v.unsqueeze(2).to_broadcast([P, NT, n])

        stats(x_res)
        with ExitStack() as st1:
            h_all = sb("h_all1", [P, NT * P], stack=st1)
            comb = sb("comb1", [P, NT, E1 + 1], stack=st1)
            lg = sb("lg1", [P, NT, E1], stack=st1)
            route("m1", x_res, c("gate1"), c("gate1b", rows=1), E1, lg, h_all)
            with ExitStack() as st:
                s1, s2 = (sb(f"m1_sel{j}", [P, NT, E1], stack=st) for j in range(2))
                m1, m2, t1 = (sb(f"m1_t{j}", [P, NT], stack=st) for j in range(3))
                with nc.Block() as block:
                    k0 = n_chain[0]

                    @block.vector
                    def _(dve):
                        link(dve, dve.memset(comb[:, :, :], 1.0))
                        pick(dve, s1[:, :, :], lg[:, :, :], m1[:, :], t1[:, :], E1)
                        link(dve, dve.scalar_tensor_tensor(lg[:, :, :], s1[:, :, :], -BIG, lg[:, :, :], ALU.mult, ALU.add))
                        pick(dve, s2[:, :, :], lg[:, :, :], m2[:, :], t1[:, :], E1)
                        link(dve, dve.tensor_tensor(m2[:, :], m2[:, :], m1[:, :], ALU.subtract))
                        n_act[0] += 1
                        dve.wait_ge(acted, n_act[0])
                        link(dve, dve.tensor_scalar(t1[:, :], m2[:, :], 1.0, None, ALU.add))
                        link(dve, dve.reciprocal(m1[:, :], t1[:, :]))
                        link(dve, dve.tensor_tensor(m2[:, :], m2[:, :], m1[:, :], ALU.mult))
                        link(dve, dve.tensor_tensor(s1[:, :, :], s1[:, :, :], over_tiles(m1[:, :], E1), ALU.mult))
                        link(dve, dve.tensor_tensor(s2[:, :, :], s2[:, :, :], over_tiles(m2[:, :], E1), ALU.mult))
                        link(dve, dve.tensor_tensor(comb[:, :, 0:E1], s1[:, :, :], s2[:, :, :], ALU.add))

                    @block.scalar
                    def _(act):
                        act.wait_ge(chained, k0 + 13)
                        act.activation(m2[:, :], m2[:, :], ACT.Exp).then_inc(acted, 1)
            experts("e1", x_res, h_all, comb, w1_in, E1 + 1, F1, ACT.Gelu)

        PQ = (0, 1, 2, 0, 1, 0)
        PK = (0, 0, 0, 1, 1, 2)
        KR = len(PQ) * HD
        KM = KR + 3

        def project(tag, src, w, keep=None):
            fr, s = projections[tag]
            low_rank = w["low"] is not None
            with ExitStack() as st:
                nrm = [sb(f"{tag}_nrm{j}", [P, UT, P], stack=st) for j in range(2)]
                hT = [sb(f"{tag}_hT{j}", [P, U], stack=st) for j in range(2)]
                low = [sb(f"{tag}_low{j}", [64, U], stack=st) for j in range(2)]
                parts = [sb(f"{tag}_parts{j}", [P, 2, 3, U], BF16, stack=st) for j in range(2)]
                rest = [sb(f"{tag}_rest{j}", [P, 2, U], stack=st) for j in range(2)]
                v1 = [sb(f"{tag}_v{j}", [P, UT, NH, HD + 1], stack=st) for j in range(2)]
                ps_t = bank(f"{tag}_ps_t", st, 2)
                ps_low = bank(f"{tag}_ps_low", st)
                ps_qk = bank(f"{tag}_ps_qk", st, 4)
                ps_v = bank(f"{tag}_ps_v", st)
                with pool.loop_block(NU // 2) as block:
                    k_set = n_chain[0] + 2

                    @block.vector
                    def _(dve):
                        for j in range(2):
                            link(dve, dve.memset(v1[j][:, :, :, :], 1.0))
                        with dve.Fori(0, NU // 2) as i:
                            for j in range(2):
                                norm_tiles(dve, fr.nrm, nrm[j], src, (i * 2 + j) * UT, UT, rstd, fr.tps.last(i, j + 1),
                                           None if keep is None else s["kept"].last(i, j + 1))
                            for j in range(2):
                                for n in range(2):
                                    k = 2 * j + n + 1
                                    dve.wait_ge(*s["hi"].now(i, k))
                                    dve.wait_ge(*s["stored"][j].last(i, 32 * len(PQ)))
                                    if w["b"][n] is None:
                                        dve.tensor_tensor(rest[j][:, n, :], ps_qk[:, 2 * j + n, :], parts[j][:, n, 0, :],
                                                          ALU.subtract).then_inc(s["r1"].sem, 1)
                                    else:
                                        dve.scalar_tensor_tensor(rest[j][:, n, :], ps_qk[:, 2 * j + n, :], w["b"][n],
                                                                 parts[j][:, n, 0, :], ALU.add, ALU.subtract
                                                                 ).then_inc(s["r1"].sem, 1)
                                    dve.wait_ge(*s["r1"].now(i, k))
                                    dve.tensor_copy(parts[j][:, n, 1, :], rest[j][:, n, :]).then_inc(s["mid"].sem, 1)
                                    dve.wait_ge(*s["mid"].now(i, k))
                                    dve.tensor_tensor(parts[j][:, n, 2, :], rest[j][:, n, :], parts[j][:, n, 1, :],
                                                      ALU.subtract).then_inc(s["lo"].sem, 1)
                                dve.wait_ge(*s["v"].now(i, j + 1))
                                dve.wait_ge(*s["v_stored"][j].last(i, 16))
                                dve.tensor_copy(v1[j][:, :, :, 0:HD],
                                                ps_v[:, 0, :].rearrange("p (t h e) -> p t h e", t=UT, h=NH)
                                                ).then_inc(s["vc"].sem, 1)

                    if keep is not None:
                        @block.gpsimd
                        def _(gp):
                            with gp.Fori(0, NU // 2) as i:
                                for j in range(2):
                                    gp.wait_ge(*fr.nrm.now(i, j + 1))
                                    gp.tensor_copy(keep[:, ds((i * 2 + j) * UT, UT), :], nrm[j][:, :, :]
                                                   ).then_inc(s["kept"].sem, 1)

                    @block.tensor
                    def _(pe):
                        with pe.Fori(0, NU // 2) as i:
                            for j in range(2):
                                turn_tiles(pe, fr.tps, ps_t[:, j, :], nrm[j], UT, fr.nrm.now(i, j + 1),
                                           fr.hT.last(i, j + 1))
                            for j in range(2):
                                pe.wait_ge(*fr.hT.now(i, j + 1))
                                q_in = kv_in = hT[j][:, :]
                                if low_rank:
                                    pe.wait_ge(*(s["lowc"].now(i, 1) if j else s["lowc"].last(i, 2)))
                                    pe.matmul(ps_low[0:64, 0, :], w["low"], hT[j][:, :], start=True, stop=True
                                              ).then_inc(s["low"].sem, 1)
                                    pe.wait_ge(*s["lowc"].now(i, j + 1))
                                    q_in, kv_in = low[j][0:32, :], low[j][32:64, :]
                                for n, x_t in enumerate((q_in, kv_in)):
                                    pe.wait_ge(*s["r1"].last(i, 2 * j + n + 1))
                                    pe.matmul(ps_qk[:, 2 * j + n, :], w["qk"][n], x_t, start=True, stop=True
                                              ).then_inc(s["pr"].sem, 1)
                                pe.wait_ge(*(s["vc"].now(i, 1) if j else s["vc"].last(i, 2)))
                                for t in range(UT):
                                    dst = ps_v[:, 0, t * D:(t + 1) * D]
                                    if w["bv"] is not None:
                                        pe.matmul(dst, c("ones", rows=1), w["bv"], start=True, stop=False)
                                    ins = pe.matmul(dst, kv_in[:, t * P:(t + 1) * P], w["v"],
                                                    start=(w["bv"] is None), stop=True)
                                ins.then_inc(s["v"].sem, 1)

                    @block.scalar
                    def _(act):
                        with act.Fori(0, NU // 2) as i:
                            for j in range(2):
                                act.wait_ge(*fr.tps.now(i, j + 1))
                                act.wait_ge(*s["v"].last(i, j + 1))
                                act.activation(hT[j][:, :], ps_t[:, j, :], ACT.Copy).then_inc(fr.hT.sem, 1)
                            for j in range(2):
                                if low_rank:
                                    act.wait_ge(*s["low"].now(i, j + 1))
                                    act.activation(low[j][:, :], ps_low[0:64, 0, :], ACT.Copy).then_inc(s["lowc"].sem, 1)
                                for n in range(2):
                                    act.wait_ge(*s["pr"].now(i, 2 * j + n + 1))
                                    act.wait_ge(*s["stored"][j].last(i, 32 * len(PQ)))
                                    if w["b"][n] is None:
                                        ins = act.activation(parts[j][:, n, 0, :], ps_qk[:, 2 * j + n, :], ACT.Copy)
                                    else:
                                        ins = act.activation(parts[j][:, n, 0, :], ps_qk[:, 2 * j + n, :], ACT.Identity,
                                                             bias=w["b"][n])
                                    ins.then_inc(s["hi"].sem, 1)

                    @block.sync
                    def _(sp):
                        sp.wait_ge(chained, k_set)
                        with sp.Fori(0, NU // 2) as i:
                            for j in range(2):
                                sp.wait_ge(*s["lo"].now(i, 2 * j + 2))
                                for n, (d, order) in enumerate(((q_stack, PQ), (k_stack, PK))):
                                    for r, a in enumerate(order):
                                        sp.dma_start(d[r * HD:(r + 1) * HD, :, ds((i * 2 + j) * U, U)].rearrange("e h t -> h e t"),
                                                     parts[j][:, n, a, :]).then_inc(s["stored"][j].sem, 16)
                                sp.wait_ge(*s["vc"].now(i, j + 1))
                                sp.dma_start(v_ones[ds((i * 2 + j) * UT, UT)].rearrange("t p w -> p t w"),
                                             v1[j][:, :, :, :].rearrange("p t h e -> p t (h e)")
                                             ).then_inc(s["v_stored"][j].sem, 16)
                        for j in range(2):
                            sp.wait_ge(*s["stored"][j].now(NU // 2 - 1, 32 * len(PQ)))
                            sp.wait_ge(*s["v_stored"][j].now(NU // 2 - 1, 16))

        HG = 4
        GROUPS = NH // HG
        SLOTS = 4

        def attend(tag, causal, dst, w):
            s = attns[tag]
            scale = HD ** -0.5
            VW = HD + 1

            def at(name, b, k):
                return s[name].now(b, k)

            with ExitStack() as st:
                sq = [sb(f"{tag}_sq{u}", [64, NH, SEQ], BF16, stack=st) for u in range(SLOTS)]
                sk = [sb(f"{tag}_sk{u}", [64, NH, SEQ], BF16, stack=st) for u in range(SLOTS)]
                vb = [sb(f"{tag}_vb{u}", [P, TPB, NH, VW], stack=st) for u in range(SLOTS)]
                mx = sb(f"{tag}_mx", [P, NH, TPB], stack=st)
                nm = sb(f"{tag}_nm", [P, TPB, NH], stack=st)
                mpart = sb(f"{tag}_mpart", [NH, 3, SEQ], BF16, stack=st)
                mrest = sb(f"{tag}_mrest", [NH, SEQ], stack=st)
                pt = [sb(f"{tag}_pt{n}", [P, HG, TPB, SEQ], stack=st) for n in range(2)]
                sums = [sb(f"{tag}_sums{n}", [P, SEQ], stack=st) for n in range(2)]
                rec = sb(f"{tag}_rec", [P, TPB, HG], stack=st)
                on = sb(f"{tag}_on", [P, TPB, NH, HD], stack=st)
                oT = sb(f"{tag}_oT", [P, SEQ], stack=st)
                if causal:
                    msk = sb(f"{tag}_msk", [P, 3 * P], stack=st)
                    mskb = sb(f"{tag}_mskb", [P, 3 * P], BF16, stack=st)
                ps_1 = bank(f"{tag}_ps_1", st, 2)
                ps_2 = bank(f"{tag}_ps_2", st, 3)
                ps_o = bank(f"{tag}_ps_o", st)
                ps_s = bank(f"{tag}_ps_s", st)
                ps_m = bank(f"{tag}_ps_m", st)

                def run(eng, step):
                    for b in range(-2, 1):
                        step(b, b % SLOTS, b // SLOTS, first=True, turn=b >= -1, body=b >= 0, tail=False)
                    with eng.Fori(0, (NB - 4) // SLOTS) as i:
                        for v in range(1, SLOTS + 1):
                            step(i * SLOTS + v, v % SLOTS, i + v // SLOTS, first=True, turn=True, body=True, tail=True)
                    for b in range(NB - 3, NB + 1):
                        step(b, b % SLOTS, b // SLOTS, first=b + 2 < NB, turn=b + 1 < NB, body=b < NB, tail=True)

                def ahead(u, r, n):
                    return (u + n) % SLOTS, r + (u + n) // SLOTS

                with pool.loop_block(NB) as block:
                    k_set = n_chain[0] + SLOTS + (2 if causal else 1)

                    @block.sync
                    def _(sp):
                        if causal:
                            sp.dma_start(msk[:, :], maskb_in).then_inc(loaded, 16)
                        sp.wait_ge(chained, k_set)

                        def load(b, u):
                            cols = ds(b * SEQ, SEQ)
                            up = s["loaded"][u].sem
                            sp.dma_start(sq[u][0:KR, :, :], q_stack[:, :, cols]).then_inc(up, 16)
                            sp.dma_start(sk[u][0:KR, :, :], k_stack[:, :, cols]).then_inc(up, 16)
                            sp.dma_start(vb[u][:, :, :, :].rearrange("p t h e -> p t (h e)"),
                                         v_ones[ds(b * TPB, TPB)].rearrange("t p w -> p t w")).then_inc(up, 16)

                        def step(b, u, r, first, turn, body, tail):
                            if first and tail and not (isinstance(b, int) and b + 3 >= NB):
                                sp.wait_ge(*at("pv", b, 0))
                                load(b + 3, ahead(u, r, 3)[0])
                            if turn:
                                sp.wait_ge(*at("mlo", b + 1, 1))
                                sp.wait_ge(*at("min", b + 1, 0))
                                sp.dma_start(m_parts.rearrange("a h t -> h a t"), mpart[:, :, :]).then_inc(s["mout"].sem, 16)
                                sp.wait_ge(*at("mout", b + 1, 16))
                                sp.dma_start(sq[ahead(u, r, 1)[0]][KR:KM, :, :], m_parts).then_inc(s["min"].sem, 16)

                        for b in range(SLOTS):
                            load(b, b)
                        run(sp, step)

                    @block.vector
                    def _(dve):
                        for u in range(SLOTS):
                            link(dve, dve.memset(sk[u][32:64, :, :], 1.0))
                        link(dve, dve.memset(ps_o[:, :, :], 0.0))
                        if causal:
                            dve.wait_ge(loaded, 48)
                            link(dve, dve.tensor_copy(mskb[:, :], msk[:, :]))

                        def maximum(b, h):
                            dve.wait_ge(*at("s1", b, h + 1))
                            if h == 0:
                                dve.wait_ge(*at("nm", b, 0))
                            sv = ps_1[:, h % 2, :].rearrange("p (q k) -> p q k", q=TPB)
                            if causal:
                                dve.tensor_reduce(mx[:, h, 0:1], sv[:, 0, 0:P], AX, ALU.max)
                                dve.tensor_reduce(mx[:, h, 1:2], sv[:, 1, :], AX, ALU.max).then_inc(s["mx"].sem, 1)
                            else:
                                dve.tensor_reduce(mx[:, h, :], sv, AX, ALU.max).then_inc(s["mx"].sem, 1)

                        def norm(b, g):
                            tv = ps_s[:, 0, 0:SEQ].rearrange("p (q j e) -> p q j e", q=TPB, j=HG)
                            dve.wait_ge(*at("tu", b, g + 1))
                            dve.wait_ge(*at("on", b, g))
                            dve.reciprocal(rec[:, :, :], tv[:, :, :, HD]).then_inc(s["rec"].sem, 1)
                            dve.wait_ge(*at("rec", b, g + 1))
                            if g == 0:
                                dve.wait_ge(*at("ot", b, 0))
                            dve.tensor_tensor(on[:, :, HG * g:HG * (g + 1), :], tv[:, :, :, 0:HD],
                                              rec[:, :, :].unsqueeze(3).to_broadcast([P, TPB, HG, HD]), ALU.mult
                                              ).then_inc(s["on"].sem, 1)

                        def step(b, u, r, first, turn, body, tail):
                            for g in range(GROUPS):
                                if first:
                                    for j in range(HG - 1):
                                        maximum(b + 2, HG * g + j)
                                if g < 2 and tail:
                                    norm(b - 1, g + 2)
                                if g >= 2 and body:
                                    norm(b, g - 2)
                                if g == 1 and turn:
                                    dve.wait_ge(*at("mhi", b + 1, 1))
                                    dve.wait_ge(*at("mlo", b + 1, 0))
                                    dve.tensor_tensor(mrest[:, :], ps_m[0:NH, 0, 0:SEQ], mpart[:, 0, :], ALU.subtract
                                                      ).then_inc(s["mr"].sem, 1)
                                if g == 3 and tail:
                                    dve.wait_ge(*at("out", b - 1, 1))
                                    xd = dst[:, ds((b - 1) * TPB, TPB), :]
                                    dve.tensor_tensor(xd, xd, ps_m[:, 0, 0:SEQ].rearrange("p (t d) -> p t d", t=TPB),
                                                      ALU.add).then_inc(s["x"].sem, 1)
                                if first:
                                    maximum(b + 2, HG * g + HG - 1)
                            if first:
                                dve.wait_ge(*at("mx", b + 2, NH))
                                dve.wait_ge(*at("mt", b + 2, 0))
                                dve.tensor_scalar(nm[:, :, :].rearrange("p q h -> p h q"), mx[:, :, :], -1.0, None, ALU.mult
                                                  ).then_inc(s["nm"].sem, 1)

                        run(dve, step)

                    @block.gpsimd
                    def _(gp):
                        def step(b, u, r, first, turn, body, tail):
                            if turn:
                                gp.wait_ge(*at("mmid", b + 1, 1))
                                gp.tensor_tensor(mpart[:, 2, :], mrest[:, :], mpart[:, 1, :], ALU.subtract
                                                 ).then_inc(s["mlo"].sem, 1)

                        run(gp, step)

                    @block.tensor
                    def _(pe):
                        pe.wait_ge(chained, k_set)

                        def max_scores(b, u, r, h):
                            if h == 0:
                                pe.wait_ge(*s["loaded"][u].now(r, 48))
                            pe.wait_ge(*at("mx", b, h - 1))
                            for q in range(TPB):
                                nk = (q + 1) * P if causal else SEQ
                                o = ps_1[:, h % 2, q * SEQ:q * SEQ + nk]
                                ins = pe.matmul(o, sq[u][0:KR, h, q * P:(q + 1) * P], sk[u][0:KR, h, 0:nk],
                                                start=True, stop=not causal)
                                if causal:
                                    ins = pe.matmul(o[:, q * P:nk], mskb[:, 0:P], mskb[:, P:2 * P],
                                                    start=False, stop=True)
                            ins.then_inc(s["s1"].sem, 1)

                        def scores(b, u, h):
                            if h == 0:
                                pe.wait_ge(*at("min", b, 16))
                            pe.wait_ge(*at("ex", b, h - 2 if h else 0))
                            for t in range(TPB):
                                q0 = t * P if causal else 0
                                o = ps_2[:, h % 3, t * SEQ:(t + 1) * SEQ]
                                ins = pe.matmul(o[:, q0:], sk[u][0:KM, h, t * P:(t + 1) * P], sq[u][0:KM, h, q0:],
                                                start=True, stop=not causal)
                                if causal:
                                    ins = pe.matmul(o[:, q0:q0 + P], mskb[:, 0:P], mskb[:, 2 * P:3 * P],
                                                    start=False, stop=True)
                            ins.then_inc(s["s2"].sem, 1)

                        def weigh(b, u, g):
                            pe.wait_ge(*at("ex", b, HG * (g + 1)))
                            pe.wait_ge(*at("ev", b, g))
                            for t in range(TPB):
                                q0 = t * P if causal else 0
                                for j in range(HG):
                                    o = ps_o[32 * j:32 * j + VW, 0, q0:SEQ]
                                    ins = pe.matmul(o, vb[u][:, t, HG * g + j, :], pt[g % 2][:, j, t, q0:], start=(t == 0),
                                                    stop=(t == TPB - 1), skip_group_check=True)
                            ins.then_inc(s["pv"].sem, 1)

                        def turn_sums(b, g):
                            pe.wait_ge(*at("ev", b, g + 1))
                            pe.wait_ge(*at("on", b, g))
                            for q in range(TPB):
                                ins = pe.transpose(ps_s[:, 0, q * P:(q + 1) * P], sums[g % 2][:, q * P:(q + 1) * P], ident)
                            ins.then_inc(s["tu"].sem, 1)

                        def turn_max(b):
                            pe.wait_ge(*at("nm", b, 1))
                            pe.wait_ge(*at("x", b, -2))
                            for q in range(TPB):
                                ins = pe.transpose(ps_m[0:NH, 0, q * P:(q + 1) * P], nm[:, q, :], ident)
                            ins.then_inc(s["mt"].sem, 1)

                        def turn_out(b, mr_wait):
                            pe.wait_ge(*at("on", b, GROUPS))
                            if mr_wait:
                                pe.wait_ge(*at("mr", b + 2, 1))
                            pe.wait_ge(*at("x", b, 0))
                            for q in range(TPB):
                                ins = pe.transpose(ps_m[:, 0, q * P:(q + 1) * P],
                                                   on[:, q, :, :].rearrange("p h e -> p (h e)"), ident)
                            ins.then_inc(s["ot"].sem, 1)

                        def project_out(b):
                            pe.wait_ge(*at("otc", b, 1))
                            for t in range(TPB):
                                o = ps_m[:, 0, t * D:(t + 1) * D]
                                if w["bo"] is not None:
                                    pe.matmul(o, c("ones", rows=1), w["bo"], start=True, stop=False)
                                ins = pe.matmul(o, oT[:, t * P:(t + 1) * P], w["o"], start=(w["bo"] is None), stop=True)
                            ins.then_inc(s["out"].sem, 1)

                        def step(b, u, r, first, turn, body, tail):
                            later = ahead(u, r, 2)
                            for g in range(GROUPS):
                                for j in range(HG):
                                    if body:
                                        scores(b, u, HG * g + j)
                                    if j == 2:
                                        if g and body:
                                            weigh(b, u, g - 1)
                                        if not g and tail:
                                            weigh(b - 1, (u - 1) % SLOTS, GROUPS - 1)
                                    if j == 3:
                                        if g < 2 and tail:
                                            turn_sums(b - 1, g + 2)
                                        if g == 0 and turn:
                                            turn_max(b + 1)
                                        if g == 2 and tail:
                                            turn_out(b - 1, turn)
                                        if g >= 2 and body:
                                            turn_sums(b, g - 2)
                                        if g == 3 and tail:
                                            project_out(b - 1)
                                    if first:
                                        max_scores(b + 2, *later, HG * g + j)

                        run(pe, step)

                    @block.scalar
                    def _(act):
                        def weights(b, h):
                            g, j = h // HG, h % HG
                            act.wait_ge(*at("s2", b, h + 1))
                            act.wait_ge(*at("pv", b, g - 1))
                            sv = ps_2[:, h % 3, :].rearrange("p (t q) -> p t q", t=TPB)
                            to = pt[g % 2][:, j]
                            if causal:
                                act.activation(to[:, 0, :], sv[:, 0, :], ACT.Exp, scale=scale)
                                act.activation(to[:, 1, P:], sv[:, 1, P:], ACT.Exp, scale=scale).then_inc(s["ex"].sem, 1)
                            else:
                                act.activation(to, sv, ACT.Exp, scale=scale).then_inc(s["ex"].sem, 1)

                        def keep_sums(b, g):
                            act.wait_ge(*at("pv", b, g + 1))
                            act.wait_ge(*at("tu", b, g - 1))
                            act.activation(sums[g % 2][:, :], ps_o[:, 0, 0:SEQ], ACT.Copy
                                           ).then_inc(s["ev"].sem, 1)

                        def step(b, u, r, first, turn, body, tail):
                            for g in range(GROUPS):
                                if body:
                                    for j in range(HG - 1):
                                        weights(b, HG * g + j)
                                if g and body:
                                    keep_sums(b, g - 1)
                                if not g and tail:
                                    keep_sums(b - 1, GROUPS - 1)
                                if body:
                                    weights(b, HG * g + HG - 1)
                                if g == 0 and turn:
                                    act.wait_ge(*at("mt", b + 1, 1))
                                    act.wait_ge(*at("mout", b + 1, 0))
                                    act.activation(mpart[:, 0, :], ps_m[0:NH, 0, 0:SEQ], ACT.Copy
                                                   ).then_inc(s["mhi"].sem, 1)
                                if g == 1 and turn:
                                    act.wait_ge(*at("mr", b + 1, 1))
                                    act.activation(mpart[:, 1, :], mrest[:, :], ACT.Copy).then_inc(s["mmid"].sem, 1)
                                if g == 2 and tail:
                                    act.wait_ge(*at("ot", b - 1, 1))
                                    act.wait_ge(*at("out", b - 1, 0))
                                    act.activation(oT[:, :], ps_m[:, 0, 0:SEQ], ACT.Copy).then_inc(s["otc"].sem, 1)

                        run(act, step)

        stats(x_res)
        project("p2", x_res, dict(low=c("wlow"), qk=(c("wuq", rows=32), pack[32:64, OFF["wuk"][0]:OFF["wuk"][0] + D]),
                                  b=(None, None), v=pack[32:64, OFF["wuv"][0]:OFF["wuv"][0] + D], bv=None))
        attend("h2", True, x_res, dict(o=c("wo2"), bo=None))

        stats(x_res)
        RA = (E2 + 1) * R2
        with ExitStack() as st2:
            h_all = sb("h_all2", [P, NT * P], stack=st2)
            comb = sb("comb2", [P, NT, E2 + 1], stack=st2)
            lg = sb("lg2", [P, NT, E2], stack=st2)
            route("m2", x_res, c("rout"), c("routb", rows=1), E2, lg, h_all)
            with ExitStack() as st:
                s1, s2, ex = (sb(f"m2_sel{j}", [P, NT, E2], stack=st) for j in range(3))
                m1, m2, t1 = (sb(f"m2_t{j}", [P, NT], stack=st) for j in range(3))
                with nc.Block() as block:
                    k0 = n_chain[0]

                    @block.vector
                    def _(dve):
                        link(dve, dve.memset(comb[:, :, :], 1.0))
                        softmax_rows(dve, lg[:, :, :], ex[:, :, :], m1[:, :], t1[:, :], E2)
                        link(dve, dve.tensor_tensor(ex[:, :, :], ex[:, :, :], over_tiles(t1[:, :], E2), ALU.mult))
                        pick(dve, s1[:, :, :], lg[:, :, :], m1[:, :], t1[:, :], E2)
                        link(dve, dve.scalar_tensor_tensor(lg[:, :, :], s1[:, :, :], -BIG, lg[:, :, :], ALU.mult, ALU.add))
                        pick(dve, s2[:, :, :], lg[:, :, :], m2[:, :], t1[:, :], E2)
                        link(dve, dve.tensor_tensor(s1[:, :, :], s1[:, :, :], s2[:, :, :], ALU.add))
                        link(dve, dve.tensor_tensor(s1[:, :, :], s1[:, :, :], ex[:, :, :], ALU.mult))
                        link(dve, dve.tensor_reduce(t1[:, :], s1[:, :, :], AX, ALU.add))
                        link(dve, dve.tensor_scalar(t1[:, :], t1[:, :], 1e-6, None, ALU.add))
                        link(dve, dve.reciprocal(t1[:, :], t1[:, :]))
                        link(dve, dve.tensor_tensor(comb[:, :, 0:E2], s1[:, :, :], over_tiles(t1[:, :], E2), ALU.mult))

                    @block.scalar
                    def _(act):
                        act.wait_ge(chained, k0 + 3)
                        act.activation(ex[:, :, :], ex[:, :, :], ACT.Exp).then_inc(acted, 1)

            with ExitStack() as st:
                hT = [sb(f"m_hT{j}", [P, U], stack=st) for j in range(2)]
                hw = [sb(f"m_hw{j}", [P, UT, RA], stack=st) for j in range(2)]
                hwT = [sb(f"m_hwT{j}", [RA, U], stack=st) for j in range(2)]
                ps_a = bank("m_ps_a", st, 2)
                ps_t = bank("m_ps_t", st, 2)
                ps_o = bank("m_ps_o", st, 2)
                with pool.loop_block(NU // 2) as block:
                    @block.vector
                    def _(dve):
                        with dve.Fori(0, NU // 2) as i:
                            for j in range(2):
                                first = (i * 2 + j) * UT
                                dve.wait_ge(*m_h.now(i, j + 1))
                                dve.wait_ge(*m_tr.last(i, j + 1))
                                for t in range(UT):
                                    cw = comb[:, ds(first + t, 1), :].rearrange("p o e -> p (o e)")
                                    ins = dve.tensor_tensor(
                                        hw[j][:, t, :].rearrange("p (e r) -> p e r", r=R2),
                                        ps_a[:, j, t * P:t * P + RA].rearrange("p (e r) -> p e r", r=R2),
                                        cw.unsqueeze(2).to_broadcast([P, E2 + 1, R2]), ALU.mult)
                                ins.then_inc(m_ts.sem, 1)
                            for j in range(2):
                                xs = x_res[:, ds((i * 2 + j) * UT, UT), :]
                                dve.wait_ge(*m_o.now(i, j + 1))
                                dve.tensor_tensor(xs, xs, ps_o[:, j, :].rearrange("p (t d) -> p t d", t=UT), ALU.add
                                                  ).then_inc(m_x.sem, 1)

                    @block.tensor
                    def _(pe):
                        with pe.Fori(0, NU // 2) as i:
                            for j in range(2):
                                pe.wait_ge(*m_c.now(i, j + 1))
                                pe.wait_ge(*m_ts.last(i, j + 1))
                                for t in range(UT):
                                    ins = pe.matmul(ps_a[:, j, t * P:t * P + RA], hT[j][:, t * P:(t + 1) * P], c("acat"),
                                                    start=True, stop=True)
                                ins.then_inc(m_h.sem, 1)
                            for j in range(2):
                                pe.wait_ge(*m_ts.now(i, j + 1))
                                pe.wait_ge(*m_tc.last(i, j + 1))
                                for t in range(UT):
                                    ins = pe.transpose(ps_t[0:RA, j, t * P:(t + 1) * P], hw[j][:, t, :], ident)
                                ins.then_inc(m_tr.sem, 1)
                            for j in range(2):
                                pe.wait_ge(*m_tc.now(i, j + 1))
                                pe.wait_ge(*m_x.last(i, j + 1))
                                for t in range(UT):
                                    o = ps_o[:, j, t * D:(t + 1) * D]
                                    pe.matmul(o, c("ones", rows=1), c("baseb", rows=1), start=True, stop=False)
                                    pe.matmul(o, hT[j][:, t * P:(t + 1) * P], c("basew"), start=False, stop=False)
                                    ins = pe.matmul(o, hwT[j][:, t * P:(t + 1) * P], c("bcat", rows=RA),
                                                    start=False, stop=True)
                                ins.then_inc(m_o.sem, 1)

                    @block.scalar
                    def _(act):
                        with act.Fori(0, NU // 2) as i:
                            for j in range(2):
                                act.wait_ge(*m_o.last(i, j + 1))
                                act.activation(hT[j][:, :], h_all[:, ds((i * 2 + j) * U, U)], ACT.Copy
                                               ).then_inc(m_c.sem, 1)
                            for j in range(2):
                                act.wait_ge(*m_tr.now(i, j + 1))
                                act.wait_ge(*m_o.last(i, j + 1))
                                act.activation(hwT[j][:, :], ps_t[0:RA, j, :], ACT.Copy).then_inc(m_tc.sem, 1)

        stats(x_res)
        with ExitStack() as st:
            nrm = [sb(f"s_nrm{j}", [P, UT, P], stack=st) for j in range(2)]
            hT = [sb(f"s_hT{j}", [P, 2, SEQ + 1], stack=st) for j in range(2)]
            mixed = [sb(f"s_mix{j}", [P, 2, SEQ], stack=st) for j in range(2)]
            rel = [sb(f"s_rel{j}", [P, 2, SEQ], stack=st) for j in range(2)]
            state = [sb(f"s_state{j}", [P, 2, SEQ], stack=st) for j in range(2)]
            dec = sb("s_dec", [P, SEQ], stack=st)
            omix = sb("s_omix", [P, 1], stack=st)
            ps_t = bank("s_ps_t", st, 2)
            ps_h = bank("s_ps_h", st, 2)
            ps_o = bank("s_ps_o", st, 2)
            with pool.loop_block(NU // 2) as block:
                k_set = n_chain[0] + 5

                @block.vector
                def _(dve):
                    for j in range(2):
                        link(dve, dve.memset(hT[j][:, :, :], 0.0))
                    link(dve, dve.memset(dec[:, :], 1.0))
                    link(dve, dve.tensor_scalar(dec[:, :], dec[:, :], c("decay"), None, ALU.mult))
                    link(dve, dve.tensor_scalar(omix[:, :], c("mix"), -1.0, 1.0, ALU.mult, ALU.add))
                    with dve.Fori(0, NU // 2) as i:
                        for j in range(2):
                            norm_tiles(dve, fr_s.nrm, nrm[j], x_res, (i * 2 + j) * UT, UT, rstd, fr_s.tps.last(i, j + 1))
                        for j in range(2):
                            dve.wait_ge(*fr_s.hT.now(i, j + 1))
                            dve.wait_ge(*s_pr.last(i, j + 1))
                            dve.tensor_scalar(mixed[j][:, :, :], hT[j][:, :, 0:SEQ], omix[:, :], None, ALU.mult
                                              ).then_inc(s_in.sem, 1)
                            dve.wait_ge(*s_in.now(i, 2 * j + 1))
                            dve.scalar_tensor_tensor(mixed[j][:, :, :], hT[j][:, :, 1:], c("mix"), mixed[j][:, :, :],
                                                     ALU.mult, ALU.add).then_inc(s_in.sem, 1)
                        for j in range(2):
                            dve.wait_ge(*s_re.now(i, j + 1))
                            dve.wait_ge(*s_o.last(i, j + 1))
                            for b in range(2):
                                dve.tensor_tensor_scan(state[j][:, b, :], dec[:, :], rel[j][:, b, :], 0.0,
                                                       ALU.mult, ALU.add).then_inc(s_sc.sem, 1)
                        for j in range(2):
                            xs = x_res[:, ds((i * 2 + j) * UT, UT), :]
                            dve.wait_ge(*s_o.now(i, j + 1))
                            dve.tensor_tensor(xs, xs, ps_o[:, j, :].rearrange("p (t d) -> p t d", t=UT), ALU.add
                                              ).then_inc(s_x.sem, 1)

                @block.tensor
                def _(pe):
                    with pe.Fori(0, NU // 2) as i:
                        for j in range(2):
                            turn_tiles(pe, fr_s.tps, ps_t[:, j, :], nrm[j], UT, fr_s.nrm.now(i, j + 1),
                                       fr_s.hT.last(i, j + 1))
                        for j in range(2):
                            pe.wait_ge(*s_in.now(i, 2 * j + 2))
                            pe.wait_ge(*s_re.last(i, j + 1))
                            pe.matmul(ps_h[:, j, :], c("win3"), mixed[j][:, :, :].rearrange("p b t -> p (b t)"),
                                      start=True, stop=True).then_inc(s_pr.sem, 1)
                        for j in range(2):
                            pe.wait_ge(*s_sc.now(i, 2 * j + 2))
                            pe.wait_ge(*s_x.last(i, j + 1))
                            for t in range(UT):
                                o = ps_o[:, j, t * D:(t + 1) * D]
                                pe.matmul(o, c("ones", rows=1), c("bout3", rows=1), start=True, stop=False)
                                ins = pe.matmul(o, state[j][:, t // TPB, (t % TPB) * P:(t % TPB + 1) * P], c("wout3"),
                                                start=False, stop=True)
                            ins.then_inc(s_o.sem, 1)

                @block.scalar
                def _(act):
                    act.wait_ge(chained, k_set)
                    with act.Fori(0, NU // 2) as i:
                        for j in range(2):
                            act.wait_ge(*fr_s.tps.now(i, j + 1))
                            act.wait_ge(*s_in.last(i, 2 * j + 2))
                            act.activation(hT[j][:, :, 1:], ps_t[:, j, :].rearrange("p (b t) -> p b t", b=2), ACT.Copy
                                           ).then_inc(fr_s.hT.sem, 1)
                        for j in range(2):
                            act.wait_ge(*s_pr.now(i, j + 1))
                            act.wait_ge(*s_sc.last(i, 2 * j + 2))
                            act.activation(rel[j][:, :, :], ps_h[:, j, :].rearrange("p (b t) -> p b t", b=2), ACT.Relu,
                                           bias=c("bin3")).then_inc(s_re.sem, 1)

        stats(x_res)
        with ExitStack() as st3:
            x2 = sb("x2", [P, NT, D], stack=st3)
            project("p3", x_res, dict(low=None, qk=(c("wq3"), c("wk3")), b=(c("bq3"), c("bk3")), v=c("wv3"),
                                      bv=c("bv3", rows=1)), keep=x2)
            attend("h3", False, x2, dict(o=c("wo3"), bo=c("bo3", rows=1)))
            stats(x2)
            with ExitStack() as st:
                h_all = sb("h_all3", [P, NT * P], stack=st)
                comb = sb("comb3", [P, NT, E3], stack=st)
                lg = sb("lg3", [P, NT, G3 + E3], stack=st)
                route("m3", x2, c("rt3"), c("rt3b", rows=1), G3 + E3, lg, h_all, (c("g1"), c("b1")))
                with ExitStack() as stm:
                    sel, ex = (sb(f"m3_g{j}", [P, NT, G3], stack=stm) for j in range(2))
                    el = sb("m3_el", [P, NT, 2], stack=stm)
                    tmp = sb("m3_tmp", [P, NT, 2], stack=stm)
                    sel2 = sb("m3_sel2", [P, NT, 2], stack=stm)
                    m1, t1, gp = (sb(f"m3_t{j}", [P, NT], stack=stm) for j in range(3))
                    with nc.Block() as block:
                        k0 = n_chain[0]

                        @block.vector
                        def _(dve):
                            softmax_rows(dve, lg[:, :, 0:G3], ex[:, :, :], m1[:, :], gp[:, :], G3)
                            pick(dve, sel[:, :, :], lg[:, :, 0:G3], m1[:, :], t1[:, :], G3)
                            for g in range(G3):
                                eg = lg[:, :, G3 + 2 * g:G3 + 2 * g + 2]
                                sg = over_tiles(sel[:, :, g], 2)
                                link(dve, dve.tensor_tensor(el[:, :, :] if g == 0 else tmp[:, :, :], eg, sg, ALU.mult))
                                if g:
                                    link(dve, dve.tensor_tensor(el[:, :, :], el[:, :, :], tmp[:, :, :], ALU.add))
                            softmax_rows(dve, el[:, :, :], tmp[:, :, :], m1[:, :], t1[:, :], 2)
                            link(dve, dve.tensor_tensor(gp[:, :], gp[:, :], t1[:, :], ALU.mult))
                            pick(dve, sel2[:, :, :], el[:, :, :], m1[:, :], t1[:, :], 2)
                            link(dve, dve.tensor_tensor(sel2[:, :, :], sel2[:, :, :], over_tiles(gp[:, :], 2), ALU.mult))
                            for g in range(G3):
                                link(dve, dve.tensor_tensor(comb[:, :, 2 * g:2 * g + 2], sel2[:, :, :],
                                                            over_tiles(sel[:, :, g], 2), ALU.mult))

                        @block.scalar
                        def _(act):
                            act.wait_ge(chained, k0 + 2)
                            act.activation(ex[:, :, :], ex[:, :, :], ACT.Exp).then_inc(acted, 1)
                            act.wait_ge(chained, k0 + 2 + 2 + 5 + 7 + 2)
                            act.activation(tmp[:, :, :], tmp[:, :, :], ACT.Exp).then_inc(acted, 1)
                experts("e3", x2, h_all, comb, w3_in, E3, F3, ACT.Relu)

            stats(x2)
            with ExitStack() as st:
                fin = [sb(f"z_fin{j}", [P, UT, D], stack=st) for j in range(2)]
                out_t = out.rearrange("(t p) d -> p t d", p=P)
                with pool.loop_block(NU // 2) as block:
                    @block.vector
                    def _(dve):
                        with dve.Fori(0, NU // 2) as i:
                            for j in range(2):
                                first = (i * 2 + j) * UT
                                norm_tiles(dve, z_n, fin[j], x2, first, UT, rstd, z_d[j].last(i, 16))
                                dve.wait_ge(*z_n.now(i, j + 1))
                                dve.tensor_tensor(fin[j][:, :, :], fin[j][:, :, :],
                                                  c("g2").unsqueeze(1).to_broadcast([P, UT, D]), ALU.mult
                                                  ).then_inc(z_a.sem, 1)
                                dve.wait_ge(*z_a.now(i, 3 * j + 1))
                                dve.tensor_tensor(fin[j][:, :, :], fin[j][:, :, :],
                                                  c("b2").unsqueeze(1).to_broadcast([P, UT, D]), ALU.add
                                                  ).then_inc(z_a.sem, 1)
                                dve.wait_ge(*z_a.now(i, 3 * j + 2))
                                dve.tensor_tensor(fin[j][:, :, :], fin[j][:, :, :], x_res[:, ds(first, UT), :], ALU.add
                                                  ).then_inc(z_a.sem, 1)

                    @block.sync
                    def _(sp):
                        with sp.Fori(0, NU // 2) as i:
                            for j in range(2):
                                sp.wait_ge(*z_a.now(i, 3 * j + 3))
                                sp.dma_start(out_t[:, ds((i * 2 + j) * UT, UT), :], fin[j][:, :, :]).then_inc(z_d[j].sem, 16)
                        for j in range(2):
                            sp.wait_ge(*z_d[j].now(NU // 2 - 1, 16))


def kernel(**inputs):
    import numpy as np
    import concourse.bacc as bacc
    from concourse.bass_utils import run_bass_kernel_spmd

    a = {k: np.ascontiguousarray(v) for k, v in inputs.items()}
    f32 = np.float32
    parts = {}

    def put(name, arr):
        parts[name] = arr if arr.ndim == 2 else arr[:, None]

    def blocks(arr):
        n = arr.shape[0] // P
        return arr.reshape(n, P, -1).transpose(1, 0, 2).reshape(P, -1)

    def row(arr):
        return arr.reshape(1, -1)

    def every(arr):
        return np.broadcast_to(arr.reshape(1, -1), (P, arr.size))

    def lower(arr):
        return np.concatenate([np.zeros((32, arr.shape[1]), f32), arr], 0)

    put("ident", np.eye(P, dtype=f32))
    put("ones", np.ones((P, P), f32))
    tri = np.triu(np.ones((P, P), f32))
    put("tri_st", np.concatenate([tri, np.ones((P, P), f32), tri], 1))
    put("iota", np.broadcast_to(np.arange(1, CAP + 1, dtype=f32), (P, CAP)))
    put("tvec", np.broadcast_to(np.arange(SEQ, dtype=f32), (P, SEQ)))
    put("rank", np.broadcast_to(np.arange(8, 0, -1, dtype=f32), (P, 8)))
    A = "L0_attn_"
    put("gam0", a[A + "norm_gamma"]); put("bet0", a[A + "norm_beta"])
    put("inw", a[A + "in_w"]); put("inb", blocks(a[A + "in_b"]))
    put("cw", blocks(a[A + "conv_w"].reshape(INNER, 3))); put("cbias", blocks(a[A + "conv_b"]))
    put("alog", blocks(a[A + "A_log"])); put("bp", blocks(a[A + "B_p"])); put("cp", blocks(a[A + "C_p"]))
    put("dp", blocks(a[A + "D_p"])); put("outw", blocks(a[A + "out_w"])); put("outb", row(a[A + "out_b"]))
    A = "L0_ffn_"
    put("gate0", a[A + "gate_w"].T); put("wsg", a[A + "Ws_g"].T); put("wsu", a[A + "Ws_u"].T)
    put("wsd", blocks(np.ascontiguousarray(a[A + "Ws_d"].T)))
    A = "L1_attn_"
    put("lng1", a[A + "ln_g"]); put("lnb1", a[A + "ln_b"]); put("qkvw", a[A + "qkv_w"])
    put("qkvb", blocks(a[A + "qkv_b"])); put("vb", row(a[A + "qkv_b"][2 * D:]))
    put("gw1", a[A + "gate_w"]); put("gb1", a[A + "gate_b"])
    A = "L1_ffn_"
    put("gate1", a[A + "gate_w"]); put("gate1b", row(a[A + "gate_b"]))
    A = "L2_attn_"
    put("wlow", np.concatenate([a[A + "W_dq"], a[A + "W_dkv"]], 1))
    put("wuq", a[A + "W_uq"]); put("wuk", lower(a[A + "W_uk"])); put("wuv", lower(a[A + "W_uv"]))
    put("wo2", a[A + "W_o"])
    A = "L2_ffn_"
    put("basew", a[A + "base_W"].T); put("baseb", row(a[A + "base_b"]))
    put("acat", np.concatenate([a[A + "routed_A"].reshape(E2 * R2, D), a[A + "shared_A"]], 0).T)
    put("bcat", np.concatenate([a[A + "routed_B"].transpose(0, 2, 1).reshape(E2 * R2, D), a[A + "shared_B"].T], 0))
    put("rout", a[A + "router_W"].T); put("routb", row(a[A + "router_b"]))
    A = "L3_attn_"
    put("win3", a[A + "W_in"].T); put("bin3", a[A + "b_in"]); put("wout3", a[A + "W_out"].T)
    put("bout3", row(a[A + "b_out"])); put("decay", every(a[A + "decay"])); put("mix", every(a[A + "mix"]))
    A = "L3_ffn_"
    w, b = a[A + "in_proj_w"], a[A + "in_proj_b"]
    put("wq3", w[:D].T); put("wk3", w[D:2 * D].T); put("wv3", w[2 * D:].T)
    put("bq3", b[:D]); put("bk3", b[D:2 * D])
    put("bv3", row(b[2 * D:])); put("wo3", a[A + "out_proj_w"].T); put("bo3", row(a[A + "out_proj_b"]))
    for n, s in (("g1", "ln1_g"), ("b1", "ln1_b"), ("g2", "ln2_g"), ("b2", "ln2_b")):
        put(n, every(a[A + s]))
    put("rt3", np.concatenate([a[A + "w_group"], a[A + "w_expert"].transpose(1, 0, 2).reshape(D, E3)], 1))
    put("rt3b", row(np.concatenate([a[A + "b_group"], a[A + "b_expert"].reshape(-1)])))
    pack = np.zeros((P, NPACK), f32)
    for name, (o, n) in OFF.items():
        m = parts[name]
        assert m.shape[1] == n, (name, m.shape, n)
        pack[:m.shape[0], o:o + n] = m

    def down(w, f):
        return w.reshape(w.shape[0], f // P, P, D).transpose(0, 2, 1, 3).reshape(w.shape[0], P, -1)

    A = "L0_ffn_"
    w0 = np.concatenate([a[A + "Wg"].transpose(0, 2, 1), a[A + "Wu"].transpose(0, 2, 1),
                         down(np.ascontiguousarray(a[A + "Wd"].transpose(0, 2, 1)), F0)], 2)

    def expert(wa, wb, ba, bb, f):
        e = wa.shape[0]
        o = np.zeros((e, P, 2 * f + f // P + U), f32)
        o[:, :, :f] = wa
        o[:, :, f:2 * f] = down(wb, f)
        o[:, :, 2 * f:2 * f + f // P] = ba.reshape(e, f // P, P).transpose(0, 2, 1)
        o[:, 0, 2 * f + f // P:] = np.broadcast_to(bb[:, None, :], (e, UT, D)).reshape(e, U)
        return o

    A = "L1_ffn_"
    w1 = expert(np.concatenate([a[A + "w1"], a[A + "ws1"][None]]), np.concatenate([a[A + "w2"], a[A + "ws2"][None]]),
                np.concatenate([a[A + "b1"], a[A + "bs1"][None]]), np.concatenate([a[A + "b2"], a[A + "bs2"][None]]), F1)
    A = "L3_ffn_"
    w3 = expert(a[A + "w1"], a[A + "w2"], a[A + "b1"], a[A + "b2"], F3)
    mask = np.where(np.arange(P)[None, :] <= np.arange(P)[:, None], 0.0, -BIG).astype(f32)
    masks = np.concatenate([np.eye(P, dtype=f32), mask, mask.T], 1)

    nc = bacc.Bacc("TRN2", target_bir_lowering=False, num_devices=1)
    arrays = {"x": a["L0_attn_x"].reshape(NB * SEQ, D), "pack": pack, "masks": masks,
              "w0": np.ascontiguousarray(w0), "w1": w1, "w3": w3}
    aps = [nc.dram_tensor("in_" + n, v.shape, F32, kind="ExternalInput").ap() for n, v in arrays.items()]
    out = nc.dram_tensor("out", (NB * SEQ, D), F32, kind="ExternalOutput").ap()
    ktab = nc.dram_tensor("ktab", (INNER, P + SEQ), F32).ap()
    ychan = nc.dram_tensor("ychan", (INNER, NB, SEQ), F32).ap()
    q_stack, k_stack = (nc.dram_tensor(n, (6 * HD, NH, NB * SEQ), BF16).ap() for n in ("q_stack", "k_stack"))
    v_ones = nc.dram_tensor("v_ones", (NT, P, NH * (HD + 1)), F32).ap()
    m_parts = nc.dram_tensor("m_parts", (3, NH, SEQ), BF16).ap()
    build(nc, *aps, out, ktab, ychan, q_stack, k_stack, v_ones, m_parts)
    r = run_bass_kernel_spmd(nc, [{"in_" + n: v for n, v in arrays.items()}], core_ids=[0])
    return r.results[0]["out"].reshape(NB, SEQ, D)
```

```python
from contextlib import ExitStack, contextmanager

import concourse.bass as bass
from concourse import mybir
from concourse.alu_op_type import AluOpType as ALU

ACT = mybir.ActivationFunctionType
AX = mybir.AxisListType.X
F32 = mybir.dt.float32
BF16 = mybir.dt.bfloat16
I32 = mybir.dt.int32
ds = bass.ds

P = 128
NB, SEQ, D = 32, 256, 128
TPB = SEQ // P
NT = NB * TPB
UT = 4
U = UT * P
NU = NT // UT
EPS = 1e-5
INNER, NSTATE = 256, 64
CB = INNER // P
E0, F0, CAP = 16, 256, SEQ * 2 // 16
E1, F1 = 8, 512
E2, R2 = 6, 16
E3, F3, G3 = 8, 256, 4
NH, HD = 16, 8
BIG = 1e30
CREDIT = 256

def tiles_of(choices):
    return -(-((NB * SEQ * choices + 8 * (P - 1)) // P) // 8) * 8


def spare_of(choices):
    return choices * NB * SEQ


def wide(f_dim):
    return 2 * f_dim + f_dim // P + D


PACK = [("ident", P), ("ones", P), ("tri_st", P + SEQ), ("iota", CAP), ("tvec", SEQ),
        ("rank", 8), ("token", tiles_of(2)),
        ("gam0", 1), ("bet0", 1), ("inw", 3 * INNER), ("inb", 3 * CB), ("cw", 3 * CB), ("cbias", CB),
        ("alog", CB * NSTATE), ("bp", CB * NSTATE), ("cp", CB * NSTATE), ("dp", CB), ("outw", CB * D), ("outb", D),
        ("gate0", E0), ("wsg", F0), ("wsu", F0), ("wsd", 2 * D),
        ("lng1", 1), ("lnb1", 1), ("qkvw", 3 * D), ("qkvb", 3), ("vb", D), ("gw1", D), ("gb1", 1),
        ("gate1", E1), ("gate1b", E1),
        ("wlow", 64), ("wuq", D), ("wuk", D), ("wuv", D), ("wo2", D),
        ("basew", D), ("acat", (E2 + 1) * R2), ("bcat", D), ("rout", E2), ("routb", E2),
        ("win3", D), ("bin3", 1), ("wout3", D), ("bout3", D), ("decay", 1), ("mix", 1),
        ("wq3", D), ("wk3", D), ("wv3", D), ("bq3", 1), ("bk3", 1), ("bv3", D), ("wo3", D), ("bo3", D),
        ("g1", D), ("b1", D), ("g2", D), ("b2", D), ("rt3", G3 + E3), ("rt3b", G3 + E3)]
OFF, NPACK = {}, 0
for _n, _c in PACK:
    OFF[_n] = (NPACK, _c)
    NPACK += _c
W0 = 3 * F0


class Signal:

    def __init__(self, semaphores, name, per):
        self.semaphores, self.name, self.per, self.held = semaphores, name, per, None

    @property
    def sem(self):
        if self.held is None:
            self.held = self.semaphores.take(self)
        return self.held[0]

    def raises(self, steps):
        return self.per * steps

    def now(self, i, k):
        return self.sem, i * self.per + (self.held[1] + k)

    def last(self, i, k):
        return self.sem, i * self.per + (self.held[1] + k - self.per)


    def ago(self, i, k, n):
        return self.sem, i * self.per + (self.held[1] + k - n * self.per)


def staggered(eng, units, slots, *stages):
    deep = max(lag for lag, _ in stages)
    rounds = (units - deep) // slots

    def step(i, s):
        for lag, work in stages:
            n = s - lag
            if i is not None:
                work(i * slots + n, n % slots, i + n // slots)
            elif 0 <= n < units:
                work(n, n % slots, n // slots)

    for s in range(deep):
        step(None, s)
    with eng.Fori(0, rounds) as i:
        for v in range(slots):
            step(i, deep + v)
    for s in range(deep + rounds * slots, units + deep):
        step(None, s)


class SlotSignal(Signal):

    def __init__(self, semaphores, name, per, u, of):
        super().__init__(semaphores, name, per)
        self.u, self.of = u, of

    def raises(self, steps):
        return self.per * len(range(self.u, steps, self.of))


class Semaphores:

    def __init__(self, nc, stack, count):
        self.nc, self.open = nc, []
        self.free = [stack.enter_context(nc.semaphore(f"signal{n}")) for n in range(count)]
        self.value = {s.num: CREDIT for s in self.free}
        with nc.Block() as block:
            @block.sync
            def _(sp):
                for s in self.free:
                    sp.sem_inc(s, CREDIT)

    def take(self, signal):
        held = self.free.pop(0)
        self.open.append((signal, held))
        return held, self.value[held.num]

    @contextmanager
    def loop_block(self, steps):
        with self.nc.Block() as block:
            yield block
        for signal, held in self.open:
            self.value[held.num] += signal.raises(steps)
            signal.held = None
            self.free.append(held)
        self.open = []


def build(nc, x_in, pack_in, maskb_in, w0_in, w1_in, w3_in, out, ktab, ychan, q_stack, k_stack, ones_rows, v_ones,
          m_parts, xs1, xs3, ys):
    ctx = ExitStack()
    with ctx:
        pool = Semaphores(nc, ctx, 48)

        def sem(name):
            return ctx.enter_context(nc.semaphore(name))

        def sig(name, per):
            return Signal(pool, name, per)

        def sb(name, shape, dt=F32, stack=ctx):
            return stack.enter_context(nc.sbuf_tensor(name, shape, dt))

        def bank(name, stack, n=1):
            return stack.enter_context(nc.psum_tensor(name, [P, n, 512], F32))

        x_res = sb("x_res", [P, NT, D])
        pack = sb("pack", [P, NPACK])
        mean = sb("mean", [P, NT])
        rstd = sb("rstd", [P, NT])
        rstd2 = sb("rstd2", [P, NT])
        bn6 = sb("bn6", [P, NT, 6])
        tmpa = sb("tmpa", [P, NT])
        tmpb = sb("tmpb", [P, NT])
        epsc = sb("epsc", [P, 1])

        def c(name, lo=0, n=None, rows=P):
            o, w = OFF[name]
            return pack[0:rows, o + lo:o + (w if n is None else lo + n)]

        ident = c("ident")
        loaded = sem("loaded")
        x_loaded = sem("x_loaded")
        ones_in = [sem(f"ones_in{n}") for n in range(2)]
        kready = sem("kready")
        chained = sem("chained")
        acted = sem("acted")
        peed = sem("peed")
        filled = sem("filled")
        scattered = [sem(f"scattered{j}") for j in range(4)]
        padded = sem("padded")
        n_chain, n_act, n_pe, n_filled, n_scattered = [0], [0], [0], [0], [0]
        idle = sb("idle", [P, 2])

        def link(dve, ins):
            n_chain[0] += 1
            ins.then_inc(chained, 1)
            dve.wait_ge(chained, n_chain[0])

        def act_done(ins):
            n_act[0] += 1
            ins.then_inc(acted, 1)

        def pe_done(ins):
            n_pe[0] += 1
            ins.then_inc(peed, 1)

        s_e = sig("decay_exp", 2 * CB)
        s_k = sig("table_sum", 2 * CB)

        class Front:
            def __init__(self, t, n):
                self.nrm = sig(t + "_normed", n)
                self.tps = sig(t + "_turned", n)
                self.hT = sig(t + "_hT_ready", n)

        fr_a = Front("a", 1)
        a_proj, a_up, a_conv, a_c3, a_c, a_silu, a_tr, a_u = (
            sig("a_" + n, CB) for n in ("proj", "up", "mid_tap", "left_tap", "convolved", "silu", "turned_u", "u_stored"))
        b_tz, b_st, b_mm, b_ev, b_ea, b_out = ([sig(f"b_toeplitz{j}", 64) for j in range(4)], sig("b_staged", 4), sig("b_conv", 8),
                                              sig("b_kept_odd", 4), sig("b_kept_even", 4), [sig(f"b_y_stored{j}", 16) for j in range(4)])
        fr_c = Front("c", 1)
        c_load = [SlotSignal(pool, f"c_y_loaded{j}", 32, j, 3) for j in range(3)]
        c_proj, c_sig, c_v, c_y, c_z, c_out, c_x = (sig("c_proj", CB), sig("c_sigmoid", 2 * CB), sig("c_silu", CB),
                                                    sig("c_y_used", CB), sig("c_z", CB), sig("c_outproj", 1), sig("c_x", 1))
        c_grown = sig("c_grown", 1)
        routes = {}
        for t in ("d", "m1", "m2", "m3"):
            routes[t] = (Front(t, 1), sig(t + "_logits", 1), sig(t + "_logits_kept", 1), sig(t + "_affine", 2),
                         sig(t + "_src_kept", 1))
        g_n, g_p, g_mm, g_x = sig("g_normed", 4), sig("g_onehot", 4), sig("g_gathered", 4), sig("g_stored", 4)
        x_w, x_gu, x_ge, x_h, x_o, x_s = ([sig(f"x_weights{j}", 16) for j in range(2)], sig("x_gate_up", 8), sig("x_gelu", 8),
                                         sig("x_hidden", 8), sig("x_down", 4), sig("x_kept", 4))
        fr_f = Front("f", 1)
        f_p, f_st, f_pt, f_ptc, f_eo, f_eoc, f_gu, f_ge, f_h, f_o, f_x = (
            sig("f_onehot", 2), sig("f_staged", 1), sig("f_turned_p", 2), sig("f_p_kept", 2), sig("f_turned_e", 1),
            sig("f_e_kept", 1), sig("f_gate_up", 1), sig("f_gelu", 1), sig("f_hidden", 1), sig("f_out", 1),
            sig("f_x", 1))
        f_h0 = sig("f_places", 2)
        fr_l = Front("l", 1)
        l_g, l_qk_in, l_tanh, l_gate, l_q, l_k, l_low, l_exp, l_v, l_vc, l_qk, l_a, l_am, l_o, l_den, l_rec, l_x = (
            sig("l_" + n, 1) for n in ("gate_proj", "qk_proj", "tanh", "gate", "q", "k", "low", "exp", "v", "v_kept", "qk_ready",
                                       "scores", "masked", "out", "den", "den_inverse", "x"))
        moes = {}
        collects = {}
        for t, nf, choices in (("e1", F1 // P, 2), ("e3", F3 // P, 1)):
            per = NT * choices // (NU // 2)
            moes[t] = (
                (sig(t + "_rows", per), sig(t + "_places", per), sig(t + "_row_hold", per)),
                ([sig(f"{t}{j}_hidden", nf) for j in range(2)], [sig(f"{t}{j}_acted", nf) for j in range(2)],
                 [sig(f"{t}{j}_out", 1) for j in range(2)], [sig(f"{t}{j}_x", 1) for j in range(2)], sem(t + "_shared_weights")),
                ([SlotSignal(pool, f"{t}_row_tiles{g}", 16, 0, 8) for g in range(2)], sig(t + "_weights", 1), sig(t + "_turned", 1),
                 sig(t + "_kept", 1), sig(t + "_tile_hidden", nf), sig(t + "_tile_acted", nf), sig(t + "_tile_out", 1),
                 SlotSignal(pool, t + "_empty", 2, 0, 8), SlotSignal(pool, t + "_keys", 2, 0, 8), sig(t + "_biased", 1), sig(t + "_result", 1),
                 sig(t + "_result_hold", 1)))
            collects[t] = ([sig(f"{t}{j}_results", 16 * choices) for j in range(4)],
                           [sig(f"{t}{j}_added", choices) for j in range(4)])
        m_ts, m_tr, m_tc, m_o, m_x = (sig("m_scaled", 1), sig("m_turned", 1), sig("m_kept", 1), sig("m_out", 1),
                                      sig("m_x", 1))
        m_c = sig("m_staged", 1)
        m_h = sig("m_low", 1)
        fr_s = Front("s", 1)
        s_in0, s_in, s_pr, s_re, s_sc, s_o, s_x = (sig("s_mixing", 1), sig("s_mixed", 1), sig("s_proj", 1), sig("s_relu", 1),
                                                   sig("s_scan", 2), sig("s_out", 1), sig("s_x", 1))
        projections = {t: (Front(t, 1), dict(
            {k: sig(f"{t}_{k}", n) for k, n in (("kept", 1), ("pr", 2), ("hi", 2), ("r1", 2),
                                               ("mid", 2), ("lo", 2), ("v", 1), ("vc", 1))},
            stored=[SlotSignal(pool, f"{t}_stored{j}", 96, j, 3) for j in range(3)],
            v_stored=[SlotSignal(pool, f"{t}_v_stored{j}", 16, j, 3) for j in range(3)])) for t in ("p2", "p3")}
        attns = {t: dict(
            {k: sig(f"{t}_{k}", n) for k, n in (
                ("s1", NH), ("mx", NH), ("nm", 1), ("mt", 1), ("mhi", 1), ("mr", 1), ("mmid", 1), ("mlo", 1), ("mout", 16),
                ("min", 16), ("s2", NH), ("ex", NH), ("pv", 4), ("ev", 4), ("tu", 4), ("rec", 4), ("on", 4), ("ot", 1),
                ("otc", 1), ("out", 1), ("x", 1))},
            loaded=[SlotSignal(pool, f"{t}_loaded{u}", 48, u, 4) for u in range(4)]) for t in ("h2", "h3")}
        z_s, z_n, z_g, z_a = sig("z_shifted", 1), sig("z_normed", 1), sig("z_gain", 1), sig("z_done", 1)
        z_d = [SlotSignal(pool, f"z_stored{j}", 16, j, 6) for j in range(6)]

        with nc.Block() as block:
            @block.sync
            def _(sp):
                sp.dma_start(pack[:, :], pack_in).then_inc(loaded, 16)
                sp.wait_ge(loaded, 16)

            @block.vector
            def _(dve):
                link(dve, dve.memset(epsc[:, :], EPS))

        def count(dve, src, first, n, *written):
            dve.wait_ge(*written)
            for t in range(n):
                dve.bn_stats(bn6[:, ds(first + t, 1), :], src[:, ds(first + t, 1), :])

        def stats(src, twice=False, counted=True):
            with nc.Block() as block:
                k0 = n_chain[0]

                @block.vector
                def _(dve):
                    if not counted:
                        with dve.Fori(0, NT // 8) as i:
                            for t in range(8):
                                dve.bn_stats(bn6[:, ds(i * 8 + t, 1), :], src[:, ds(i * 8 + t, 1), :])
                    link(dve, dve.tensor_copy(tmpa[:, 0:1], epsc[:, 0:1]))
                    link(dve, dve.tensor_tensor(mean[:, :], bn6[:, :, 1], bn6[:, :, 4], ALU.add))
                    link(dve, dve.tensor_tensor(tmpa[:, :], bn6[:, :, 1], bn6[:, :, 4], ALU.subtract))
                    link(dve, dve.tensor_tensor(tmpb[:, :], bn6[:, :, 2], bn6[:, :, 5], ALU.add))
                    link(dve, dve.tensor_scalar(mean[:, :], mean[:, :], 0.5, None, ALU.mult))
                    link(dve, dve.tensor_tensor(tmpa[:, :], tmpa[:, :], tmpa[:, :], ALU.mult))
                    link(dve, dve.tensor_scalar(tmpa[:, :], tmpa[:, :], 0.25, EPS, ALU.mult, ALU.add))
                    link(dve, dve.scalar_tensor_tensor(tmpa[:, :], tmpb[:, :], 1.0 / D, tmpa[:, :], ALU.mult, ALU.add))

                    def root(dst):
                        n_act[0] += 1
                        dve.wait_ge(acted, n_act[0])
                        link(dve, dve.reciprocal(dst[:, :], dst[:, :]))
                        link(dve, dve.tensor_tensor(tmpb[:, :], dst[:, :], dst[:, :], ALU.mult))
                        link(dve, dve.tensor_tensor(tmpb[:, :], tmpb[:, :], tmpa[:, :], ALU.mult))
                        link(dve, dve.tensor_scalar(tmpb[:, :], tmpb[:, :], -0.5, 1.5, ALU.mult, ALU.add))
                        link(dve, dve.tensor_tensor(dst[:, :], dst[:, :], tmpb[:, :], ALU.mult))

                    root(rstd)
                    if twice:
                        link(dve, dve.tensor_scalar(tmpa[:, :], tmpa[:, :], EPS, None, ALU.subtract))
                        link(dve, dve.tensor_tensor(tmpa[:, :], tmpa[:, :], rstd[:, :], ALU.mult))
                        link(dve, dve.tensor_tensor(tmpa[:, :], tmpa[:, :], rstd[:, :], ALU.mult))
                        link(dve, dve.tensor_scalar(tmpa[:, :], tmpa[:, :], EPS, None, ALU.add))
                        root(rstd2)
                        link(dve, dve.tensor_tensor(rstd2[:, :], rstd2[:, :], rstd[:, :], ALU.mult))

                @block.scalar
                def _(act):
                    act.wait_ge(chained, k0 + 8)
                    act.activation(rstd[:, :], tmpa[:, :], ACT.Sqrt).then_inc(acted, 1)
                    if twice:
                        act.wait_ge(chained, k0 + 8 + 5 + 4)
                        act.activation(rstd2[:, :], tmpa[:, :], ACT.Sqrt).then_inc(acted, 1)

        def norm_tiles(dve, done, dst, src, first, n, r, ready_to_write, extra=None):
            dve.wait_ge(*ready_to_write)
            if extra is not None:
                dve.wait_ge(*extra)
            for t in range(n):
                ins = dve.tensor_scalar(dst[:, t, :], src[:, ds(first + t, 1), :].rearrange("p o d -> p (o d)"),
                                        mean[:, ds(first + t, 1)], r[:, ds(first + t, 1)], ALU.subtract, ALU.mult)
            ins.then_inc(done.sem, 1)

        def turn_tiles(pe, done, ps, nrm, n, *waits):
            for w in waits:
                pe.wait_ge(*w)
            for t in range(n):
                ins = pe.transpose(ps[:, t * P:(t + 1) * P], nrm[:, t, :], ident)
            ins.then_inc(done.sem, 1)

        with ExitStack() as st:
            aexp = sb("aexp", [P, CB * NSTATE], stack=st)
            cbp = sb("cbp", [P, CB * NSTATE], stack=st)
            esb = sb("esb", [P, 2 * CB, SEQ], stack=st)
            ksb = sb("ksb", [P, CB, P + SEQ], stack=st)
            rows_of = ((2, xs1), (1, xs3))
            pad = [sb(f"pad{n}", [P, 8, D + 2], stack=st) for n in range(2)]
            pad_key = sb("pad_key", [P, 1], I32, stack=st)
            k_ones = sb("k_ones", [3 * NH, SEQ], BF16, stack=st)
            with pool.loop_block(NSTATE // 2) as block:
                a0 = n_act[0]
                k_neg = n_chain[0] + 3

                @block.scalar
                def _(act):
                    act_done(act.activation(aexp[:, :], c("alog"), ACT.Exp))
                    act.wait_ge(chained, k_neg)
                    with act.Fori(0, NSTATE // 2) as i:
                        for n in range(2 * CB):
                            act.wait_ge(*s_k.last(i, n + 1))
                            act.activation(esb[:, n, :], c("tvec"), ACT.Exp,
                                           scale=aexp[:, ds(i * 2 + (n // CB + n % CB * NSTATE), 1)]).then_inc(s_e.sem, 1)

                @block.vector
                def _(dve):
                    link(dve, dve.memset(ksb[:, :, :], 0.0))
                    link(dve, dve.tensor_tensor(cbp[:, :], c("bp"), c("cp"), ALU.mult))
                    dve.wait_ge(acted, a0 + 1)
                    link(dve, dve.tensor_scalar(aexp[:, :], aexp[:, :], -1.0, None, ALU.mult))
                    with dve.Fori(0, NSTATE // 2) as i:
                        for n in range(2 * CB):
                            b = n % CB
                            dve.wait_ge(*s_k.now(i, n + 1 - CB))
                            dve.wait_ge(*s_e.now(i, n + 1))
                            dve.scalar_tensor_tensor(ksb[:, b, P:], esb[:, n, :],
                                                     cbp[:, ds(i * 2 + (n // CB + b * NSTATE), 1)],
                                                     ksb[:, b, P:], ALU.mult, ALU.add).then_inc(s_k.sem, 1)
                    dve.wait_ge(*s_k.now(NSTATE // 2 - 1, 2 * CB))
                    link(dve, dve.tensor_tensor(ksb[:, :, P], ksb[:, :, P], c("dp"), ALU.add))

                @block.gpsimd
                def _(gp):
                    for n, (choices, _) in enumerate(rows_of):
                        gp.memset(pad[n][:, :, 0:D + 1], 0.0)
                        gp.memset(pad[n][:, :, D + 1:D + 2], float(spare_of(choices)))
                    gp.tensor_scalar(pad_key[:, :], c("token", 0, 1), float(spare_of(2)), None, ALU.add)
                    gp.memset(k_ones[:, :], 1.0)
                    gp.memset(idle[:, :], 0.0).then_inc(padded, 1)
                    gp.wait_ge(padded, 1)
                    for j in range(4):
                        gp.indirect_dma_start(ys[:, :], bass.IndirectOffsetOnAxis(ap=pad_key[:, :], axis=0),
                                              pad[0][:, 0, 0:D], None).then_inc(scattered[j], 16)
                        gp.wait_ge(scattered[j], 16)
                    n_scattered[0] = 16

                @block.sync
                def _(sp):
                    sp.dma_start(x_res[:, :, :], x_in.rearrange("(t p) d -> p t d", p=P)).then_inc(x_loaded, 16)
                    sp.wait_ge(padded, 1)
                    for n, (choices, rows) in enumerate(rows_of):
                        for t in range(0, tiles_of(choices), 8):
                            n_filled[0] += 16
                            sp.dma_start(rows[t * P:(t + 8) * P, :].rearrange("(t p) w -> p t w", p=P), pad[n][:, :, :]
                                         ).then_inc(filled, 16)
                    n_filled[0] += 16
                    sp.dma_start(ones_rows.rearrange("r h t -> (r h) t"), k_ones[:, :]).then_inc(filled, 16)
                    sp.wait_ge(filled, n_filled[0])
                    sp.wait_ge(chained, k_neg + 1)
                    sp.dma_start(ktab.rearrange("(b p) l -> p b l", p=P), ksb[:, :, :]).then_inc(kready, 16)
                    sp.wait_ge(kready, 16)
                    sp.wait_ge(x_loaded, 16)

        stats(x_res, twice=True, counted=False)

        with ExitStack() as st_u:
            u_all = sb("u_all", [P, TPB, NB, INNER], stack=st_u)
            with ExitStack() as st:
                S = 4
                nrm = sb("a_nrm", [P, UT, P], stack=st)
                hT = [sb(f"a_hT{j}", [P, U], stack=st) for j in range(S)]
                up = [sb(f"a_up{j}", [P, CB, 2, SEQ + 2], stack=st) for j in range(S)]
                cv = [sb(f"a_cv{j}", [P, CB, 2, SEQ], stack=st) for j in range(S)]
                rv = [sb(f"a_rv{j}", [P, CB, 2, SEQ], stack=st) for j in range(S)]
                ps_t = bank("a_ps_t", st)
                ps_u = bank("a_ps_u", st, CB)
                ps_r = bank("a_ps_r", st, CB)
                with pool.loop_block(NU) as block:
                    ch0 = n_chain[0] + S

                    @block.vector
                    def _(dve):
                        for j in range(S):
                            link(dve, dve.memset(up[j][:, :, :, :], 0.0))

                        def normed(n, j, r):
                            norm_tiles(dve, fr_a.nrm, nrm, x_res, n * UT, UT, rstd2, fr_a.tps.last(n, 1))

                        def keep(n, j, r):
                            for b in range(CB):
                                dve.wait_ge(*a_tr.now(n, b + 1))
                                dst = u_all[:, :, ds(n * 2, 2), b * P:(b + 1) * P]
                                dve.tensor_copy(dst.rearrange("p h b c -> p b h c"),
                                                ps_r[:, b, :].rearrange("p (b h c) -> p b h c", b=2, h=TPB)
                                                ).then_inc(a_u.sem, 1)

                        def convolve(n, j, r):
                            for b in range(CB):
                                dve.wait_ge(*a_up.now(n, b + 1))
                                dve.wait_ge(*a_silu.ago(n, b + 1, S))
                                dve.tensor_scalar(cv[j][:, b], up[j][:, b, :, 1:SEQ + 1], c("cw", b * 3 + 1, 1),
                                                  c("cbias", b, 1), ALU.mult, ALU.add).then_inc(a_conv.sem, 1)
                            for b in range(CB):
                                dve.wait_ge(*a_conv.now(n, b + 1))
                                dve.scalar_tensor_tensor(cv[j][:, b], up[j][:, b, :, 0:SEQ], c("cw", b * 3, 1),
                                                         cv[j][:, b], ALU.mult, ALU.add).then_inc(a_c3.sem, 1)
                            for b in range(CB):
                                dve.wait_ge(*a_c3.now(n, b + 1))
                                dve.scalar_tensor_tensor(cv[j][:, b], up[j][:, b, :, 2:SEQ + 2],
                                                         c("cw", b * 3 + 2, 1), cv[j][:, b],
                                                         ALU.mult, ALU.add).then_inc(a_c.sem, 1)

                        staggered(dve, NU, S, (0, normed), (4, keep), (2, convolve))

                    @block.tensor
                    def _(pe):
                        pe.wait_ge(chained, ch0)

                        def turn(n, j, r):
                            turn_tiles(pe, fr_a.tps, ps_t[:, 0, :], nrm, UT, fr_a.nrm.now(n, 1), fr_a.hT.last(n, 1))

                        def project(n, j, r):
                            pe.wait_ge(*fr_a.hT.now(n, 1))
                            for b in range(CB):
                                pe.wait_ge(*a_up.last(n, b + 1))
                                pe.matmul(ps_u[:, b, :], c("inw", b * P, P), hT[j][:, :], start=True, stop=True
                                          ).then_inc(a_proj.sem, 1)

                        def turn_u(n, j, r):
                            for b in range(CB):
                                pe.wait_ge(*a_silu.now(n, b + 1))
                                pe.wait_ge(*a_u.last(n, b + 1))
                                for t in range(UT):
                                    h = TPB - 1 - t % TPB
                                    ins = pe.transpose(ps_r[:, b, t * P:(t + 1) * P],
                                                       rv[j][:, b, t // TPB, h * P:(h + 1) * P], ident)
                                ins.then_inc(a_tr.sem, 1)

                        staggered(pe, NU, S, (1, project), (0, turn), (3, turn_u))

                    @block.scalar
                    def _(act):
                        act.wait_ge(chained, ch0)

                        def keep(n, j, r):
                            act.wait_ge(*fr_a.tps.now(n, 1))
                            act.wait_ge(*a_proj.ago(n, CB, S))
                            act.activation(hT[j][:, :], ps_t[:, 0, :], ACT.Identity, bias=c("bet0"), scale=c("gam0")
                                           ).then_inc(fr_a.hT.sem, 1)

                        def biased(n, j, r):
                            for b in range(CB):
                                act.wait_ge(*a_proj.now(n, b + 1))
                                act.wait_ge(*a_c.ago(n, b + 1, S))
                                act.activation(up[j][:, b, :, 1:SEQ + 1], ps_u[:, b, :].rearrange("p (b t) -> p b t", b=2),
                                               ACT.Identity, bias=c("inb", b, 1)).then_inc(a_up.sem, 1)

                        def silu(n, j, r):
                            for b in range(CB):
                                act.wait_ge(*a_c.now(n, b + 1))
                                act.wait_ge(*a_tr.ago(n, b + 1, S))
                                end = cv[j][:, b, 0, SEQ - 1:SEQ]
                                down = bass.AP(end.tensor, end.offset, [list(end.ap[0]), [SEQ, 2], [-1, SEQ]])
                                act.activation(rv[j][:, b], down, ACT.Silu).then_inc(a_silu.sem, 1)

                        staggered(act, NU, S, (1, biased), (0, keep), (3, silu))

            with ExitStack() as st:
                GC = 8
                QUADS = GC // 4
                STRIP = 32
                SLOTS = 4
                STEPS = INNER // GC // SLOTS
                tz = [sb(f"b_tz{j}", [P, GC, SEQ], stack=st) for j in range(SLOTS)]
                us = [sb(f"b_us{j}", [P, TPB, GC, NB], stack=st) for j in range(SLOTS)]
                ysb = [sb(f"b_y{j}", [P, QUADS, SEQ], stack=st) for j in range(SLOTS)]
                ps_y = bank("b_ps_y", st, 2 * QUADS)
                with pool.loop_block(STEPS) as block:
                    k_zero = n_chain[0] + SLOTS

                    @block.sync
                    def _(sp):
                        sp.wait_ge(chained, k_zero)
                        with sp.Fori(0, STEPS) as i:
                            for j in range(SLOTS):
                                sp.wait_ge(*b_mm.last(i, QUADS * (j + 1)))
                                rows = ktab[ds((i * SLOTS + j) * GC, GC), :]
                                for q in range(P // STRIP):
                                    late = P - (q + 1) * STRIP
                                    strip = bass.AP(rows.tensor, rows.offset + 1 + q * STRIP + late,
                                                    [[1, STRIP], [P + SEQ, GC], [1, SEQ - late]])
                                    sp.dma_start(tz[j][q * STRIP:(q + 1) * STRIP, :, late:], strip).then_inc(b_tz[j].sem, 16)
                        for j in range(SLOTS):
                            sp.wait_ge(*b_out[j].now(STEPS - 1, 16))

                    @block.vector
                    def _(dve):
                        for j in range(SLOTS):
                            link(dve, dve.memset(tz[j][:, :, 0:P - STRIP], 0.0))

                        with dve.Fori(0, STEPS) as i:
                            def stage(j):
                                dve.wait_ge(*b_mm.last(i, QUADS * (j + 1)))
                                dve.tensor_copy(us[j][:, :, :, :].rearrange("p h c b -> p h b c"),
                                                u_all[:, :, :, ds((i * SLOTS + j) * GC, GC)]).then_inc(b_st.sem, 1)

                            stage(0)
                            for j in range(SLOTS):
                                if j + 1 < SLOTS:
                                    stage(j + 1)
                                dve.wait_ge(*b_mm.now(i, QUADS * j + 2))
                                dve.wait_ge(*b_out[j].last(i, 16))
                                dve.tensor_copy(ysb[j][:, 1, :], ps_y[:, j % 2 * QUADS + 1, 0:SEQ]).then_inc(b_ev.sem, 1)

                    @block.tensor
                    def _(pe):
                        with pe.Fori(0, STEPS) as i:
                            for j in range(SLOTS):
                                pe.wait_ge(*b_tz[j].now(i, 16 * (P // STRIP)))
                                pe.wait_ge(*b_st.now(i, j + 1))
                                if j >= 2:
                                    pe.wait_ge(*b_ev.now(i, j - 1))
                                    pe.wait_ge(*b_ea.now(i, j - 1))
                                else:
                                    pe.wait_ge(*b_ev.last(i, j + SLOTS - 1))
                                    pe.wait_ge(*b_ea.last(i, j + SLOTS - 1))
                                for q in range(QUADS):
                                    for g in range(4):
                                        ch = 4 * q + g
                                        strip = ps_y[32 * g:32 * g + 32, j % 2 * QUADS + q, :]
                                        pe.matmul(strip[:, 0:SEQ], us[j][:, 0, ch, :], tz[j][:, ch, :],
                                                  start=True, stop=False)
                                        ins = pe.matmul(strip[:, P:SEQ], us[j][:, 1, ch, :], tz[j][:, ch, 0:P],
                                                        start=False, stop=True)
                                    ins.then_inc(b_mm.sem, 1)

                    @block.scalar
                    def _(act):
                        with act.Fori(0, STEPS) as i:
                            for j in range(SLOTS):
                                act.wait_ge(*b_mm.now(i, QUADS * j + 1))
                                act.wait_ge(*b_out[j].last(i, 16))
                                act.activation(ysb[j][:, 0, :], ps_y[:, j % 2 * QUADS, 0:SEQ], ACT.Copy).then_inc(b_ea.sem, 1)
                                act.wait_ge(*b_ea.now(i, j + 1))
                                act.wait_ge(*b_ev.now(i, j + 1))
                                dst = ychan[ds((i * SLOTS + j) * GC, GC)].rearrange("(q g) b t -> (g b) q t", g=4)
                                act.dma_start(dst, ysb[j][:, :, :]).then_inc(b_out[j].sem, 16)

        with ExitStack() as st:
            S = 3
            nrm = sb("c_nrm", [P, UT, P], stack=st)
            hT = [sb(f"c_hT{j}", [P, U], stack=st) for j in range(S)]
            yT = [sb(f"c_yT{j}", [P, CB, U], stack=st) for j in range(S)]
            sv = [sb(f"c_sv{j}", [P, CB, U], stack=st) for j in range(S)]
            sg = [sb(f"c_sg{j}", [P, CB, U], stack=st) for j in range(S)]
            grow = sb("c_grow", [P, NT], stack=st)
            sink = sb("c_sink", [P, NT], stack=st)
            ps_t = bank("c_ps_t", st)
            ps_v = bank("c_ps_v", st, CB)
            ps_g = bank("c_ps_g", st, CB)
            ps_o = bank("c_ps_o", st, S)
            with pool.loop_block(NU) as block:
                k_set = n_chain[0] + 2

                @block.sync
                def _(sp):
                    def load(n, j, r):
                        sp.wait_ge(*c_y.ago(n, CB, S))
                        for b in range(CB):
                            src = ychan[b * P:(b + 1) * P, ds(n * 2, 2), :]
                            sp.dma_start(yT[j][:, b, :].rearrange("p (b t) -> p b t", b=2), src
                                         ).then_inc(c_load[j].sem, 16)

                    staggered(sp, NU, S, (0, load))

                @block.vector
                def _(dve):
                    link(dve, dve.tensor_scalar(grow[:, :], rstd[:, :], 1.0, None, ALU.add))
                    link(dve, dve.scalar_tensor_tensor(sink[:, :], mean[:, :], -1.0, rstd[:, :], ALU.mult, ALU.mult))

                    def normed(n, j, r):
                        norm_tiles(dve, fr_c.nrm, nrm, x_res, n * UT, UT, rstd2, fr_c.tps.last(n, 1))

                    def gated(n, j, r):
                        dve.wait_ge(*c_load[j].now(r, 32))
                        for b in range(CB):
                            dve.wait_ge(*c_sig.now(n, 2 * b + 2))
                            dve.scalar_tensor_tensor(sv[j][:, b, :], ps_v[:, b, :], c("inb", CB + b, 1),
                                                     sv[j][:, b, :], ALU.add, ALU.mult).then_inc(c_v.sem, 1)
                            dve.tensor_tensor(sg[j][:, b, :], sg[j][:, b, :], yT[j][:, b, :],
                                              ALU.mult).then_inc(c_y.sem, 1)
                            dve.wait_ge(*c_v.now(n, b + 1))
                            dve.wait_ge(*c_y.now(n, b + 1))
                            dve.tensor_tensor(sv[j][:, b, :], sv[j][:, b, :], sg[j][:, b, :],
                                              ALU.add).then_inc(c_z.sem, 1)

                    def added(n, j, r):
                        dve.wait_ge(*c_grown.now(n, 1))
                        dve.wait_ge(*c_out.now(n, 1))
                        xs = x_res[:, ds(n * UT, UT), :]
                        dve.tensor_tensor(xs, xs, ps_o[:, j, :].rearrange("p (t d) -> p t d", t=UT), ALU.add
                                          ).then_inc(c_x.sem, 1)
                        count(dve, x_res, n * UT, UT, *c_x.now(n, 1))

                    staggered(dve, NU, S, (0, normed), (3, added), (1, gated))

                @block.tensor
                def _(pe):
                    def turn(n, j, r):
                        turn_tiles(pe, fr_c.tps, ps_t[:, 0, :], nrm, UT, fr_c.nrm.now(n, 1), fr_c.hT.last(n, 1))

                    def project(n, j, r):
                        pe.wait_ge(*fr_c.hT.now(n, 1))
                        for b in range(CB):
                            pe.wait_ge(*c_z.last(n, b + 1))
                            pe.matmul(ps_v[:, b, :], c("inw", (CB + b) * P, P), hT[j][:, :], start=True, stop=True)
                            pe.matmul(ps_g[:, b, :], c("inw", (2 * CB + b) * P, P), hT[j][:, :],
                                      start=True, stop=True).then_inc(c_proj.sem, 1)

                    def project_out(n, j, r):
                        pe.wait_ge(*c_z.now(n, CB))
                        pe.wait_ge(*c_x.ago(n, 1, S))
                        for t in range(UT):
                            dst = ps_o[:, j, t * P:(t + 1) * P]
                            pe.matmul(dst, c("ones", rows=1), c("outb", rows=1), start=True, stop=False)
                            for b in range(CB):
                                ins = pe.matmul(dst, sv[j][:, b, t * P:(t + 1) * P], c("outw", b * D, D),
                                                start=False, stop=(b == CB - 1))
                        ins.then_inc(c_out.sem, 1)

                    staggered(pe, NU, S, (1, project), (0, turn), (2, project_out))

                @block.scalar
                def _(act):
                    def keep(n, j, r):
                        act.wait_ge(*fr_c.tps.now(n, 1))
                        act.wait_ge(*c_proj.ago(n, CB, S))
                        act.activation(hT[j][:, :], ps_t[:, 0, :], ACT.Identity, bias=c("bet0"), scale=c("gam0")
                                       ).then_inc(fr_c.hT.sem, 1)

                    def gated(n, j, r):
                        for b in range(CB):
                            act.wait_ge(*c_proj.now(n, b + 1))
                            act.wait_ge(*c_out.ago(n, 1, S))
                            act.activation(sv[j][:, b, :], ps_v[:, b, :], ACT.Sigmoid, bias=c("inb", CB + b, 1)
                                           ).then_inc(c_sig.sem, 1)
                            act.activation(sg[j][:, b, :], ps_g[:, b, :], ACT.Sigmoid, bias=c("inb", 2 * CB + b, 1)
                                           ).then_inc(c_sig.sem, 1)

                    def grown(n, j, r):
                        act.wait_ge(*fr_c.nrm.now(n, 1))
                        for t in range(UT):
                            tile = ds(n * UT + t, 1)
                            x_t = x_res[:, tile, :].rearrange("p o d -> p (o d)")
                            ins = act.activation(x_t, x_t, ACT.Identity, scale=grow[:, tile], bias=sink[:, tile])
                        ins.then_inc(c_grown.sem, 1)

                    act.wait_ge(chained, k_set)
                    staggered(act, NU, S, (1, gated), (0, keep), (1, grown))

        def route(tag, src, weights, bias, n_out, logits, h_all=None, affine=None, fetch=None):
            fr, lg, kept, aff, put = routes[tag]
            S = 3
            with ExitStack() as st:
                nrm = [sb(f"{tag}_nrm{j}", [P, UT, P], stack=st) for j in range(S)]
                hT = [sb(f"{tag}_hT{j}", [P, U], stack=st) for j in range(S)]
                ps_t = bank(f"{tag}_ps_t", st, S)
                ps_l = bank(f"{tag}_ps_l", st, S)
                with pool.loop_block(NU) as block:
                    if fetch is not None:
                        @block.sync
                        def _(sp):
                            w, w_in = fetch
                            for e in range(w.shape[1]):
                                n_filled[0] += 16
                                sp.dma_start(w[:, e, :], w_in[e]).then_inc(filled, 16)
                            sp.wait_ge(filled, n_filled[0])

                    @block.vector
                    def _(dve):
                        def normed(n, j, r):
                            free = fr.tps.ago(n, 1, S)
                            if affine is None:
                                norm_tiles(dve, fr.nrm, nrm[j], src, n * UT, UT, rstd, free)
                                return
                            dve.wait_ge(*put.ago(n, 1, S))
                            norm_tiles(dve, aff, nrm[j], src, n * UT, UT, rstd, free)
                            dve.wait_ge(*aff.now(n, 1))
                            dve.tensor_tensor(nrm[j][:, :, :], nrm[j][:, :, :],
                                              affine[0].unsqueeze(1).to_broadcast([P, UT, D]), ALU.mult).then_inc(aff.sem, 1)
                            dve.wait_ge(*aff.now(n, 2))
                            dve.tensor_tensor(nrm[j][:, :, :], nrm[j][:, :, :],
                                              affine[1].unsqueeze(1).to_broadcast([P, UT, D]), ALU.add
                                              ).then_inc(fr.nrm.sem, 1)

                        def keep(n, j, r):
                            dve.wait_ge(*lg.now(n, 1))
                            to, got = logits[:, ds(n * UT, UT), :], ps_l[:, j, 0:UT * n_out].rearrange("p (t e) -> p t e", t=UT)
                            if bias is None:
                                ins = dve.tensor_copy(to, got)
                            else:
                                ins = dve.tensor_tensor(to, got, bias.unsqueeze(1).to_broadcast([P, UT, n_out]), ALU.add)
                            ins.then_inc(kept.sem, 1)

                        staggered(dve, NU, S, (0, normed), (3, keep))

                    @block.tensor
                    def _(pe):
                        def turn(n, j, r):
                            turn_tiles(pe, fr.tps, ps_t[:, j, :], nrm[j], UT, fr.nrm.now(n, 1), fr.hT.ago(n, 1, S))

                        def project(n, j, r):
                            pe.wait_ge(*fr.hT.now(n, 1))
                            pe.wait_ge(*kept.ago(n, 1, S))
                            for t in range(UT):
                                ins = pe.matmul(ps_l[:, j, t * n_out:(t + 1) * n_out], hT[j][:, t * P:(t + 1) * P], weights,
                                                start=True, stop=True)
                            ins.then_inc(lg.sem, 1)

                        staggered(pe, NU, S, (2, project), (0, turn))

                    @block.scalar
                    def _(act):
                        def keep(n, j, r):
                            act.wait_ge(*fr.tps.now(n, 1))
                            act.wait_ge(*lg.ago(n, 1, S))
                            if h_all is not None:
                                act.activation(h_all[:, ds(n * U, U)], ps_t[:, j, :], ACT.Copy)
                            act.activation(hT[j][:, :], ps_t[:, j, :], ACT.Copy).then_inc(fr.hT.sem, 1)
                            if affine is not None:
                                act.activation(src[:, ds(n * UT, UT), :], nrm[j][:, :, :], ACT.Copy).then_inc(put.sem, 1)

                        staggered(act, NU, S, (0, keep))

        def softmax_rows(dve, lg, out_e, m, s, n):
            link(dve, dve.tensor_reduce(m, lg, AX, ALU.max))
            link(dve, dve.tensor_tensor(out_e, lg, m.unsqueeze(2).to_broadcast([P, NT, n]), ALU.subtract))
            n_act[0] += 1
            dve.wait_ge(acted, n_act[0])
            link(dve, dve.tensor_reduce(s, out_e, AX, ALU.add))
            link(dve, dve.reciprocal(s, s))

        stats(x_res)
        NG = NB // 8
        with ExitStack() as st_d:
            score = sb("d_score", [P, NT, E0], stack=st_d)
            place = sb("d_place", [P, NT, E0], stack=st_d)
            route("d", x_res, c("gate0"), None, E0, score)
            with ExitStack() as st:
                mx = sb("d_max", [P, NT], stack=st)
                rs = sb("d_rsum", [P, NT], stack=st)
                rows = sb("d_rows", [P, NG, SEQ], stack=st)
                work = sb("d_work", [P, NG, SEQ], stack=st)
                taken = sb("d_taken", [P, NG, SEQ], stack=st)
                zero = sb("d_zero", [P, SEQ], stack=st)
                top = sb("d_top", [P, NG, 8], stack=st)
                lin = sb("d_lin", [P, TPB * NG, P], stack=st)
                ps_s = bank("d_ps_s", st, 2)
                ps_p = bank("d_ps_p", st, 2)
                with nc.Block() as block:
                    k0, p0 = n_chain[0], n_pe[0]

                    @block.vector
                    def _(dve):
                        link(dve, dve.memset(zero[:, :], 0.0))
                        softmax_rows(dve, score[:, :, :], score[:, :, :], mx[:, :], rs[:, :], E0)
                        link(dve, dve.tensor_tensor(score[:, :, :], score[:, :, :],
                                                    rs[:, :].unsqueeze(2).to_broadcast([P, NT, E0]), ALU.mult))
                        lv = lin[:, :, :].rearrange("p (g h) (b e) -> p g h b e", g=NG, b=8)
                        sv = score[:, :, :].rearrange("p (g b h) e -> p g h b e", g=NG, b=8)
                        for g in range(NG):
                            link(dve, dve.tensor_copy(lv[:, g], sv[:, g]))
                        dve.wait_ge(peed, p0 + 1)
                        link(dve, dve.tensor_copy(rows[:, :, :].rearrange("p g t -> p (g t)"),
                                                  ps_s[:, :, :].rearrange("p k n -> p (k n)")))
                        for g in range(NG):
                            src = rows
                            for _ in range(CAP // 8):
                                link(dve, dve.max(top[:, g, :], src[:, g, :]))
                                link(dve, dve.match_replace(work[:, g, :], top[:, g, :], src[:, g, :], -1.0))
                                src = work
                            link(dve, dve.tensor_scalar(taken[:, g, :], work[:, g, :], 0.0, None, ALU.is_lt))
                            link(dve, dve.tensor_tensor_scan(work[:, g, :], taken[:, g, :], zero[:, :], 0.0,
                                                             ALU.add, ALU.add))
                            link(dve, dve.tensor_tensor(rows[:, g, :], work[:, g, :], taken[:, g, :], ALU.mult))
                        dve.wait_ge(peed, p0 + 2)
                        pv = place[:, :, :].rearrange("p (g b h) e -> p g h b e", g=NG, b=8)
                        for g in range(NG):
                            half = ps_p[:, g // 2, (g % 2) * SEQ:(g % 2 + 1) * SEQ]
                            link(dve, dve.tensor_copy(pv[:, g], half.rearrange("p (h b e) -> p h b e", h=TPB, b=8)))

                    k_lin = k0 + 1 + 4 + 1 + NG
                    k_rows = k_lin + 1 + NG * (2 * (CAP // 8) + 3)

                    @block.scalar
                    def _(act):
                        act.wait_ge(chained, k0 + 3)
                        act.activation(score[:, :, :], score[:, :, :], ACT.Exp).then_inc(acted, 1)

                    @block.tensor
                    def _(pe):
                        pe.wait_ge(chained, k_lin)
                        for g in range(NG):
                            for h in range(TPB):
                                ins = pe.transpose(ps_s[:, g // 2, (g % 2) * SEQ + h * P:(g % 2) * SEQ + (h + 1) * P],
                                                   lin[:, g * TPB + h, :], ident)
                        pe_done(ins)
                        pe.wait_ge(chained, k_rows)
                        for g in range(NG):
                            for h in range(TPB):
                                ins = pe.transpose(ps_p[:, g // 2, (g % 2) * SEQ + h * P:(g % 2) * SEQ + (h + 1) * P],
                                                   rows[:, g, h * P:(h + 1) * P], ident)
                        pe_done(ins)

            SLOTS = E0 * CAP
            with ExitStack() as st_x:
                xg = sb("xg", [P, E0, NB, CAP], stack=st_x)

                with ExitStack() as st:
                    S = 4
                    nrm = [sb(f"g_nrm{j}", [P, TPB, P], stack=st) for j in range(S)]
                    hot = [sb(f"g_hot{j}", [P, TPB, E0, CAP], stack=st) for j in range(S)]
                    ps_x = bank("g_ps_x", st, S)
                    with pool.loop_block(NB // S) as block:
                        @block.vector
                        def _(dve):
                            with dve.Fori(0, NB // S) as i:
                                for j in range(S):
                                    norm_tiles(dve, g_n, nrm[j], x_res, (i * S + j) * TPB, TPB, rstd,
                                               g_mm.last(i, j + 1))
                                    for h in range(TPB):
                                        pl = place[:, ds((i * S + j) * TPB + h, 1), :].rearrange("p o e -> p (o e)")
                                        ins = dve.tensor_tensor(hot[j][:, h], pl.unsqueeze(2).to_broadcast([P, E0, CAP]),
                                                                c("iota").unsqueeze(1).to_broadcast([P, E0, CAP]),
                                                                ALU.is_equal)
                                    ins.then_inc(g_p.sem, 1)

                        @block.tensor
                        def _(pe):
                            with pe.Fori(0, NB // S) as i:
                                for j in range(S):
                                    pe.wait_ge(*g_n.now(i, j + 1))
                                    pe.wait_ge(*g_p.now(i, j + 1))
                                    pe.wait_ge(*g_x.last(i, j + 1))
                                    for h in range(TPB):
                                        ins = pe.matmul(ps_x[:, j, :], nrm[j][:, h, :],
                                                        hot[j][:, h].rearrange("p e s -> p (e s)"),
                                                        start=(h == 0), stop=(h == TPB - 1))
                                    ins.then_inc(g_mm.sem, 1)

                        @block.scalar
                        def _(act):
                            with act.Fori(0, NB // S) as i:
                                for j in range(S):
                                    act.wait_ge(*g_mm.now(i, j + 1))
                                    act.activation(xg[:, :, ds(i * S + j, 1), :].rearrange("p e o s -> p e (o s)"),
                                                   ps_x[:, j, :].rearrange("p (e s) -> p e s", e=E0),
                                                   ACT.Copy).then_inc(g_x.sem, 1)

                with ExitStack() as st:
                    w0 = [sb(f"x_w{j}", [P, W0], stack=st) for j in range(2)]
                    ge = [sb(f"x_gelu{f}", [P, 512], stack=st) for f in range(2)]
                    hu = [sb(f"x_hid{n}", [P, 2, 512], stack=st) for n in range(2)]
                    ps_g = bank("x_ps_g", st, 2)
                    ps_u = bank("x_ps_u", st, 2)
                    ps_o = bank("x_ps_o", st, 2)
                    xe = xg[:, :, :, :].rearrange("p e b s -> p (e b s)")
                    with pool.loop_block(E0 // 2) as block:
                        @block.sync
                        def _(sp):
                            with sp.Fori(0, E0 // 2) as i:
                                for j in range(2):
                                    sp.wait_ge(*x_o.last(i, 2 * j + 2))
                                    sp.dma_start(w0[j][:, :], w0_in[ds(i * 2 + j, 1)].rearrange("o p w -> p (o w)")
                                                 ).then_inc(x_w[j].sem, 16)

                        def at(i, n):
                            return xe[:, ds(i * (2 * NB * CAP) + n * 512, 512)]

                        @block.tensor
                        def _(pe):
                            with pe.Fori(0, E0 // 2) as i:
                                def down_proj(n):
                                    pe.wait_ge(*x_h.now(i, 2 * n + 2))
                                    if n >= 2:
                                        pe.wait_ge(*x_s.now(i, n - 1))
                                    else:
                                        pe.wait_ge(*x_s.last(i, n + 3))
                                    for f in range(2):
                                        ins = pe.matmul(ps_o[:, n % 2, :], w0[n // 2][:, 2 * F0 + f * D:2 * F0 + (f + 1) * D],
                                                        hu[n % 2][:, f, :], start=(f == 0), stop=(f == 1))
                                    ins.then_inc(x_o.sem, 1)

                                for n in range(4):
                                    if n % 2 == 0:
                                        pe.wait_ge(*x_w[n // 2].now(i, 16))
                                    for f in range(2):
                                        if n:
                                            pe.wait_ge(*x_h.now(i, 2 * n - 1 + f))
                                        else:
                                            pe.wait_ge(*x_h.last(i, 7 + f))
                                        pe.matmul(ps_g[:, f, :], w0[n // 2][:, f * P:(f + 1) * P], at(i, n),
                                                  start=True, stop=True)
                                        pe.matmul(ps_u[:, f, :], w0[n // 2][:, F0 + f * P:F0 + (f + 1) * P], at(i, n),
                                                  start=True, stop=True).then_inc(x_gu.sem, 1)
                                    if n:
                                        down_proj(n - 1)
                                down_proj(3)

                        @block.scalar
                        def _(act):
                            with act.Fori(0, E0 // 2) as i:
                                def keep(n):
                                    act.wait_ge(*x_o.now(i, n + 1))
                                    act.activation(at(i, n), ps_o[:, n % 2, :], ACT.Copy).then_inc(x_s.sem, 1)

                                for n in range(4):
                                    for f in range(2):
                                        k = 2 * n + f + 1
                                        act.wait_ge(*x_gu.now(i, k))
                                        if n:
                                            act.wait_ge(*x_h.now(i, k - 2))
                                        else:
                                            act.wait_ge(*x_h.last(i, 7 + f))
                                        act.activation(ge[f][:, :], ps_g[:, f, :], ACT.Gelu).then_inc(x_ge.sem, 1)
                                    if n:
                                        keep(n - 1)
                                keep(3)

                        @block.vector
                        def _(dve):
                            with dve.Fori(0, E0 // 2) as i:
                                for n in range(4):
                                    for f in range(2):
                                        dve.wait_ge(*x_ge.now(i, 2 * n + f + 1))
                                        if n >= 2:
                                            dve.wait_ge(*x_o.now(i, n - 1))
                                        else:
                                            dve.wait_ge(*x_o.last(i, n + 3))
                                        dve.tensor_tensor(hu[n % 2][:, f, :], ge[f][:, :], ps_u[:, f, :],
                                                          ALU.mult).then_inc(x_h.sem, 1)

                with ExitStack() as st:
                    S = 3
                    nrm = sb("f_nrm", [P, TPB, P], stack=st)
                    eoT = sb("f_eoT", [P, SLOTS], stack=st)
                    hot = sb("f_hot", [P, TPB, E0, CAP], stack=st)
                    hT, hotT, eo, ge, hs = ([sb(f"f_{n}{j}", [P] + shape, stack=st) for j in range(S)] for n, shape in (
                        ("hT", [SEQ]), ("hotT", [4, SEQ]), ("eo", [4, D]), ("ge", [2, SEQ]), ("hs", [2, SEQ])))
                    ps_t = bank("f_ps_t", st)
                    ps_p = bank("f_ps_p", st, 2)
                    ps_e = bank("f_ps_e", st)
                    ps_g = bank("f_ps_g", st)
                    ps_u = bank("f_ps_u", st)
                    ps_o = bank("f_ps_o", st)
                    with pool.loop_block(NB) as block:
                        @block.vector
                        def _(dve):
                            def normed(n, j, r):
                                norm_tiles(dve, fr_f.nrm, nrm, x_res, n * TPB, TPB, rstd, fr_f.tps.last(n, 1))

                            def weighted(n, j, r):
                                dve.wait_ge(*f_pt.last(n, 2))
                                for h in range(TPB):
                                    pl = place[:, ds(n * TPB + h, 1), :].rearrange("p o e -> p (o e)")
                                    dve.tensor_tensor(hot[:, h], pl.unsqueeze(2).to_broadcast([P, E0, CAP]),
                                                      c("iota").unsqueeze(1).to_broadcast([P, E0, CAP]),
                                                      ALU.is_equal).then_inc(f_h0.sem, 1)
                                for h in range(TPB):
                                    dve.wait_ge(*f_h0.now(n, h + 1))
                                    sc = score[:, ds(n * TPB + h, 1), :].rearrange("p o e -> p (o e)")
                                    dve.tensor_tensor(hot[:, h], hot[:, h], sc.unsqueeze(2).to_broadcast([P, E0, CAP]),
                                                      ALU.mult).then_inc(f_p.sem, 1)
                                dve.wait_ge(*f_eo.last(n, 1))
                                dve.tensor_copy(eoT[:, :].rearrange("p (e s) -> p e s", e=E0),
                                                xg[:, :, ds(n, 1), :].rearrange("p e o s -> p e (o s)")
                                                ).then_inc(f_st.sem, 1)

                            def hidden(n, j, r):
                                dve.wait_ge(*f_ge.now(n, 1))
                                dve.wait_ge(*f_o.ago(n, 1, S))
                                dve.tensor_tensor(hs[j][:, :, :], ge[j][:, :, :],
                                                  ps_u[:, 0, :].rearrange("p (f t) -> p f t", f=2), ALU.mult
                                                  ).then_inc(f_h.sem, 1)

                            def added(n, j, r):
                                dve.wait_ge(*f_o.now(n, 1))
                                xs = x_res[:, ds(n * TPB, TPB), :]
                                dve.tensor_tensor(xs, xs, ps_o[:, 0, 0:SEQ].rearrange("p (t d) -> p t d", t=TPB),
                                                  ALU.add).then_inc(f_x.sem, 1)
                                count(dve, x_res, n * TPB, TPB, *f_x.now(n, 1))

                            staggered(dve, NB, S, (0, normed), (0, weighted), (1, hidden), (2, added))

                        @block.tensor
                        def _(pe):
                            def turn(n, j, r):
                                turn_tiles(pe, fr_f.tps, ps_t[:, 0, :], nrm, TPB, fr_f.nrm.now(n, 1), fr_f.hT.last(n, 1))

                            def project(n, j, r):
                                pe.wait_ge(*fr_f.hT.now(n, 1))
                                pe.wait_ge(*f_h.last(n, 1))
                                for f in range(2):
                                    pe.matmul(ps_g[:, 0, f * SEQ:(f + 1) * SEQ], c("wsg", f * P, P), hT[j][:, :],
                                              start=True, stop=True)
                                    ins = pe.matmul(ps_u[:, 0, f * SEQ:(f + 1) * SEQ], c("wsu", f * P, P), hT[j][:, :],
                                                    start=True, stop=True)
                                ins.then_inc(f_gu.sem, 1)

                            def turn_weights(n, j, r):
                                for m in range(2):
                                    pe.wait_ge(*f_p.now(n, 2))
                                    pe.wait_ge(*f_ptc.last(n, m + 1))
                                    for k in range(2 * m, 2 * m + 2):
                                        for h in range(TPB):
                                            ins = pe.transpose(
                                                ps_p[:, m, (k % 2) * SEQ + h * P:(k % 2) * SEQ + (h + 1) * P],
                                                hot[:, h].rearrange("p e s -> p (e s)")[:, k * P:(k + 1) * P], ident)
                                    ins.then_inc(f_pt.sem, 1)
                                pe.wait_ge(*f_st.now(n, 1))
                                pe.wait_ge(*f_eoc.last(n, 1))
                                for k in range(4):
                                    ins = pe.transpose(ps_e[:, 0, k * D:(k + 1) * D], eoT[:, k * P:(k + 1) * P], ident)
                                ins.then_inc(f_eo.sem, 1)

                            def project_out(n, j, r):
                                pe.wait_ge(*f_h.now(n, 1))
                                pe.wait_ge(*f_ptc.now(n, 2))
                                pe.wait_ge(*f_eoc.now(n, 1))
                                pe.wait_ge(*f_x.last(n, 1))
                                for h in range(TPB):
                                    dst = ps_o[:, 0, h * D:(h + 1) * D]
                                    for f in range(2):
                                        pe.matmul(dst, hs[j][:, f, h * P:(h + 1) * P], c("wsd", f * D, D),
                                                  start=(f == 0), stop=False)
                                    for k in range(4):
                                        ins = pe.matmul(dst, hotT[j][:, k, h * P:(h + 1) * P], eo[j][:, k, :],
                                                        start=False, stop=(k == 3))
                                ins.then_inc(f_o.sem, 1)

                            staggered(pe, NB, S, (1, project), (0, turn), (2, project_out), (0, turn_weights))

                        @block.scalar
                        def _(act):
                            def keep(n, j, r):
                                act.wait_ge(*fr_f.tps.now(n, 1))
                                act.wait_ge(*f_gu.ago(n, 1, S))
                                act.activation(hT[j][:, :], ps_t[:, 0, 0:SEQ], ACT.Copy).then_inc(fr_f.hT.sem, 1)

                            def gelu(n, j, r):
                                act.wait_ge(*f_gu.now(n, 1))
                                act.wait_ge(*f_h.ago(n, 1, S))
                                act.activation(ge[j][:, :, :], ps_g[:, 0, :].rearrange("p (f t) -> p f t", f=2),
                                               ACT.Gelu).then_inc(f_ge.sem, 1)

                            def keep_weights(n, j, r):
                                for m in range(2):
                                    act.wait_ge(*f_pt.now(n, m + 1))
                                    act.wait_ge(*f_o.ago(n, 1, S))
                                    act.activation(hotT[j][:, 2 * m:2 * m + 2, :],
                                                   ps_p[:, m, :].rearrange("p (k t) -> p k t", k=2), ACT.Copy
                                                   ).then_inc(f_ptc.sem, 1)
                                act.wait_ge(*f_eo.now(n, 1))
                                act.activation(eo[j][:, :, :].rearrange("p k d -> p (k d)"), ps_e[:, 0, :], ACT.Copy
                                               ).then_inc(f_eoc.sem, 1)

                            staggered(act, NB, S, (1, gelu), (0, keep), (0, keep_weights))

        stats(x_res, twice=True)
        with ExitStack() as st:
            VW = D + 4
            S = 6
            nrm, hT, egate, gate, qk, low, v1, am = (
                [sb(f"l_{n}{j}", [P] + shape, stack=st) for j in range(S)] for n, shape in (
                    ("nrm", [TPB, P]), ("hT", [SEQ]), ("egate", [SEQ]), ("gate", [SEQ]), ("qk", [2, SEQ]), ("low", [2, SEQ]),
                    ("v", [TPB, VW]), ("am", [P + SEQ])))
            hgb = sb("l_hgb", [P, 1], stack=st)
            den = sb("l_den", [P, TPB], stack=st)
            ps_t = bank("l_ps_t", st)
            ps_q = bank("l_ps_q", st, 2)
            ps_g = bank("l_ps_g", st, 2)
            ps_v = bank("l_ps_v", st)
            ps_a = bank("l_ps_a", st)
            ps_o = bank("l_ps_o", st)
            with pool.loop_block(NB) as block:
                k_set = n_chain[0] + 1 + S

                @block.vector
                def _(dve):
                    link(dve, dve.tensor_scalar(hgb[:, :], c("gb1"), 0.5, None, ALU.mult))
                    for j in range(S):
                        link(dve, dve.memset(v1[j][:, :, :], 1.0))

                    def normed(b, j, r):
                        norm_tiles(dve, fr_l.nrm, nrm[j], x_res, b * TPB, TPB, rstd2, fr_l.tps.ago(b, 1, S))

                    def gated(b, j, r):
                        dve.wait_ge(*l_tanh.now(b, 1))
                        dve.wait_ge(*l_k.ago(b, 1, S))
                        dve.tensor_scalar(gate[j][:, :], egate[j][:, :], 0.5, 0.5, ALU.mult, ALU.add).then_inc(l_gate.sem, 1)

                    def keys(b, j, r):
                        dve.wait_ge(*l_gate.now(b, 1))
                        dve.wait_ge(*l_q.now(b, 1))
                        dve.wait_ge(*l_a.ago(b, 1, S))
                        dve.scalar_tensor_tensor(qk[j][:, 1, :], ps_q[:, j % 2, SEQ:2 * SEQ], c("qkvb", 1, 1), gate[j][:, :],
                                                 ALU.add, ALU.mult).then_inc(l_k.sem, 1)

                    def negative(b, j, r):
                        dve.wait_ge(*l_k.now(b, 1))
                        dve.wait_ge(*l_qk.ago(b, 1, S))
                        dve.tensor_scalar(low[j][:, :, :], qk[j][:, :, :], 0.0, None, ALU.min).then_inc(l_low.sem, 1)

                    def positive(b, j, r):
                        dve.wait_ge(*l_exp.now(b, 1))
                        dve.scalar_tensor_tensor(qk[j][:, :, :], qk[j][:, :, :], 0.0, low[j][:, :, :], ALU.max, ALU.add
                                                 ).then_inc(l_qk.sem, 1)

                    def masked(b, j, r):
                        dve.wait_ge(*l_a.now(b, 1))
                        dve.wait_ge(*l_o.ago(b, 1, S))
                        dve.tensor_tensor(am[j][:, :], ps_a[:, 0, 0:P + SEQ], c("tri_st"), ALU.mult).then_inc(l_am.sem, 1)

                    ov = ps_o[:, 0, 0:TPB * VW].rearrange("p (t w) -> p t w", t=TPB)

                    def denominator(b, j, r):
                        dve.wait_ge(*l_o.now(b, 1))
                        dve.wait_ge(*l_x.last(b, 1))
                        dve.tensor_scalar(den[:, :], ov[:, :, D], 1e-6, None, ALU.add).then_inc(l_den.sem, 1)

                    def inverse(b, j, r):
                        dve.wait_ge(*l_den.now(b, 1))
                        dve.reciprocal(den[:, :], den[:, :]).then_inc(l_rec.sem, 1)

                    def added(b, j, r):
                        dve.wait_ge(*l_rec.now(b, 1))
                        for t in range(TPB):
                            xs = x_res[:, ds(b * TPB + t, 1), :].rearrange("p o d -> p (o d)")
                            ins = dve.scalar_tensor_tensor(xs, ov[:, t, 0:D], den[:, t:t + 1], xs, ALU.mult, ALU.add)
                        ins.then_inc(l_x.sem, 1)

                    def counted(b, j, r):
                        count(dve, x_res, b * TPB, TPB, *l_x.now(b, 1))

                    staggered(dve, NB, S, (7, denominator), (3, positive), (7, inverse), (5, masked), (7, added), (0, normed),
                              (2, gated), (7, counted), (2, keys), (2, negative))

                @block.tensor
                def _(pe):
                    pe.wait_ge(chained, k_set)

                    def turn(b, j, r):
                        turn_tiles(pe, fr_l.tps, ps_t[:, 0, :], nrm[j], TPB, fr_l.nrm.now(b, 1), fr_l.hT.last(b, 1))

                    def project(b, j, r):
                        pe.wait_ge(*fr_l.hT.now(b, 1))
                        pe.wait_ge(*l_tanh.ago(b, 1, 2))
                        pe.matmul(ps_g[:, j % 2, 0:SEQ], c("gw1"), hT[j][:, :], start=True, stop=True).then_inc(l_g.sem, 1)
                        pe.wait_ge(*l_k.ago(b, 1, 2))
                        pe.matmul(ps_q[:, j % 2, 0:SEQ], c("qkvw", 0, D), hT[j][:, :], start=True, stop=True)
                        pe.matmul(ps_q[:, j % 2, SEQ:2 * SEQ], c("qkvw", D, D), hT[j][:, :], start=True, stop=True
                                  ).then_inc(l_qk_in.sem, 1)
                        pe.wait_ge(*l_vc.last(b, 1))
                        for t in range(TPB):
                            dst = ps_v[:, 0, t * D:(t + 1) * D]
                            pe.matmul(dst, c("ones", rows=1), c("vb", rows=1), start=True, stop=False)
                            ins = pe.matmul(dst, hT[j][:, t * P:(t + 1) * P], c("qkvw", 2 * D, D), start=False, stop=True)
                        ins.then_inc(l_v.sem, 1)

                    def scores(b, j, r):
                        pe.wait_ge(*l_qk.now(b, 1))
                        pe.wait_ge(*l_am.last(b, 1))
                        pe.matmul(ps_a[:, 0, 0:SEQ], qk[j][:, 1, 0:P], qk[j][:, 0, :], start=True, stop=True)
                        pe.matmul(ps_a[:, 0, SEQ:SEQ + P], qk[j][:, 1, P:SEQ], qk[j][:, 0, P:SEQ], start=True, stop=True
                                  ).then_inc(l_a.sem, 1)

                    def weigh(b, j, r):
                        pe.wait_ge(*l_am.now(b, 1))
                        pe.wait_ge(*l_vc.now(b, 1))
                        pe.wait_ge(*l_x.last(b, 1))
                        pe.matmul(ps_o[:, 0, 0:VW], am[j][:, 0:P], v1[j][:, 0, :], start=True, stop=True)
                        pe.matmul(ps_o[:, 0, VW:2 * VW], am[j][:, P:SEQ], v1[j][:, 0, :], start=True, stop=False)
                        pe.matmul(ps_o[:, 0, VW:2 * VW], am[j][:, SEQ:SEQ + P], v1[j][:, 1, :], start=False, stop=True
                                  ).then_inc(l_o.sem, 1)

                    staggered(pe, NB, S, (2, project), (0, turn), (4, scores), (6, weigh))

                @block.scalar
                def _(act):
                    act.wait_ge(chained, k_set)

                    def keep(b, j, r):
                        act.wait_ge(*fr_l.tps.now(b, 1))
                        act.wait_ge(*l_v.ago(b, 1, S))
                        act.activation(hT[j][:, :], ps_t[:, 0, 0:SEQ], ACT.Identity, bias=c("lnb1"), scale=c("lng1")
                                       ).then_inc(fr_l.hT.sem, 1)

                    def gated(b, j, r):
                        act.wait_ge(*l_g.now(b, 1))
                        act.wait_ge(*l_gate.ago(b, 1, S))
                        act.activation(egate[j][:, :], ps_g[:, j % 2, 0:SEQ], ACT.Tanh, bias=hgb[:, :], scale=0.5
                                       ).then_inc(l_tanh.sem, 1)
                        act.wait_ge(*l_qk_in.now(b, 1))
                        act.wait_ge(*l_a.ago(b, 1, S))
                        act.activation(qk[j][:, 0, :], ps_q[:, j % 2, 0:SEQ], ACT.Identity, bias=c("qkvb", 0, 1)
                                       ).then_inc(l_q.sem, 1)
                        act.wait_ge(*l_v.now(b, 1))
                        act.wait_ge(*l_o.ago(b, 1, S))
                        act.activation(v1[j][:, :, 0:D], ps_v[:, 0, 0:SEQ].rearrange("p (t d) -> p t d", t=TPB), ACT.Copy
                                       ).then_inc(l_vc.sem, 1)

                    def powers(b, j, r):
                        act.wait_ge(*l_low.now(b, 1))
                        act.activation(low[j][:, :, :], low[j][:, :, :], ACT.Exp).then_inc(l_exp.sem, 1)

                    staggered(act, NB, S, (2, gated), (0, keep), (2, powers))

        def sorted_experts(tag, sel, weight, src, xs, w, w_in, f_dim, func, normed=None):
            choices = len(sel)
            n_exp = 8
            n_tiles = tiles_of(choices)
            nf = f_dim // P
            wc = wide(f_dim)
            o_b1, o_b2 = 2 * f_dim, 2 * f_dim + nf
            ga, gb, gc = moes[tag]
            spare = spare_of(choices)
            with ExitStack() as st:
                pos = sb(f"{tag}_pos", [P, choices, NT], I32, stack=st)
                meta = sb(f"{tag}_meta", [P, choices, NT, 2], stack=st)
                place = sb(f"{tag}_place", [P, n_tiles], I32, stack=st)
                with ExitStack() as sta:
                    both = sb(f"{tag}_both", [P, NT, n_exp], stack=sta)
                    loc = sb(f"{tag}_loc", [P, NT, n_exp], stack=sta)
                    tot = sb(f"{tag}_tot", [P, NT, n_exp], stack=sta)
                    cum = sb(f"{tag}_cum", [P, n_exp, NT], stack=sta)
                    step_of = sb(f"{tag}_step", [P, n_exp, NT], stack=sta)
                    edge = sb(f"{tag}_edge", [P, NT], stack=sta)
                    tiles, tend, base = (sb(f"{tag}_{n}", [P, n_exp], stack=sta) for n in ("tiles", "tend", "base"))
                    posf = sb(f"{tag}_posf", [P, NT], stack=sta)
                    past = sb(f"{tag}_past", [P, n_tiles, n_exp - 1], stack=sta)
                    placef = sb(f"{tag}_placef", [P, n_tiles], stack=sta)
                    ps_c = bank(f"{tag}_ps_c", sta, 2)
                    with nc.Block() as block:
                        k0, p0 = n_chain[0], n_pe[0]
                        @block.vector
                        def _(dve):
                            if choices == 2:
                                link(dve, dve.tensor_tensor(both[:, :, :], sel[0], sel[1], ALU.add))
                            else:
                                link(dve, dve.tensor_copy(both[:, :, :], sel[0]))
                            n_pe[0] += 1
                            dve.wait_ge(peed, n_pe[0])
                            link(dve, dve.tensor_copy(loc[:, :, :].rearrange("p t e -> p (t e)"), ps_c[:, 0, :]))
                            link(dve, dve.tensor_copy(tot[:, :, :].rearrange("p t e -> p (t e)"), ps_c[:, 1, :]))
                            for e in range(n_exp):
                                link(dve, dve.tensor_tensor_scan(cum[:, e, :], c("ones", 0, NT), tot[:, :, e], 0.0,
                                                                 ALU.mult, ALU.add))
                            link(dve, dve.tensor_scalar(edge[:, :], c("tvec", 0, NT), float(P), None, ALU.mult))
                            link(dve, dve.tensor_tensor(step_of[:, :, :],
                                                        cum[:, :, NT - 1].unsqueeze(2).to_broadcast([P, n_exp, NT]),
                                                        edge[:, :].unsqueeze(1).to_broadcast([P, n_exp, NT]), ALU.is_gt))
                            link(dve, dve.tensor_reduce(tiles[:, :], step_of[:, :, :], AX, ALU.add))
                            link(dve, dve.tensor_tensor_scan(tend[:, :], c("ones", 0, n_exp), tiles[:, :], 0.0,
                                                             ALU.mult, ALU.add))
                            link(dve, dve.tensor_tensor(base[:, :], tend[:, :], tiles[:, :], ALU.subtract))
                            link(dve, dve.tensor_scalar(base[:, :], base[:, :], float(P), -1.0, ALU.mult, ALU.add))
                            link(dve, dve.tensor_tensor(loc[:, :, :], loc[:, :, :],
                                                        cum[:, :, :].rearrange("p e t -> p t e"), ALU.add))
                            link(dve, dve.tensor_tensor(loc[:, :, :], loc[:, :, :], tot[:, :, :], ALU.subtract))
                            link(dve, dve.tensor_tensor(loc[:, :, :], loc[:, :, :],
                                                        base[:, :].unsqueeze(1).to_broadcast([P, NT, n_exp]), ALU.add))
                            for k in range(choices):
                                link(dve, dve.tensor_tensor(tot[:, :, :], sel[k], loc[:, :, :], ALU.mult))
                                link(dve, dve.tensor_reduce(posf[:, :], tot[:, :, :], AX, ALU.add))
                                link(dve, dve.tensor_copy(pos[:, k, :], posf[:, :]))
                                link(dve, dve.tensor_copy(meta[:, k, :, 0], weight[k]))
                                link(dve, dve.tensor_scalar(meta[:, k, :, 1], c("token", 0, NT), float(k * NB * SEQ), None, ALU.add))
                            link(dve, dve.tensor_tensor(past[:, :, :],
                                                        c("tvec", 0, n_tiles).unsqueeze(2).to_broadcast([P, n_tiles, n_exp - 1]),
                                                        tend[:, 0:n_exp - 1].unsqueeze(1).to_broadcast([P, n_tiles, n_exp - 1]),
                                                        ALU.is_ge))
                            link(dve, dve.tensor_reduce(placef[:, :], past[:, :, :], AX, ALU.add))
                            link(dve, dve.tensor_scalar(placef[:, :], placef[:, :], float(wc), None, ALU.mult))
                            link(dve, dve.tensor_copy(place[:, :], placef[:, :]))

                        @block.tensor
                        def _(pe):
                            pe.wait_ge(chained, k0 + 1)
                            flat = both[:, :, :].rearrange("p t e -> p (t e)")
                            pe.matmul(ps_c[:, 0, :], c("tri_st", 0, P), flat, start=True, stop=True)
                            pe.matmul(ps_c[:, 1, :], c("ones"), flat, start=True, stop=True).then_inc(peed, 1)

                def hold(gp, held, own, *waits):
                    for wt in waits:
                        gp.wait_ge(*wt)
                    gp.wait_ge(*own)
                    gp.tensor_tensor(idle[:, 0:1], idle[:, 1:2], idle[:, 1:2], ALU.add).then_inc(held.sem, 1)

                steps = NU // 2
                per = NT * choices // steps
                with ExitStack() as sts:
                    row = [sb(f"{tag}_row{j}", [P, D + 2], stack=sts) for j in range(4)]
                    key = [sb(f"{tag}_key{j}", [P, 1], I32, stack=sts) for j in range(4)]
                    g_row, g_meta, g_hold = ga
                    if normed is not None:
                        h_all, acc = normed
                        hid, acted_h, outs, added, w_load = gb
                        ws = sb(f"{tag}_ws", [P, wc], stack=sts)
                        hs = [sb(f"{tag}_hs{j}", [P, nf, U], stack=sts) for j in range(2)]
                        ps_h = bank(f"{tag}_ps_h", sts, 4)
                        ps_o = bank(f"{tag}_ps_o", sts, 2)
                    done = n_scattered[0]

                    def slot_free(i, n):
                        return scattered[n % 4], i * (16 * per // 4) + (done + 16 * (n // 4))

                    with pool.loop_block(steps) as block:
                        @block.vector
                        def _(dve):
                            with dve.Fori(0, steps) as i:
                                for n in range(per):
                                    tile = i * (NT // steps) + n // choices
                                    x_t = src[:, ds(tile, 1), :].rearrange("p o d -> p (o d)")
                                    dve.wait_ge(*slot_free(i, n))
                                    if normed is None:
                                        ins = dve.tensor_scalar(row[n % 4][:, 0:D], x_t, 1.0, None, ALU.mult)
                                    else:
                                        ins = dve.tensor_scalar(row[n % 4][:, 0:D], x_t, mean[:, ds(tile, 1)],
                                                                rstd[:, ds(tile, 1)], ALU.subtract, ALU.mult)
                                    ins.then_inc(g_row.sem, 1)
                                if normed is not None:
                                    dve.wait_ge(*g_row.now(i, per))
                                    for j in range(2):
                                        dve.wait_ge(*outs[j].now(i, 1))
                                        xs_u = acc[:, ds((i * 2 + j) * UT, UT), :]
                                        dve.tensor_tensor(xs_u, xs_u, ps_o[:, j, :].rearrange("p (t d) -> p t d", t=UT),
                                                          ALU.add).then_inc(added[j].sem, 1)

                        @block.gpsimd
                        def _(gp):
                            with gp.Fori(0, steps) as i:
                                for n in range(per):
                                    hold(gp, g_hold, g_hold.now(i, n), g_row.now(i, n + 1), g_meta.now(i, n + 1))
                                    gp.indirect_dma_start(xs[:, :], bass.IndirectOffsetOnAxis(ap=key[n % 4][:, :], axis=0),
                                                          row[n % 4][:, :], None).then_inc(scattered[n % 4], 16)
                            for j in range(4):
                                gp.wait_ge(scattered[j], done + 16 * steps * per // 4)

                        @block.scalar
                        def _(act):
                            if normed is not None:
                                act.wait_ge(w_load, 16)
                            with act.Fori(0, steps) as i:
                                for n in range(per):
                                    tile = i * (NT // steps) + n // choices
                                    k = n % choices
                                    act.wait_ge(*slot_free(i, n))
                                    act.activation(key[n % 4][:, :], pos[:, k, ds(tile, 1)], ACT.Copy)
                                    act.activation(row[n % 4][:, D:D + 2], meta[:, k, ds(tile, 1), :].rearrange("p o m -> p (o m)"),
                                                   ACT.Copy).then_inc(g_meta.sem, 1)
                                    if normed is not None and n < 2 * nf:
                                        j, f = divmod(n, nf)
                                        act.wait_ge(*hid[j].now(i, f + 1))
                                        act.wait_ge(*outs[j].last(i, 1))
                                        act.activation(hs[j][:, f, :], ps_h[:, f, :], func, bias=ws[:, o_b1 + f:o_b1 + f + 1]
                                                       ).then_inc(acted_h[j].sem, 1)

                        if normed is not None:
                            @block.sync
                            def _(sp):
                                sp.dma_start(ws[:, :], w_in[n_exp]).then_inc(w_load, 16)

                            @block.tensor
                            def _(pe):
                                pe.wait_ge(w_load, 16)
                                with pe.Fori(0, steps) as i:
                                    for j in range(2):
                                        for f in range(nf):
                                            pe.wait_ge(*(acted_h[1].last(i, f + 1) if j == 0 else acted_h[0].now(i, f + 1)))
                                            pe.matmul(ps_h[:, f, :], ws[:, f * P:(f + 1) * P],
                                                      h_all[:, ds((i * 2 + j) * U, U)], start=True, stop=True
                                                      ).then_inc(hid[j].sem, 1)
                                    for j in range(2):
                                        pe.wait_ge(*added[j].last(i, 1))
                                        pe.wait_ge(*acted_h[j].now(i, nf))
                                        for t in range(UT):
                                            o = ps_o[:, j, t * D:(t + 1) * D]
                                            pe.matmul(o, c("ones", rows=1), ws[0:1, o_b2:o_b2 + D], start=True, stop=False)
                                            for f in range(nf):
                                                ins = pe.matmul(o, hs[j][:, f, t * P:(t + 1) * P],
                                                                ws[:, f_dim + f * D:f_dim + (f + 1) * D],
                                                                start=False, stop=(f == nf - 1))
                                        ins.then_inc(outs[j].sem, 1)
                    n_scattered[0] = done + 16 * steps * per // 4

                with ExitStack() as ste:
                    wt = [sb(f"{tag}_wt{j}", [P, wc], stack=ste) for j in range(4)]
                    xt = [sb(f"{tag}_xt{g}", [P, 4, D + 2], stack=ste) for g in range(2)]
                    hT = [sb(f"{tag}_hT{j}", [P, P], stack=ste) for j in range(4)]
                    hid_t = [sb(f"{tag}_hid{j}", [P, nf, P], stack=ste) for j in range(4)]
                    y = [sb(f"{tag}_y{j}", [P, D], stack=ste) for j in range(4)]
                    key = [sb(f"{tag}_ykey{g}", [P, 4], I32, stack=ste) for g in range(2)]
                    empty = [sb(f"{tag}_empty{g}", [P, 4], stack=ste) for g in range(2)]
                    ps_t = bank(f"{tag}_ps_t2", ste, 2)
                    ps_h = bank(f"{tag}_ps_h2", ste, 4)
                    ps_o = bank(f"{tag}_ps_o2", ste, 2)
                    e_load, e_w, e_t, e_tc, e_h, e_a, e_o, e_empty, e_key, e_b, e_y, e_hold = gc
                    done = n_scattered[0]

                    def run(eng, step):
                        step(-1, 7, -1, True, False, False)
                        step(0, 0, 0, True, True, False)
                        with eng.Fori(0, n_tiles // 8 - 1) as i:
                            for v in range(1, 9):
                                step(i * 8 + v, v % 8, i + v // 8, True, True, True)
                        for v in range(n_tiles - 7, n_tiles):
                            step(v, v % 8, v // 8, v + 1 < n_tiles, True, True)
                        step(n_tiles, 0, n_tiles // 8, False, False, True)

                    def next_of(j, r, n):
                        return (j + n) % 8, r + (j + n) // 8

                    with pool.loop_block(n_tiles) as block:
                        @block.sync
                        def _(sp):
                            def load(n, g):
                                sp.dma_start(xt[g][:, :, :], xs[ds(n * P, 4 * P), :].rearrange("(t p) w -> p t w", p=P)
                                             ).then_inc(e_load[g].sem, 16)

                            def step(n, j, r, ahead, now, behind):
                                if behind and j % 4 == 0 and not (isinstance(n, int) and n + 4 >= n_tiles):
                                    sp.wait_ge(*e_y.now(n, 0))
                                    load(n + 4, (j // 4 + 1) % 2)

                            load(0, 0)
                            load(4, 1)
                            run(sp, step)

                        @block.vector
                        def _(dve):
                            def weights(n, j):
                                at = nc.values_load(place[0:1, ds(n, 1)], engines=(mybir.EngineType.DVE,), min_val=0,
                                                    max_val=(n_exp - 1) * wc,
                                                    skip_runtime_bounds_check_because="an expert's number times its width")
                                dve.wait_ge(*e_y.now(n, -3))
                                dve.tensor_scalar(wt[j % 4][:, :], w[:, :, :].rearrange("p e w -> p (e w)")[:, ds(at, wc)],
                                                  1.0, None, ALU.mult).then_inc(e_w.sem, 1)

                            def step(n, j, r, ahead, now, behind):
                                if isinstance(n, int) and n == -1:
                                    weights(0, 0)
                                if ahead and not (isinstance(n, int) and n + 2 >= n_tiles):
                                    weights(n + 2, (j + 2) % 8)
                                if ahead and j % 4 == 3:
                                    m, rm = next_of(j, r, 1)
                                    g = m // 4
                                    to = xt[g][:, :, D + 1]
                                    dve.wait_ge(*e_load[g].now(rm, 16))
                                    dve.wait_ge(*e_key.now(rm, g - 1))
                                    dve.scalar_tensor_tensor(empty[g][:, :], to, float(spare),
                                                             c("token", 0, n_tiles)[:, ds(n + 1, 4)], ALU.is_ge, ALU.mult
                                                             ).then_inc(e_empty.sem, 1)
                                    dve.wait_ge(*e_empty.now(rm, g + 1))
                                    for k in (2, 3):
                                        dve.wait_ge(scattered[k], rm * 32 + (done + 16 * (g - 1)))
                                    dve.tensor_tensor(key[g][:, :], empty[g][:, :], to, ALU.add).then_inc(e_key.sem, 1)
                                if behind:
                                    m, rm = next_of(j, r, -1)
                                    dve.wait_ge(scattered[m % 4], rm * 32 + (done + 16 * (m // 4)))
                                    dve.wait_ge(*e_o.now(n, 0))
                                    dve.tensor_tensor(y[m % 4][:, :], ps_o[:, m % 2, 0:D], wt[m % 4][:, o_b2:o_b2 + D], ALU.add
                                                      ).then_inc(e_b.sem, 1)
                                    dve.wait_ge(*e_b.now(n, 0))
                                    dve.tensor_scalar(y[m % 4][:, :], y[m % 4][:, :], xt[m // 4][:, m % 4, D:D + 1], None,
                                                      ALU.mult).then_inc(e_y.sem, 1)

                            run(dve, step)

                        @block.gpsimd
                        def _(gp):
                            def step(n, j, r, ahead, now, behind):
                                if behind:
                                    m, rm = next_of(j, r, -1)
                                    hold(gp, e_hold, e_hold.now(n - 1, 0), e_y.now(n, 0), e_key.now(rm, m // 4 + 1))
                                    gp.indirect_dma_start(ys[:, :], bass.IndirectOffsetOnAxis(
                                        ap=key[m // 4][:, m % 4:m % 4 + 1], axis=0), y[m % 4][:, :], None
                                        ).then_inc(scattered[m % 4], 16)

                            run(gp, step)
                            for j in range(4):
                                gp.wait_ge(scattered[j], done + 16 * n_tiles // 4)

                        @block.tensor
                        def _(pe):
                            def step(n, j, r, ahead, now, behind):
                                if ahead:
                                    m, rm = next_of(j, r, 1)
                                    if m % 4 == 0:
                                        pe.wait_ge(*e_load[m // 4].now(rm, 16))
                                    pe.wait_ge(*e_tc.now(n + 1, -1))
                                    pe.transpose(ps_t[:, m % 2, 0:P], xt[m // 4][:, m % 4, 0:D], ident).then_inc(e_t.sem, 1)
                                if now:
                                    pe.wait_ge(*e_tc.now(n, 1))
                                    pe.wait_ge(*e_w.now(n, 1))
                                    for f in range(nf):
                                        k = (j * nf + f) % 4
                                        pe.wait_ge(*e_a.now(n, f + 1 - 4))
                                        pe.matmul(ps_h[:, k, 0:P], wt[j % 4][:, f * P:(f + 1) * P], hT[j % 4][:, :],
                                                  start=True, stop=True).then_inc(e_h.sem, 1)
                                if behind:
                                    m = (j - 1) % 4
                                    pe.wait_ge(*e_y.now(n, -2))
                                    o = ps_o[:, m % 2, 0:D]
                                    for f in range(nf):
                                        pe.wait_ge(*e_a.now(n, f + 1 - nf))
                                        ins = pe.matmul(o, hid_t[m][:, f, :], wt[m][:, f_dim + f * D:f_dim + (f + 1) * D],
                                                        start=(f == 0), stop=(f == nf - 1))
                                    ins.then_inc(e_o.sem, 1)

                            run(pe, step)

                        @block.scalar
                        def _(act):
                            def step(n, j, r, ahead, now, behind):
                                if ahead:
                                    m = (j + 1) % 4
                                    act.wait_ge(*e_t.now(n + 1, 1))
                                    act.wait_ge(*e_h.now(n + 1, -3 * nf))
                                    act.activation(hT[m][:, :], ps_t[:, m % 2, 0:P], ACT.Copy).then_inc(e_tc.sem, 1)
                                if now:
                                    act.wait_ge(*e_o.now(n, -3))
                                    for f in range(nf):
                                        act.wait_ge(*e_h.now(n, f + 1))
                                        act.activation(hid_t[j % 4][:, f, :], ps_h[:, (j * nf + f) % 4, 0:P], func,
                                                       bias=wt[j % 4][:, o_b1 + f:o_b1 + f + 1]).then_inc(e_a.sem, 1)

                            run(act, step)
                    n_scattered[0] = done + 16 * n_tiles // 4

        def collect(tag, choices, acc):
            loads, adds = collects[tag]
            S = len(loads)
            with ExitStack() as st:
                got = [sb(f"{tag}_got{j}", [P, choices, UT, D], stack=st) for j in range(S)]
                with pool.loop_block(NU // S) as block:
                    @block.sync
                    def _(sp):
                        with sp.Fori(0, NU // S) as i:
                            for j in range(S):
                                sp.wait_ge(*adds[j].last(i, choices))
                                for k in range(choices):
                                    sp.dma_start(got[j][:, k], ys[ds((i * S + j) * U + k * NB * SEQ, U), :]
                                                 .rearrange("(t p) d -> p t d", p=P)).then_inc(loads[j].sem, 16)

                    @block.vector
                    def _(dve):
                        with dve.Fori(0, NU // S) as i:
                            for k in range(choices):
                                for j in range(S):
                                    xs_u = acc[:, ds((i * S + j) * UT, UT), :]
                                    dve.wait_ge(*loads[j].now(i, 16 * choices))
                                    if k:
                                        dve.wait_ge(*adds[j].now(i, k))
                                    dve.tensor_tensor(xs_u, xs_u, got[j][:, k], ALU.add).then_inc(adds[j].sem, 1)
                            for j in range(S):
                                count(dve, acc, (i * S + j) * UT, UT, *adds[j].now(i, choices))

        def pick(dve, sel, lg, m, w3, n):
            link(dve, dve.tensor_reduce(m, lg, AX, ALU.max))
            link(dve, dve.tensor_tensor(sel, lg, m.unsqueeze(2).to_broadcast([P, NT, n]), ALU.is_equal))
            rank = c("rank", 0, n).unsqueeze(1).to_broadcast([P, NT, n])
            link(dve, dve.tensor_tensor(sel, sel, rank, ALU.mult))
            link(dve, dve.tensor_reduce(w3, sel, AX, ALU.max))
            link(dve, dve.tensor_tensor(sel, sel, w3.unsqueeze(2).to_broadcast([P, NT, n]), ALU.is_equal))

        def over_tiles(v, n):
            return v.unsqueeze(2).to_broadcast([P, NT, n])

        stats(x_res)
        with ExitStack() as st1:
            h_all = sb("h_all1", [P, NT * P], stack=st1)
            s1, s2 = (sb(f"m1_sel{j}", [P, NT, E1], stack=st1) for j in range(2))
            m1, m2 = (sb(f"m1_t{j}", [P, NT], stack=st1) for j in range(2))
            lg = sb("lg1", [P, NT, E1], stack=st1)
            w = sb("w1", [P, E1, wide(F1)], stack=st1)
            route("m1", x_res, c("gate1"), c("gate1b"), E1, lg, h_all, fetch=(w, w1_in))
            with ExitStack() as st:
                t1 = sb("m1_t", [P, NT], stack=st)
                with nc.Block() as block:
                    k0 = n_chain[0]

                    @block.vector
                    def _(dve):
                        pick(dve, s1[:, :, :], lg[:, :, :], m1[:, :], t1[:, :], E1)
                        link(dve, dve.scalar_tensor_tensor(lg[:, :, :], s1[:, :, :], -BIG, lg[:, :, :], ALU.mult, ALU.add))
                        pick(dve, s2[:, :, :], lg[:, :, :], m2[:, :], t1[:, :], E1)
                        link(dve, dve.tensor_tensor(m2[:, :], m2[:, :], m1[:, :], ALU.subtract))
                        n_act[0] += 1
                        dve.wait_ge(acted, n_act[0])
                        link(dve, dve.tensor_scalar(t1[:, :], m2[:, :], 1.0, None, ALU.add))
                        link(dve, dve.reciprocal(m1[:, :], t1[:, :]))
                        link(dve, dve.tensor_tensor(m2[:, :], m2[:, :], m1[:, :], ALU.mult))

                    @block.scalar
                    def _(act):
                        act.wait_ge(chained, k0 + 12)
                        act.activation(m2[:, :], m2[:, :], ACT.Exp).then_inc(acted, 1)
            sorted_experts("e1", (s1[:, :, :], s2[:, :, :]), (m1[:, :], m2[:, :]), x_res, xs1, w, w1_in, F1, ACT.Gelu,
                           normed=(h_all, x_res))
        collect("e1", 2, x_res)

        KR = 6 * HD
        KM = KR + 3

        def project(tag, src, w, keep=None):
            fr, s = projections[tag]
            with ExitStack() as st:
                S = 3
                PARTS = 6 * 16
                nrm = [sb(f"{tag}_nrm{j}", [P, UT, P], stack=st) for j in range(S)]
                hT = [sb(f"{tag}_hT{j}", [P, U], stack=st) for j in range(S)]
                parts = [sb(f"{tag}_parts{j}", [P, 2, 3, U], BF16, stack=st) for j in range(S)]
                rest = [sb(f"{tag}_rest{j}", [P, 2, U], stack=st) for j in range(S)]
                v1 = [sb(f"{tag}_v{j}", [P, UT, NH, HD + 1], stack=st) for j in range(S)]
                ps_t = bank(f"{tag}_ps_t", st)
                ps_qk = bank(f"{tag}_ps_qk", st, 2)
                ps_v = bank(f"{tag}_ps_v", st)
                with pool.loop_block(NU) as block:
                    k_set = n_chain[0] + S

                    @block.vector
                    def _(dve):
                        for j in range(S):
                            link(dve, dve.memset(v1[j][:, :, :, :], 1.0))

                        def normed(n, j, r):
                            norm_tiles(dve, fr.nrm, nrm[j], src, n * UT, UT, rstd, fr.tps.ago(n, 1, S),
                                       None if keep is None else s["kept"].ago(n, 1, S))

                        def split(n, j, r):
                            for m in range(2):
                                dve.wait_ge(*s["hi"].now(n, m + 1))
                                dve.wait_ge(*s["lo"].ago(n, m + 1, S))
                                if w["b"][m] is None:
                                    dve.tensor_tensor(rest[j][:, m, :], ps_qk[:, m, :], parts[j][:, m, 0, :],
                                                      ALU.subtract).then_inc(s["r1"].sem, 1)
                                else:
                                    dve.scalar_tensor_tensor(rest[j][:, m, :], ps_qk[:, m, :], w["b"][m],
                                                             parts[j][:, m, 0, :], ALU.add, ALU.subtract
                                                             ).then_inc(s["r1"].sem, 1)

                        def split_on(n, j, r):
                            for m in range(2):
                                dve.wait_ge(*s["mid"].now(n, m + 1))
                                dve.tensor_tensor(parts[j][:, m, 2, :], rest[j][:, m, :], parts[j][:, m, 1, :],
                                                  ALU.subtract).then_inc(s["lo"].sem, 1)
                            dve.wait_ge(*s["v"].now(n, 1))
                            dve.wait_ge(*s["v_stored"][j].last(r, 16))
                            dve.tensor_copy(v1[j][:, :, :, 0:HD], ps_v[:, 0, :].rearrange("p (t h e) -> p t h e", t=UT, h=NH)
                                            ).then_inc(s["vc"].sem, 1)

                        staggered(dve, NU, S, (0, normed), (2, split_on), (1, split))

                    if keep is not None:
                        @block.gpsimd
                        def _(gp):
                            def kept(n, j, r):
                                gp.wait_ge(*fr.nrm.now(n, 1))
                                gp.tensor_copy(keep[:, ds(n * UT, UT), :], nrm[j][:, :, :]).then_inc(s["kept"].sem, 1)

                            staggered(gp, NU, S, (0, kept))

                    @block.tensor
                    def _(pe):
                        def turn(n, j, r):
                            turn_tiles(pe, fr.tps, ps_t[:, 0, :], nrm[j], UT, fr.nrm.now(n, 1), fr.hT.last(n, 1))

                        def project(n, j, r):
                            pe.wait_ge(*fr.hT.now(n, 1))
                            for m in range(2):
                                pe.wait_ge(*s["r1"].last(n, m + 1))
                                pe.matmul(ps_qk[:, m, :], w["qk"][m], hT[j][:, :], start=True, stop=True
                                          ).then_inc(s["pr"].sem, 1)
                            pe.wait_ge(*s["vc"].last(n, 1))
                            for t in range(UT):
                                dst = ps_v[:, 0, t * D:(t + 1) * D]
                                if w["bv"] is not None:
                                    pe.matmul(dst, c("ones", rows=1), w["bv"], start=True, stop=False)
                                ins = pe.matmul(dst, hT[j][:, t * P:(t + 1) * P], w["v"], start=(w["bv"] is None), stop=True)
                            ins.then_inc(s["v"].sem, 1)

                        staggered(pe, NU, S, (1, project), (0, turn))

                    @block.scalar
                    def _(act):
                        def turned(n, j, r):
                            act.wait_ge(*fr.tps.now(n, 1))
                            act.wait_ge(*s["v"].ago(n, 1, S))
                            act.activation(hT[j][:, :], ps_t[:, 0, :], ACT.Copy).then_inc(fr.hT.sem, 1)

                        def first_part(n, j, r):
                            for m in range(2):
                                act.wait_ge(*s["pr"].now(n, m + 1))
                                act.wait_ge(*s["stored"][j].last(r, PARTS))
                                if w["b"][m] is None:
                                    ins = act.activation(parts[j][:, m, 0, :], ps_qk[:, m, :], ACT.Copy)
                                else:
                                    ins = act.activation(parts[j][:, m, 0, :], ps_qk[:, m, :], ACT.Identity, bias=w["b"][m])
                                ins.then_inc(s["hi"].sem, 1)

                        def second_part(n, j, r):
                            for m in range(2):
                                act.wait_ge(*s["r1"].now(n, m + 1))
                                act.activation(parts[j][:, m, 1, :], rest[j][:, m, :], ACT.Copy).then_inc(s["mid"].sem, 1)

                        staggered(act, NU, S, (1, first_part), (0, turned), (1, second_part))

                    @block.sync
                    def _(sp):
                        sp.wait_ge(chained, k_set)

                        def store(n, j, r):
                            sp.wait_ge(*s["lo"].now(n, 2))
                            row = 0
                            for i in range(3):
                                to = [d.rearrange("h e a t -> (h e) a t")[:, row:row + 3 - i, ds(n * U, U)]
                                      for d in (q_stack, k_stack)]
                                sp.dma_start(to[0], parts[j][:, 0, 0:3 - i, :]).then_inc(s["stored"][j].sem, 16)
                                sp.dma_start(to[1], parts[j][:, 1, i:i + 1, :].to_broadcast([P, 3 - i, U])
                                             ).then_inc(s["stored"][j].sem, 16)
                                row += 3 - i
                            sp.wait_ge(*s["vc"].now(n, 1))
                            sp.dma_start(v_ones[ds(n * UT, UT)].rearrange("t p w -> p t w"),
                                         v1[j][:, :, :, :].rearrange("p t h e -> p t (h e)")
                                         ).then_inc(s["v_stored"][j].sem, 16)

                        staggered(sp, NU, S, (0, store))
                        for j in range(S):
                            last = len(range(j, NU, S)) - 1
                            sp.wait_ge(*s["stored"][j].now(last, PARTS))
                            sp.wait_ge(*s["v_stored"][j].now(last, 16))

        HG = 4
        GROUPS = NH // HG
        SLOTS = 4

        def attend(tag, causal, dst, w):
            s = attns[tag]
            n_att = list(attns).index(tag)
            scale = HD ** -0.5
            VW = HD + 1

            def at(name, b, k):
                return s[name].now(b, k)

            with ExitStack() as st:
                sq = [sb(f"{tag}_sq{u}", [64, NH, SEQ], BF16, stack=st) for u in range(SLOTS)]
                sk = [sb(f"{tag}_sk{u}", [64, NH, SEQ], BF16, stack=st) for u in range(SLOTS)]
                vb = [sb(f"{tag}_vb{u}", [P, TPB, NH, VW], stack=st) for u in range(SLOTS)]
                mx = sb(f"{tag}_mx", [P, NH, TPB], stack=st)
                nm = sb(f"{tag}_nm", [P, TPB, NH], stack=st)
                mpart = sb(f"{tag}_mpart", [NH, 3, SEQ], BF16, stack=st)
                mrest = sb(f"{tag}_mrest", [NH, SEQ], stack=st)
                pt = [sb(f"{tag}_pt{n}", [P, HG, TPB, SEQ], stack=st) for n in range(2)]
                sums = [sb(f"{tag}_sums{n}", [P, SEQ], stack=st) for n in range(2)]
                rec = sb(f"{tag}_rec", [P, TPB, HG], stack=st)
                on = sb(f"{tag}_on", [P, TPB, NH, HD], stack=st)
                oT = sb(f"{tag}_oT", [P, SEQ], stack=st)
                if causal:
                    msk = sb(f"{tag}_msk", [P, 3 * P], stack=st)
                    mskb = sb(f"{tag}_mskb", [P, 3 * P], BF16, stack=st)
                ps_1 = bank(f"{tag}_ps_1", st, 2)
                ps_2 = bank(f"{tag}_ps_2", st, 3)
                ps_o = bank(f"{tag}_ps_o", st)
                ps_s = bank(f"{tag}_ps_s", st)
                ps_m = bank(f"{tag}_ps_m", st)

                def run(eng, step):
                    for b in range(-2, 1):
                        step(b, b % SLOTS, b // SLOTS, first=True, turn=b >= -1, body=b >= 0, tail=False)
                    with eng.Fori(0, (NB - 4) // SLOTS) as i:
                        for v in range(1, SLOTS + 1):
                            step(i * SLOTS + v, v % SLOTS, i + v // SLOTS, first=True, turn=True, body=True, tail=True)
                    for b in range(NB - 3, NB + 1):
                        step(b, b % SLOTS, b // SLOTS, first=b + 2 < NB, turn=b + 1 < NB, body=b < NB, tail=True)

                def ahead(u, r, n):
                    return (u + n) % SLOTS, r + (u + n) // SLOTS

                with pool.loop_block(NB) as block:
                    k_set = n_chain[0] + (2 if causal else 1)

                    @block.sync
                    def _(sp):
                        if causal:
                            sp.dma_start(msk[:, :], maskb_in).then_inc(loaded, 16)
                        for u in range(SLOTS):
                            sp.dma_start(sk[u][KR:KM, :, :], ones_rows).then_inc(ones_in[n_att], 16)

                        def load(b, u):
                            cols = ds(b * SEQ, SEQ)
                            up = s["loaded"][u].sem
                            sp.dma_start(sq[u][0:KR, :, :], q_stack.rearrange("h e a t -> (e a) h t")[:, :, cols]
                                         ).then_inc(up, 16)
                            sp.dma_start(sk[u][0:KR, :, :], k_stack.rearrange("h e a t -> (e a) h t")[:, :, cols]
                                         ).then_inc(up, 16)
                            sp.dma_start(vb[u][:, :, :, :].rearrange("p t h e -> p t (h e)"),
                                         v_ones[ds(b * TPB, TPB)].rearrange("t p w -> p t w")).then_inc(up, 16)

                        def step(b, u, r, first, turn, body, tail):
                            if first and tail and not (isinstance(b, int) and b + 3 >= NB):
                                sp.wait_ge(*at("pv", b, 0))
                                load(b + 3, ahead(u, r, 3)[0])
                            if turn:
                                sp.wait_ge(*at("mlo", b + 1, 1))
                                sp.wait_ge(*at("min", b + 1, 0))
                                sp.dma_start(m_parts.rearrange("a h t -> h a t"), mpart[:, :, :]).then_inc(s["mout"].sem, 16)
                                sp.wait_ge(*at("mout", b + 1, 16))
                                sp.dma_start(sq[ahead(u, r, 1)[0]][KR:KM, :, :], m_parts).then_inc(s["min"].sem, 16)

                        for b in range(SLOTS):
                            load(b, b)
                        run(sp, step)

                    @block.vector
                    def _(dve):
                        link(dve, dve.memset(ps_o[:, :, :], 0.0))
                        if causal:
                            dve.wait_ge(loaded, 32)
                            link(dve, dve.tensor_copy(mskb[:, :], msk[:, :]))

                        def maximum(b, h):
                            dve.wait_ge(*at("s1", b, h + 1))
                            if h == 0:
                                dve.wait_ge(*at("nm", b, 0))
                            sv = ps_1[:, h % 2, :].rearrange("p (q k) -> p q k", q=TPB)
                            if causal:
                                dve.tensor_reduce(mx[:, h, 0:1], sv[:, 0, 0:P], AX, ALU.max)
                                dve.tensor_reduce(mx[:, h, 1:2], sv[:, 1, :], AX, ALU.max).then_inc(s["mx"].sem, 1)
                            else:
                                dve.tensor_reduce(mx[:, h, :], sv, AX, ALU.max).then_inc(s["mx"].sem, 1)

                        def norm(b, g):
                            tv = ps_s[:, 0, 0:SEQ].rearrange("p (q j e) -> p q j e", q=TPB, j=HG)
                            dve.wait_ge(*at("tu", b, g + 1))
                            dve.wait_ge(*at("on", b, g))
                            dve.reciprocal(rec[:, :, :], tv[:, :, :, HD]).then_inc(s["rec"].sem, 1)
                            dve.wait_ge(*at("rec", b, g + 1))
                            if g == 0:
                                dve.wait_ge(*at("ot", b, 0))
                            dve.tensor_tensor(on[:, :, HG * g:HG * (g + 1), :], tv[:, :, :, 0:HD],
                                              rec[:, :, :].unsqueeze(3).to_broadcast([P, TPB, HG, HD]), ALU.mult
                                              ).then_inc(s["on"].sem, 1)

                        def step(b, u, r, first, turn, body, tail):
                            for g in range(GROUPS):
                                for j in range(HG):
                                    if j == 2 and g == 1 and turn:
                                        dve.wait_ge(*at("mhi", b + 1, 1))
                                        dve.wait_ge(*at("mlo", b + 1, 0))
                                        dve.tensor_tensor(mrest[:, :], ps_m[0:NH, 0, 0:SEQ], mpart[:, 0, :], ALU.subtract
                                                          ).then_inc(s["mr"].sem, 1)
                                    if j == 2 and g == 3 and tail:
                                        dve.wait_ge(*at("out", b - 1, 1))
                                        xd = dst[:, ds((b - 1) * TPB, TPB), :]
                                        dve.tensor_tensor(xd, xd, ps_m[:, 0, 0:SEQ].rearrange("p (t d) -> p t d", t=TPB),
                                                          ALU.add).then_inc(s["x"].sem, 1)
                                    if j == 3 and g < 2 and tail:
                                        norm(b - 1, g + 2)
                                    if j == 3 and g >= 2 and body:
                                        norm(b, g - 2)
                                    if first:
                                        maximum(b + 2, HG * g + j)
                            if tail:
                                count(dve, dst, (b - 1) * TPB, TPB, *at("x", b - 1, 1))
                            if first:
                                dve.wait_ge(*at("mx", b + 2, NH))
                                dve.wait_ge(*at("mt", b + 2, 0))
                                dve.tensor_scalar(nm[:, :, :].rearrange("p q h -> p h q"), mx[:, :, :], -1.0, None, ALU.mult
                                                  ).then_inc(s["nm"].sem, 1)

                        run(dve, step)

                    @block.gpsimd
                    def _(gp):
                        def step(b, u, r, first, turn, body, tail):
                            if turn:
                                gp.wait_ge(*at("mmid", b + 1, 1))
                                gp.tensor_tensor(mpart[:, 2, :], mrest[:, :], mpart[:, 1, :], ALU.subtract
                                                 ).then_inc(s["mlo"].sem, 1)

                        run(gp, step)

                    @block.tensor
                    def _(pe):
                        pe.wait_ge(chained, k_set)
                        pe.wait_ge(ones_in[n_att], 16 * SLOTS)

                        def max_scores(b, u, r, h):
                            if h == 0:
                                pe.wait_ge(*s["loaded"][u].now(r, 48))
                            pe.wait_ge(*at("mx", b, h - 1))
                            for q in range(TPB):
                                nk = (q + 1) * P if causal else SEQ
                                o = ps_1[:, h % 2, q * SEQ:q * SEQ + nk]
                                ins = pe.matmul(o, sq[u][0:KR, h, q * P:(q + 1) * P], sk[u][0:KR, h, 0:nk],
                                                start=True, stop=not causal)
                                if causal:
                                    ins = pe.matmul(o[:, q * P:nk], mskb[:, 0:P], mskb[:, P:2 * P],
                                                    start=False, stop=True)
                            ins.then_inc(s["s1"].sem, 1)

                        def scores(b, u, h):
                            if h == 0:
                                pe.wait_ge(*at("min", b, 16))
                            pe.wait_ge(*at("ex", b, h - 2 if h else 0))
                            for t in range(TPB):
                                q0 = t * P if causal else 0
                                o = ps_2[:, h % 3, t * SEQ:(t + 1) * SEQ]
                                ins = pe.matmul(o[:, q0:], sk[u][0:KM, h, t * P:(t + 1) * P], sq[u][0:KM, h, q0:],
                                                start=True, stop=not causal)
                                if causal:
                                    ins = pe.matmul(o[:, q0:q0 + P], mskb[:, 0:P], mskb[:, 2 * P:3 * P],
                                                    start=False, stop=True)
                            ins.then_inc(s["s2"].sem, 1)

                        def weigh(b, u, g):
                            pe.wait_ge(*at("ex", b, HG * (g + 1)))
                            pe.wait_ge(*at("ev", b, g))
                            for t in range(TPB):
                                q0 = t * P if causal else 0
                                for j in range(HG):
                                    o = ps_o[32 * j:32 * j + VW, 0, q0:SEQ]
                                    ins = pe.matmul(o, vb[u][:, t, HG * g + j, :], pt[g % 2][:, j, t, q0:], start=(t == 0),
                                                    stop=(t == TPB - 1), skip_group_check=True)
                            ins.then_inc(s["pv"].sem, 1)

                        def turn_sums(b, g):
                            pe.wait_ge(*at("ev", b, g + 1))
                            pe.wait_ge(*at("on", b, g))
                            for q in range(TPB):
                                ins = pe.transpose(ps_s[:, 0, q * P:(q + 1) * P], sums[g % 2][:, q * P:(q + 1) * P], ident)
                            ins.then_inc(s["tu"].sem, 1)

                        def turn_max(b):
                            pe.wait_ge(*at("nm", b, 1))
                            pe.wait_ge(*at("x", b, -2))
                            for q in range(TPB):
                                ins = pe.transpose(ps_m[0:NH, 0, q * P:(q + 1) * P], nm[:, q, :], ident)
                            ins.then_inc(s["mt"].sem, 1)

                        def turn_out(b, mr_wait):
                            pe.wait_ge(*at("on", b, GROUPS))
                            if mr_wait:
                                pe.wait_ge(*at("mr", b + 2, 1))
                            pe.wait_ge(*at("x", b, 0))
                            for q in range(TPB):
                                ins = pe.transpose(ps_m[:, 0, q * P:(q + 1) * P],
                                                   on[:, q, :, :].rearrange("p h e -> p (h e)"), ident)
                            ins.then_inc(s["ot"].sem, 1)

                        def project_out(b):
                            pe.wait_ge(*at("otc", b, 1))
                            for t in range(TPB):
                                o = ps_m[:, 0, t * D:(t + 1) * D]
                                if w["bo"] is not None:
                                    pe.matmul(o, c("ones", rows=1), w["bo"], start=True, stop=False)
                                ins = pe.matmul(o, oT[:, t * P:(t + 1) * P], w["o"], start=(w["bo"] is None), stop=True)
                            ins.then_inc(s["out"].sem, 1)

                        def step(b, u, r, first, turn, body, tail):
                            later = ahead(u, r, 2)
                            for g in range(GROUPS):
                                for j in range(HG):
                                    if body:
                                        scores(b, u, HG * g + j)
                                    if j == 1 and g == 2 and tail:
                                        turn_out(b - 1, turn)
                                    if j == 0 and g == 3 and tail:
                                        project_out(b - 1)
                                    if j == 2:
                                        if g and body:
                                            weigh(b, u, g - 1)
                                        if not g and tail:
                                            weigh(b - 1, (u - 1) % SLOTS, GROUPS - 1)
                                    if j == 3:
                                        if g < 2 and tail:
                                            turn_sums(b - 1, g + 2)
                                        if g == 0 and turn:
                                            turn_max(b + 1)
                                        if g >= 2 and body:
                                            turn_sums(b, g - 2)
                                    if first:
                                        max_scores(b + 2, *later, HG * g + j)

                        run(pe, step)

                    @block.scalar
                    def _(act):
                        def weights(b, h):
                            g, j = h // HG, h % HG
                            act.wait_ge(*at("s2", b, h + 1))
                            act.wait_ge(*at("pv", b, g - 1))
                            sv = ps_2[:, h % 3, :].rearrange("p (t q) -> p t q", t=TPB)
                            to = pt[g % 2][:, j]
                            if causal:
                                act.activation(to[:, 0, :], sv[:, 0, :], ACT.Exp, scale=scale)
                                act.activation(to[:, 1, P:], sv[:, 1, P:], ACT.Exp, scale=scale).then_inc(s["ex"].sem, 1)
                            else:
                                act.activation(to, sv, ACT.Exp, scale=scale).then_inc(s["ex"].sem, 1)

                        def keep_sums(b, g):
                            act.wait_ge(*at("pv", b, g + 1))
                            act.wait_ge(*at("tu", b, g - 1))
                            act.activation(sums[g % 2][:, :], ps_o[:, 0, 0:SEQ], ACT.Copy
                                           ).then_inc(s["ev"].sem, 1)

                        def step(b, u, r, first, turn, body, tail):
                            for g in range(GROUPS):
                                if body:
                                    for j in range(HG - 1):
                                        weights(b, HG * g + j)
                                if g and body:
                                    keep_sums(b, g - 1)
                                if not g and tail:
                                    keep_sums(b - 1, GROUPS - 1)
                                if body:
                                    weights(b, HG * g + HG - 1)
                                if g == 0 and turn:
                                    act.wait_ge(*at("mt", b + 1, 1))
                                    act.wait_ge(*at("mout", b + 1, 0))
                                    act.activation(mpart[:, 0, :], ps_m[0:NH, 0, 0:SEQ], ACT.Copy
                                                   ).then_inc(s["mhi"].sem, 1)
                                if g == 1 and turn:
                                    act.wait_ge(*at("mr", b + 1, 1))
                                    act.activation(mpart[:, 1, :], mrest[:, :], ACT.Copy).then_inc(s["mmid"].sem, 1)
                                if g == 2 and tail:
                                    act.wait_ge(*at("ot", b - 1, 1))
                                    act.wait_ge(*at("out", b - 1, 0))
                                    act.activation(oT[:, :], ps_m[:, 0, 0:SEQ], ACT.Copy).then_inc(s["otc"].sem, 1)

                        run(act, step)

        stats(x_res)
        with ExitStack() as st2:
            w_qkv = sb("w_qkv2", [P, 3, D], stack=st2)
            with ExitStack() as st:
                w_turned = sb("w_turned2", [64, D], stack=st)
                ps_w = bank("w_ps2", st, 4)
                with nc.Block() as block:
                    k0, p0 = n_chain[0], n_pe[0]

                    @block.tensor
                    def _(pe):
                        pe_done(pe.transpose(ps_w[0:64, 0, 0:D], c("wlow"), ident))
                        pe.wait_ge(chained, k0 + 1)
                        pe.matmul(ps_w[:, 1, 0:D], w_turned[0:32, :], c("wuq", rows=32), start=True, stop=True)
                        for n, name in ((1, "wuk"), (2, "wuv")):
                            first = OFF[name][0]
                            ins = pe.matmul(ps_w[:, 1 + n, 0:D], w_turned[32:64, :], pack[32:64, first:first + D],
                                            start=True, stop=True)
                        pe_done(ins)

                    @block.vector
                    def _(dve):
                        dve.wait_ge(peed, p0 + 1)
                        link(dve, dve.tensor_copy(w_turned[:, :], ps_w[0:64, 0, 0:D]))
                        dve.wait_ge(peed, p0 + 2)
                        link(dve, dve.tensor_copy(w_qkv[:, :, :], ps_w[:, 1:4, 0:D]))

            project("p2", x_res, dict(qk=(w_qkv[:, 0, :], w_qkv[:, 1, :]), b=(None, None), v=w_qkv[:, 2, :], bv=None))
        attend("h2", True, x_res, dict(o=c("wo2"), bo=None))

        stats(x_res)
        RA = (E2 + 1) * R2
        with ExitStack() as st2:
            h_all = sb("h_all2", [P, NT * P], stack=st2)
            comb = sb("comb2", [P, NT, E2 + 1], stack=st2)
            lg = sb("lg2", [P, NT, E2], stack=st2)
            route("m2", x_res, c("rout"), c("routb"), E2, lg, h_all)
            with ExitStack() as st:
                s1, s2, ex = (sb(f"m2_sel{j}", [P, NT, E2], stack=st) for j in range(3))
                m1, m2, t1 = (sb(f"m2_t{j}", [P, NT], stack=st) for j in range(3))
                with nc.Block() as block:
                    k0 = n_chain[0]

                    @block.vector
                    def _(dve):
                        link(dve, dve.memset(comb[:, :, :], 1.0))
                        softmax_rows(dve, lg[:, :, :], ex[:, :, :], m1[:, :], t1[:, :], E2)
                        link(dve, dve.tensor_tensor(ex[:, :, :], ex[:, :, :], over_tiles(t1[:, :], E2), ALU.mult))
                        pick(dve, s1[:, :, :], lg[:, :, :], m1[:, :], t1[:, :], E2)
                        link(dve, dve.scalar_tensor_tensor(lg[:, :, :], s1[:, :, :], -BIG, lg[:, :, :], ALU.mult, ALU.add))
                        pick(dve, s2[:, :, :], lg[:, :, :], m2[:, :], t1[:, :], E2)
                        link(dve, dve.tensor_tensor(s1[:, :, :], s1[:, :, :], s2[:, :, :], ALU.add))
                        link(dve, dve.tensor_tensor(s1[:, :, :], s1[:, :, :], ex[:, :, :], ALU.mult))
                        link(dve, dve.tensor_reduce(t1[:, :], s1[:, :, :], AX, ALU.add))
                        link(dve, dve.tensor_scalar(t1[:, :], t1[:, :], 1e-6, None, ALU.add))
                        link(dve, dve.reciprocal(t1[:, :], t1[:, :]))
                        link(dve, dve.tensor_tensor(comb[:, :, 0:E2], s1[:, :, :], over_tiles(t1[:, :], E2), ALU.mult))

                    @block.scalar
                    def _(act):
                        act.wait_ge(chained, k0 + 3)
                        act.activation(ex[:, :, :], ex[:, :, :], ACT.Exp).then_inc(acted, 1)

            with ExitStack() as st:
                S = 3
                hT = [sb(f"m_hT{j}", [P, U], stack=st) for j in range(S)]
                hw = [sb(f"m_hw{j}", [P, UT, RA + 1], stack=st) for j in range(S)]
                hwT = [sb(f"m_hwT{j}", [RA + 1, U], stack=st) for j in range(S)]
                ps_a = bank("m_ps_a", st, S)
                ps_t = bank("m_ps_t", st)
                ps_o = bank("m_ps_o", st, S)
                with pool.loop_block(NU) as block:
                    k_set = n_chain[0] + S

                    @block.vector
                    def _(dve):
                        for j in range(S):
                            link(dve, dve.memset(hw[j][:, :, :], 1.0))

                        def combined(n, j, r):
                            dve.wait_ge(*m_h.now(n, 1))
                            dve.wait_ge(*m_tr.ago(n, 1, S))
                            for t in range(UT):
                                cw = comb[:, ds(n * UT + t, 1), :].rearrange("p o e -> p (o e)")
                                ins = dve.tensor_tensor(
                                    hw[j][:, t, 0:RA].rearrange("p (e r) -> p e r", r=R2),
                                    ps_a[:, j, t * P:t * P + RA].rearrange("p (e r) -> p e r", r=R2),
                                    cw.unsqueeze(2).to_broadcast([P, E2 + 1, R2]), ALU.mult)
                            ins.then_inc(m_ts.sem, 1)

                        def added(n, j, r):
                            xs = x_res[:, ds(n * UT, UT), :]
                            dve.wait_ge(*m_o.now(n, 1))
                            dve.tensor_tensor(xs, xs, ps_o[:, j, :].rearrange("p (t d) -> p t d", t=UT), ALU.add
                                              ).then_inc(m_x.sem, 1)
                            count(dve, x_res, n * UT, UT, *m_x.now(n, 1))

                        staggered(dve, NU, S, (0, combined), (2, added))

                    @block.tensor
                    def _(pe):
                        pe.wait_ge(chained, k_set)

                        def reduce(n, j, r):
                            pe.wait_ge(*m_c.now(n, 1))
                            pe.wait_ge(*m_ts.ago(n, 1, S))
                            for t in range(UT):
                                ins = pe.matmul(ps_a[:, j, t * P:t * P + RA], hT[j][:, t * P:(t + 1) * P], c("acat"),
                                                start=True, stop=True)
                            ins.then_inc(m_h.sem, 1)

                        def turn(n, j, r):
                            pe.wait_ge(*m_ts.now(n, 1))
                            pe.wait_ge(*m_tc.last(n, 1))
                            for t in range(UT):
                                ins = pe.transpose(ps_t[0:RA + 1, 0, t * P:(t + 1) * P], hw[j][:, t, :], ident)
                            ins.then_inc(m_tr.sem, 1)

                        def expand(n, j, r):
                            pe.wait_ge(*m_tc.now(n, 1))
                            pe.wait_ge(*m_x.ago(n, 1, S))
                            for t in range(UT):
                                o = ps_o[:, j, t * D:(t + 1) * D]
                                pe.matmul(o, hT[j][:, t * P:(t + 1) * P], c("basew"), start=True, stop=False)
                                ins = pe.matmul(o, hwT[j][:, t * P:(t + 1) * P], c("bcat", rows=RA + 1),
                                                start=False, stop=True)
                            ins.then_inc(m_o.sem, 1)

                        staggered(pe, NU, S, (0, reduce), (1, turn), (2, expand))

                    @block.scalar
                    def _(act):
                        def keep(n, j, r):
                            act.wait_ge(*m_o.ago(n, 1, S))
                            act.activation(hT[j][:, :], h_all[:, ds(n * U, U)], ACT.Copy).then_inc(m_c.sem, 1)

                        def turned(n, j, r):
                            act.wait_ge(*m_tr.now(n, 1))
                            act.wait_ge(*m_o.ago(n, 1, S))
                            act.activation(hwT[j][:, :], ps_t[0:RA + 1, 0, :], ACT.Copy).then_inc(m_tc.sem, 1)

                        staggered(act, NU, S, (0, keep), (1, turned))

        stats(x_res)
        with ExitStack() as st:
            S = 3
            nrm = sb("s_nrm", [P, UT, P], stack=st)
            hT = [sb(f"s_hT{j}", [P, 2, SEQ + 1], stack=st) for j in range(S)]
            mixed = [sb(f"s_mix{j}", [P, 2, SEQ], stack=st) for j in range(S)]
            rel = [sb(f"s_rel{j}", [P, 2, SEQ], stack=st) for j in range(S)]
            state = [sb(f"s_state{j}", [P, 2, SEQ], stack=st) for j in range(S)]
            dec = sb("s_dec", [P, SEQ], stack=st)
            omix = sb("s_omix", [P, 1], stack=st)
            ps_t = bank("s_ps_t", st)
            ps_h = bank("s_ps_h", st)
            ps_o = bank("s_ps_o", st, S)
            with pool.loop_block(NU) as block:
                k_set = n_chain[0] + 3 + S

                @block.vector
                def _(dve):
                    for j in range(S):
                        link(dve, dve.memset(hT[j][:, :, :], 0.0))
                    link(dve, dve.memset(dec[:, :], 1.0))
                    link(dve, dve.tensor_scalar(dec[:, :], dec[:, :], c("decay"), None, ALU.mult))
                    link(dve, dve.tensor_scalar(omix[:, :], c("mix"), -1.0, 1.0, ALU.mult, ALU.add))

                    def normed(n, j, r):
                        norm_tiles(dve, fr_s.nrm, nrm, x_res, n * UT, UT, rstd, fr_s.tps.last(n, 1))

                    def mix(n, j, r):
                        dve.wait_ge(*fr_s.hT.now(n, 1))
                        dve.wait_ge(*s_pr.ago(n, 1, S))
                        dve.tensor_scalar(mixed[j][:, :, :], hT[j][:, :, 0:SEQ], omix[:, :], None, ALU.mult
                                          ).then_inc(s_in0.sem, 1)
                        dve.wait_ge(*s_in0.now(n, 1))
                        dve.scalar_tensor_tensor(mixed[j][:, :, :], hT[j][:, :, 1:], c("mix"), mixed[j][:, :, :],
                                                 ALU.mult, ALU.add).then_inc(s_in.sem, 1)

                    def scan(n, j, r):
                        dve.wait_ge(*s_re.now(n, 1))
                        dve.wait_ge(*s_o.ago(n, 1, S))
                        for b in range(2):
                            dve.tensor_tensor_scan(state[j][:, b, :], dec[:, :], rel[j][:, b, :], 0.0,
                                                   ALU.mult, ALU.add).then_inc(s_sc.sem, 1)

                    def added(n, j, r):
                        xs = x_res[:, ds(n * UT, UT), :]
                        dve.wait_ge(*s_o.now(n, 1))
                        dve.tensor_tensor(xs, xs, ps_o[:, j, :].rearrange("p (t d) -> p t d", t=UT), ALU.add
                                          ).then_inc(s_x.sem, 1)
                        count(dve, x_res, n * UT, UT, *s_x.now(n, 1))

                    staggered(dve, NU, S, (0, normed), (4, added), (2, scan), (1, mix))

                @block.tensor
                def _(pe):
                    def turn(n, j, r):
                        turn_tiles(pe, fr_s.tps, ps_t[:, 0, :], nrm, UT, fr_s.nrm.now(n, 1), fr_s.hT.last(n, 1))

                    def project(n, j, r):
                        pe.wait_ge(*s_in.now(n, 1))
                        pe.wait_ge(*s_re.last(n, 1))
                        pe.matmul(ps_h[:, 0, :], c("win3"), mixed[j][:, :, :].rearrange("p b t -> p (b t)"),
                                  start=True, stop=True).then_inc(s_pr.sem, 1)

                    def project_out(n, j, r):
                        pe.wait_ge(*s_sc.now(n, 2))
                        pe.wait_ge(*s_x.ago(n, 1, S))
                        for t in range(UT):
                            o = ps_o[:, j, t * D:(t + 1) * D]
                            pe.matmul(o, c("ones", rows=1), c("bout3", rows=1), start=True, stop=False)
                            ins = pe.matmul(o, state[j][:, t // TPB, (t % TPB) * P:(t % TPB + 1) * P], c("wout3"),
                                            start=False, stop=True)
                        ins.then_inc(s_o.sem, 1)

                    staggered(pe, NU, S, (2, project), (0, turn), (3, project_out))

                @block.scalar
                def _(act):
                    act.wait_ge(chained, k_set)

                    def turned(n, j, r):
                        act.wait_ge(*fr_s.tps.now(n, 1))
                        act.wait_ge(*s_in.ago(n, 1, S))
                        act.activation(hT[j][:, :, 1:], ps_t[:, 0, :].rearrange("p (b t) -> p b t", b=2), ACT.Copy
                                       ).then_inc(fr_s.hT.sem, 1)

                    def positive(n, j, r):
                        act.wait_ge(*s_pr.now(n, 1))
                        act.wait_ge(*s_sc.ago(n, 2, S))
                        act.activation(rel[j][:, :, :], ps_h[:, 0, :].rearrange("p (b t) -> p b t", b=2), ACT.Relu,
                                       bias=c("bin3")).then_inc(s_re.sem, 1)

                    staggered(act, NU, S, (2, positive), (0, turned))

        stats(x_res)
        with ExitStack() as st3:
            x2 = sb("x2", [P, NT, D], stack=st3)
            project("p3", x_res, dict(qk=(c("wq3"), c("wk3")), b=(c("bq3"), c("bk3")), v=c("wv3"),
                                      bv=c("bv3", rows=1)), keep=x2)
            attend("h3", False, x2, dict(o=c("wo3"), bo=c("bo3", rows=1)))
            stats(x2)
            with ExitStack() as st:
                chosen = sb("chosen3", [P, NT, E3], stack=st)
                gp = sb("m3_gp", [P, NT], stack=st)
                lg = sb("lg3", [P, NT, G3 + E3], stack=st)
                w = sb("w3", [P, E3, wide(F3)], stack=st)
                route("m3", x2, c("rt3"), c("rt3b"), G3 + E3, lg, None, (c("g1"), c("b1")), fetch=(w, w3_in))
                with ExitStack() as stm:
                    sel, ex = (sb(f"m3_g{j}", [P, NT, G3], stack=stm) for j in range(2))
                    el = sb("m3_el", [P, NT, 2], stack=stm)
                    tmp = sb("m3_tmp", [P, NT, 2], stack=stm)
                    sel2 = sb("m3_sel2", [P, NT, 2], stack=stm)
                    m1, t1 = (sb(f"m3_t{j}", [P, NT], stack=stm) for j in range(2))
                    with nc.Block() as block:
                        k0 = n_chain[0]

                        @block.vector
                        def _(dve):
                            softmax_rows(dve, lg[:, :, 0:G3], ex[:, :, :], m1[:, :], gp[:, :], G3)
                            pick(dve, sel[:, :, :], lg[:, :, 0:G3], m1[:, :], t1[:, :], G3)
                            for g in range(G3):
                                eg = lg[:, :, G3 + 2 * g:G3 + 2 * g + 2]
                                sg = over_tiles(sel[:, :, g], 2)
                                link(dve, dve.tensor_tensor(el[:, :, :] if g == 0 else tmp[:, :, :], eg, sg, ALU.mult))
                                if g:
                                    link(dve, dve.tensor_tensor(el[:, :, :], el[:, :, :], tmp[:, :, :], ALU.add))
                            softmax_rows(dve, el[:, :, :], tmp[:, :, :], m1[:, :], t1[:, :], 2)
                            link(dve, dve.tensor_tensor(gp[:, :], gp[:, :], t1[:, :], ALU.mult))
                            pick(dve, sel2[:, :, :], el[:, :, :], m1[:, :], t1[:, :], 2)
                            for g in range(G3):
                                link(dve, dve.tensor_tensor(chosen[:, :, 2 * g:2 * g + 2], sel2[:, :, :],
                                                            over_tiles(sel[:, :, g], 2), ALU.mult))

                        @block.scalar
                        def _(act):
                            act.wait_ge(chained, k0 + 2)
                            act.activation(ex[:, :, :], ex[:, :, :], ACT.Exp).then_inc(acted, 1)
                            act.wait_ge(chained, k0 + 2 + 2 + 5 + 7 + 2)
                            act.activation(tmp[:, :, :], tmp[:, :, :], ACT.Exp).then_inc(acted, 1)
                sorted_experts("e3", (chosen[:, :, :],), (gp[:, :],), x2, xs3, w, w3_in, F3, ACT.Relu)
            collect("e3", 1, x2)

            stats(x2)
            with ExitStack() as st:
                S = 6
                fin = [sb(f"z_fin{j}", [P, UT, D], stack=st) for j in range(S)]
                sink = sb("z_sink", [P, NT], stack=st)
                out_t = out.rearrange("(t p) d -> p t d", p=P)
                with pool.loop_block(NU) as block:
                    k_sink = n_chain[0] + 1

                    @block.gpsimd
                    def _(gp):
                        def shift(n, j, r):
                            xs = x_res[:, ds(n * UT, UT), :]
                            gp.tensor_tensor(xs, xs, c("b2").unsqueeze(1).to_broadcast([P, UT, D]), ALU.add).then_inc(z_s.sem, 1)

                        staggered(gp, NU, S, (0, shift))

                    @block.vector
                    def _(dve):
                        link(dve, dve.scalar_tensor_tensor(sink[:, :], mean[:, :], -1.0, rstd[:, :], ALU.mult, ALU.mult))

                        def finish(n, j, r):
                            dve.wait_ge(*z_n.now(n, 1))
                            dve.tensor_tensor(fin[j][:, :, :], fin[j][:, :, :], c("g2").unsqueeze(1).to_broadcast([P, UT, D]),
                                              ALU.mult).then_inc(z_g.sem, 1)

                        def add(n, j, r):
                            dve.wait_ge(*z_g.now(n, 1))
                            dve.wait_ge(*z_s.now(n, 1))
                            dve.tensor_tensor(fin[j][:, :, :], fin[j][:, :, :], x_res[:, ds(n * UT, UT), :], ALU.add
                                              ).then_inc(z_a.sem, 1)

                        staggered(dve, NU, S, (0, finish), (1, add))

                    @block.scalar
                    def _(act):
                        act.wait_ge(chained, k_sink)

                        def normed(n, j, r):
                            act.wait_ge(*z_d[j].last(r, 16))
                            for t in range(UT):
                                tile = ds(n * UT + t, 1)
                                ins = act.activation(fin[j][:, t, :], x2[:, tile, :].rearrange("p o d -> p (o d)"), ACT.Identity,
                                                     scale=rstd[:, tile], bias=sink[:, tile])
                            ins.then_inc(z_n.sem, 1)

                        staggered(act, NU, S, (0, normed))

                    @block.sync
                    def _(sp):
                        def store(n, j, r):
                            sp.wait_ge(*z_a.now(n, 1))
                            sp.dma_start(out_t[:, ds(n * UT, UT), :], fin[j][:, :, :]).then_inc(z_d[j].sem, 16)

                        staggered(sp, NU, S, (0, store))
                        for j in range(S):
                            sp.wait_ge(*z_d[j].now(len(range(j, NU, S)) - 1, 16))


def kernel(**inputs):
    import numpy as np
    import concourse.bacc as bacc
    from concourse.bass_utils import run_bass_kernel_spmd

    a = {k: np.ascontiguousarray(v) for k, v in inputs.items()}
    f32 = np.float32
    parts = {}

    def put(name, arr):
        parts[name] = arr if arr.ndim == 2 else arr[:, None]

    def blocks(arr):
        n = arr.shape[0] // P
        return arr.reshape(n, P, -1).transpose(1, 0, 2).reshape(P, -1)

    def row(arr):
        return arr.reshape(1, -1)

    def every(arr):
        return np.broadcast_to(arr.reshape(1, -1), (P, arr.size))

    def lower(arr):
        return np.concatenate([np.zeros((32, arr.shape[1]), f32), arr], 0)

    put("ident", np.eye(P, dtype=f32))
    put("ones", np.ones((P, P), f32))
    tri = np.triu(np.ones((P, P), f32))
    put("tri_st", np.concatenate([tri, np.ones((P, P), f32), tri], 1))
    put("iota", np.broadcast_to(np.arange(1, CAP + 1, dtype=f32), (P, CAP)))
    put("tvec", np.broadcast_to(np.arange(SEQ, dtype=f32), (P, SEQ)))
    put("rank", np.broadcast_to(np.arange(8, 0, -1, dtype=f32), (P, 8)))
    put("token", np.arange(tiles_of(2) * P, dtype=f32).reshape(-1, P).T)
    A = "L0_attn_"
    put("gam0", a[A + "norm_gamma"]); put("bet0", a[A + "norm_beta"])
    put("inw", a[A + "in_w"]); put("inb", blocks(a[A + "in_b"]))
    put("cw", blocks(a[A + "conv_w"].reshape(INNER, 3))); put("cbias", blocks(a[A + "conv_b"]))
    put("alog", blocks(a[A + "A_log"])); put("bp", blocks(a[A + "B_p"])); put("cp", blocks(a[A + "C_p"]))
    put("dp", blocks(a[A + "D_p"])); put("outw", blocks(a[A + "out_w"])); put("outb", row(a[A + "out_b"]))
    A = "L0_ffn_"
    put("gate0", a[A + "gate_w"].T); put("wsg", a[A + "Ws_g"].T); put("wsu", a[A + "Ws_u"].T)
    put("wsd", blocks(np.ascontiguousarray(a[A + "Ws_d"].T)))
    A = "L1_attn_"
    put("lng1", a[A + "ln_g"]); put("lnb1", a[A + "ln_b"]); put("qkvw", a[A + "qkv_w"])
    put("qkvb", blocks(a[A + "qkv_b"])); put("vb", row(a[A + "qkv_b"][2 * D:]))
    put("gw1", a[A + "gate_w"]); put("gb1", a[A + "gate_b"])
    A = "L1_ffn_"
    put("gate1", a[A + "gate_w"]); put("gate1b", every(a[A + "gate_b"]))
    A = "L2_attn_"
    put("wlow", np.concatenate([a[A + "W_dq"], a[A + "W_dkv"]], 1))
    put("wuq", a[A + "W_uq"]); put("wuk", lower(a[A + "W_uk"])); put("wuv", lower(a[A + "W_uv"]))
    put("wo2", a[A + "W_o"])
    A = "L2_ffn_"
    put("basew", a[A + "base_W"].T)
    put("acat", np.concatenate([a[A + "routed_A"].reshape(E2 * R2, D), a[A + "shared_A"]], 0).T)
    put("bcat", np.concatenate([a[A + "routed_B"].transpose(0, 2, 1).reshape(E2 * R2, D), a[A + "shared_B"].T,
                               row(a[A + "base_b"])], 0))
    put("rout", a[A + "router_W"].T); put("routb", every(a[A + "router_b"]))
    A = "L3_attn_"
    put("win3", a[A + "W_in"].T); put("bin3", a[A + "b_in"]); put("wout3", a[A + "W_out"].T)
    put("bout3", row(a[A + "b_out"])); put("decay", every(a[A + "decay"])); put("mix", every(a[A + "mix"]))
    A = "L3_ffn_"
    w, b = a[A + "in_proj_w"], a[A + "in_proj_b"]
    put("wq3", w[:D].T); put("wk3", w[D:2 * D].T); put("wv3", w[2 * D:].T)
    put("bq3", b[:D]); put("bk3", b[D:2 * D])
    put("bv3", row(b[2 * D:])); put("wo3", a[A + "out_proj_w"].T); put("bo3", row(a[A + "out_proj_b"]))
    for n, s in (("g1", "ln1_g"), ("b1", "ln1_b"), ("g2", "ln2_g"), ("b2", "ln2_b")):
        put(n, every(a[A + s]))
    put("rt3", np.concatenate([a[A + "w_group"], a[A + "w_expert"].transpose(1, 0, 2).reshape(D, E3)], 1))
    put("rt3b", every(np.concatenate([a[A + "b_group"], a[A + "b_expert"].reshape(-1)])))
    pack = np.zeros((P, NPACK), f32)
    for name, (o, n) in OFF.items():
        m = parts[name]
        assert m.shape[1] == n, (name, m.shape, n)
        pack[:m.shape[0], o:o + n] = m

    def down(w, f):
        return w.reshape(w.shape[0], f // P, P, D).transpose(0, 2, 1, 3).reshape(w.shape[0], P, -1)

    A = "L0_ffn_"
    w0 = np.concatenate([a[A + "Wg"].transpose(0, 2, 1), a[A + "Wu"].transpose(0, 2, 1),
                         down(np.ascontiguousarray(a[A + "Wd"].transpose(0, 2, 1)), F0)], 2)

    def expert(wa, wb, ba, bb, f):
        e = wa.shape[0]
        o = np.zeros((e, P, 2 * f + f // P + D), f32)
        o[:, :, :f] = wa
        o[:, :, f:2 * f] = down(wb, f)
        o[:, :, 2 * f:2 * f + f // P] = ba.reshape(e, f // P, P).transpose(0, 2, 1)
        o[:, :, 2 * f + f // P:] = bb[:, None, :]
        return o

    A = "L1_ffn_"
    w1 = expert(np.concatenate([a[A + "w1"], a[A + "ws1"][None]]), np.concatenate([a[A + "w2"], a[A + "ws2"][None]]),
                np.concatenate([a[A + "b1"], a[A + "bs1"][None]]), np.concatenate([a[A + "b2"], a[A + "bs2"][None]]), F1)
    A = "L3_ffn_"
    w3 = expert(a[A + "w1"], a[A + "w2"], a[A + "b1"], a[A + "b2"], F3)
    mask = np.where(np.arange(P)[None, :] <= np.arange(P)[:, None], 0.0, -BIG).astype(f32)
    masks = np.concatenate([np.eye(P, dtype=f32), mask, mask.T], 1)

    nc = bacc.Bacc("TRN2", target_bir_lowering=False, num_devices=1)
    arrays = {"x": a["L0_attn_x"].reshape(NB * SEQ, D), "pack": pack, "masks": masks,
              "w0": np.ascontiguousarray(w0), "w1": w1, "w3": w3}
    aps = [nc.dram_tensor("in_" + n, v.shape, F32, kind="ExternalInput").ap() for n, v in arrays.items()]
    out = nc.dram_tensor("out", (NB * SEQ, D), F32, kind="ExternalOutput").ap()
    ktab = nc.dram_tensor("ktab", (INNER, P + SEQ), F32).ap()
    ychan = nc.dram_tensor("ychan", (INNER, NB, SEQ), F32).ap()
    q_stack, k_stack = (nc.dram_tensor(n, (NH, HD, 6, NB * SEQ), BF16).ap() for n in ("q_stack", "k_stack"))
    ones_rows = nc.dram_tensor("ones_rows", (3, NH, SEQ), BF16).ap()
    v_ones = nc.dram_tensor("v_ones", (NT, P, NH * (HD + 1)), F32).ap()
    m_parts = nc.dram_tensor("m_parts", (3, NH, SEQ), BF16).ap()
    xs1, xs3 = (nc.dram_tensor(f"sorted_rows{n}", (tiles_of(n) * P, D + 2), F32).ap() for n in (2, 1))
    ys = nc.dram_tensor("results", (2 * NB * SEQ + tiles_of(2) * P, D), F32).ap()
    build(nc, *aps, out, ktab, ychan, q_stack, k_stack, ones_rows, v_ones, m_parts, xs1, xs3, ys)
    r = run_bass_kernel_spmd(nc, [{"in_" + n: v for n, v in arrays.items()}], core_ids=[0])
    return r.results[0]["out"].reshape(NB, SEQ, D)
```
